# Optimizing a Trainium2 kernel written in Bass

```python
import numpy as np
import jax
import jax.numpy as jnp

def _softmax(x, axis=-1):
    return jax.nn.softmax(x, axis=axis)

def _gelu(x):
    return jax.nn.gelu(x, approximate=True)

def _silu(x):
    return jax.nn.silu(x)

def _sigmoid(x):
    return jax.nn.sigmoid(x)

def _layernorm(x, axis=-1, eps=1e-05):
    m = jnp.mean(x, axis=axis, keepdims=True)
    v = jnp.var(x, axis=axis, keepdims=True)
    return (x - m) / jnp.sqrt(v + eps)

def _scatter_add(tgt, idx, src, axis=0):
    return tgt.at[idx].add(src)

def _segment_sum(src, seg, n):
    return jax.ops.segment_sum(src, seg, n)
kernel_name = 'mk_perceiver_d2_seqx_r4_fb6885'

def setup_inputs(seed: int=0):
    np.random.seed(seed)
    _w = jnp.asarray

    def _rec_inputs():
        import jax
        import jax.numpy as jnp
        _rk = jax.random.key(seed)
        x = -0.0005146 + 1 * jax.random.normal(jax.random.fold_in(_rk, 1), (64, 32, 256), jnp.float32)
        _lenS = 32 - jax.random.randint(jax.random.fold_in(_rk, 7), (64,), 0, max(1, 32 // 4) + 1, jnp.int32)
        _lenS2 = 257 - jax.random.randint(jax.random.fold_in(_rk, 8), (64,), 0, max(1, 257 // 4) + 1, jnp.int32)
        _ctx_768P = jax.random.normal(jax.random.fold_in(_rk, 11), (64, 16, 192), jnp.float32)
        _ctx_768c = jax.random.dirichlet(jax.random.fold_in(_rk, 511), 0.3 * jnp.ones((16,), jnp.float32), (64, 257))
        _ctx_768t = jnp.einsum('bsk,bkd->bsd', _ctx_768c, _ctx_768P)
        _ctx_768t = _ctx_768t * jax.lax.rsqrt(jnp.mean(jnp.square(_ctx_768t)) + 1e-12) * 0.953939
        ctx_768 = -0.00040386 + 0.999972 * (_ctx_768t + 0.3 * jax.random.normal(jax.random.fold_in(_rk, 611), (64, 257, 192), jnp.float32))
        _validS = jnp.arange(32)[None, :] < _lenS[:, None]
        _validS2 = jnp.arange(257)[None, :] < _lenS2[:, None]
        _causal = jnp.tril(jnp.ones((32, 32), dtype=bool))
        mask_BxS2_bk0 = jnp.logical_not(jnp.broadcast_to(_validS2[:, :], (64, 257)))
        return (x, ctx_768, mask_BxS2_bk0)
    x, ctx_768, mask_BxS2_bk0 = _rec_inputs()

    def _L0_xattn_setup():
        import jax, jax.numpy as jnp
        import numpy as np
        DIM_IN, DIM_LAT, DIM_HEAD = (192, 256, 64)
        INNER = max(DIM_LAT, DIM_IN)
        HEADS = INNER // DIM_HEAD
        SCALE = DIM_HEAD ** (-0.5)
        RMS_EPS = 1e-08
        LN_EPS = 1e-05

        def layernorm(x, g, b):
            mu = jnp.mean(x, axis=-1, keepdims=True)
            var = jnp.mean((x - mu) ** 2, axis=-1, keepdims=True)
            return (x - mu) * jax.lax.rsqrt(var + LN_EPS) * g + b

        def rmsnorm(x, gamma):
            norm = jnp.sqrt(jnp.sum(x * x, axis=-1, keepdims=True)) * x.shape[-1] ** (-0.5)
            return x / jnp.maximum(norm, RMS_EPS) * gamma
        key = jax.random.key(seed)
        ks = jax.random.split(key, 12)
        b, n, m = (4, 1024, 128)
        x = jax.random.normal(ks[0], (b, n, DIM_IN), jnp.float32)
        latents = jax.random.normal(ks[1], (b, m, DIM_LAT), jnp.float32)
        mask = jax.random.randint(ks[2], (b, n), 0, 2).astype(bool)
        s = lambda k, sh, fan: jax.random.normal(k, sh, jnp.float32) * fan ** (-0.5)
        return {'x': x, 'latents': latents, 'mask': mask, 'ln_x_g': jnp.ones((DIM_IN,), jnp.float32), 'ln_x_b': jnp.zeros((DIM_IN,), jnp.float32), 'ln_l_g': jnp.ones((DIM_LAT,), jnp.float32), 'ln_l_b': jnp.zeros((DIM_LAT,), jnp.float32), 'qn_g': jnp.ones((DIM_HEAD,), jnp.float32), 'kn_g': jnp.ones((DIM_HEAD,), jnp.float32), 'Wq': s(ks[3], (INNER, DIM_LAT), DIM_LAT), 'Wkv': s(ks[4], (2 * INNER, DIM_IN), DIM_IN), 'Wlkv': s(ks[5], (2 * INNER, DIM_LAT), DIM_LAT), 'Wo': s(ks[6], (DIM_LAT, INNER), INNER), 'bo': jnp.zeros((DIM_LAT,), jnp.float32)}
    _L0_xattn_all = _L0_xattn_setup()
    _L0_xattn_in = {k: v for k, v in _L0_xattn_all.items() if k in ('ln_x_g', 'ln_x_b', 'ln_l_g', 'ln_l_b', 'qn_g', 'kn_g', 'Wq', 'Wkv', 'Wlkv', 'Wo', 'bo')}
    del _L0_xattn_all

    def _L0_attn_setup():
        import jax, jax.numpy as jnp
        import numpy as np
        HEADS, DK, DV = (16, 16, 64)
        EPS = 1e-12

        def l2norm(t):
            n = jnp.linalg.norm(t, axis=-1, keepdims=True)
            return t / jnp.maximum(n, EPS)

        def tanh_norm(t):
            n = jnp.linalg.norm(t, axis=-1, keepdims=True)
            return jnp.tanh(n) * (t / jnp.maximum(n, EPS))

        def split_heads(x, h):
            b, n, hd = x.shape
            return x.reshape(b, n, h, hd // h).transpose(0, 2, 1, 3)
        key = jax.random.key(seed)
        k1, k2, k3, k4 = jax.random.split(key, 4)
        b, n, dim = (2, 512, 256)
        tokens = jax.random.normal(k1, (b, n, dim), dtype=jnp.float32)
        Wq = jax.random.normal(k2, (dim, DK * HEADS), dtype=jnp.float32) * 0.02
        Wkv = jax.random.normal(k3, (dim, (DK + DV) * HEADS), dtype=jnp.float32) * 0.02
        Wout = jax.random.normal(k4, (DV * HEADS, dim), dtype=jnp.float32) * 0.02
        return {'tokens': tokens, 'Wq': Wq, 'Wkv': Wkv, 'Wout': Wout}
    _L0_attn_all = _L0_attn_setup()
    _L0_attn_in = {k: v for k, v in _L0_attn_all.items() if k in ('Wq', 'Wkv', 'Wout')}
    del _L0_attn_all

    def _L0_ffn_setup():
        import jax, jax.numpy as jnp
        import numpy as np
        H = 8
        KD = 128
        TOPK = 8
        NUM_KEYS = 64
        N_EXPERTS = NUM_KEYS * NUM_KEYS
        N_DIM = 256
        BN_EPS = 1e-05

        def gelu_new(x):
            c = jnp.sqrt(jnp.asarray(2.0 / jnp.pi, x.dtype))
            return 0.5 * x * (1.0 + jnp.tanh(c * (x + 0.044715 * x * x * x)))
        key = jax.random.key(seed)
        ks = jax.random.split(key, 5)
        b, s = (2, 256)
        x = jax.random.normal(ks[0], (b, s, N_DIM), dtype=jnp.float32)
        w_q = jax.random.normal(ks[1], (N_DIM, 2 * H * KD), dtype=jnp.float32) * 0.02
        bn_gamma = jnp.ones((2 * H * KD,), dtype=jnp.float32)
        bn_beta = jnp.zeros((2 * H * KD,), dtype=jnp.float32)
        keys = jax.random.normal(ks[2], (H, NUM_KEYS, 2, KD), dtype=jnp.float32) * 0.02
        down_embed = jax.random.normal(ks[3], (N_EXPERTS, N_DIM), dtype=jnp.float32) * 0.02
        up_embed = jax.random.normal(ks[4], (N_EXPERTS, N_DIM), dtype=jnp.float32) * 0.02
        return {'x': x, 'w_q': w_q, 'bn_gamma': bn_gamma, 'bn_beta': bn_beta, 'keys': keys, 'down_embed': down_embed, 'up_embed': up_embed}
    _L0_ffn_all = _L0_ffn_setup()
    _L0_ffn_in = {k: v for k, v in _L0_ffn_all.items() if k in ('w_q', 'bn_gamma', 'bn_beta', 'keys', 'down_embed', 'up_embed')}
    del _L0_ffn_all

    def _L1_xattn_setup():
        import jax, jax.numpy as jnp
        import numpy as np
        NUM_HEADS = 16
        CLAMP = 10000.0
        key = jax.random.key(seed)
        ks = jax.random.split(key, 8)
        B, Nq, Nkv, Cq, Ckv = (4, 512, 512, 256, 192)
        s_q = 1.0 / np.sqrt(Cq)
        s_kv = 1.0 / np.sqrt(Ckv)
        return {'query': jax.random.normal(ks[0], (B, Nq, Cq), jnp.float32), 'key_value': jax.random.normal(ks[1], (B, Nkv, Ckv), jnp.float32), 'Wq': jax.random.normal(ks[2], (Cq, Cq), jnp.float32) * s_q, 'bq': jnp.zeros((Cq,), jnp.float32), 'Wk': jax.random.normal(ks[3], (Ckv, Cq), jnp.float32) * s_kv, 'bk': jnp.zeros((Cq,), jnp.float32), 'Wv': jax.random.normal(ks[4], (Ckv, Cq), jnp.float32) * s_kv, 'bv': jnp.zeros((Cq,), jnp.float32), 'Wo': jax.random.normal(ks[5], (Cq, Cq), jnp.float32) * s_q, 'bo': jnp.zeros((Cq,), jnp.float32)}
    _L1_xattn_all = _L1_xattn_setup()
    _L1_xattn_in = {k: v for k, v in _L1_xattn_all.items() if k in ('Wq', 'bq', 'Wk', 'bk', 'Wv', 'bv', 'Wo', 'bo')}
    del _L1_xattn_all

    def _L1_attn_setup():
        import jax, jax.numpy as jnp
        import numpy as np
        D_MODEL = 256
        D_STATE = 16
        EXPAND = 2
        D_INNER = EXPAND * D_MODEL
        DT_RANK = 64
        D_CONV = 4

        def _silu(v):
            return v * jax.nn.sigmoid(v)
        key = jax.random.key(seed)
        ks = jax.random.split(key, 8)
        s = 0.02
        x = jax.random.normal(ks[0], (2, 512, D_MODEL), dtype=jnp.float32)
        W_in = jax.random.normal(ks[1], (D_MODEL, 2 * D_INNER), dtype=jnp.float32) * s
        W_conv = jax.random.normal(ks[2], (D_CONV, D_INNER), dtype=jnp.float32) * s
        b_conv = jnp.zeros((D_INNER,), dtype=jnp.float32)
        W_xproj = jax.random.normal(ks[3], (D_INNER, DT_RANK + 2 * D_STATE), dtype=jnp.float32) * s
        W_dt = jax.random.normal(ks[4], (DT_RANK, D_INNER), dtype=jnp.float32) * s
        b_dt = jnp.zeros((D_INNER,), dtype=jnp.float32)
        A_log = jnp.broadcast_to(jnp.log(jnp.arange(1, D_STATE + 1, dtype=jnp.float32)), (D_INNER, D_STATE))
        D = jnp.ones((D_INNER,), dtype=jnp.float32)
        W_out = jax.random.normal(ks[5], (D_INNER, D_MODEL), dtype=jnp.float32) * s
        return {'x': x, 'W_in': W_in, 'W_conv': W_conv, 'b_conv': b_conv, 'W_xproj': W_xproj, 'W_dt': W_dt, 'b_dt': b_dt, 'A_log': A_log, 'D': D, 'W_out': W_out}
    _L1_attn_all = _L1_attn_setup()
    _L1_attn_in = {k: v for k, v in _L1_attn_all.items() if k in ('W_in', 'W_conv', 'b_conv', 'W_xproj', 'W_dt', 'b_dt', 'A_log', 'D', 'W_out')}
    del _L1_attn_all

    def _L1_ffn_setup():
        import jax, jax.numpy as jnp
        import numpy as np
        D_MODEL = 256
        D_FF = 1024
        NUM_EXPERTS = 8
        TOP_K = 2
        BATCH = 4
        SEQ = 512
        key = jax.random.key(seed)
        ks = jax.random.split(key, 8)
        s = 0.02
        x = jax.random.normal(ks[0], (BATCH, SEQ, D_MODEL), dtype=jnp.float32)
        router_w = jax.random.normal(ks[1], (D_MODEL, NUM_EXPERTS), dtype=jnp.float32) * s
        router_b = jnp.zeros((NUM_EXPERTS,), dtype=jnp.float32)
        W1 = jax.random.normal(ks[2], (NUM_EXPERTS, D_MODEL, D_FF), dtype=jnp.float32) * s
        b1 = jnp.zeros((NUM_EXPERTS, D_FF), dtype=jnp.float32)
        W2 = jax.random.normal(ks[3], (NUM_EXPERTS, D_FF, D_MODEL), dtype=jnp.float32) * s
        b2 = jnp.zeros((NUM_EXPERTS, D_MODEL), dtype=jnp.float32)
        return {'x': x, 'router_w': router_w, 'router_b': router_b, 'W1': W1, 'b1': b1, 'W2': W2, 'b2': b2}
    _L1_ffn_all = _L1_ffn_setup()
    _L1_ffn_in = {k: v for k, v in _L1_ffn_all.items() if k in ('router_w', 'router_b', 'W1', 'b1', 'W2', 'b2')}
    del _L1_ffn_all
    return {'x': x, 'ctx_768': ctx_768, 'mask_BxS2_bk0': mask_BxS2_bk0, 'L0_xattn_ln_x_g': _L0_xattn_in['ln_x_g'], 'L0_xattn_ln_x_b': _L0_xattn_in['ln_x_b'], 'L0_xattn_ln_l_g': _L0_xattn_in['ln_l_g'], 'L0_xattn_ln_l_b': _L0_xattn_in['ln_l_b'], 'L0_xattn_qn_g': _L0_xattn_in['qn_g'], 'L0_xattn_kn_g': _L0_xattn_in['kn_g'], 'L0_xattn_Wq': _L0_xattn_in['Wq'], 'L0_xattn_Wkv': _L0_xattn_in['Wkv'], 'L0_xattn_Wlkv': _L0_xattn_in['Wlkv'], 'L0_xattn_Wo': _L0_xattn_in['Wo'], 'L0_xattn_bo': _L0_xattn_in['bo'], 'L0_attn_Wq': _L0_attn_in['Wq'], 'L0_attn_Wkv': _L0_attn_in['Wkv'], 'L0_attn_Wout': _L0_attn_in['Wout'], 'L0_ffn_w_q': _L0_ffn_in['w_q'], 'L0_ffn_bn_gamma': _L0_ffn_in['bn_gamma'], 'L0_ffn_bn_beta': _L0_ffn_in['bn_beta'], 'L0_ffn_keys': _L0_ffn_in['keys'], 'L0_ffn_down_embed': _L0_ffn_in['down_embed'], 'L0_ffn_up_embed': _L0_ffn_in['up_embed'], 'L1_xattn_Wq': _L1_xattn_in['Wq'], 'L1_xattn_bq': _L1_xattn_in['bq'], 'L1_xattn_Wk': _L1_xattn_in['Wk'], 'L1_xattn_bk': _L1_xattn_in['bk'], 'L1_xattn_Wv': _L1_xattn_in['Wv'], 'L1_xattn_bv': _L1_xattn_in['bv'], 'L1_xattn_Wo': _L1_xattn_in['Wo'], 'L1_xattn_bo': _L1_xattn_in['bo'], 'L1_attn_W_in': _L1_attn_in['W_in'], 'L1_attn_W_conv': _L1_attn_in['W_conv'], 'L1_attn_b_conv': _L1_attn_in['b_conv'], 'L1_attn_W_xproj': _L1_attn_in['W_xproj'], 'L1_attn_W_dt': _L1_attn_in['W_dt'], 'L1_attn_b_dt': _L1_attn_in['b_dt'], 'L1_attn_A_log': _L1_attn_in['A_log'], 'L1_attn_D': _L1_attn_in['D'], 'L1_attn_W_out': _L1_attn_in['W_out'], 'L1_ffn_router_w': _L1_ffn_in['router_w'], 'L1_ffn_router_b': _L1_ffn_in['router_b'], 'L1_ffn_W1': _L1_ffn_in['W1'], 'L1_ffn_b1': _L1_ffn_in['b1'], 'L1_ffn_W2': _L1_ffn_in['W2'], 'L1_ffn_b2': _L1_ffn_in['b2']}

def reference(x, ctx_768, mask_BxS2_bk0, L0_xattn_ln_x_g, L0_xattn_ln_x_b, L0_xattn_ln_l_g, L0_xattn_ln_l_b, L0_xattn_qn_g, L0_xattn_kn_g, L0_xattn_Wq, L0_xattn_Wkv, L0_xattn_Wlkv, L0_xattn_Wo, L0_xattn_bo, L0_attn_Wq, L0_attn_Wkv, L0_attn_Wout, L0_ffn_w_q, L0_ffn_bn_gamma, L0_ffn_bn_beta, L0_ffn_keys, L0_ffn_down_embed, L0_ffn_up_embed, L1_xattn_Wq, L1_xattn_bq, L1_xattn_Wk, L1_xattn_bk, L1_xattn_Wv, L1_xattn_bv, L1_xattn_Wo, L1_xattn_bo, L1_attn_W_in, L1_attn_W_conv, L1_attn_b_conv, L1_attn_W_xproj, L1_attn_W_dt, L1_attn_b_dt, L1_attn_A_log, L1_attn_D, L1_attn_W_out, L1_ffn_router_w, L1_ffn_router_b, L1_ffn_W1, L1_ffn_b1, L1_ffn_W2, L1_ffn_b2):
    import jax
    import jax.numpy as jnp

    def _L0_xattn_ref(x, latents, mask, ln_x_g, ln_x_b, ln_l_g, ln_l_b, qn_g, kn_g, Wq, Wkv, Wlkv, Wo, bo):
        import jax, jax.numpy as jnp
        import numpy as np
        DIM_IN, DIM_LAT, DIM_HEAD = (192, 256, 64)
        INNER = max(DIM_LAT, DIM_IN)
        HEADS = INNER // DIM_HEAD
        SCALE = DIM_HEAD ** (-0.5)
        RMS_EPS = 1e-08
        LN_EPS = 1e-05

        def layernorm(x, g, b):
            mu = jnp.mean(x, axis=-1, keepdims=True)
            var = jnp.mean((x - mu) ** 2, axis=-1, keepdims=True)
            return (x - mu) * jax.lax.rsqrt(var + LN_EPS) * g + b

        def rmsnorm(x, gamma):
            norm = jnp.sqrt(jnp.sum(x * x, axis=-1, keepdims=True)) * x.shape[-1] ** (-0.5)
            return x / jnp.maximum(norm, RMS_EPS) * gamma
        b, n, _ = x.shape
        m = latents.shape[1]
        xn = layernorm(x, ln_x_g, ln_x_b)
        ln = layernorm(latents, ln_l_g, ln_l_b)
        q = ln @ Wq.T
        kv = jnp.concatenate([xn @ Wkv.T, ln @ Wlkv.T], axis=1)
        k, v = (kv[..., :INNER], kv[..., INNER:])
        split_heads = lambda t: t.reshape(t.shape[0], t.shape[1], HEADS, DIM_HEAD).transpose(0, 2, 1, 3)
        q, k, v = (split_heads(q), split_heads(k), split_heads(v))
        qn = rmsnorm(q, qn_g) * SCALE
        kn = rmsnorm(k, kn_g)
        attn = jnp.einsum('bhid,bhjd->bhij', qn, kn)
        full_mask = jnp.pad(mask, ((0, 0), (0, m)), constant_values=True)
        attn = jnp.where(full_mask[:, None, None, :], attn, -jnp.finfo(attn.dtype).max)
        attn = jax.nn.softmax(attn, axis=-1)
        out = jnp.einsum('bhij,bhjd->bhid', attn, v)
        out = out.transpose(0, 2, 1, 3).reshape(b, m, INNER)
        return out @ Wo.T + bo

    def _L0_attn_ref(tokens, Wq, Wkv, Wout):
        import jax, jax.numpy as jnp
        import numpy as np
        HEADS, DK, DV = (16, 16, 64)
        EPS = 1e-12

        def l2norm(t):
            n = jnp.linalg.norm(t, axis=-1, keepdims=True)
            return t / jnp.maximum(n, EPS)

        def tanh_norm(t):
            n = jnp.linalg.norm(t, axis=-1, keepdims=True)
            return jnp.tanh(n) * (t / jnp.maximum(n, EPS))

        def split_heads(x, h):
            b, n, hd = x.shape
            return x.reshape(b, n, h, hd // h).transpose(0, 2, 1, 3)
        q = split_heads(tokens @ Wq, HEADS)
        kv = split_heads(tokens @ Wkv, HEADS)
        k, v = (kv[..., :DK], kv[..., DK:])
        q, k, v = (l2norm(q), l2norm(k), l2norm(v))
        sim = jnp.einsum('bhid,bhjd->bhij', q, k)
        attn = jnp.square(jax.nn.relu(sim))
        out = jnp.einsum('bhij,bhjd->bhid', attn, v)
        out = tanh_norm(out)
        b, h, n, d = out.shape
        out = out.transpose(0, 2, 1, 3).reshape(b, n, h * d)
        return out @ Wout

    def _L0_ffn_ref(x, w_q, bn_gamma, bn_beta, keys, down_embed, up_embed):
        import jax, jax.numpy as jnp
        import numpy as np
        H = 8
        KD = 128
        TOPK = 8
        NUM_KEYS = 64
        N_EXPERTS = NUM_KEYS * NUM_KEYS
        N_DIM = 256
        BN_EPS = 1e-05

        def gelu_new(x):
            c = jnp.sqrt(jnp.asarray(2.0 / jnp.pi, x.dtype))
            return 0.5 * x * (1.0 + jnp.tanh(c * (x + 0.044715 * x * x * x)))
        b, n, d = x.shape
        q = jnp.einsum('bnd,de->bne', x, w_q)
        mean = jnp.mean(q, axis=(0, 1))
        var = jnp.var(q, axis=(0, 1))
        q = (q - mean) * jax.lax.rsqrt(var + BN_EPS) * bn_gamma + bn_beta
        q = q.reshape(b, n, 2, H, KD).transpose(2, 0, 1, 3, 4)
        sim = jnp.einsum('pbnhd,hkpd->pbnhk', q, keys)
        sx, ix = jax.lax.top_k(sim[0], TOPK)
        sy, iy = jax.lax.top_k(sim[1], TOPK)
        all_scores = (sx[..., :, None] + sy[..., None, :]).reshape(b, n, H, TOPK * TOPK)
        all_indices = (ix[..., :, None] * NUM_KEYS + iy[..., None, :]).reshape(b, n, H, TOPK * TOPK)
        scores, pk = jax.lax.top_k(all_scores, TOPK)
        indices = jnp.take_along_axis(all_indices, pk, axis=-1)
        wd = down_embed[indices]
        wu = up_embed[indices]
        h = jnp.einsum('bnd,bnhkd->bnhk', x, wd)
        h = gelu_new(h)
        h = jax.nn.softmax(scores, axis=-1) * h
        out = jnp.einsum('bnhk,bnhkd->bnd', h, wu)
        return out

    def _L1_xattn_ref(query, key_value, Wq, bq, Wk, bk, Wv, bv, Wo, bo):
        import jax, jax.numpy as jnp
        import numpy as np
        NUM_HEADS = 16
        CLAMP = 10000.0
        B, Nq, Cq = query.shape
        Nkv = key_value.shape[1]
        H = NUM_HEADS
        D = Cq // H
        scale = D ** (-0.5)
        q = (query @ Wq + bq).reshape(B, Nq, H, D).transpose(0, 2, 1, 3)
        k = (key_value @ Wk + bk).reshape(B, Nkv, H, D).transpose(0, 2, 1, 3)
        v = (key_value @ Wv + bv).reshape(B, Nkv, H, D).transpose(0, 2, 1, 3)
        attn = jnp.einsum('bhqd,bhkd->bhqk', q, k) * scale
        attn = jnp.clip(attn, -CLAMP, CLAMP)
        attn = jax.nn.softmax(attn, axis=-1)
        attn = jnp.where(jnp.any(jnp.isnan(attn)), jnp.asarray(1.0 / Nkv, attn.dtype), attn)
        x = jnp.einsum('bhqk,bhkd->bqhd', attn, v).reshape(B, Nq, Cq)
        return x @ Wo + bo

    def _L1_attn_ref(x, W_in, W_conv, b_conv, W_xproj, W_dt, b_dt, A_log, D, W_out):
        import jax, jax.numpy as jnp
        import numpy as np
        D_MODEL = 256
        D_STATE = 16
        EXPAND = 2
        D_INNER = EXPAND * D_MODEL
        DT_RANK = 64
        D_CONV = 4

        def _silu(v):
            return v * jax.nn.sigmoid(v)
        B_, L, _ = x.shape
        xz = x @ W_in
        x_in, z = jnp.split(xz, 2, axis=-1)
        pad = D_CONV - 1
        x_pad = jnp.pad(x_in, ((0, 0), (pad, 0), (0, 0)))
        x_conv = b_conv
        x_conv = sum((x_pad[:, k:k + L, :] * W_conv[k] for k in range(D_CONV))) + b_conv
        x_in = _silu(x_conv)
        dbc = x_in @ W_xproj
        dt = jax.nn.softplus(dbc[..., :DT_RANK] @ W_dt + b_dt)
        Bm = dbc[..., DT_RANK:DT_RANK + D_STATE]
        Cm = dbc[..., DT_RANK + D_STATE:]
        A = -jnp.exp(A_log)

        def step(state, inp):
            x_t, dt_t, B_t, C_t = inp
            dA = jnp.exp(jnp.clip(dt_t[:, :, None] * A[None], -10.0, 10.0))
            dB = dt_t[:, :, None] * B_t[:, None, :]
            state = jnp.clip(state * dA + x_t[:, :, None] * dB, -10.0, 10.0)
            y_t = jnp.einsum('bdn,bn->bd', state, C_t) + D * x_t
            return (state, y_t)
        tm = lambda a: jnp.swapaxes(a, 0, 1)
        state0 = jnp.zeros((B_, D_INNER, D_STATE), dtype=x.dtype)
        _, ys = jax.lax.scan(step, state0, (tm(x_in), tm(dt), tm(Bm), tm(Cm)))
        y = jnp.swapaxes(ys, 0, 1)
        y = y * _silu(z)
        return y @ W_out

    def _L1_ffn_ref(x, router_w, router_b, W1, b1, W2, b2):
        import jax, jax.numpy as jnp
        import numpy as np
        D_MODEL = 256
        D_FF = 1024
        NUM_EXPERTS = 8
        TOP_K = 2
        BATCH = 4
        SEQ = 512
        logits = jnp.einsum('bsd,de->bse', x, router_w) + router_b
        topk_scores, topk_idx = jax.lax.top_k(logits, TOP_K)
        topk_gates = jax.nn.softmax(topk_scores, axis=-1)
        onehot = jax.nn.one_hot(topk_idx, NUM_EXPERTS, dtype=x.dtype)
        combine = jnp.einsum('bsk,bske->bse', topk_gates, onehot)
        combine_e = jnp.moveaxis(combine, -1, 0)

        def expert_step(acc, params):
            w1, bb1, w2, bb2, c = params
            h = jax.nn.relu(jnp.einsum('bsd,df->bsf', x, w1) + bb1)
            y = jnp.einsum('bsf,fd->bsd', h, w2) + bb2
            return (acc + y * c[..., None], None)
        out, _ = jax.lax.scan(expert_step, jnp.zeros_like(x), (W1, b1, W2, b2, combine_e))
        return out
    x = x + _L0_xattn_ref(ctx_768, _layernorm(x, axis=-1), mask_BxS2_bk0, L0_xattn_ln_x_g, L0_xattn_ln_x_b, L0_xattn_ln_l_g, L0_xattn_ln_l_b, L0_xattn_qn_g, L0_xattn_kn_g, L0_xattn_Wq, L0_xattn_Wkv, L0_xattn_Wlkv, L0_xattn_Wo, L0_xattn_bo)
    x = x + _L0_attn_ref(_layernorm(x, axis=-1), L0_attn_Wq, L0_attn_Wkv, L0_attn_Wout)
    x = x + _L0_ffn_ref(_layernorm(x, axis=-1), L0_ffn_w_q, L0_ffn_bn_gamma, L0_ffn_bn_beta, L0_ffn_keys, L0_ffn_down_embed, L0_ffn_up_embed)
    x = x + _L1_xattn_ref(_layernorm(x, axis=-1), ctx_768, L1_xattn_Wq, L1_xattn_bq, L1_xattn_Wk, L1_xattn_bk, L1_xattn_Wv, L1_xattn_bv, L1_xattn_Wo, L1_xattn_bo)
    x = x + _L1_attn_ref(_layernorm(x, axis=-1), L1_attn_W_in, L1_attn_W_conv, L1_attn_b_conv, L1_attn_W_xproj, L1_attn_W_dt, L1_attn_b_dt, L1_attn_A_log, L1_attn_D, L1_attn_W_out)
    x = x + _L1_ffn_ref(_layernorm(x, axis=-1), L1_ffn_router_w, L1_ffn_router_b, L1_ffn_W1, L1_ffn_b1, L1_ffn_W2, L1_ffn_b2)
    return x

_drawn_inputs = setup_inputs


def setup_inputs(seed=0):
    import zlib

    import numpy as np

    out = dict(_drawn_inputs(seed))
    spreads = {'L0_xattn_ln_x_g': (1.0, 0.2),
     'L0_xattn_ln_x_b': (0.0, 0.1),
     'L0_xattn_ln_l_g': (1.0, 0.2),
     'L0_xattn_ln_l_b': (0.0, 0.1),
     'L0_xattn_qn_g': (1.0, 0.2),
     'L0_xattn_kn_g': (1.0, 0.2),
     'L0_xattn_bo': (0.0, 0.1),
     'L0_ffn_bn_gamma': (1.0, 0.6),
     'L0_ffn_bn_beta': (0.0, 0.8),
     'L1_xattn_bq': (0.0, 0.331),
     'L1_xattn_bk': (0.0, 2.0),
     'L1_xattn_bv': (0.0, 0.1),
     'L1_xattn_bo': (0.0, 0.1),
     'L1_attn_b_conv': (0.0, 0.8),
     'L1_attn_b_dt': (0.0, 0.8),
     'L1_attn_D': (1.0, 0.6),
     'L1_ffn_router_b': (0.0, 2.0),
     'L1_ffn_b1': (0.0, 2.0),
     'L1_ffn_b2': (0.0, 2.0)}
    factors = {'L0_ffn_w_q': 8.0,
     'L0_ffn_keys': 8.0,
     'L0_ffn_down_embed': 8.0,
     'L0_ffn_up_embed': 8.0,
     'L1_attn_W_in': 8.0,
     'L1_attn_W_conv': 8.0,
     'L1_attn_W_xproj': 8.0,
     'L1_attn_W_dt': 8.0,
     'L1_attn_A_log': 8.0,
     'L1_attn_W_out': 8.0,
     'L1_ffn_router_w': 8.0,
     'L1_ffn_W1': 8.0,
     'L1_ffn_W2': 8.0}
    for name, (base, spread) in spreads.items():
        noise = np.random.default_rng([zlib.crc32(name.encode()), seed]).standard_normal(out[name].shape)
        drawn = base * np.exp(spread * noise) if base else spread * noise
        out[name] = jnp.asarray(drawn.astype(out[name].dtype))
    for name, factor in factors.items():
        out[name] = (out[name] * factor).astype(out[name].dtype)
    return out
```

```python
from contextlib import ExitStack

import numpy as np
import concourse.bass as bass
from concourse import mybir

ALU = mybir.AluOpType
ACT = mybir.ActivationFunctionType
AXX = mybir.AxisListType.X
F32 = mybir.dt.float32
U32 = mybir.dt.uint32
U8 = mybir.dt.uint8

P = 128
B, S, D = 64, 32, 256
T = B * S
NT = T // P
BT = P // S
KT = D // P
CTX, DC = 257, 192
DH = DC // 2
C = 512
NC = T // C
LN_EPS = 1e-5
U = 2


class Link:

    def __init__(self, eng, sem):
        self.eng, self.sem, self.base, self.n = eng, sem, 0, 0

    def __call__(self, ins):
        self.n += 1
        ins.then_inc(self.sem, 1)
        self.eng.wait_ge(self.sem, self.base + self.n)

    def loop(self, i, per):
        self.start, self.per = self.n, per
        self.base, self.n = i * per + self.start, 0

    def end(self, trips):
        assert self.n == self.per, (self.n, self.per)
        self.base, self.n = 0, self.start + trips * self.per


def signals(n):
    return n + 1


def dma_signals(n):
    return 16 * (n + 1)


def opens(eng, *sems):
    for s in sems:
        eng.sem_inc(s, 1)


def bc(ap, *shape):
    return ap.broadcast_to(list(shape))


def tok(t):
    return bass.ts(t, P)


class Scope:

    def __init__(self, nc, ctx, name):
        self.nc, self.ctx, self.name = nc, ctx, name

    def sb(self, name, shape, dt=F32):
        return self.ctx.enter_context(self.nc.sbuf_tensor(f"{self.name}_{name}", shape, dt))

    def sem(self, name):
        return self.nc.alloc_semaphore(f"{self.name}_{name}")

    def sems(self, names):
        return [self.sem(n) for n in names.split()]

    def psum(self):
        return self.ctx.enter_context(self.nc.psum_tensor(f"{self.name}_ps", [P, 8, 512], F32))


def row_stats(dve, link, x, stats, mv, var, eps):
    for t in range(NT):
        last = dve.bn_stats(stats[:, t, :], x[:, t, :])
    link(last)
    for t in range(NT):
        last = dve.bn_aggr(mv[:, t, :], stats[:, t, :])
    link(last)
    return dve.tensor_scalar(var[:, :], mv[:, :, 1], eps, None, ALU.add)


def project_out(nc, g, name, ps, OT, wo, bias, kt=KT):
    X = g.X
    with ExitStack() as ctx:
        s = Scope(nc, ctx, name)
        yT = s.sb("yT", [P, KT, C])
        product, yT_ready, y_tr, x_ready = s.sems("product yT_ready y_tr x_ready")
        block = ctx.enter_context(nc.Block())

        @block.tensor
        def _(pe):
            opens(pe, product, y_tr)
            with pe.Fori(0, NC) as c:
                pe.wait_ge(yT_ready, signals(c))
                for m in range(KT):
                    for k in range(kt):
                        mm = pe.matmul(ps[:, m, :], lhsT=wo[:, k, m * P:(m + 1) * P], rhs=OT[:, k, bass.ts(c, C)],
                                       start=k == 0, stop=k == kt - 1)
                mm.then_inc(product, 1)
                pe.wait_ge(yT_ready, signals(c + 1))
                pe.wait_ge(x_ready, signals(c))
                for t in range(C // P):
                    for m in range(KT):
                        at = (t % 2) * D + m * P
                        mm = pe.transpose(ps[:, 2 + t // 2, at:at + P], yT[:, m, t * P:(t + 1) * P], g.ident[:])
                mm.then_inc(y_tr, 1)

        @block.scalar
        def _(act):
            opens(act, yT_ready)
            with act.Fori(0, NC) as c:
                act.wait_ge(product, signals(c + 1))
                act.wait_ge(y_tr, signals(c))
                for m in range(KT):
                    if bias is None:
                        ins = act.activation(yT[:, m, :], ps[:, m, :], ACT.Copy)
                    else:
                        ins = act.activation(yT[:, m, :], ps[:, m, :], ACT.Identity, bias=bias[:, m:m + 1])
                ins.then_inc(yT_ready, 1)

        @block.vector
        def _(dve):
            opens(dve, x_ready)
            with dve.Fori(0, NC) as c:
                dve.wait_ge(y_tr, signals(c + 1))
                xs = X[:, bass.ts(c, C // P), :].rearrange("p (a t) d -> p a (t d)", a=2)
                dve.tensor_tensor(xs, xs, ps[:, 2:4, :], ALU.add).then_inc(x_ready, 1)


class Normed:

    def __init__(self, s):
        self.stats, self.mv = s.sb("stats", [P, NT, 6]), s.sb("mv", [P, NT, 2])
        self.var, self.rstd, self.half = s.sb("var", [P, NT]), s.sb("rstd", [P, NT]), s.sb("half", [P, 1])

    def apply(self, dve, out, X, t):
        return dve.tensor_scalar(out, X[:, t, :], self.mv[:, t, 0:1], self.rstd[:, bass.ds(t, 1)], ALU.subtract, ALU.mult)


def normed_transposed(nc, g, s, ps, n, xT):
    X = g.X
    with ExitStack() as ctx:
        a = Scope(nc, ctx, s.name + "n")
        xn = a.sb("xn", [P, U, D])
        half_ready, stat_ready, rstd_ready, dve_link, ln_ready, x_tr, xT_ready = a.sems(
            "half_ready stat_ready rstd_ready dve_link ln_ready x_tr xT_ready")
        block = ctx.enter_context(nc.Block())

        @block.gpsimd
        def _(pool):
            pool.memset(n.half[:], -0.5).then_inc(half_ready, 1)
            pool.wait_ge(half_ready, 1)
            pool.wait_ge(stat_ready, 1)
            pool.tensor_tensor(n.rstd[:], n.var[:], bc(n.half[:], P, NT), ALU.pow).then_inc(rstd_ready, 1)

        @block.vector
        def _(dve):
            link = Link(dve, dve_link)
            row_stats(dve, link, X, n.stats, n.mv, n.var, LN_EPS).then_inc(stat_ready, 1)
            dve.wait_ge(rstd_ready, 1)
            opens(dve, ln_ready)
            with dve.Fori(0, NT // U) as i:
                for u in range(U):
                    dve.wait_ge(x_tr, signals(i * U))
                    n.apply(dve, xn[:, u, :], X, i * U + u).then_inc(ln_ready, 1)

        @block.tensor
        def _(pe):
            opens(pe, x_tr)
            with pe.Fori(0, NT // U) as i:
                for u in range(U):
                    t = i * U + u
                    pe.wait_ge(ln_ready, signals(t + 1))
                    pe.wait_ge(xT_ready, signals(i * U))
                    for k in range(KT):
                        mm = pe.transpose(ps[:, u, tok(k)], xn[:, u, tok(k)], g.ident[:])
                    mm.then_inc(x_tr, 1)

        @block.scalar
        def _(act):
            opens(act, xT_ready)
            with act.Fori(0, NT // U) as i:
                for u in range(U):
                    t = i * U + u
                    act.wait_ge(x_tr, signals(t + 1))
                    act.activation(xT[:, :, tok(t)], ps[:, u, 0:KT * P].rearrange("p (k q) -> p k q", k=KT), ACT.Copy).then_inc(xT_ready, 1)


def phase1(nc, g):
    I, X, ident = g.I, g.X, g.ident
    H, HD = 4, 64
    NK = CTX + S
    with ExitStack() as ctx:
        def sb(name, shape, dt=F32):
            return ctx.enter_context(nc.sbuf_tensor("s1_" + name, shape, dt))

        def sem(name):
            return nc.alloc_semaphore("p1_" + name)

        banks = ctx.enter_context(nc.psum_tensor("p1_ps", [P, 8, 512], F32))
        ps = banks[:].rearrange("p (u n) c -> p u n c", u=U)
        QT = sb("QT", [P, KT, B * S])
        KLT = sb("KLT", [P, KT, B * S])
        KXT = sb("KXT", [P, KT, B])
        V3 = sb("V3", [S + 1, B, D])
        OT = sb("OT", [P, KT, B * S])
        wq = sb("wq", [P, KT, D])
        wlkv = sb("wlkv", [P, KT, 2 * D])
        wkv = sb("wkv", [DH, 2, 2 * D])
        wo = sb("wo", [P, KT, D])
        vec = sb("vec", [P, 5, KT])
        cvec = sb("cvec", [DH, 2, 2])
        headmask = sb("headmask", [P, KT, H])
        blockmask = sb("blockmask", [P, D])
        sel = sb("sel", [P, S])
        half = sb("half", [P, 1])
        mask8 = sb("mask8", [P, B, CTX], U8)

        load = sem("load")
        dve_link = sem("dve_link")

        with ExitStack() as actx:
            def sa(name, shape, dt=F32):
                return actx.enter_context(nc.sbuf_tensor("p1a_" + name, shape, dt))

            stats = sa("stats", [P, NT, 6])
            mv = sa("mv", [P, NT, 2])
            var = sa("var", [P, NT])
            rstd = sa("rstd", [P, NT])
            lat = sa("lat", [P, NT, D])
            ln = sa("ln", [P, U, D])
            lnT = sa("lnT", [P, U, KT, P])
            sq = sa("sq", [P, U, 2 * D])
            ss = sa("ss", [P, U, 8])
            rn = sa("rn", [P, U, 8])
            qk = sa("qk", [P, U, 2 * D])
            vl = sa("vl", [P, U, D])
            cx = sa("cx", [B, DC])
            cst = sa("cst", [B, 6])
            cmv = sa("cmv", [B, 2])
            cve = sa("cve", [B, 1])
            crs = sa("crs", [B, 1])
            cn = sa("cn", [B, DC])
            cT = sa("cT", [DH, 2, B])
            csq = sa("csq", [B, D])
            css = sa("css", [B, 4])
            crn = sa("crn", [B, 4])
            ck = sa("ck", [B, D])
            cv = sa("cv", [B, D])
            stat_ready, rstd_ready = sem("stat_ready"), sem("rstd_ready")
            half_ready = sem("half_ready")
            cstat_ready, crstd_ready, cn_ready = sem("cstat_ready"), sem("crstd_ready"), sem("cn_ready")
            c_tr, cT_ready, c_proj, csq_ready = sem("c_tr"), sem("cT_ready"), sem("c_proj"), sem("csq_ready")
            css_ready, crn_ready, ck_ready, c_tr2 = sem("css_ready"), sem("crn_ready"), sem("ck_ready"), sem("c_tr2")
            cv_ready, kx_ready, cv_loaded = sem("cv_ready"), sem("kx_ready"), sem("cv_loaded")
            v3_loaded = [sem(f"v3_loaded{u}") for u in range(U)]
            ln_ready, ln_tr, lnT_ready, proj = sem("ln_ready"), sem("ln_tr"), sem("lnT_ready"), sem("proj")
            sq_ready, ss_ready, rn_ready, qk_ready = sem("sq_ready"), sem("ss_ready"), sem("rn_ready"), sem("qk_ready")
            qk_tr, qT_ready, kT_ready, vl_ready = sem("qk_tr"), sem("qT_ready"), sem("kT_ready"), sem("vl_ready")
            NLOAD = 11
            block = actx.enter_context(nc.Block())

            @block.sync
            def _(sp):
                for dst, src in ((vec, "p1_vec"), (cvec, "p1_cvec"), (wq, "p1_wq"), (wlkv, "p1_wlkv"), (wkv, "p1_wkv"),
                                 (headmask, "headmask4"), (blockmask, "blockmask4"), (sel, "sel"), (wo, "p1_wo")):
                    sp.dma_start(dst[:], I[src]).then_inc(load, 16)
                sp.dma_start(cx[:], I["ctx_768"][:, CTX - 1, :]).then_inc(load, 16)
                sp.dma_start(mask8[:].rearrange("p b k -> p (b k)"),
                             I["mask_BxS2_bk0"].rearrange("b k -> (b k)").unsqueeze(0).broadcast_to([P, B * CTX])).then_inc(load, 16)
                sp.wait_ge(cv_ready, 1)
                sp.dma_start(V3[0:1, :, :], cv[:]).then_inc(cv_loaded, 16)
                for q in v3_loaded:
                    sp.sem_inc(q, 16)
                with sp.Fori(0, NT // U) as i:
                    for u in range(U):
                        t = i * U + u
                        sp.wait_ge(vl_ready, signals(t + 1))
                        for b in range(BT):
                            sp.dma_start(V3[1:S + 1, t * BT + b, :], vl[b * S:b * S + S, u, :]).then_inc(v3_loaded[u], 16)
                sp.wait_ge(cv_loaded, 16)
                for q in v3_loaded:
                    sp.wait_ge(q, dma_signals(BT * NT // U))

            @block.gpsimd
            def _(pool):
                pool.memset(half[:], -0.5).then_inc(half_ready, 1)
                pool.wait_ge(half_ready, 1)
                for n in range(2):
                    pool.wait_ge(stat_ready, n + 1)
                    pool.tensor_tensor(rstd[:], var[:], bc(half[:], P, NT), ALU.pow).then_inc(rstd_ready, 1)
                pool.wait_ge(cstat_ready, 1)
                pool.tensor_tensor(crs[:], cve[:], half[0:B, :], ALU.pow).then_inc(crstd_ready, 1)
                pool.wait_ge(css_ready, 1)
                pool.tensor_tensor(crn[:], css[:], bc(half[0:B, :], B, 4), ALU.pow).then_inc(crn_ready, 1)
                opens(pool, rn_ready)
                with pool.Fori(0, NT // U) as i:
                    for u in range(U):
                        t = i * U + u
                        pool.wait_ge(ss_ready, signals(t + 1))
                        pool.tensor_tensor(rn[:, u, :], ss[:, u, :], bc(half[:], P, 8), ALU.pow).then_inc(rn_ready, 1)

            @block.tensor
            def _(pe):
                pe.wait_ge(load, 16 * NLOAD)
                pe.wait_ge(cn_ready, 1)
                for k in range(2):
                    mm = pe.transpose(ps[0:DH, 0, 0, k * B:(k + 1) * B], cn[:, k * DH:(k + 1) * DH], g.ident[0:B, 0:B])
                mm.then_inc(c_tr, 1)
                pe.wait_ge(cT_ready, 1)
                for k in range(2):
                    mm = pe.matmul(ps[0:B, 0, 1, :], lhsT=cT[:, k, :], rhs=wkv[:, k, :], start=k == 0, stop=k == 1)
                mm.then_inc(c_proj, 1)
                pe.wait_ge(ck_ready, 1)
                for k in range(KT):
                    mm = pe.transpose(ps[:, 0, 2, k * B:(k + 1) * B], ck[:, k * P:(k + 1) * P], g.ident[0:B, 0:B])
                mm.then_inc(c_tr2, 1)
                pe.wait_ge(kx_ready, 1)
                opens(pe, ln_tr, proj, qk_tr)
                with pe.Fori(0, NT // U) as i:
                    for u in range(U):
                        t = i * U + u
                        pe.wait_ge(ln_ready, signals(t + 1))
                        pe.wait_ge(qT_ready, signals(i * U))
                        pe.wait_ge(kT_ready, signals(i * U))
                        for k in range(KT):
                            mm = pe.transpose(ps[:, u, 0, k * P:(k + 1) * P], ln[:, u, k * P:(k + 1) * P], g.ident[:])
                        mm.then_inc(ln_tr, 1)
                    for u in range(U):
                        t = i * U + u
                        pe.wait_ge(lnT_ready, signals(t + 1))
                        for k in range(KT):
                            pe.matmul(ps[:, u, 1, 0:D], lhsT=lnT[:, u, k, :], rhs=wq[:, k, :], start=k == 0, stop=k == KT - 1)
                        for k in range(KT):
                            mm = pe.matmul(ps[:, u, 2, :], lhsT=lnT[:, u, k, :], rhs=wlkv[:, k, :], start=k == 0, stop=k == KT - 1)
                        mm.then_inc(proj, 1)
                    for u in range(U):
                        t = i * U + u
                        pe.wait_ge(qk_ready, signals(t + 1))
                        for k in range(2 * KT):
                            mm = pe.transpose(ps[:, u, 0, k * P:(k + 1) * P], qk[:, u, k * P:(k + 1) * P], g.ident[:])
                        mm.then_inc(qk_tr, 1)

            @block.scalar
            def _(act):
                act.wait_ge(load, 16 * NLOAD)
                act.wait_ge(c_tr, 1)
                for k in range(2):
                    ins = act.activation(cT[:, k, :], ps[0:DH, 0, 0, k * B:(k + 1) * B], ACT.Identity,
                                         bias=cvec[:, 1, k:k + 1], scale=cvec[:, 0, k:k + 1])
                ins.then_inc(cT_ready, 1)
                act.wait_ge(c_proj, 1)
                act.activation(csq[:], ps[0:B, 0, 1, 0:D], ACT.Square).then_inc(csq_ready, 1)
                act.activation(cv[:], ps[0:B, 0, 1, D:2 * D], ACT.Copy).then_inc(cv_ready, 1)
                act.wait_ge(c_tr2, 1)
                for k in range(KT):
                    ins = act.activation(KXT[:, k, :], ps[:, 0, 2, k * B:(k + 1) * B], ACT.Identity, scale=vec[:, 3, k:k + 1])
                ins.then_inc(kx_ready, 1)
                opens(act, lnT_ready, sq_ready, vl_ready, kT_ready)
                with act.Fori(0, NT // U) as i:
                    for u in range(U):
                        t = i * U + u
                        act.wait_ge(ln_tr, signals(t + 1))
                        for k in range(KT):
                            ins = act.activation(lnT[:, u, k, :], ps[:, u, 0, k * P:(k + 1) * P], ACT.Identity,
                                                 bias=vec[:, 1, k:k + 1], scale=vec[:, 0, k:k + 1])
                        ins.then_inc(lnT_ready, 1)
                    for u in range(U):
                        t = i * U + u
                        act.wait_ge(proj, signals(t + 1))
                        act.wait_ge(ss_ready, signals(i * U))
                        act.activation(sq[:, u, 0:D], ps[:, u, 1, 0:D], ACT.Square)
                        act.activation(sq[:, u, D:2 * D], ps[:, u, 2, 0:D], ACT.Square).then_inc(sq_ready, 1)
                        act.wait_ge(v3_loaded[u], dma_signals(i * BT))
                        act.activation(vl[:, u, :], ps[:, u, 2, D:2 * D], ACT.Copy).then_inc(vl_ready, 1)
                    for u in range(U):
                        t = i * U + u
                        act.wait_ge(qk_tr, signals(t + 1))
                        act.wait_ge(qT_ready, signals(t + 1))
                        for k in range(KT):
                            ins = act.activation(KLT[:, k, tok(t)], ps[:, u, 0, D + k * P:D + (k + 1) * P], ACT.Identity,
                                                 scale=vec[:, 3, k:k + 1])
                        ins.then_inc(kT_ready, 1)

            @block.vector
            def _(dve):
                link = Link(dve, dve_link)
                row_stats(dve, link, X, stats, mv, var, LN_EPS).then_inc(stat_ready, 1)
                dve.wait_ge(rstd_ready, 1)
                for t in range(NT):
                    ins = dve.tensor_scalar(lat[:, t, :], X[:, t, :], mv[:, t, 0:1], rstd[:, t:t + 1], ALU.subtract, ALU.mult)
                link(ins)
                row_stats(dve, link, lat, stats, mv, var, LN_EPS).then_inc(stat_ready, 1)
                dve.wait_ge(load, 16 * NLOAD)
                link(dve.bn_stats(cst[:], cx[:]))
                link(dve.bn_aggr(cmv[:], cst[:]))
                dve.tensor_scalar(cve[:], cmv[:, 1:2], LN_EPS, None, ALU.add).then_inc(cstat_ready, 1)
                dve.wait_ge(crstd_ready, 1)
                dve.tensor_scalar(cn[:], cx[:], cmv[:, 0:1], crs[:], ALU.subtract, ALU.mult).then_inc(cn_ready, 1)
                dve.wait_ge(csq_ready, 1)
                link(dve.tensor_reduce(css[:], csq[:].rearrange("p (h d) -> p h d", h=H), AXX, ALU.add))
                dve.tensor_scalar(css[:], css[:], 1.0 / HD, 1e-16, ALU.mult, ALU.max).then_inc(css_ready, 1)
                dve.wait_ge(crn_ready, 1)
                dve.wait_ge(cv_ready, 1)
                dve.tensor_tensor(ck[:].rearrange("p (h d) -> p h d", h=H), ps[0:B, 0, 1, 0:D].rearrange("p (h d) -> p h d", h=H),
                                  bc(crn[:].unsqueeze(2), B, H, HD), ALU.mult).then_inc(ck_ready, 1)
                dve.wait_ge(rstd_ready, 2)
                opens(dve, ln_ready, ss_ready, qk_ready, qT_ready)
                with dve.Fori(0, NT // U) as i:
                    link.loop(i, U * 1)
                    for u in range(U):
                        t = i * U + u
                        dve.wait_ge(ln_tr, signals(i * U))
                        dve.tensor_scalar(ln[:, u, :], lat[:, t, :], mv[:, t, 0:1], rstd[:, bass.ds(t, 1)],
                                          ALU.subtract, ALU.mult).then_inc(ln_ready, 1)
                    for u in range(U):
                        t = i * U + u
                        dve.wait_ge(sq_ready, signals(t + 1))
                        dve.wait_ge(rn_ready, signals(i * U))
                        link(dve.tensor_reduce(ss[:, u, :], sq[:, u, :].rearrange("p (h d) -> p h d", h=2 * H), AXX, ALU.add))
                        dve.tensor_scalar(ss[:, u, :], ss[:, u, :], 1.0 / HD, 1e-16, ALU.mult, ALU.max).then_inc(ss_ready, 1)
                    for u in range(U):
                        t = i * U + u
                        dve.wait_ge(rn_ready, signals(t + 1))
                        dve.wait_ge(vl_ready, signals(t + 1))
                        dve.wait_ge(qk_tr, signals(i * U))
                        for j in range(2):
                            ins = dve.tensor_tensor(qk[:, u, j * D:(j + 1) * D].rearrange("p (h d) -> p h d", h=H),
                                                    ps[:, u, 1 + j, 0:D].rearrange("p (h d) -> p h d", h=H),
                                                    bc(rn[:, u, j * H:(j + 1) * H].unsqueeze(2), P, H, HD), ALU.mult)
                        ins.then_inc(qk_ready, 1)
                    for u in range(U):
                        t = i * U + u
                        dve.wait_ge(qk_tr, signals(t + 1))
                        for k in range(KT):
                            ins = dve.tensor_scalar(QT[:, k, tok(t)], ps[:, u, 0, k * P:(k + 1) * P], vec[:, 2, k:k + 1],
                                                    HD ** -0.5, ALU.mult, ALU.mult)
                        ins.then_inc(qT_ready, 1)
                link.end(NT // U)
        phase1_attention(nc, g, ps, dict(
            H=H, HD=HD, NK=NK, QT=QT, KLT=KLT, KXT=KXT, V3=V3, OT=OT, wkv=wkv, cvec=cvec, vec=vec,
            headmask=headmask, blockmask=blockmask, sel=sel, half=half, mask8=mask8))
        project_out(nc, g, "p1o", banks, OT, wo, vec[:, 4, :])


def phase1_attention(nc, g, ps, v):
    I, X = g.I, g.X
    BIG = 1e30
    H, HD, NK = v["H"], v["HD"], v["NK"]
    QT, KLT, KXT, V3, OT, wkv, cvec, vec = (v[n] for n in ("QT", "KLT", "KXT", "V3", "OT", "wkv", "cvec", "vec"))
    headmask, blockmask, sel, half, mask8 = (v[n] for n in ("headmask", "blockmask", "sel", "half", "mask8"))
    with ExitStack() as ctx:
        def sb(name, shape, dt=F32):
            return ctx.enter_context(nc.sbuf_tensor("p1b_" + name, shape, dt))

        def sem(name):
            return nc.alloc_semaphore("p1b_" + name)

        carry = sb("carry", [P, U])
        cx = sb("cx", [P, U, 2, DC])
        cst = sb("cst", [P, U, 2, 6])
        cmv = sb("cmv", [P, U, 2, 2])
        cve = sb("cve", [P, U, 2])
        crs = sb("crs", [P, U, 2])
        cn = sb("cn", [P, U, 2, DC])
        cT = sb("cT", [DH, U, 2, 2 * P])
        sq = sb("sq", [P, U, 2, D])
        ss = sb("ss", [P, U, 2 * H])
        rn = sb("rn", [P, U, 2 * H])
        kn = sb("kn", [P, U, 2, D])
        vv = sb("vv", [P, U, 2, D])
        kT = sb("kT", [P, U, KT, 2 * P])
        qb = sb("qb", [P, U, KT, P])
        mb = sb("mb", [P, U, NK])
        sc = sb("sc", [P, U, NK])
        mx = sb("mx", [P, U, 1])
        nm = sb("nm", [P, U, 1])
        pr = sb("pr", [P, U, NK])
        rs = sb("rs", [P, U, 1])
        ri = sb("ri", [P, U, 1])
        pT = sb("pT", [P, U, 3, P])
        om = sb("om", [P, U, D])
        (cve_ready, crs_ready, cn_ready, c_tr, cT_ready, kv, sq_ready, vv_ready, ss_ready, rn_ready, kn_ready,
         k_tr, kT_ready, qb_ready, mb_zeroed, mb_written, scores, sc_ready, pr_ready, p_tr, pT_ready, pv, om_ready, o_tr, oT_ready,
         dl) = (sem(n) for n in (
             "cve_ready crs_ready cn_ready c_tr cT_ready kv sq_ready vv_ready ss_ready rn_ready kn_ready "
             "k_tr kT_ready qb_ready mb_zeroed mb_written scores sc_ready pr_ready p_tr pT_ready pv om_ready o_tr oT_ready dl").split())
        cx_loaded = [sem(f"cx_loaded{u}") for u in range(U)]
        G = B // U
        block = ctx.enter_context(nc.Block())

        @block.sync
        def _(sp):
            with sp.Fori(0, G) as i:
                for u in range(U):
                    b = i * U + u
                    sp.wait_ge(cn_ready, signals(i * U))
                    sp.dma_start(cx[:, u, :, :], I["ctx_768"][b, 0:2 * P, :].rearrange("(j p) c -> p j c", p=P)).then_inc(cx_loaded[u], 16)

        @block.gpsimd
        def _(pool):
            pool.memset(mb[:], 0.0).then_inc(mb_zeroed, 1)
            opens(pool, crs_ready, qb_ready, rn_ready)
            with pool.Fori(0, G) as i:
                for u in range(U):
                    b = i * U + u
                    pool.wait_ge(cve_ready, signals(b + 1))
                    pool.tensor_tensor(crs[:, u, :], cve[:, u, :], bc(half[:], P, 2), ALU.pow).then_inc(crs_ready, 1)
                for u in range(U):
                    b = i * U + u
                    pool.wait_ge(scores, signals(i * U))
                    pool.tensor_tensor(qb[:, u, :, :].rearrange("p k (h q) -> p k h q", h=H),
                                       bc(QT[:, :, bass.ts(b, S)].unsqueeze(2), P, KT, H, S),
                                       bc(headmask[:].unsqueeze(3), P, KT, H, S), ALU.mult).then_inc(qb_ready, 1)
                for u in range(U):
                    b = i * U + u
                    pool.wait_ge(ss_ready, signals(b + 1))
                    pool.tensor_tensor(rn[:, u, :], ss[:, u, :], bc(half[:], P, 2 * H), ALU.pow).then_inc(rn_ready, 1)

        @block.tensor
        def _(pe):
            opens(pe, c_tr, kv, k_tr, scores, p_tr, pv, o_tr)
            with pe.Fori(0, G) as i:
                for u in range(U):
                    b = i * U + u
                    pe.wait_ge(cn_ready, signals(b + 1))
                    pe.wait_ge(pT_ready, signals(i * U))
                    for k in range(2):
                        for j in range(2):
                            mm = pe.transpose(ps[0:DH, u, 0, (2 * k + j) * P:(2 * k + j + 1) * P], cn[:, u, j, k * DH:(k + 1) * DH], g.ident[:])
                    mm.then_inc(c_tr, 1)
                for u in range(U):
                    b = i * U + u
                    pe.wait_ge(cT_ready, signals(b + 1))
                    pe.wait_ge(oT_ready, signals(i * U))
                    for j in range(2):
                        for k in range(2):
                            mm = pe.matmul(ps[:, u, 1 + j, :], lhsT=cT[:, u, k, j * P:(j + 1) * P], rhs=wkv[:, k, :], start=k == 0, stop=k == 1)
                    mm.then_inc(kv, 1)
                for u in range(U):
                    b = i * U + u
                    pe.wait_ge(kn_ready, signals(b + 1))
                    for k in range(KT):
                        for j in range(2):
                            mm = pe.transpose(ps[:, u, 0, (2 * k + j) * P:(2 * k + j + 1) * P], kn[:, u, j, k * P:(k + 1) * P], g.ident[:])
                    mm.then_inc(k_tr, 1)
                for u in range(U):
                    b = i * U + u
                    pe.wait_ge(kT_ready, signals(b + 1))
                    pe.wait_ge(qb_ready, signals(b + 1))
                    for lo, hi, rhs in ((0, 2 * P, lambda k: kT[:, u, k, :]), (2 * P, CTX, lambda k: KXT[:, k, bass.ds(b, 1)]),
                                        (CTX, NK, lambda k: KLT[:, k, bass.ts(b, S)])):
                        for k in range(KT):
                            mm = pe.matmul(ps[:, u, 3, lo:hi], lhsT=qb[:, u, k, :], rhs=rhs(k), start=k == 0, stop=k == KT - 1)
                    mm.then_inc(scores, 1)
                for u in range(U):
                    b = i * U + u
                    pe.wait_ge(pr_ready, signals(b + 1))
                    for j in range(3):
                        w = min(P, NK - j * P)
                        mm = pe.transpose(ps[0:w, u, 0, j * P:(j + 1) * P], pr[:, u, j * P:j * P + w], g.ident[:])
                    mm.then_inc(p_tr, 1)
                for u in range(U):
                    b = i * U + u
                    pe.wait_ge(pT_ready, signals(b + 1))
                    pe.wait_ge(vv_ready, signals(b + 1))
                    for j in range(2):
                        pe.matmul(ps[:, u, 3, 0:D], lhsT=pT[:, u, j, :], rhs=vv[:, u, j, :], start=j == 0, stop=False)
                    pe.matmul(ps[:, u, 3, 0:D], lhsT=pT[0:S + 1, u, 2, :], rhs=V3[:, b, :], start=False, stop=True).then_inc(pv, 1)
                for u in range(U):
                    b = i * U + u
                    pe.wait_ge(om_ready, signals(b + 1))
                    for k in range(KT):
                        mm = pe.matmul(ps[:, u, 1, k * S:(k + 1) * S], lhsT=om[:, u, k * P:(k + 1) * P], rhs=sel[:], start=True, stop=True)
                    mm.then_inc(o_tr, 1)

        @block.scalar
        def _(act):
            opens(act, cT_ready, sq_ready, vv_ready, kT_ready, pr_ready, pT_ready, oT_ready)
            with act.Fori(0, G) as i:
                for u in range(U):
                    b = i * U + u
                    act.wait_ge(c_tr, signals(b + 1))
                    for k in range(2):
                        ins = act.activation(cT[:, u, k, :], ps[0:DH, u, 0, 2 * k * P:2 * (k + 1) * P], ACT.Identity,
                                             bias=cvec[:, 1, k:k + 1], scale=cvec[:, 0, k:k + 1])
                    ins.then_inc(cT_ready, 1)
                for u in range(U):
                    b = i * U + u
                    act.wait_ge(kv, signals(b + 1))
                    act.activation(sq[:, u, :, :], ps[:, u, 1:3, 0:D], ACT.Square).then_inc(sq_ready, 1)
                    act.activation(vv[:, u, :, :], ps[:, u, 1:3, D:2 * D], ACT.Copy).then_inc(vv_ready, 1)
                for u in range(U):
                    b = i * U + u
                    act.wait_ge(k_tr, signals(b + 1))
                    for k in range(KT):
                        ins = act.activation(kT[:, u, k, :], ps[:, u, 0, 2 * k * P:2 * (k + 1) * P], ACT.Identity, scale=vec[:, 3, k:k + 1])
                    ins.then_inc(kT_ready, 1)
                for u in range(U):
                    b = i * U + u
                    act.wait_ge(sc_ready, signals(b + 1))
                    act.activation(pr[:, u, :], sc[:, u, :], ACT.Exp, bias=nm[:, u, :], accum_out=rs[:, u, :]).then_inc(pr_ready, 1)
                for u in range(U):
                    b = i * U + u
                    act.wait_ge(p_tr, signals(b + 1))
                    act.activation(pT[:, u, 0:2, :], ps[:, u, 0, 0:2 * P].rearrange("p (j q) -> p j q", j=2), ACT.Copy)
                    act.activation(pT[0:S + 1, u, 2, :], ps[0:S + 1, u, 0, 2 * P:3 * P], ACT.Copy).then_inc(pT_ready, 1)
                for u in range(U):
                    b = i * U + u
                    act.wait_ge(o_tr, signals(b + 1))
                    act.activation(OT[:, :, bass.ts(b, S)], ps[:, u, 1, 0:KT * S].rearrange("p (k q) -> p k q", k=KT), ACT.Copy).then_inc(oT_ready, 1)

        @block.vector
        def _(dve):
            link = Link(dve, dl)
            opens(dve, cve_ready, cn_ready, ss_ready, kn_ready, sc_ready, om_ready, mb_written)
            dve.wait_ge(mb_zeroed, 1)
            with dve.Fori(0, G) as i:
                link.loop(i, 6 * U)
                for u in range(U):
                    b = i * U + u
                    dve.wait_ge(sc_ready, signals(i * U))
                    dve.tensor_scalar(mb[:, u, 0:CTX], mask8[:, b, :], BIG, -BIG, ALU.mult, ALU.add).then_inc(mb_written, 1)
                for u in range(U):
                    b = i * U + u
                    dve.wait_ge(cx_loaded[u], 16 * (i + 1))
                    for j in range(2):
                        ins = dve.bn_stats(cst[:, u, j, :], cx[:, u, j, :])
                    link(ins)
                    dve.memset(carry[:, u:u + 1], 0.0)
                    for j in range(2):
                        ins = dve.bn_aggr(cmv[:, u, j, :], cst[:, u, j, :])
                    link(ins)
                    dve.tensor_scalar(cve[:, u, :], cmv[:, u, :, 1], LN_EPS, None, ALU.add).then_inc(cve_ready, 1)
                for u in range(U):
                    b = i * U + u
                    dve.wait_ge(crs_ready, signals(b + 1))
                    dve.wait_ge(c_tr, signals(i * U))
                    for j in range(2):
                        ins = dve.tensor_scalar(cn[:, u, j, :], cx[:, u, j, :], cmv[:, u, j, 0:1], crs[:, u, j:j + 1], ALU.subtract, ALU.mult)
                    ins.then_inc(cn_ready, 1)
                for u in range(U):
                    b = i * U + u
                    dve.wait_ge(sq_ready, signals(b + 1))
                    link(dve.tensor_reduce(ss[:, u, :], sq[:, u, :, :].rearrange("p j (h d) -> p (j h) d", h=H), AXX, ALU.add))
                    dve.tensor_scalar(ss[:, u, :], ss[:, u, :], 1.0 / HD, 1e-16, ALU.mult, ALU.max).then_inc(ss_ready, 1)
                for u in range(U):
                    b = i * U + u
                    dve.wait_ge(rn_ready, signals(b + 1))
                    dve.wait_ge(vv_ready, signals(b + 1))
                    for j in range(2):
                        ins = dve.tensor_tensor(kn[:, u, j, :].rearrange("p (h d) -> p h d", h=H),
                                                ps[:, u, 1 + j, 0:D].rearrange("p (h d) -> p h d", h=H),
                                                bc(rn[:, u, j * H:(j + 1) * H].unsqueeze(2), P, H, HD), ALU.mult)
                    ins.then_inc(kn_ready, 1)
                for u in range(U):
                    b = i * U + u
                    dve.wait_ge(scores, signals(b + 1))
                    dve.wait_ge(mb_written, signals(b + 1))
                    dve.wait_ge(pr_ready, signals(i * U))
                    link(dve.tensor_tensor(sc[:, u, :], ps[:, u, 3, 0:NK], mb[:, u, :], ALU.add))
                    link(dve.tensor_reduce(mx[:, u, :], sc[:, u, :], AXX, ALU.max))
                    dve.tensor_scalar(nm[:, u, :], mx[:, u, :], -1.0, None, ALU.mult).then_inc(sc_ready, 1)
                for u in range(U):
                    b = i * U + u
                    dve.wait_ge(pr_ready, signals(b + 1))
                    link(dve.reciprocal(ri[:, u, :], rs[:, u, :]))
                for u in range(U):
                    b = i * U + u
                    dve.wait_ge(pv, signals(b + 1))
                    dve.scalar_tensor_tensor(om[:, u, :], ps[:, u, 3, 0:D], ri[:, u, :], blockmask[:], ALU.mult, ALU.mult).then_inc(om_ready, 1)
            link.end(G)


def phase2(nc, g):
    I, X = g.I, g.X
    H, DK, DV = 16, 16, 64
    HK = P // DK
    QKV = H * (2 * DK + DV)
    VT = H * DV // P
    with ExitStack() as ctx:
        s = Scope(nc, ctx, "s2")
        sb, sem = s.sb, s.sem
        ps = s.psum()[:].rearrange("p (u n) c -> p u n c", u=U)
        w = sb("w", [P, KT, QKV])
        wo = sb("wo", [P, VT, D])
        headmask = sb("headmask", [P, HK])
        batchmask = sb("batchmask", [P, P])
        half = sb("half", [P, 1])
        stats, mv, var, rstd = sb("stats", [P, NT, 6]), sb("mv", [P, NT, 2]), sb("var", [P, NT]), sb("rstd", [P, NT])
        xn = sb("xn", [P, U, D])
        xT = sb("xT", [P, U, KT, P])
        sq = sb("sq", [P, U, QKV])
        ss, nrm, rn = sb("ss", [P, U, 3 * H]), sb("nrm", [P, U, 3 * H]), sb("rn", [P, U, 3 * H])
        qk = sb("qk", [P, U, 2 * D])
        vv = sb("vv", [P, U, H * DV])
        kT = sb("kT", [P, U, KT, P])
        qb = sb("qb", [P, U, KT, HK, P])
        at = sb("at", [P, U, H, P])
        so, no, th, fac = sb("so", [P, U, H]), sb("no", [P, U, H]), sb("th", [P, U, H]), sb("fac", [P, U, H])
        on = sb("on", [P, U, H * DV])
        oT = sb("oT", [P, U, VT, P])
        load, half_ready, stat_ready, rstd_ready, dve_link, act_link = s.sems(
            "load half_ready stat_ready rstd_ready dve_link act_link")
        (ln_ready, x_tr, xT_ready, proj, sq_ready, ss_ready, nrm_ready, qk_ready, qk_tr, kT_ready, qb_ready, scores, relu_ready,
         at_ready, o_ready, sqo_ready, so_ready, th_ready, on_ready, o_tr, oT_ready, y_ready, x_done) = s.sems(
            "ln_ready x_tr xT_ready proj sq_ready ss_ready nrm_ready qk_ready qk_tr kT_ready qb_ready scores relu_ready "
            "at_ready o_ready sqo_ready so_ready th_ready on_ready o_tr oT_ready y_ready x_done")
        G = NT // U
        NLOAD = 4
        block = ctx.enter_context(nc.Block())

        def heads(ap, n):
            return ap.rearrange("p (h d) -> p h d", h=n)

        @block.sync
        def _(sp):
            for dst, src in ((w, "p2_w"), (wo, "p2_wo"), (headmask, "headmask8"), (batchmask, "batchmask")):
                sp.dma_start(dst[:], I[src]).then_inc(load, 16)
            sp.wait_ge(load, 16 * NLOAD)

        @block.gpsimd
        def _(pool):
            pool.memset(half[:], -0.5).then_inc(half_ready, 1)
            pool.wait_ge(half_ready, 1)
            pool.wait_ge(stat_ready, 1)
            pool.tensor_tensor(rstd[:], var[:], bc(half[:], P, NT), ALU.pow).then_inc(rstd_ready, 1)

        @block.tensor
        def _(pe):
            opens(pe, x_tr, proj, qk_tr, scores, o_ready, o_tr, y_ready)
            pe.wait_ge(load, 16 * NLOAD)
            with pe.Fori(0, G) as i:
                for u in range(U):
                    t = i * U + u
                    pe.wait_ge(ln_ready, signals(t + 1))
                    pe.wait_ge(oT_ready, signals(i * U))
                    for k in range(KT):
                        mm = pe.transpose(ps[:, u, 3, tok(k)], xn[:, u, tok(k)], g.ident[:])
                    mm.then_inc(x_tr, 1)
                for u in range(U):
                    t = i * U + u
                    pe.wait_ge(xT_ready, signals(t + 1))
                    pe.wait_ge(x_done, signals(i * U))
                    for n in range(QKV // C):
                        for k in range(KT):
                            mm = pe.matmul(ps[:, u, n, :], lhsT=xT[:, u, k, :], rhs=w[:, k, n * C:(n + 1) * C], start=k == 0, stop=k == KT - 1)
                    mm.then_inc(proj, 1)
                for u in range(U):
                    t = i * U + u
                    pe.wait_ge(qk_ready, signals(t + 1))
                    for k in range(2 * KT):
                        mm = pe.transpose(ps[:, u, 3, tok(k)], qk[:, u, tok(k)], g.ident[:])
                    mm.then_inc(qk_tr, 1)
                for u in range(U):
                    t = i * U + u
                    pe.wait_ge(qb_ready, signals(t + 1))
                    for n in range(4):
                        k, h = divmod(4 * n, HK)
                        mm = pe.matmul(ps[:, u, n, :], lhsT=kT[:, u, k, :], rhs=qb[:, u, k, h:h + 4, :], start=True, stop=True)
                    mm.then_inc(scores, 1)
                for u in range(U):
                    t = i * U + u
                    pe.wait_ge(at_ready, signals(t + 1))
                    for h in range(H):
                        mm = pe.matmul(ps[:, u, h // 8, h % 8 * DV:(h % 8 + 1) * DV], lhsT=at[:, u, h, :], rhs=vv[:, u, h * DV:(h + 1) * DV],
                                       start=True, stop=True)
                    mm.then_inc(o_ready, 1)
                for u in range(U):
                    t = i * U + u
                    pe.wait_ge(on_ready, signals(t + 1))
                    for k in range(VT):
                        mm = pe.transpose(ps[:, u, 2 + k // 4, tok(k % 4)], on[:, u, tok(k)], g.ident[:])
                    mm.then_inc(o_tr, 1)
                for u in range(U):
                    t = i * U + u
                    pe.wait_ge(oT_ready, signals(t + 1))
                    for k in range(VT):
                        mm = pe.matmul(ps[:, u, 0, 0:D], lhsT=oT[:, u, k, :], rhs=wo[:, k, :], start=k == 0, stop=k == VT - 1)
                    mm.then_inc(y_ready, 1)

        @block.scalar
        def _(act):
            link = Link(act, act_link)
            opens(act, xT_ready, sq_ready, nrm_ready, kT_ready, at_ready, sqo_ready, th_ready, oT_ready)
            with act.Fori(0, G) as i:
                link.loop(i, U)
                for u in range(U):
                    t = i * U + u
                    act.wait_ge(x_tr, signals(t + 1))
                    act.activation(xT[:, u, :, :], ps[:, u, 3, 0:KT * P].rearrange("p (k q) -> p k q", k=KT), ACT.Copy).then_inc(xT_ready, 1)
                for u in range(U):
                    t = i * U + u
                    act.wait_ge(proj, signals(t + 1))
                    act.activation(sq[:, u, :], ps[:, u, 0:3, :].rearrange("p n c -> p (n c)"), ACT.Square).then_inc(sq_ready, 1)
                for u in range(U):
                    t = i * U + u
                    act.wait_ge(ss_ready, signals(t + 1))
                    act.activation(nrm[:, u, :], ss[:, u, :], ACT.Sqrt).then_inc(nrm_ready, 1)
                for u in range(U):
                    t = i * U + u
                    act.wait_ge(qk_tr, signals(t + 1))
                    act.activation(kT[:, u, :, :], ps[:, u, 3, KT * P:2 * KT * P].rearrange("p (k q) -> p k q", k=KT), ACT.Copy).then_inc(kT_ready, 1)
                for u in range(U):
                    t = i * U + u
                    act.wait_ge(relu_ready, signals(t + 1))
                    act.activation(at[:, u, :, :], at[:, u, :, :], ACT.Square).then_inc(at_ready, 1)
                for u in range(U):
                    t = i * U + u
                    act.wait_ge(o_ready, signals(t + 1))
                    act.activation(sq[:, u, 0:H * DV], ps[:, u, 0:2, :].rearrange("p n c -> p (n c)"), ACT.Square).then_inc(sqo_ready, 1)
                for u in range(U):
                    t = i * U + u
                    act.wait_ge(so_ready, signals(t + 1))
                    link(act.activation(no[:, u, :], so[:, u, :], ACT.Sqrt))
                for u in range(U):
                    act.activation(th[:, u, :], no[:, u, :], ACT.Tanh).then_inc(th_ready, 1)
                for u in range(U):
                    t = i * U + u
                    act.wait_ge(o_tr, signals(t + 1))
                    act.activation(oT[:, u, :, :], ps[:, u, 2:4, :].rearrange("p n (k q) -> p (n k) q", k=4), ACT.Copy).then_inc(oT_ready, 1)
            link.end(G)

        @block.vector
        def _(dve):
            link = Link(dve, dve_link)
            row_stats(dve, link, X, stats, mv, var, LN_EPS).then_inc(stat_ready, 1)
            dve.wait_ge(rstd_ready, 1)
            dve.wait_ge(load, 16 * NLOAD)
            opens(dve, ln_ready, ss_ready, qk_ready, qb_ready, relu_ready, so_ready, on_ready, x_done)
            with dve.Fori(0, G) as i:
                link.loop(i, 5 * U)
                for u in range(U):
                    t = i * U + u
                    dve.wait_ge(x_tr, signals(i * U))
                    dve.tensor_scalar(xn[:, u, :], X[:, t, :], mv[:, t, 0:1], rstd[:, bass.ds(t, 1)],
                                      ALU.subtract, ALU.mult).then_inc(ln_ready, 1)
                for u in range(U):
                    t = i * U + u
                    dve.wait_ge(sq_ready, signals(t + 1))
                    dve.tensor_reduce(ss[:, u, 0:2 * H], heads(sq[:, u, 0:2 * D], 2 * H), AXX, ALU.add)
                    link(dve.tensor_reduce(ss[:, u, 2 * H:3 * H], heads(sq[:, u, 2 * D:QKV], H), AXX, ALU.add))
                    dve.tensor_scalar(ss[:, u, :], ss[:, u, :], 1e-24, None, ALU.max).then_inc(ss_ready, 1)
                for u in range(U):
                    t = i * U + u
                    dve.wait_ge(nrm_ready, signals(t + 1))
                    link(dve.reciprocal(rn[:, u, :], nrm[:, u, :]))
                    dve.tensor_tensor(heads(vv[:, u, :], H), ps[:, u, 1:3, :].rearrange("p n (h d) -> p (n h) d", d=DV),
                                      bc(rn[:, u, 2 * H:3 * H].unsqueeze(2), P, H, DV), ALU.mult)
                    dve.tensor_tensor(heads(qk[:, u, :], 2 * H), heads(ps[:, u, 0, :], 2 * H),
                                      bc(rn[:, u, 0:2 * H].unsqueeze(2), P, 2 * H, DK), ALU.mult).then_inc(qk_ready, 1)
                for u in range(U):
                    t = i * U + u
                    dve.wait_ge(kT_ready, signals(t + 1))
                    for k in range(KT):
                        ins = dve.tensor_tensor(qb[:, u, k, :, :], bc(ps[:, u, 3, tok(k)].unsqueeze(1), P, HK, P),
                                                bc(headmask[:].unsqueeze(2), P, HK, P), ALU.mult)
                    ins.then_inc(qb_ready, 1)
                for u in range(U):
                    t = i * U + u
                    dve.wait_ge(scores, signals(t + 1))
                    dve.scalar_tensor_tensor(at[:, u, :, :], ps[:, u, :, :].rearrange("p n (h q) -> p (n h) q", q=P), 0.0,
                                             bc(batchmask[:].unsqueeze(1), P, H, P), ALU.max, ALU.mult).then_inc(relu_ready, 1)
                for u in range(U):
                    t = i * U + u
                    dve.wait_ge(sqo_ready, signals(t + 1))
                    dve.tensor_reduce(so[:, u, :], heads(sq[:, u, 0:H * DV], H), AXX, ALU.add).then_inc(so_ready, 1)
                for u in range(U):
                    t = i * U + u
                    dve.wait_ge(th_ready, signals(t + 1))
                    link(dve.tensor_scalar(no[:, u, :], no[:, u, :], 1e-12, None, ALU.max))
                    link(dve.reciprocal(fac[:, u, :], no[:, u, :]))
                    link(dve.tensor_tensor(fac[:, u, :], fac[:, u, :], th[:, u, :], ALU.mult))
                    dve.tensor_tensor(heads(on[:, u, :], H), ps[:, u, 0:2, :].rearrange("p n (h d) -> p (n h) d", d=DV),
                                      bc(fac[:, u, :].unsqueeze(2), P, H, DV), ALU.mult).then_inc(on_ready, 1)
                for u in range(U):
                    t = i * U + u
                    dve.wait_ge(y_ready, signals(t + 1))
                    dve.tensor_tensor(X[:, t, :], X[:, t, :], ps[:, u, 0, 0:D], ALU.add).then_inc(x_done, 1)
            link.end(G)


def phase3(nc, g):
    I, X = g.I, g.X
    H, K, NK = 8, 8, 64
    PH = 2 * H
    M = H * K
    BN_EPS = 1e-5
    with ExitStack() as ctx:
        s = Scope(nc, ctx, "s3")
        sb, sems = s.sb, s.sems
        banks = s.psum()
        n = Normed(s)
        weights = sb("weights", [P, NT, M])
        experts = sb("experts", [P, NT, M], U32)
        with ExitStack() as sctx:
            q = Scope(nc, sctx, "s3s")
            xT = q.sb("xT", [P, KT, T])
            best = q.sb("best", [P, PH, NT, K])
            place = q.sb("place", [P, PH, NT, K], U32)
            normed_transposed(nc, g, s, banks, n, xT)
            key_scores(nc, g, banks, xT, best, place, BN_EPS)
            choose(nc, g, best, place, weights, experts)
        experts_of(nc, g, banks, n, weights, experts)


def key_scores(nc, g, banks, xT, best, place, eps):
    I = g.I
    PH, NK, K = 16, 64, 8
    with ExitStack() as ctx:
        s = Scope(nc, ctx, "s3k")
        sb = s.sb
        wq = sb("wq", [P, U, KT, P])
        keys = sb("keys", [P, U, NK])
        gb = sb("gb", [P, 2, PH])
        half = sb("half", [P, 1])
        st, mv, ve, rs = sb("st", [P, U, NC, 6]), sb("mv", [P, U, 2]), sb("ve", [P, U]), sb("rs", [P, U])
        gain, shift = sb("gain", [P, U]), sb("shift", [P, U])
        carry = sb("carry", [P, U, 3])
        qn = sb("qn", [P, U, T])
        sim = sb("sim", [P, U, NT, NK])
        bst = sb("bst", [P, U, NT, K])
        plc = sb("plc", [P, U, NT, K], U32)
        w_loaded = [s.sem(f"w_loaded{u}") for u in range(U)]
        (gb_loaded, half_ready, dve_link, q_ready, ve_ready, rs_ready, aff_ready, qn_ready, sim_ready, sim_copied) = s.sems(
            "gb_loaded half_ready dve_link q_ready ve_ready rs_ready aff_ready qn_ready sim_ready sim_copied")
        G = PH // U
        simb = banks[:, 4:8, :].rearrange("p (u n) (t k) -> p u (n t) k", u=U, k=NK)
        block = ctx.enter_context(nc.Block())

        @block.sync
        def _(sp):
            sp.dma_start(gb[:], I["p3_gb"]).then_inc(gb_loaded, 16)
            with sp.Fori(0, G) as i:
                for u in range(U):
                    c = i * U + u
                    sp.wait_ge(sim_ready, signals(i * U))
                    sp.dma_start(wq[:, u, :, :], I["p3_wq"][c]).then_inc(w_loaded[u], 16)
                    sp.dma_start(keys[:, u, :], I["p3_keys"][c]).then_inc(w_loaded[u], 16)

        @block.gpsimd
        def _(pool):
            pool.memset(half[:], -0.5).then_inc(half_ready, 1)
            pool.wait_ge(half_ready, 1)
            opens(pool, rs_ready)
            with pool.Fori(0, G) as i:
                for u in range(U):
                    pool.wait_ge(ve_ready, signals(i * U + u + 1))
                    pool.tensor_tensor(rs[:, u:u + 1], ve[:, u:u + 1], half[:], ALU.pow).then_inc(rs_ready, 1)

        @block.tensor
        def _(pe):
            opens(pe, q_ready, sim_ready)
            with pe.Fori(0, G) as i:
                for u in range(U):
                    c = i * U + u
                    pe.wait_ge(w_loaded[u], 32 * (i + 1))
                    pe.wait_ge(qn_ready, signals(c))
                    for n in range(NC):
                        for k in range(KT):
                            mm = pe.matmul(banks[:, n, :], lhsT=wq[:, u, k, :], rhs=xT[:, k, n * C:(n + 1) * C], start=k == 0, stop=k == KT - 1)
                    mm.then_inc(q_ready, 1)
                    pe.wait_ge(qn_ready, signals(c + 1))
                    pe.wait_ge(sim_copied, signals(i * U))
                    for t in range(NT):
                        mm = pe.matmul(simb[:, u, t, :], lhsT=qn[:, u, tok(t)], rhs=keys[:, u, :], start=True, stop=True)
                    mm.then_inc(sim_ready, 1)

        @block.scalar
        def _(act):
            opens(act, qn_ready, sim_copied)
            with act.Fori(0, G) as i:
                for u in range(U):
                    c = i * U + u
                    act.wait_ge(aff_ready, signals(c + 1))
                    act.activation(qn[:, u, :], banks[:, 0:4, :].rearrange("p n c -> p (n c)"), ACT.Identity,
                                   bias=shift[:, u:u + 1], scale=gain[:, u:u + 1]).then_inc(qn_ready, 1)
                    act.wait_ge(sim_ready, signals(c + 1))
                    act.activation(sim[:, u, :, :], simb[:, u, :, :], ACT.Copy).then_inc(sim_copied, 1)

        @block.vector
        def _(dve):
            link = Link(dve, dve_link)
            dve.wait_ge(gb_loaded, 16)
            opens(dve, ve_ready, aff_ready)
            with dve.Fori(0, G) as i:
                link.loop(i, 7 * U)
                for u in range(U):
                    c = i * U + u
                    dve.wait_ge(q_ready, signals(c + 1))
                    for n in range(NC):
                        ins = dve.bn_stats(st[:, u, n, :], banks[:, n, :])
                    link(ins)
                    dve.memset(carry[:, u, 0:1], 0.0)
                    link(dve.bn_aggr(mv[:, u, :], st[:, u, :, :]))
                    dve.tensor_scalar(ve[:, u:u + 1], mv[:, u, 1:2], eps, None, ALU.add).then_inc(ve_ready, 1)
                    dve.wait_ge(rs_ready, signals(c + 1))
                    link(dve.tensor_tensor(gain[:, u:u + 1], rs[:, u:u + 1], gb[:, 0, bass.ds(c, 1)], ALU.mult))
                    link(dve.tensor_tensor(shift[:, u:u + 1], mv[:, u, 0:1], gain[:, u:u + 1], ALU.mult))
                    dve.tensor_tensor(shift[:, u:u + 1], gb[:, 1, bass.ds(c, 1)], shift[:, u:u + 1], ALU.subtract).then_inc(aff_ready, 1)
                    dve.wait_ge(sim_copied, signals(c + 1))
                    dve.memset(carry[:, u, 1:2], 0.0)
                    for t in range(NT):
                        ins = dve.max(bst[:, u, t, :], sim[:, u, t, :])
                    link(ins)
                    dve.memset(carry[:, u, 2:3], 0.0)
                    for t in range(NT):
                        ins = dve.max_index(plc[:, u, t, :], bst[:, u, t, :], sim[:, u, t, :])
                    link(ins)
                    dve.tensor_copy(best[:, c, :, :], bst[:, u, :, :])
                    link(dve.tensor_copy(place[:, c, :, :], plc[:, u, :, :]))
            link.end(G)


def choose(nc, g, best, place, weights, experts):
    H, K, NK = 8, 8, 64
    with ExitStack() as ctx:
        s = Scope(nc, ctx, "s3c")
        sb = s.sb
        cand = sb("cand", [P, NT, K * K])
        top = sb("top", [P, NT, K])
        pos = sb("pos", [P, NT, K], U32)
        part = sb("part", [P, 2, NT, K], U32)
        partf = sb("partf", [P, 2, NT * K])
        keyf = sb("keyf", [P, 2, NT, K])
        count = sb("count", [P, K])
        hit = sb("hit", [P, 2, NT, K, K])
        key = sb("key", [P, 2, NT, K])
        ex, den, rden = sb("ex", [P, NT, K]), sb("den", [P, NT]), sb("rden", [P, NT])
        idx = sb("idx", [P, NT, K])
        carry = sb("carry", [P, 2])
        dve_link, count_loaded, diff_ready, ex_ready = s.sems("dve_link count_loaded diff_ready ex_ready")
        block = ctx.enter_context(nc.Block())

        @block.sync
        def _(sp):
            sp.dma_start(count[:], g.I["count8"]).then_inc(count_loaded, 16)

        @block.scalar
        def _(act):
            opens(act, ex_ready)
            with act.Fori(0, H) as h:
                act.wait_ge(diff_ready, signals(h + 1))
                act.activation(ex[:], ex[:], ACT.Exp).then_inc(ex_ready, 1)

        @block.vector
        def _(dve):
            link = Link(dve, dve_link)
            dve.wait_ge(count_loaded, 16)
            opens(dve, diff_ready)
            with dve.Fori(0, H) as h:
                link.loop(h, 13)
                link(dve.tensor_tensor(cand[:].rearrange("p t (a b) -> p t a b", a=K), bc(best[:, h, :, :].unsqueeze(3), P, NT, K, K),
                                       bc(best[:, h + H, :, :].unsqueeze(2), P, NT, K, K), ALU.add))
                dve.memset(carry[:, 0:1], 0.0)
                for t in range(NT):
                    ins = dve.max(top[:, t, :], cand[:, t, :])
                link(ins)
                dve.tensor_tensor(ex[:], top[:], bc(top[:, :, 0:1], P, NT, K), ALU.subtract).then_inc(diff_ready, 1)
                for t in range(NT):
                    ins = dve.max_index(pos[:, t, :], top[:, t, :], cand[:, t, :])
                link(ins)
                dve.tensor_scalar(part[:, 0, :, :], pos[:], 3, None, ALU.logical_shift_right)
                link(dve.tensor_scalar(part[:, 1, :, :], pos[:], K - 1, None, ALU.bitwise_and))
                dve.tensor_copy(partf[:], part[:].rearrange("p j t k -> p j (t k)"))
                dve.tensor_copy(keyf[:, 0, :, :], place[:, h, :, :])
                link(dve.tensor_copy(keyf[:, 1, :, :], place[:, h + H, :, :]))
                for j in range(2):
                    ins = dve.tensor_tensor(hit[:, j, :, :, :].rearrange("p t k a -> p (t k) a"), bc(partf[:, j, :].unsqueeze(2), P, NT * K, K),
                                            bc(count[:].unsqueeze(1), P, NT * K, K), ALU.is_equal)
                link(ins)
                for j in range(2):
                    ins = dve.tensor_tensor(hit[:, j, :, :, :], hit[:, j, :, :, :], bc(keyf[:, j, :, :].unsqueeze(2), P, NT, K, K), ALU.mult)
                link(ins)
                link(dve.tensor_reduce(key[:], hit[:], AXX, ALU.add))
                link(dve.scalar_tensor_tensor(idx[:], key[:, 0, :, :], float(NK), key[:, 1, :, :], ALU.mult, ALU.add))
                link(dve.tensor_copy(experts[:, :, bass.ts(h, K)], idx[:]))
                dve.wait_ge(ex_ready, signals(h + 1))
                link(dve.tensor_reduce(den[:], ex[:], AXX, ALU.add))
                link(dve.reciprocal(rden[:], den[:]))
                link(dve.tensor_tensor(weights[:, :, bass.ts(h, K)], ex[:], bc(rden[:].unsqueeze(2), P, NT, K), ALU.mult))
            link.end(H)


def experts_of(nc, g, banks, n, weights, experts):
    I, X = g.I, g.X
    H, K = 8, 8
    R = 4
    with ExitStack() as ctx:
        s = Scope(nc, ctx, "s3e")
        sb = s.sb
        xn = sb("xn", [P, U, D])
        idx = sb("idx", [P, U, H * K], U32)
        wts = sb("wts", [P, U, H * K])
        rows = sb("rows", [P, R, K, 2 * D])
        hd, hg, hw = sb("hd", [P, R, K]), sb("hg", [P, R, K]), sb("hw", [P, R, K])
        one = sb("one", [P, 2])
        gathered = [s.sem(f"gathered{r}") for r in range(R)]
        carried, dve_link, idx_ready, dots, hg_ready, scaled, summed, x_done = s.sems("carried dve_link idx_ready dots hg_ready scaled summed x_done")
        G = NT // U
        block = ctx.enter_context(nc.Block())

        @block.gpsimd
        def _(pool):
            pool.memset(one[:], 1.0).then_inc(carried, 1)
            with pool.Fori(0, G) as i:
                for u in range(U):
                    t = i * U + u
                    pool.wait_ge(idx_ready, signals(t + 1))
                    for h in range(H):
                        r = h % R
                        pool.wait_ge(summed, t * H + h + 1)
                        pool.wait_ge(carried, t * H + h + 1)
                        pool.tensor_tensor(one[:, 1:2], one[:, 0:1], one[:, 0:1], ALU.mult).then_inc(carried, 1)
                        for k in range(K):
                            m = h * K + k
                            pool.indirect_dma_start(rows[:, r, k, :], None, I["p3_table"],
                                                    bass.IndirectOffsetOnAxis(idx[:, u, m:m + 1], 0)).then_inc(gathered[r], 16)

        @block.scalar
        def _(act):
            opens(act, hg_ready)
            with act.Fori(0, G) as i:
                for u in range(U):
                    for h in range(H):
                        v = (i * U + u) * H + h
                        act.wait_ge(dots, signals(v + 1))
                        act.activation(hg[:, h % R, :], hd[:, h % R, :], ACT.Gelu_apprx_tanh).then_inc(hg_ready, 1)

        @block.tensor
        def _(pe):
            pe.sem_inc(summed, R)
            with pe.Fori(0, G) as i:
                for u in range(U):
                    t = i * U + u
                    pe.wait_ge(x_done, signals(i * U))
                    for h in range(H):
                        pe.wait_ge(scaled, signals(t * H + h + 1))
                        for k in range(K):
                            mm = pe.matmul(banks[:, u, 0:D], lhsT=g.ident[:], rhs=rows[:, h % R, k, D:2 * D],
                                           start=h == 0 and k == 0, stop=h == H - 1 and k == K - 1)
                        mm.then_inc(summed, 1)

        @block.vector
        def _(dve):
            link = Link(dve, dve_link)
            opens(dve, idx_ready, dots, scaled, x_done)
            with dve.Fori(0, G) as i:
                link.loop(i, U * (H + 1))

                def scale(u, h):
                    v = (i * U + u) * H + h
                    r = h % R
                    dve.wait_ge(hg_ready, signals(v + 1))
                    link(dve.tensor_tensor(hw[:, r, :], hg[:, r, :], wts[:, u, h * K:(h + 1) * K], ALU.mult))
                    for k in range(K):
                        ins = dve.tensor_scalar(rows[:, r, k, D:2 * D], rows[:, r, k, D:2 * D], hw[:, r, k:k + 1], None, ALU.mult)
                    ins.then_inc(scaled, 1)

                for u in range(U):
                    t = i * U + u
                    dve.tensor_copy(wts[:, u, :], weights[:, t, :])
                    n.apply(dve, xn[:, u, :], X, t)
                    dve.tensor_copy(idx[:, u, :], experts[:, t, :]).then_inc(idx_ready, 1)
                for u in range(U):
                    t = i * U + u
                    dve.wait_ge(idx_ready, signals(t + 1))
                    for h in range(H):
                        r = h % R
                        dve.wait_ge(gathered[r], (t * (H // R) + h // R + 1) * (16 * K))
                        for k in range(K):
                            ins = dve.tensor_tensor_reduce(rows[:, r, k, 0:D], rows[:, r, k, 0:D], xn[:, u, :], 1.0, 0.0, ALU.mult, ALU.add, hd[:, r, k:k + 1])
                        ins.then_inc(dots, 1)
                        if h:
                            scale(u, h - 1)
                    scale(u, H - 1)
                    dve.wait_ge(summed, t * H + H + R)
                    link(dve.tensor_tensor(X[:, t, :], X[:, t, :], banks[:, u, 0:D], ALU.add))
                    dve.sem_inc(x_done, 1)
            link.end(G)


def phase4(nc, g):
    I, X = g.I, g.X
    H, HD = 16, 16
    HK = P // HD
    HG = P // S
    NG = H // HG
    GD = HG * HD
    CLAMP = 10000.0
    with ExitStack() as ctx:
        s = Scope(nc, ctx, "s4")
        sb, sem = s.sb, s.sem
        banks = s.psum()
        ps = banks[:].rearrange("p (u n) c -> p u n c", u=U)
        OT = sb("OT", [P, KT, T])
        wo = sb("wo", [P, KT, D])
        vec = sb("vec", [P, 4, KT])
        load = sem("load")
        NLOAD = 10
        with ExitStack() as actx:
            a = Scope(nc, actx, "s4a")
            sb = a.sb
            QT = sb("QT", [P, KT, T])
            wq = sb("wq", [P, KT, D])
            wk, wv = sb("wk", [DH, 2, D]), sb("wv", [DH, 2, D])
            headmask = sb("headmask", [P, HK])
            blockmask = sb("blockmask", [P, GD])
            sel = sb("sel", [P, S])
            KXT = sb("KXT", [P, KT, B])
            VX = sb("VX", [1, B, D])
            VM = sb("VM", [P, KT, B])
            VXT = sb("VXT", [P, KT, B])
            sums = sb("sums", [P, B, NG])
            cx = sb("cx", [B, DC])
            cxT = sb("cxT", [DH, 2, B])
            vx = sb("vx", [B, D])
            with ExitStack() as nctx:
                q = Scope(nc, nctx, "s4q")
                n = Normed(q)
                xT = q.sb("xT", [P, KT, T])
                normed_transposed(nc, g, q, banks, n, xT)
                c_tr, cT_ready, c_proj, kx_ready, vx_ready, vx_loaded, q_ready, q_read = a.sems(
                    "c_tr cT_ready c_proj kx_ready vx_ready vx_loaded q_ready q_read")
                block = nctx.enter_context(nc.Block())

                @block.sync
                def _(sp):
                    for dst, src in ((vec, "p4_vec"), (wq, "p4_wq"), (wk, "p4_wk"), (wv, "p4_wv"), (wo, "p4_wo"), (headmask, "headmask8"),
                                     (blockmask, "blockmask16"), (sel, "sel")):
                        sp.dma_start(dst[:], I[src]).then_inc(load, 16)
                    sp.dma_start(cx[:], I["ctx_768"][:, CTX - 1, :]).then_inc(load, 16)
                    sp.wait_ge(load, 16 * (NLOAD - 1))
                    sp.wait_ge(vx_ready, 1)
                    sp.dma_start(VX[:], vx[:]).then_inc(vx_loaded, 16)
                    sp.wait_ge(vx_loaded, 16)

                @block.tensor
                def _(pe):
                    pe.wait_ge(load, 16 * (NLOAD - 1))
                    opens(pe, q_ready)
                    for k in range(2):
                        mm = pe.transpose(banks[0:DH, 4, k * B:(k + 1) * B], cx[:, k * DH:(k + 1) * DH], g.ident[0:B, 0:B])
                    mm.then_inc(c_tr, 1)
                    pe.wait_ge(cT_ready, 1)
                    for m in range(KT):
                        for k in range(2):
                            pe.matmul(banks[:, 5, m * B:(m + 1) * B], lhsT=wk[:, k, tok(m)], rhs=cxT[:, k, :], start=k == 0, stop=k == 1)
                    for m in range(KT):
                        for k in range(2):
                            pe.matmul(banks[:, 7, m * B:(m + 1) * B], lhsT=wv[:, k, tok(m)], rhs=cxT[:, k, :], start=k == 0, stop=k == 1)
                    for k in range(2):
                        mm = pe.matmul(banks[0:B, 6, 0:D], lhsT=cxT[:, k, :], rhs=wv[:, k, :], start=k == 0, stop=k == 1)
                    mm.then_inc(c_proj, 1)
                    with pe.Fori(0, NC) as c:
                        pe.wait_ge(q_read, signals(c))
                        for m in range(KT):
                            for k in range(KT):
                                mm = pe.matmul(banks[:, m, :], lhsT=wq[:, k, tok(m)], rhs=xT[:, k, bass.ts(c, C)], start=k == 0, stop=k == KT - 1)
                        mm.then_inc(q_ready, 1)

                @block.scalar
                def _(act):
                    act.wait_ge(load, 16 * (NLOAD - 1))
                    act.wait_ge(c_tr, 1)
                    act.activation(cxT[:], banks[0:DH, 4, 0:2 * B].rearrange("p (k b) -> p k b", k=2), ACT.Copy).then_inc(cT_ready, 1)
                    act.wait_ge(c_proj, 1)
                    for m in range(KT):
                        ins = act.activation(KXT[:, m, :], banks[:, 5, m * B:(m + 1) * B], ACT.Identity, bias=vec[:, 1, m:m + 1])
                    ins.then_inc(kx_ready, 1)
                    act.activation(VXT[:], banks[:, 7, 0:KT * B].rearrange("p (k b) -> p k b", k=KT), ACT.Copy)
                    act.activation(vx[:], banks[0:B, 6, 0:D], ACT.Copy).then_inc(vx_ready, 1)
                    act.wait_ge(kx_ready, 1)

                @block.vector
                def _(dve):
                    dve.wait_ge(load, 16 * (NLOAD - 1))
                    opens(dve, q_read)
                    with dve.Fori(0, NC) as c:
                        dve.wait_ge(q_ready, signals(c + 1))
                        for m in range(KT):
                            ins = dve.tensor_scalar(QT[:, m, bass.ts(c, C)], banks[:, m, :], vec[:, 0, m:m + 1], HD ** -0.5, ALU.add, ALU.mult)
                        ins.then_inc(q_read, 1)

            attend(nc, g, ps, dict(
                H=H, HG=HG, NG=NG, GD=GD, HK=HK, CLAMP=CLAMP, QT=QT, OT=OT, wk=wk, wv=wv, vec=vec, KXT=KXT, VX=VX, VM=VM,
                sums=sums, headmask=headmask, blockmask=blockmask, sel=sel))
            guard(nc, g, sums, VM, VXT, vec, OT)
        project_out(nc, g, "s4o", banks, OT, wo, vec[:, 3, :])


def attend(nc, g, ps, v):
    I = g.I
    H, HG, NG, GD, HK, CLAMP = (v[n] for n in "H HG NG GD HK CLAMP".split())
    QT, OT, wk, wv, vec, KXT, VX, VM, sums = (v[n] for n in "QT OT wk wv vec KXT VX VM sums".split())
    headmask, blockmask, sel = (v[n] for n in "headmask blockmask sel".split())
    with ExitStack() as ctx:
        s = Scope(nc, ctx, "s4b")
        sb = s.sb
        cx = sb("cx", [P, U, 2, DC])
        cT = sb("cT", [DH, U, 2, 2 * P])
        kT = sb("kT", [P, U, KT, 2 * P])
        vv = sb("vv", [P, U, 2, D])
        qb = sb("qb", [P, U, KT, HK, S])
        sc = sb("sc", [P, U, NG, CTX])
        mx, nm, ri = sb("mx", [P, U, NG]), sb("nm", [P, U, NG]), sb("ri", [P, U, NG])
        pr = sb("pr", [P, U, NG, CTX])
        rs = sb("rs", [P, U, NG])
        pT = sb("pT", [P, U, 2, NG * P])
        pX = sb("pX", [1, U, NG * P])
        om = sb("om", [P, U, NG, GD])
        ones = sb("ones", [P, 2])
        cx_loaded = [s.sem(f"cx_loaded{u}") for u in range(U)]
        (c_tr, cT_ready, kv, kT_ready, vv_ready, qb_ready, scores, sc_ready, pr_ready, p_tr, pT_ready, pX_ready, pv, om_ready, o_tr, oT_ready,
         vm_ready, dve_link, ones_ready) = s.sems(
            "c_tr cT_ready kv kT_ready vv_ready qb_ready scores sc_ready pr_ready p_tr pT_ready pX_ready pv om_ready o_tr oT_ready "
            "vm_ready dve_link ones_ready")
        G = B // U
        block = ctx.enter_context(nc.Block())

        @block.sync
        def _(sp):
            with sp.Fori(0, G) as i:
                for u in range(U):
                    b = i * U + u
                    sp.wait_ge(c_tr, signals(i * U))
                    sp.dma_start(cx[:, u, :, :], I["ctx_768"][b, 0:2 * P, :].rearrange("(j p) c -> p j c", p=P)).then_inc(cx_loaded[u], 16)

        @block.gpsimd
        def _(pool):
            pool.memset(ones[:], 1.0).then_inc(ones_ready, 1)
            opens(pool, qb_ready)
            with pool.Fori(0, G) as i:
                for u in range(U):
                    b = i * U + u
                    pool.wait_ge(scores, signals(i * U))
                    pool.tensor_tensor(qb[:, u, :, :, :], bc(QT[:, :, bass.ts(b, S)].unsqueeze(2), P, KT, HK, S),
                                       bc(headmask[:].unsqueeze(1).unsqueeze(3), P, KT, HK, S), ALU.mult).then_inc(qb_ready, 1)

        @block.tensor
        def _(pe):
            pe.wait_ge(ones_ready, 1)
            opens(pe, c_tr, kv, scores, p_tr, pv, o_tr)
            with pe.Fori(0, G) as i:
                for u in range(U):
                    b = i * U + u
                    pe.wait_ge(cx_loaded[u], 16 * (i + 1))
                    pe.wait_ge(vm_ready, signals(i * U))
                    pe.wait_ge(pT_ready, signals(i * U))
                    for k in range(2):
                        for j in range(2):
                            mm = pe.transpose(ps[0:DH, u, 0, tok(2 * k + j)], cx[:, u, j, k * DH:(k + 1) * DH], g.ident[:])
                    mm.then_inc(c_tr, 1)
                for u in range(U):
                    b = i * U + u
                    pe.wait_ge(cT_ready, signals(b + 1))
                    for m in range(KT):
                        for k in range(2):
                            pe.matmul(ps[:, u, 1, m * 2 * P:(m + 1) * 2 * P], lhsT=wk[:, k, tok(m)], rhs=cT[:, u, k, :], start=k == 0, stop=k == 1)
                    for j in range(2):
                        for k in range(2):
                            mm = pe.matmul(ps[:, u, 2, j * D:(j + 1) * D], lhsT=cT[:, u, k, tok(j)], rhs=wv[:, k, :], start=k == 0, stop=k == 1)
                    mm.then_inc(kv, 1)
                for u in range(U):
                    b = i * U + u
                    pe.wait_ge(kT_ready, signals(b + 1))
                    pe.wait_ge(vv_ready, signals(b + 1))
                    pe.wait_ge(qb_ready, signals(b + 1))
                    for n in range(NG):
                        k, h = divmod(n * HG, HK)
                        pe.matmul(ps[:, u, n, 0:2 * P], lhsT=qb[:, u, k, h:h + HG, :], rhs=kT[:, u, k, :], start=True, stop=True)
                        mm = pe.matmul(ps[:, u, n, 2 * P:CTX], lhsT=qb[:, u, k, h:h + HG, :], rhs=KXT[:, k, bass.ds(b, 1)], start=True, stop=True)
                    mm.then_inc(scores, 1)
                for u in range(U):
                    b = i * U + u
                    pe.wait_ge(pr_ready, signals(b + 1))
                    for n in range(NG):
                        for j in range(2):
                            pe.transpose(ps[:, u, j, tok(n)], pr[:, u, n, tok(j)], g.ident[:])
                    for n in range(NG):
                        mm = pe.transpose(ps[0:1, u, 2, tok(n)], pr[:, u, n, 2 * P:CTX], g.ident[:])
                    mm.then_inc(p_tr, 1)
                for u in range(U):
                    b = i * U + u
                    pe.wait_ge(pT_ready, signals(b + 1))
                    pe.wait_ge(pX_ready, signals(b + 1))
                    for n in range(NG):
                        gd = slice(n * GD, (n + 1) * GD)
                        for j in range(2):
                            pe.matmul(ps[:, u, 3, gd], lhsT=pT[:, u, j, tok(n)], rhs=vv[:, u, j, gd], start=j == 0, stop=False)
                        mm = pe.matmul(ps[:, u, 3, gd], lhsT=pX[:, u, tok(n)], rhs=VX[:, b, gd], start=False, stop=True)
                    mm.then_inc(pv, 1)
                for u in range(U):
                    b = i * U + u
                    pe.wait_ge(om_ready, signals(b + 1))
                    for k in range(KT):
                        pe.matmul(ps[:, u, 0, k * S:(k + 1) * S], lhsT=om[:, u, 2 * k:2 * k + 2, :], rhs=sel[:], start=True, stop=True)
                    for k in range(KT):
                        for j in range(2):
                            mm = pe.matmul(ps[:, u, 0, KT * S + k:KT * S + k + 1], lhsT=vv[:, u, j, tok(k)], rhs=ones[:, 0:1], start=j == 0, stop=j == 1)
                    mm.then_inc(o_tr, 1)

        @block.scalar
        def _(act):
            opens(act, cT_ready, kT_ready, pr_ready, pT_ready, oT_ready, vm_ready)
            with act.Fori(0, G) as i:
                for u in range(U):
                    b = i * U + u
                    act.wait_ge(c_tr, signals(b + 1))
                    act.activation(cT[:, u, :, :], ps[0:DH, u, 0, :].rearrange("p (k q) -> p k q", k=2), ACT.Copy).then_inc(cT_ready, 1)
                for u in range(U):
                    b = i * U + u
                    act.wait_ge(kv, signals(b + 1))
                    for m in range(KT):
                        ins = act.activation(kT[:, u, m, :], ps[:, u, 1, m * 2 * P:(m + 1) * 2 * P], ACT.Identity, bias=vec[:, 1, m:m + 1])
                    ins.then_inc(kT_ready, 1)
                for u in range(U):
                    b = i * U + u
                    act.wait_ge(sc_ready, signals(b + 1))
                    for n in range(NG):
                        ins = act.activation(pr[:, u, n, :], sc[:, u, n, :], ACT.Exp, bias=nm[:, u, n:n + 1], accum_out=rs[:, u, n:n + 1])
                    ins.then_inc(pr_ready, 1)
                for u in range(U):
                    b = i * U + u
                    act.wait_ge(p_tr, signals(b + 1))
                    act.activation(pT[:, u, :, :], ps[:, u, 0:2, :], ACT.Copy).then_inc(pT_ready, 1)
                for u in range(U):
                    b = i * U + u
                    act.wait_ge(o_tr, signals(b + 1))
                    for k in range(KT):
                        ins = act.activation(OT[:, k, bass.ts(b, S)], ps[:, u, 0, k * S:(k + 1) * S], ACT.Identity, bias=vec[:, 2, k:k + 1])
                    act.activation(VM[:, :, bass.ds(b, 1)], ps[:, u, 0, KT * S:KT * S + KT].unsqueeze(2), ACT.Copy).then_inc(vm_ready, 1)

        @block.vector
        def _(dve):
            link = Link(dve, dve_link)
            opens(dve, vv_ready, sc_ready, pX_ready, om_ready)
            with dve.Fori(0, G) as i:
                link.loop(i, 4 * U)
                for u in range(U):
                    b = i * U + u
                    dve.wait_ge(kv, signals(b + 1))
                    dve.tensor_copy(vv[:, u, :, :], ps[:, u, 2, :].rearrange("p (j d) -> p j d", j=2)).then_inc(vv_ready, 1)
                for u in range(U):
                    b = i * U + u
                    dve.wait_ge(scores, signals(b + 1))
                    dve.wait_ge(pr_ready, signals(i * U))
                    link(dve.tensor_scalar(sc[:, u, :, :], ps[:, u, :, 0:CTX], CLAMP, -CLAMP, ALU.min, ALU.max))
                    link(dve.tensor_reduce(mx[:, u, :], sc[:, u, :, :], AXX, ALU.max))
                    dve.tensor_scalar(nm[:, u, :], mx[:, u, :], -1.0, None, ALU.mult).then_inc(sc_ready, 1)
                for u in range(U):
                    b = i * U + u
                    dve.wait_ge(p_tr, signals(b + 1))
                    dve.tensor_copy(pX[:, u, :], ps[0:1, u, 2, :]).then_inc(pX_ready, 1)
                for u in range(U):
                    b = i * U + u
                    dve.tensor_copy(sums[:, b, :], rs[:, u, :])
                    link(dve.reciprocal(ri[:, u, :], rs[:, u, :]))
                    dve.wait_ge(pv, signals(b + 1))
                    link(dve.tensor_tensor(om[:, u, :, :], ps[:, u, 3, 0:D].rearrange("p (n c) -> p n c", n=NG),
                                           bc(ri[:, u, :].unsqueeze(2), P, NG, GD), ALU.mult))
                    dve.tensor_tensor(om[:, u, :, :], om[:, u, :, :], bc(blockmask[:].unsqueeze(1), P, NG, GD), ALU.mult).then_inc(om_ready, 1)
            link.end(G)


def guard(nc, g, sums, VM, VXT, vec, OT):
    with ExitStack() as ctx:
        s = Scope(nc, ctx, "s4g")
        nan, any_p, any_all = s.sb("nan", [P, B * 4]), s.sb("any_p", [P, 1]), s.sb("any_all", [P, 1])
        flag = s.sb("flag", [P, 1], U32)
        mean = s.sb("mean", [P, KT, B])
        full = s.sb("full", [P, KT, T])
        flags = s.sb("flags", [P, T], U32)
        dve_link, any_ready, all_ready = s.sems("dve_link any_ready all_ready")
        block = ctx.enter_context(nc.Block())

        @block.gpsimd
        def _(pool):
            pool.wait_ge(any_ready, 1)
            pool.partition_all_reduce(any_all[:], any_p[:], P, bass.bass_isa.ReduceOp.max).then_inc(all_ready, 1)

        @block.vector
        def _(dve):
            link = Link(dve, dve_link)
            flat = sums[:].rearrange("p b n -> p (b n)")
            link(dve.tensor_tensor(nan[:], flat, flat, ALU.not_equal))
            dve.tensor_reduce(any_p[:], nan[:], AXX, ALU.max).then_inc(any_ready, 1)
            link(dve.tensor_tensor(VM[:], VM[:], VXT[:], ALU.add))
            for k in range(KT):
                ins = dve.tensor_scalar(mean[:, k, :], VM[:, k, :], 1.0 / CTX, vec[:, 2, k:k + 1], ALU.mult, ALU.add)
            link(ins)
            link(dve.tensor_copy(full[:].rearrange("p k (b q) -> p (k b) q", q=S), bc(mean[:].rearrange("p k b -> p (k b)").unsqueeze(2), P, KT * B, S)))
            dve.wait_ge(all_ready, 1)
            link(dve.tensor_copy(flag[:], any_all[:]))
            link(dve.tensor_copy(flags[:], bc(flag[:], P, T)))
            for k in range(KT):
                ins = dve.copy_predicated(OT[:, k, :], flags[:], full[:, k, :])
            link(ins)


def phase5(nc, g):
    I, X = g.I, g.X
    DI, DS, R, TAPS = 512, 16, 64, 4
    DT = DI // P
    with ExitStack() as ctx:
        s = Scope(nc, ctx, "s5")
        sb = s.sb
        banks = s.psum()
        xi = sb("xi", [P, DT, T])
        vec = sb("vec", [P, DT, TAPS + 3])
        wo = sb("wo", [P, DT, D])
        zd = nc.dram_tensor("s5_silu_z", [DT, P, T], F32, kind="Internal").ap()
        vec_loaded = s.sem("vec_loaded")
        with ExitStack() as actx:
            a = Scope(nc, actx, "s5a")
            n = Normed(a)
            xT = a.sb("xT", [P, KT, T])
            normed_transposed(nc, g, a, banks, n, xT)
            project_in(nc, g, banks, xT, xi, vec, wo, zd, vec_loaded)
        with ExitStack() as bctx:
            b = Scope(nc, bctx, "s5b")
            dt = b.sb("dt", [P, DT, T])
            dtx = b.sb("dtx", [P, DT, T])
            bcs = b.sb("bcs", [P, T])
            step_sizes(nc, g, banks, xi, dt, dtx, bcs, vec)
            scan(nc, g, banks, xi, dt, dtx, bcs)
        gate(nc, g, xi, zd)
        project_out(nc, g, "s5o", banks, xi, wo, None, kt=DT)


def project_in(nc, g, banks, xT, xi, vec, wo, zd, vec_loaded):
    I = g.I
    DT, TAPS = 4, 4
    with ExitStack() as ctx:
        s = Scope(nc, ctx, "s5p")
        sb = s.sb
        w = sb("w", [P, U, KT, 2, P])
        conv = sb("conv", [P, U, B, S])
        sz = sb("sz", [P, U, T])
        w_loaded = [s.sem(f"w_loaded{u}") for u in range(U)]
        z_stored = [s.sem(f"z_stored{u}") for u in range(U)]
        x_ready, z_ready, conv_ready, xi_ready, sz_ready, dve_link = s.sems("x_ready z_ready conv_ready xi_ready sz_ready dve_link")
        G = DT // U
        xb = banks[:, 0:4, :].rearrange("p n (b t) -> p (n b) t", t=S)
        block = ctx.enter_context(nc.Block())

        @block.sync
        def _(sp):
            sp.dma_start(vec[:], I["p5_vec"]).then_inc(vec_loaded, 16)
            sp.dma_start(wo[:], I["p5_wo"]).then_inc(vec_loaded, 16)
            for q in z_stored:
                sp.sem_inc(q, 16)
            with sp.Fori(0, G) as i:
                for u in range(U):
                    d = i * U + u
                    sp.wait_ge(z_ready, signals(i * U))
                    sp.dma_start(w[:, u, :, :, :], I["p5_win"][d]).then_inc(w_loaded[u], 16)
                for u in range(U):
                    d = i * U + u
                    sp.wait_ge(sz_ready, signals(d + 1))
                    sp.dma_start(zd[d], sz[:, u, :]).then_inc(z_stored[u], 16)
            for q in z_stored:
                sp.wait_ge(q, dma_signals(G))

        @block.tensor
        def _(pe):
            opens(pe, x_ready, z_ready)
            with pe.Fori(0, G) as i:
                for u in range(U):
                    d = i * U + u
                    pe.wait_ge(w_loaded[u], 16 * (i + 1))
                    pe.wait_ge(conv_ready, signals(d))
                    pe.wait_ge(sz_ready, signals(d))
                    for half, done in ((0, x_ready), (1, z_ready)):
                        for n in range(NC):
                            for k in range(KT):
                                mm = pe.matmul(banks[:, 4 * half + n, :], lhsT=w[:, u, k, half, :], rhs=xT[:, k, n * C:(n + 1) * C],
                                               start=k == 0, stop=k == KT - 1)
                        mm.then_inc(done, 1)

        @block.scalar
        def _(act):
            opens(act, sz_ready, xi_ready)
            with act.Fori(0, G) as i:
                for u in range(U):
                    d = i * U + u
                    act.wait_ge(z_ready, signals(d + 1))
                    act.wait_ge(z_stored[u], dma_signals(i))
                    act.activation(sz[:, u, :], banks[:, 4:8, :].rearrange("p n c -> p (n c)"), ACT.Silu).then_inc(sz_ready, 1)
                    act.wait_ge(conv_ready, signals(d + 1))
                    act.activation(xi[:, d, :], conv[:, u, :, :].rearrange("p b t -> p (b t)"), ACT.Silu).then_inc(xi_ready, 1)

        @block.vector
        def _(dve):
            link = Link(dve, dve_link)
            opens(dve, conv_ready)
            dve.wait_ge(vec_loaded, 32)
            with dve.Fori(0, G) as i:
                link.loop(i, U * (TAPS - 1))
                for u in range(U):
                    d = i * U + u
                    dve.wait_ge(x_ready, signals(d + 1))
                    dve.wait_ge(xi_ready, signals(i * U))
                    link(dve.tensor_scalar(conv[:, u, :, :], xb, vec[:, bass.ds(d, 1), TAPS - 1], vec[:, bass.ds(d, 1), TAPS], ALU.mult, ALU.add))
                    for back in range(1, TAPS):
                        ins = dve.scalar_tensor_tensor(conv[:, u, :, back:S], xb[:, :, 0:S - back], vec[:, bass.ds(d, 1), TAPS - 1 - back],
                                                       conv[:, u, :, back:S], ALU.mult, ALU.add)
                        if back < TAPS - 1:
                            link(ins)
                    ins.then_inc(conv_ready, 1)
            link.end(G)


def step_sizes(nc, g, banks, xi, dt, dtx, bcs, vec):
    I = g.I
    DT, DS, R, TAPS = 4, 16, 64, 4
    with ExitStack() as ctx:
        s = Scope(nc, ctx, "s5s")
        sb = s.sb
        wx = sb("wx", [P, DT, R + 2 * DS])
        wdt = sb("wdt", [R, DT * P])
        dr = sb("dr", [R, C])
        mag, ex, pos = sb("mag", [P, DT, C]), sb("ex", [P, DT, C]), sb("pos", [P, DT, C])
        loaded, zeroed, dbc, dr_ready, v_ready, pos_ready, ln_ready, dt_ready, act_link, dve_link = s.sems(
            "loaded zeroed dbc dr_ready v_ready pos_ready ln_ready dt_ready act_link dve_link")
        block = ctx.enter_context(nc.Block())

        @block.sync
        def _(sp):
            sp.dma_start(wx[:], I["p5_wx"]).then_inc(loaded, 16)
            sp.dma_start(wdt[:], I["p5_wdt"]).then_inc(loaded, 16)

        @block.gpsimd
        def _(pool):
            pool.memset(bcs[:], 0.0).then_inc(zeroed, 1)

        @block.tensor
        def _(pe):
            opens(pe, dbc, v_ready)
            pe.wait_ge(loaded, 32)
            with pe.Fori(0, NC) as c:
                pe.wait_ge(dr_ready, signals(c))
                for lo, hi, bank in ((0, R, 0), (R, R + 2 * DS, 1)):
                    for k in range(DT):
                        mm = pe.matmul(banks[0:hi - lo, bank, :], lhsT=wx[:, k, lo:hi], rhs=xi[:, k, bass.ts(c, C)], start=k == 0, stop=k == DT - 1)
                mm.then_inc(dbc, 1)
                pe.wait_ge(dr_ready, signals(c + 1))
                pe.wait_ge(ln_ready, signals(c))
                for m in range(DT):
                    mm = pe.matmul(banks[:, 2 + m, :], lhsT=wdt[:, tok(m)], rhs=dr[:], start=True, stop=True)
                mm.then_inc(v_ready, 1)

        @block.scalar
        def _(act):
            link = Link(act, act_link)
            opens(act, dr_ready, ln_ready)
            act.wait_ge(zeroed, 1)
            with act.Fori(0, NC) as c:
                link.loop(c, 2)
                act.wait_ge(dbc, signals(c + 1))
                act.wait_ge(v_ready, signals(c))
                act.activation(bcs[0:2 * DS, bass.ts(c, C)], banks[0:2 * DS, 1, :], ACT.Copy)
                act.activation(dr[:], banks[0:R, 0, :], ACT.Copy).then_inc(dr_ready, 1)
                act.wait_ge(pos_ready, signals(c + 1))
                act.wait_ge(dt_ready, signals(c))
                for m in range(DT):
                    ins = act.activation(mag[:, m, :], banks[:, 2 + m, :], ACT.Abs, bias=vec[:, m, TAPS + 1:TAPS + 2])
                link(ins)
                link(act.activation(ex[:], mag[:], ACT.Exp, scale=-1.0))
                act.activation(ex[:], ex[:], ACT.Ln, bias=1.0).then_inc(ln_ready, 1)

        @block.vector
        def _(dve):
            link = Link(dve, dve_link)
            opens(dve, pos_ready, dt_ready)
            with dve.Fori(0, NC) as c:
                link.loop(c, 2)
                cs = bass.ts(c, C)
                dve.wait_ge(v_ready, signals(c + 1))
                for m in range(DT):
                    ins = dve.tensor_scalar(pos[:, m, :], banks[:, 2 + m, :], vec[:, m, TAPS + 1:TAPS + 2], 0.0, ALU.add, ALU.max)
                ins.then_inc(pos_ready, 1)
                dve.wait_ge(ln_ready, signals(c + 1))
                link(dve.tensor_tensor(dt[:, :, cs], pos[:], ex[:], ALU.add))
                link(dve.tensor_tensor(dtx[:, :, cs], dt[:, :, cs], xi[:, :, cs], ALU.mult))
                for m in range(DT):
                    ins = dve.tensor_scalar(xi[:, m, cs], xi[:, m, cs], vec[:, m, TAPS + 2:TAPS + 3], None, ALU.mult)
                ins.then_inc(dt_ready, 1)
            link.end(NC)


def scan(nc, g, banks, xi, dt, dtx, bcs):
    I = g.I
    DT, DS = 4, 16
    W = DS * B
    CLIP = 10.0
    with ExitStack() as ctx:
        s = Scope(nc, ctx, "s5c")
        sb = s.sb
        alog = sb("alog", [P, DT, DS])
        rate = sb("rate", [P, DT, DS])
        pick = sb("pick", [P, 2 * DS, P])
        decay = sb("decay", [P, U, DT, DS, B])
        state = sb("state", [P, DT, DS, B])
        inp = sb("inp", [P, DT, DS, B])
        flo = sb("flo", [P, 2])
        loaded, rate_ready, zeroed, rise_ready, decay_ready, decay_used, b_ready, c_ready, b_used, c_used, prod_ready, y_ready, y_added, dve_link = s.sems(
            "loaded rate_ready zeroed rise_ready decay_ready decay_used b_ready c_ready b_used c_used prod_ready y_ready y_added dve_link")
        G = S // U

        def at(ap, t):
            return ap[:].rearrange("p k (b t) -> p k b t", t=S)[:, :, :, bass.ds(t, 1)].rearrange("p k b t -> p k (b t)")

        def wide(j):
            return bc(banks[:, 2 * j:2 * j + 2, :].rearrange("p n (m b) -> p (n m) b", b=B).unsqueeze(1), P, DT, DS, B)
        block = ctx.enter_context(nc.Block())

        @block.sync
        def _(sp):
            sp.dma_start(alog[:], I["p5_alog"]).then_inc(loaded, 16)
            sp.dma_start(pick[:], I["pick32"]).then_inc(loaded, 16)

        @block.gpsimd
        def _(pool):
            pool.memset(state[:], 0.0).then_inc(zeroed, 1)
            pool.wait_ge(rate_ready, 1)
            opens(pool, rise_ready)
            with pool.Fori(0, G) as i:
                for u in range(U):
                    t = i * U + u
                    pool.wait_ge(decay_used, signals(i * U))
                    pool.tensor_tensor(decay[:, u, :, :, :], bc(rate[:].unsqueeze(3), P, DT, DS, B), bc(at(dt, t).unsqueeze(2), P, DT, DS, B),
                                       ALU.mult).then_inc(rise_ready, 1)

        @block.scalar
        def _(act):
            act.wait_ge(loaded, 32)
            act.activation(rate[:], alog[:], ACT.Exp).then_inc(rate_ready, 1)
            opens(act, decay_ready)
            with act.Fori(0, G) as i:
                for u in range(U):
                    t = i * U + u
                    act.wait_ge(rise_ready, signals(t + 1))
                    act.activation(decay[:, u, :, :, :], decay[:, u, :, :, :], ACT.Exp, scale=-1.0).then_inc(decay_ready, 1)

        @block.tensor
        def _(pe):
            pe.wait_ge(loaded, 32)
            opens(pe, b_ready, c_ready, y_ready)
            bt = bcs[:].rearrange("n (b t) -> n b t", t=S)
            with pe.Fori(0, G) as i:
                for u in range(U):
                    t = i * U + u
                    for j, ready, used in ((0, b_ready, b_used), (1, c_ready, c_used)):
                        pe.wait_ge(used, signals(t))
                        for n in range(DS):
                            mm = pe.matmul(banks[:, 2 * j + n // 8, n % 8 * B:(n % 8 + 1) * B], lhsT=pick[:, j * DS + n, :],
                                           rhs=bt[:, :, bass.ds(t, 1)].rearrange("n b t -> n (b t)"), start=True, stop=True)
                        mm.then_inc(ready, 1)
                    pe.wait_ge(prod_ready, signals(t + 1))
                    pe.wait_ge(y_added, signals(i * U))
                    for n in range(DS):
                        mm = pe.matmul(banks[:, 4 + u, 0:DT * B], lhsT=g.ident[:], rhs=inp[:, :, n, :], start=n == 0, stop=n == DS - 1)
                    mm.then_inc(y_ready, 1)

        @block.vector
        def _(dve):
            link = Link(dve, dve_link)
            dve.wait_ge(zeroed, 1)
            opens(dve, decay_used, b_used, c_used, prod_ready, y_added)
            floor = float(np.exp(-10.0))

            def add(t, u):
                dve.wait_ge(y_ready, signals(t + 1))
                xs = at(xi, t)
                dve.tensor_tensor(xs, xs, banks[:, 4 + u, 0:DT * B].rearrange("p (k b) -> p k b", k=DT), ALU.add).then_inc(y_added, 1)
            with dve.Fori(0, G) as i:
                link.loop(i, 2 * U)
                for u in range(U):
                    t = i * U + u
                    dve.wait_ge(b_ready, signals(t + 1))
                    dve.wait_ge(y_ready, signals(t))
                    dve.tensor_tensor(inp[:], bc(at(dtx, t).unsqueeze(2), P, DT, DS, B), wide(0), ALU.mult).then_inc(b_used, 1)
                    dve.wait_ge(decay_ready, signals(t + 1))
                    dve.scalar_tensor_tensor(state[:].rearrange("p k n b -> p (k n b)"), decay[:, u, :, :, :].rearrange("p k n b -> p (k n b)"), floor,
                                             state[:].rearrange("p k n b -> p (k n b)"), ALU.max, ALU.mult).then_inc(decay_used, 1)
                    dve.wait_ge(b_used, signals(t + 1))
                    dve.wait_ge(decay_used, signals(t + 1))
                    link(dve.tensor_tensor(state[:], state[:], inp[:], ALU.add))
                    link(dve.tensor_scalar(state[:], state[:], -CLIP, CLIP, ALU.max, ALU.min))
                    dve.wait_ge(c_ready, signals(t + 1))
                    dve.tensor_tensor(inp[:], state[:], wide(1), ALU.mult).then_inc(prod_ready, 1)
                    dve.wait_ge(prod_ready, signals(t + 1))
                    dve.sem_inc(c_used, 1)
                    add(t, u)
            link.end(G)


def gate(nc, g, xi, zd):
    DT = 4
    with ExitStack() as ctx:
        s = Scope(nc, ctx, "s5g")
        sz = s.sb("sz", [P, DT, T])
        z_loaded = [s.sem(f"z_loaded{d}") for d in range(DT)]
        gated = s.sem("gated")
        block = ctx.enter_context(nc.Block())

        @block.sync
        def _(sp):
            for d in range(DT):
                sp.dma_start(sz[:, d, :], zd[d]).then_inc(z_loaded[d], 16)

        @block.vector
        def _(dve):
            for d in range(DT):
                dve.wait_ge(z_loaded[d], 16)
                dve.tensor_tensor(xi[:, d, :], xi[:, d, :], sz[:, d, :], ALU.mult).then_inc(gated, 1)
            dve.wait_ge(gated, DT)


def phase6(nc, g):
    E, FF = 8, 1024
    with ExitStack() as ctx:
        s = Scope(nc, ctx, "s6")
        banks = s.psum()
        xT = s.sb("xT", [P, KT, T])
        comb = s.sb("comb", [P, E, NT])
        n = Normed(s)
        normed_transposed(nc, g, s, banks, n, xT)
        route(nc, g, banks, xT, comb, E)
        experts(nc, g, banks, xT, comb, E, FF)


def route(nc, g, banks, xT, comb, E):
    I, X = g.I, g.X
    with ExitStack() as ctx:
        s = Scope(nc, ctx, "s6r")
        sb = s.sb
        rw, rb = sb("rw", [P, KT, E]), sb("rb", [E, 1])
        count = sb("count", [P, E])
        b2, tile_of = sb("b2", [P, D]), sb("tile_of", [P, NT])
        b2_wide = sb("b2_wide", [P, NT, D])
        lgT = sb("lgT", [E, T])
        lg = sb("lg", [P, NT, E])
        best, best_at = sb("best", [P, NT, E]), sb("best_at", [P, NT, E], U32)
        at = sb("at", [P, 2, NT])
        diff, ex, gates = sb("diff", [P, NT]), sb("ex", [P, NT]), sb("gates", [P, 2, NT])
        hit = sb("hit", [P, 2, E, NT])
        combT = sb("combT", [P, P])
        loaded, product, lgT_ready, lg_tr, diff_ready, ex_ready, comb_ready, comb_tr, combT_ready, biased, added, dve_link = s.sems(
            "loaded product lgT_ready lg_tr diff_ready ex_ready comb_ready comb_tr combT_ready biased added dve_link")
        block = ctx.enter_context(nc.Block())

        @block.sync
        def _(sp):
            for dst, src in ((rw, "p6_rw"), (rb, "p6_rb"), (count, "count8"), (b2, "p6_b2"), (tile_of, "tile_of")):
                sp.dma_start(dst[:], I[src]).then_inc(loaded, 16)

        @block.tensor
        def _(pe):
            pe.wait_ge(loaded, 80)
            for c in range(NC):
                for k in range(KT):
                    mm = pe.matmul(banks[0:E, c, :], lhsT=rw[:, k, :], rhs=xT[:, k, c * C:(c + 1) * C], start=k == 0, stop=k == KT - 1)
                mm.then_inc(product, 1)
            pe.wait_ge(lgT_ready, 1)
            for t in range(NT):
                mm = pe.transpose(banks[:, 4, t * E:(t + 1) * E], lgT[:, tok(t)], g.ident[0:E, 0:E])
            mm.then_inc(lg_tr, 1)
            pe.wait_ge(comb_ready, 1)
            pe.transpose(banks[:, 5, 0:P], comb[:].rearrange("p e t -> p (e t)"), g.ident[:]).then_inc(comb_tr, 1)
            pe.wait_ge(combT_ready, 1)
            for j in range(8):
                mm = pe.matmul(banks[:, j, :], lhsT=combT[:], rhs=b2_wide[:, 2 * j:2 * j + 2, :].rearrange("p t d -> p (t d)"),
                               start=True, stop=True)
            mm.then_inc(biased, 1)

        @block.scalar
        def _(act):
            act.wait_ge(loaded, 80)
            act.wait_ge(product, NC)
            act.activation(lgT[:], banks[0:E, 0:NC, :].rearrange("e n c -> e (n c)"), ACT.Identity, bias=rb[:]).then_inc(lgT_ready, 1)
            act.wait_ge(diff_ready, 1)
            act.activation(ex[:], diff[:], ACT.Exp).then_inc(ex_ready, 1)
            act.wait_ge(comb_tr, 1)
            act.activation(combT[:], banks[:, 5, 0:P], ACT.Copy).then_inc(combT_ready, 1)

        @block.vector
        def _(dve):
            link = Link(dve, dve_link)
            dve.wait_ge(loaded, 80)
            dve.tensor_tensor(b2_wide[:], bc(b2[:].unsqueeze(1), P, NT, D), bc(tile_of[:].unsqueeze(2), P, NT, D), ALU.mult)
            dve.wait_ge(lg_tr, 1)
            link(dve.tensor_copy(lg[:].rearrange("p t e -> p (t e)"), banks[:, 4, 0:NT * E]))
            for t in range(NT):
                ins = dve.max(best[:, t, :], lg[:, t, :])
            link(ins)
            dve.tensor_tensor(diff[:], best[:, :, 1], best[:, :, 0], ALU.subtract).then_inc(diff_ready, 1)
            for t in range(NT):
                ins = dve.max_index(best_at[:, t, :], best[:, t, :], lg[:, t, :])
            link(ins)
            link(dve.tensor_copy(at[:], best_at[:, :, 0:2].rearrange("p t n -> p n t")))
            dve.wait_ge(ex_ready, 1)
            link(dve.tensor_scalar(diff[:], ex[:], 1.0, None, ALU.add))
            link(dve.reciprocal(gates[:, 0, :], diff[:]))
            link(dve.tensor_tensor(gates[:, 1, :], gates[:, 0, :], ex[:], ALU.mult))
            for n in range(2):
                ins = dve.tensor_tensor(hit[:, n, :, :], bc(count[:].unsqueeze(2), P, E, NT), bc(at[:, n, :].unsqueeze(1), P, E, NT), ALU.is_equal)
            link(ins)
            for n in range(2):
                ins = dve.tensor_tensor(hit[:, n, :, :], hit[:, n, :, :], bc(gates[:, n, :].unsqueeze(1), P, E, NT), ALU.mult)
            link(ins)
            dve.tensor_tensor(comb[:], hit[:, 0, :, :], hit[:, 1, :, :], ALU.add).then_inc(comb_ready, 1)
            dve.wait_ge(biased, 1)
            x2 = X[:].rearrange("p (j t) d -> p j (t d)", t=2)
            dve.tensor_tensor(x2, x2, banks[:], ALU.add).then_inc(added, 1)
            dve.wait_ge(added, 1)


def experts(nc, g, banks, xT, comb, E, FF):
    I, X = g.I, g.X
    FT = FF // P
    HB = 4
    YB = C // P
    EY = NC * YB
    G = E // U
    with ExitStack() as ctx:
        s = Scope(nc, ctx, "s6e")
        sb = s.sb
        w1, w2 = sb("w1", [P, U, KT, FF]), sb("w2", [P, U, FT, D])
        b1 = sb("b1", [P, E, FT])
        hT = sb("hT", [P, FT, C])
        w_loaded = [s.sem(f"w_loaded{u}") for u in range(U)]
        b1_loaded, hidden, h_ready, y_ready, y_added = s.sems("b1_loaded hidden h_ready y_ready y_added")
        flat = comb[:].rearrange("p e t -> p (e t)")
        block = ctx.enter_context(nc.Block())

        @block.sync
        def _(sp):
            sp.dma_start(b1[:], I["p6_b1"]).then_inc(b1_loaded, 16)
            with sp.Fori(0, G) as i:
                for u in range(U):
                    e = i * U + u
                    sp.wait_ge(y_ready, (e + 1) * EY)
                    sp.dma_start(w1[:, u, :, :], I["p6_w1"][e]).then_inc(w_loaded[u], 16)
                    sp.dma_start(w2[:, u, :, :], I["p6_w2"][e]).then_inc(w_loaded[u], 16)

        @block.tensor
        def _(pe):
            opens(pe, hidden)
            pe.sem_inc(y_ready, U * EY)
            with pe.Fori(0, G) as i:
                for u in range(U):
                    with pe.Fori(0, NC) as c:
                        pe.wait_ge(w_loaded[u], 32 * (i + 1))
                        n = (i * U + u) * NC + c
                        for f in range(FT):
                            pe.wait_ge(h_ready, n * FT + f + 1)
                            for k in range(KT):
                                mm = pe.matmul(banks[:, f % HB, :], lhsT=w1[:, u, k, tok(f)], rhs=xT[:, k, bass.ts(c, C)], start=k == 0, stop=k == KT - 1)
                            mm.then_inc(hidden, 1)
                        for t in range(YB):
                            pe.wait_ge(y_added, n * YB + t + 1)
                            for f in range(FT):
                                if t == 0:
                                    pe.wait_ge(h_ready, HB + n * FT + f + 1)
                                mm = pe.matmul(banks[:, HB + t, 0:D], lhsT=hT[:, f, tok(t)], rhs=w2[:, u, f, :], start=f == 0, stop=f == FT - 1)
                            mm.then_inc(y_ready, 1)

        @block.scalar
        def _(act):
            act.sem_inc(h_ready, HB)
            act.wait_ge(b1_loaded, 16)
            with act.Fori(0, G) as i:
                for u in range(U):
                    e = i * U + u
                    with act.Fori(0, NC) as c:
                        n = e * NC + c
                        act.wait_ge(y_ready, U * EY + n * YB)
                        for f in range(FT):
                            act.wait_ge(hidden, signals(n * FT + f + 1))
                            act.activation(hT[:, f, :], banks[:, f % HB, :], ACT.Relu, bias=b1[:, bass.ds(e, 1), f]).then_inc(h_ready, 1)

        @block.vector
        def _(dve):
            dve.sem_inc(y_added, YB)
            with dve.Fori(0, G) as i:
                for u in range(U):
                    e = i * U + u
                    with dve.Fori(0, NC) as c:
                        n = e * NC + c
                        for t in range(YB):
                            x_t = X[:, c * YB + t, :]
                            dve.wait_ge(y_ready, U * EY + n * YB + t + 1)
                            dve.scalar_tensor_tensor(x_t, banks[:, HB + t, 0:D], flat[:, bass.ds(e * NT + c * YB + t, 1)], x_t,
                                                     ALU.mult, ALU.add).then_inc(y_added, 1)


class Env:

    def __init__(self, inputs, x, ident):
        self.I, self.X, self.ident = inputs, x, ident


def layers(nc, out, inputs):
    with ExitStack() as ctx:
        s = Scope(nc, ctx, "x")
        g = Env(inputs, s.sb("rows", [P, NT, D]), s.sb("ident", [P, P]))
        loaded, stored = s.sems("loaded stored")
        with nc.Block() as block:
            @block.sync
            def _(sp):
                sp.dma_start(g.X[:], inputs["x"]).then_inc(loaded, 16)
                sp.dma_start(g.ident[:], inputs["ident"]).then_inc(loaded, 16)
                sp.wait_ge(loaded, 32)
        for phase in (phase1, phase2, phase3, phase4, phase5, phase6):
            before = nc.snapshot_sems()
            phase(nc, g)
            nc.clear_and_free_semaphores(nc.allocated_since(before))
            nc.all_engine_barrier()
        with nc.Block() as block:
            @block.sync
            def _(sp):
                sp.dma_start(out.rearrange("(t p) d -> p t d", p=P), g.X[:]).then_inc(stored, 16)
                sp.wait_ge(stored, 16)


def layout(a):
    import numpy as np
    c = np.ascontiguousarray
    P, H1, HD1 = 128, 4, 64
    kp = lambda w, p=P: c(w.reshape(w.shape[0] // p, p, -1).transpose(1, 0, 2))
    col = lambda v, p=P: v.reshape(-1, p).T
    r = {}
    r["x"] = c(a["x"].reshape(16, P, 256).transpose(1, 0, 2))
    r["ctx_768"] = c(a["ctx_768"])
    r["mask_BxS2_bk0"] = c(a["mask_BxS2_bk0"])
    r["ident"] = np.eye(P, dtype=np.float32)
    ch, row = np.arange(256), np.arange(P)
    r["headmask4"] = c((ch[:, None] // HD1 == np.arange(H1)).astype(np.float32).reshape(2, P, H1).transpose(1, 0, 2))
    r["blockmask4"] = (row[:, None] // 32 == ch // HD1).astype(np.float32)
    r["sel"] = (row[:, None] % 32 == np.arange(32)).astype(np.float32)
    p = "L0_xattn_"
    two = lambda v: np.concatenate([v, v])
    r["p1_vec"] = c(np.stack([col(a[p + "ln_l_g"]), col(a[p + "ln_l_b"]), col(np.tile(a[p + "qn_g"], 4)),
                              col(np.tile(a[p + "kn_g"], 4)), col(a[p + "bo"])], axis=1))
    r["p1_cvec"] = c(np.stack([col(a[p + "ln_x_g"], 96), col(a[p + "ln_x_b"], 96)], axis=1))
    r["p1_wq"], r["p1_wlkv"], r["p1_wo"] = (kp(a[p + n].T) for n in ("Wq", "Wlkv", "Wo"))
    r["p1_wkv"] = kp(a[p + "Wkv"].T, 96)
    r["p2_w"] = kp(np.concatenate([a["L0_attn_Wq"], *(a["L0_attn_Wkv"].reshape(256, 16, 80)[:, :, lo:hi].reshape(256, -1)
                                                     for lo, hi in ((0, 16), (16, 80)))], axis=1))
    r["p2_wo"] = kp(a["L0_attn_Wout"])
    r["headmask8"] = (row[:, None] // 16 == np.arange(8)).astype(np.float32)
    r["batchmask"] = (row[:, None] // 32 == row // 32).astype(np.float32)
    p = "L0_ffn_"
    r["p3_wq"] = c(a[p + "w_q"].reshape(2, P, 16, P).transpose(2, 1, 0, 3))
    r["p3_gb"] = c(np.stack([col(a[p + "bn_gamma"]), col(a[p + "bn_beta"])], axis=1))
    r["p3_keys"] = c(a[p + "keys"].transpose(2, 0, 3, 1).reshape(16, P, 64))
    r["p3_table"] = np.concatenate([a[p + "down_embed"], a[p + "up_embed"]], axis=1)
    r["count8"] = np.tile(np.arange(8, dtype=np.float32), (P, 1))
    p = "L1_xattn_"
    r["p4_vec"] = c(np.stack([col(a[p + n]) for n in ("bq", "bk", "bv", "bo")], axis=1))
    r["p4_wq"], r["p4_wo"] = kp(a[p + "Wq"]), kp(a[p + "Wo"])
    r["p4_wk"], r["p4_wv"] = kp(a[p + "Wk"], 96), kp(a[p + "Wv"], 96)
    r["blockmask16"] = (row[:, None] // 32 == np.arange(64) // 16).astype(np.float32)
    p = "L1_attn_"
    r["p5_vec"] = c(np.stack([col(v) for v in (*a[p + "W_conv"], a[p + "b_conv"], a[p + "b_dt"], a[p + "D"])], axis=2))
    r["p5_win"] = c(a[p + "W_in"].reshape(2, P, 2, 4, P).transpose(3, 1, 0, 2, 4))
    r["p5_wo"], r["p5_wx"], r["p5_wdt"] = kp(a[p + "W_out"]), kp(a[p + "W_xproj"]), c(a[p + "W_dt"])
    r["p5_alog"] = kp(a[p + "A_log"])
    r["pick32"] = np.repeat(np.eye(P, 32, dtype=np.float32), P, axis=1).reshape(P, 32, P)
    r["p6_rw"], r["p6_rb"] = kp(a["L1_ffn_router_w"]), c(a["L1_ffn_router_b"].reshape(8, 1))
    r["p6_b2"], r["tile_of"] = np.repeat(a["L1_ffn_b2"], 16, axis=0), (row[:, None] % 16 == np.arange(16)).astype(np.float32)
    r["p6_w1"] = c(a["L1_ffn_W1"].reshape(8, 2, P, 1024).transpose(0, 2, 1, 3))
    r["p6_w2"] = c(a["L1_ffn_W2"].reshape(8, 8, P, 256).transpose(0, 2, 1, 3))
    r["p6_b1"] = c(a["L1_ffn_b1"].reshape(8, 8, P).transpose(2, 0, 1))
    return r


def kernel(**inputs):
    import numpy as _np
    import concourse.bacc as _bacc
    from concourse import mybir as _mybir
    from concourse.bass_utils import run_bass_kernel_spmd as _run

    nc = _bacc.Bacc("TRN2", target_bir_lowering=False, num_devices=1)
    arrays = layout({name: _np.asarray(a) for name, a in inputs.items()})
    aps = {name: nc.dram_tensor(name, a.shape, _mybir.dt.from_np(a.dtype), kind="ExternalInput").ap() for name, a in arrays.items()}
    out = nc.dram_tensor("out", (T, D), _mybir.dt.float32, kind="ExternalOutput").ap()
    layers(nc, out, aps)
    r = _run(nc, [arrays], core_ids=[0])
    return _np.asarray(r.results[0]["out"]).reshape(B, S, D)
```

```python
from contextlib import ExitStack

import numpy as np
import concourse.bass as bass
from concourse import mybir

ALU = mybir.AluOpType
ACT = mybir.ActivationFunctionType
AXX = mybir.AxisListType.X
F32 = mybir.dt.float32
U32 = mybir.dt.uint32
U8 = mybir.dt.uint8

P = 128
B, S, D = 64, 32, 256
T = B * S
NT = T // P
BT = P // S
KT = D // P
CTX, DC = 257, 192
DH = DC // 2
C = 512
NC = T // C
LN_EPS = 1e-5
U = 2


class Link:

    def __init__(self, eng, sem):
        self.eng, self.sem, self.base, self.n = eng, sem, 0, 0

    def __call__(self, ins):
        self.n += 1
        ins.then_inc(self.sem, 1)
        self.eng.wait_ge(self.sem, self.base + self.n)

    def loop(self, i, per):
        self.start, self.per = self.n, per
        self.base, self.n = i * per + self.start, 0

    def end(self, trips):
        assert self.n == self.per, (self.n, self.per)
        self.base, self.n = 0, self.start + trips * self.per


def signals(n):
    return n + 1


def dma_signals(n):
    return 16 * (n + 1)


def opens(eng, *sems):
    for s in sems:
        eng.sem_inc(s, 1)


def bc(ap, *shape):
    return ap.broadcast_to(list(shape))


def tok(t):
    return bass.ts(t, P)


class Scope:

    def __init__(self, nc, ctx, name):
        self.nc, self.ctx, self.name = nc, ctx, name

    def sb(self, name, shape, dt=F32):
        return self.ctx.enter_context(self.nc.sbuf_tensor(f"{self.name}_{name}", shape, dt))

    def sem(self, name):
        return self.nc.alloc_semaphore(f"{self.name}_{name}")

    def sems(self, names):
        return [self.sem(n) for n in names.split()]

    def psum(self):
        return self.ctx.enter_context(self.nc.psum_tensor(f"{self.name}_ps", [P, 8, 512], F32))


def row_stats(dve, link, x, stats, mv, var, eps):
    for t in range(NT):
        last = dve.bn_stats(stats[:, t, :], x[:, t, :])
    link(last)
    for t in range(NT):
        last = dve.bn_aggr(mv[:, t, :], stats[:, t, :])
    link(last)
    return dve.tensor_scalar(var[:, :], mv[:, :, 1], eps, None, ALU.add)


def project_out(nc, g, name, ps, OT, wo, bias, kt=KT):
    X = g.X
    with ExitStack() as ctx:
        s = Scope(nc, ctx, name)
        yT = s.sb("yT", [P, KT, C])
        product, yT_ready, y_tr, x_ready = s.sems("product yT_ready y_tr x_ready")
        block = ctx.enter_context(nc.Block())

        @block.tensor
        def _(pe):
            opens(pe, product, y_tr)
            with pe.Fori(0, NC) as c:
                pe.wait_ge(yT_ready, signals(c))
                for m in range(KT):
                    for k in range(kt):
                        mm = pe.matmul(ps[:, m, :], lhsT=wo[:, k, m * P:(m + 1) * P], rhs=OT[:, k, bass.ts(c, C)],
                                       start=k == 0, stop=k == kt - 1)
                mm.then_inc(product, 1)
                pe.wait_ge(yT_ready, signals(c + 1))
                pe.wait_ge(x_ready, signals(c))
                for t in range(C // P):
                    for m in range(KT):
                        at = (t % 2) * D + m * P
                        mm = pe.transpose(ps[:, 2 + t // 2, at:at + P], yT[:, m, t * P:(t + 1) * P], g.ident[:])
                mm.then_inc(y_tr, 1)

        @block.scalar
        def _(act):
            opens(act, yT_ready)
            with act.Fori(0, NC) as c:
                act.wait_ge(product, signals(c + 1))
                act.wait_ge(y_tr, signals(c))
                for m in range(KT):
                    if bias is None:
                        ins = act.activation(yT[:, m, :], ps[:, m, :], ACT.Copy)
                    else:
                        ins = act.activation(yT[:, m, :], ps[:, m, :], ACT.Identity, bias=bias[:, m:m + 1])
                ins.then_inc(yT_ready, 1)

        @block.vector
        def _(dve):
            opens(dve, x_ready)
            with dve.Fori(0, NC) as c:
                dve.wait_ge(y_tr, signals(c + 1))
                xs = X[:, bass.ts(c, C // P), :].rearrange("p (a t) d -> p a (t d)", a=2)
                dve.tensor_tensor(xs, xs, ps[:, 2:4, :], ALU.add).then_inc(x_ready, 1)


class Normed:

    def __init__(self, s):
        self.stats, self.mv = s.sb("stats", [P, NT, 6]), s.sb("mv", [P, NT, 2])
        self.var, self.rstd, self.half = s.sb("var", [P, NT]), s.sb("rstd", [P, NT]), s.sb("half", [P, 1])

    def apply(self, dve, out, X, t):
        return dve.tensor_scalar(out, X[:, t, :], self.mv[:, t, 0:1], self.rstd[:, bass.ds(t, 1)], ALU.subtract, ALU.mult)


def normed_transposed(nc, g, s, ps, n, xT):
    X = g.X
    with ExitStack() as ctx:
        a = Scope(nc, ctx, s.name + "n")
        xn = a.sb("xn", [P, U, D])
        half_ready, stat_ready, rstd_ready, dve_link, ln_ready, x_tr, xT_ready = a.sems(
            "half_ready stat_ready rstd_ready dve_link ln_ready x_tr xT_ready")
        block = ctx.enter_context(nc.Block())

        @block.gpsimd
        def _(pool):
            pool.memset(n.half[:], -0.5).then_inc(half_ready, 1)
            pool.wait_ge(half_ready, 1)
            pool.wait_ge(stat_ready, 1)
            pool.tensor_tensor(n.rstd[:], n.var[:], bc(n.half[:], P, NT), ALU.pow).then_inc(rstd_ready, 1)

        @block.vector
        def _(dve):
            link = Link(dve, dve_link)
            row_stats(dve, link, X, n.stats, n.mv, n.var, LN_EPS).then_inc(stat_ready, 1)
            dve.wait_ge(rstd_ready, 1)
            opens(dve, ln_ready)
            with dve.Fori(0, NT // U) as i:
                for u in range(U):
                    dve.wait_ge(x_tr, signals(i * U))
                    n.apply(dve, xn[:, u, :], X, i * U + u).then_inc(ln_ready, 1)

        @block.tensor
        def _(pe):
            opens(pe, x_tr)
            with pe.Fori(0, NT // U) as i:
                for u in range(U):
                    t = i * U + u
                    pe.wait_ge(ln_ready, signals(t + 1))
                    pe.wait_ge(xT_ready, signals(i * U))
                    for k in range(KT):
                        mm = pe.transpose(ps[:, u, tok(k)], xn[:, u, tok(k)], g.ident[:])
                    mm.then_inc(x_tr, 1)

        @block.scalar
        def _(act):
            opens(act, xT_ready)
            with act.Fori(0, NT // U) as i:
                for u in range(U):
                    t = i * U + u
                    act.wait_ge(x_tr, signals(t + 1))
                    act.activation(xT[:, :, tok(t)], ps[:, u, 0:KT * P].rearrange("p (k q) -> p k q", k=KT), ACT.Copy).then_inc(xT_ready, 1)


class Item:

    def __init__(self, i, offset):
        self.b, self.u, self.turn = i * 2 + offset, offset % 2, i + offset // 2


def skewed(eng, n, depth, step, link=None, links=0):
    lead = depth + 2 + depth % 2

    def lone(v):
        step(lambda s: Item(0, v - s) if 0 <= v - s < n else None)
    for v in range(lead):
        lone(v)
    trips = (n - lead) // 2
    with eng.Fori(0, trips) as i:
        if link:
            link.loop(i, 2 * links)
        for u in range(2):
            step(lambda s: Item(i, lead + u - s))
    if link:
        link.end(trips)
    for v in range(n, n + depth):
        lone(v)


def after(eng, sem, n):
    if not (isinstance(n, int) and n <= 0):
        eng.wait_ge(sem, n)


def phase1(nc, g):
    I, X, ident = g.I, g.X, g.ident
    H, HD = 4, 64
    NK = CTX + S
    with ExitStack() as ctx:
        def sb(name, shape, dt=F32):
            return ctx.enter_context(nc.sbuf_tensor("s1_" + name, shape, dt))

        def sem(name):
            return nc.alloc_semaphore("p1_" + name)

        banks = ctx.enter_context(nc.psum_tensor("p1_ps", [P, 8, 512], F32))
        ps = banks[:].rearrange("p (u n) c -> p u n c", u=U)
        QT = sb("QT", [P, KT, B * S])
        KE = sb("KE", [P, KT, B, S + 1])
        V3 = sb("V3", [S + 1, B, D])
        OT = sb("OT", [P, KT, B * S])
        wq = sb("wq", [P, KT, D])
        wlkv = sb("wlkv", [P, KT, 2 * D])
        wkv = sb("wkv", [DH, 2, 2 * D])
        wo = sb("wo", [P, KT, D])
        vec = sb("vec", [P, 5, KT])
        cvec = sb("cvec", [DH, 2, 2])
        headmask = sb("headmask", [P, KT, H])
        blockmask = sb("blockmask", [P, D])
        sel = sb("sel", [P, S])
        half = sb("half", [P, 1])
        mask8 = sb("mask8", [P, B, CTX], U8)

        load = sem("load")
        dve_link = sem("dve_link")

        with ExitStack() as actx:
            def sa(name, shape, dt=F32):
                return actx.enter_context(nc.sbuf_tensor("p1a_" + name, shape, dt))

            stats = sa("stats", [P, NT, 6])
            mv = sa("mv", [P, NT, 2])
            var = sa("var", [P, NT])
            rstd = sa("rstd", [P, NT])
            lat = sa("lat", [P, NT, D])
            ln = sa("ln", [P, U, D])
            lnT = sa("lnT", [P, U, KT, P])
            sq = sa("sq", [P, U, 2 * D])
            ss = sa("ss", [P, U, 8])
            rn = sa("rn", [P, U, 8])
            qk = sa("qk", [P, U, 2 * D])
            vl = sa("vl", [P, U, D])
            cx = sa("cx", [B, DC])
            cst = sa("cst", [B, 6])
            cmv = sa("cmv", [B, 2])
            cve = sa("cve", [B, 1])
            crs = sa("crs", [B, 1])
            cn = sa("cn", [B, DC])
            cT = sa("cT", [DH, 2, B])
            csq = sa("csq", [B, D])
            css = sa("css", [B, 4])
            crn = sa("crn", [B, 4])
            ck = sa("ck", [B, D])
            cv = sa("cv", [B, D])
            stat_ready, rstd_ready = sem("stat_ready"), sem("rstd_ready")
            half_ready = sem("half_ready")
            cstat_ready, crstd_ready, cn_ready = sem("cstat_ready"), sem("crstd_ready"), sem("cn_ready")
            c_tr, cT_ready, c_proj, csq_ready = sem("c_tr"), sem("cT_ready"), sem("c_proj"), sem("csq_ready")
            css_ready, crn_ready, ck_ready, c_tr2 = sem("css_ready"), sem("crn_ready"), sem("ck_ready"), sem("c_tr2")
            cv_ready, kx_ready, cv_loaded = sem("cv_ready"), sem("kx_ready"), sem("cv_loaded")
            v3_loaded = [sem(f"v3_loaded{u}") for u in range(U)]
            ln_ready, ln_tr, lnT_ready, proj = sem("ln_ready"), sem("ln_tr"), sem("lnT_ready"), sem("proj")
            sq_ready, ss_ready, rn_ready, qk_ready = sem("sq_ready"), sem("ss_ready"), sem("rn_ready"), sem("qk_ready")
            qk_tr, qT_ready, kT_ready, vl_ready = sem("qk_tr"), sem("qT_ready"), sem("kT_ready"), sem("vl_ready")
            NLOAD = 11
            block = actx.enter_context(nc.Block())

            @block.sync
            def _(sp):
                for dst, src in ((vec, "p1_vec"), (cvec, "p1_cvec"), (wq, "p1_wq"), (wlkv, "p1_wlkv"), (wkv, "p1_wkv"),
                                 (headmask, "headmask4"), (blockmask, "blockmask4"), (sel, "sel"), (wo, "p1_wo")):
                    sp.dma_start(dst[:], I[src]).then_inc(load, 16)
                sp.dma_start(cx[:], I["ctx_768"][:, CTX - 1, :]).then_inc(load, 16)
                sp.dma_start(mask8[:].rearrange("p b k -> p (b k)"),
                             I["mask_BxS2_bk0"].rearrange("b k -> (b k)").unsqueeze(0).broadcast_to([P, B * CTX])).then_inc(load, 16)
                sp.wait_ge(cv_ready, 1)
                sp.dma_start(V3[0:1, :, :], cv[:]).then_inc(cv_loaded, 16)
                for q in v3_loaded:
                    sp.sem_inc(q, 16)
                with sp.Fori(0, NT // U) as i:
                    for u in range(U):
                        t = i * U + u
                        sp.wait_ge(vl_ready, signals(t + 1))
                        for b in range(BT):
                            sp.dma_start(V3[1:S + 1, t * BT + b, :], vl[b * S:b * S + S, u, :]).then_inc(v3_loaded[u], 16)
                sp.wait_ge(cv_loaded, 16)
                for q in v3_loaded:
                    sp.wait_ge(q, dma_signals(BT * NT // U))

            @block.gpsimd
            def _(pool):
                pool.memset(half[:], -0.5).then_inc(half_ready, 1)
                pool.wait_ge(half_ready, 1)
                for n in range(2):
                    pool.wait_ge(stat_ready, n + 1)
                    pool.tensor_tensor(rstd[:], var[:], bc(half[:], P, NT), ALU.pow).then_inc(rstd_ready, 1)
                pool.wait_ge(cstat_ready, 1)
                pool.tensor_tensor(crs[:], cve[:], half[0:B, :], ALU.pow).then_inc(crstd_ready, 1)
                pool.wait_ge(css_ready, 1)
                pool.tensor_tensor(crn[:], css[:], bc(half[0:B, :], B, 4), ALU.pow).then_inc(crn_ready, 1)
                opens(pool, rn_ready)
                with pool.Fori(0, NT // U) as i:
                    for u in range(U):
                        t = i * U + u
                        pool.wait_ge(ss_ready, signals(t + 1))
                        pool.tensor_tensor(rn[:, u, :], ss[:, u, :], bc(half[:], P, 8), ALU.pow).then_inc(rn_ready, 1)

            @block.tensor
            def _(pe):
                pe.wait_ge(load, 16 * NLOAD)
                pe.wait_ge(cn_ready, 1)
                for k in range(2):
                    mm = pe.transpose(ps[0:DH, 0, 0, k * B:(k + 1) * B], cn[:, k * DH:(k + 1) * DH], g.ident[0:B, 0:B])
                mm.then_inc(c_tr, 1)
                pe.wait_ge(cT_ready, 1)
                for k in range(2):
                    mm = pe.matmul(ps[0:B, 0, 1, :], lhsT=cT[:, k, :], rhs=wkv[:, k, :], start=k == 0, stop=k == 1)
                mm.then_inc(c_proj, 1)
                pe.wait_ge(ck_ready, 1)
                for k in range(KT):
                    mm = pe.transpose(ps[:, 0, 2, k * B:(k + 1) * B], ck[:, k * P:(k + 1) * P], g.ident[0:B, 0:B])
                mm.then_inc(c_tr2, 1)
                pe.wait_ge(kx_ready, 1)
                opens(pe, ln_tr, proj, qk_tr)
                with pe.Fori(0, NT // U) as i:
                    for u in range(U):
                        t = i * U + u
                        pe.wait_ge(ln_ready, signals(t + 1))
                        pe.wait_ge(qT_ready, signals(i * U))
                        pe.wait_ge(kT_ready, signals(i * U))
                        for k in range(KT):
                            mm = pe.transpose(ps[:, u, 0, k * P:(k + 1) * P], ln[:, u, k * P:(k + 1) * P], g.ident[:])
                        mm.then_inc(ln_tr, 1)
                    for u in range(U):
                        t = i * U + u
                        pe.wait_ge(lnT_ready, signals(t + 1))
                        for k in range(KT):
                            pe.matmul(ps[:, u, 1, 0:D], lhsT=lnT[:, u, k, :], rhs=wq[:, k, :], start=k == 0, stop=k == KT - 1)
                        for k in range(KT):
                            mm = pe.matmul(ps[:, u, 2, :], lhsT=lnT[:, u, k, :], rhs=wlkv[:, k, :], start=k == 0, stop=k == KT - 1)
                        mm.then_inc(proj, 1)
                    for u in range(U):
                        t = i * U + u
                        pe.wait_ge(qk_ready, signals(t + 1))
                        for k in range(2 * KT):
                            mm = pe.transpose(ps[:, u, 0, k * P:(k + 1) * P], qk[:, u, k * P:(k + 1) * P], g.ident[:])
                        mm.then_inc(qk_tr, 1)

            @block.scalar
            def _(act):
                act.wait_ge(load, 16 * NLOAD)
                act.wait_ge(c_tr, 1)
                for k in range(2):
                    ins = act.activation(cT[:, k, :], ps[0:DH, 0, 0, k * B:(k + 1) * B], ACT.Identity,
                                         bias=cvec[:, 1, k:k + 1], scale=cvec[:, 0, k:k + 1])
                ins.then_inc(cT_ready, 1)
                act.wait_ge(c_proj, 1)
                act.activation(csq[:], ps[0:B, 0, 1, 0:D], ACT.Square).then_inc(csq_ready, 1)
                act.activation(cv[:], ps[0:B, 0, 1, D:2 * D], ACT.Copy).then_inc(cv_ready, 1)
                act.wait_ge(c_tr2, 1)
                for k in range(KT):
                    ins = act.activation(KE[:, k, :, 0:1], ps[:, 0, 2, k * B:(k + 1) * B].unsqueeze(2), ACT.Identity, scale=vec[:, 3, k:k + 1])
                ins.then_inc(kx_ready, 1)
                opens(act, lnT_ready, sq_ready, vl_ready, kT_ready)
                with act.Fori(0, NT // U) as i:
                    for u in range(U):
                        t = i * U + u
                        act.wait_ge(ln_tr, signals(t + 1))
                        for k in range(KT):
                            ins = act.activation(lnT[:, u, k, :], ps[:, u, 0, k * P:(k + 1) * P], ACT.Identity,
                                                 bias=vec[:, 1, k:k + 1], scale=vec[:, 0, k:k + 1])
                        ins.then_inc(lnT_ready, 1)
                    for u in range(U):
                        t = i * U + u
                        act.wait_ge(proj, signals(t + 1))
                        act.wait_ge(ss_ready, signals(i * U))
                        act.activation(sq[:, u, 0:D], ps[:, u, 1, 0:D], ACT.Square)
                        act.activation(sq[:, u, D:2 * D], ps[:, u, 2, 0:D], ACT.Square).then_inc(sq_ready, 1)
                        act.wait_ge(v3_loaded[u], dma_signals(i * BT))
                        act.activation(vl[:, u, :], ps[:, u, 2, D:2 * D], ACT.Copy).then_inc(vl_ready, 1)
                    for u in range(U):
                        t = i * U + u
                        act.wait_ge(qk_tr, signals(t + 1))
                        act.wait_ge(qT_ready, signals(t + 1))
                        for k in range(KT):
                            ins = act.activation(KE[:, k, bass.ts(t, BT), 1:S + 1], ps[:, u, 0, D + k * P:D + (k + 1) * P].rearrange("p (b q) -> p b q", q=S), ACT.Identity,
                                                 scale=vec[:, 3, k:k + 1])
                        ins.then_inc(kT_ready, 1)

            @block.vector
            def _(dve):
                link = Link(dve, dve_link)
                row_stats(dve, link, X, stats, mv, var, LN_EPS).then_inc(stat_ready, 1)
                dve.wait_ge(rstd_ready, 1)
                for t in range(NT):
                    ins = dve.tensor_scalar(lat[:, t, :], X[:, t, :], mv[:, t, 0:1], rstd[:, t:t + 1], ALU.subtract, ALU.mult)
                link(ins)
                row_stats(dve, link, lat, stats, mv, var, LN_EPS).then_inc(stat_ready, 1)
                dve.wait_ge(load, 16 * NLOAD)
                link(dve.bn_stats(cst[:], cx[:]))
                link(dve.bn_aggr(cmv[:], cst[:]))
                dve.tensor_scalar(cve[:], cmv[:, 1:2], LN_EPS, None, ALU.add).then_inc(cstat_ready, 1)
                dve.wait_ge(crstd_ready, 1)
                dve.tensor_scalar(cn[:], cx[:], cmv[:, 0:1], crs[:], ALU.subtract, ALU.mult).then_inc(cn_ready, 1)
                dve.wait_ge(csq_ready, 1)
                link(dve.tensor_reduce(css[:], csq[:].rearrange("p (h d) -> p h d", h=H), AXX, ALU.add))
                dve.tensor_scalar(css[:], css[:], 1.0 / HD, 1e-16, ALU.mult, ALU.max).then_inc(css_ready, 1)
                dve.wait_ge(crn_ready, 1)
                dve.wait_ge(cv_ready, 1)
                dve.tensor_tensor(ck[:].rearrange("p (h d) -> p h d", h=H), ps[0:B, 0, 1, 0:D].rearrange("p (h d) -> p h d", h=H),
                                  bc(crn[:].unsqueeze(2), B, H, HD), ALU.mult).then_inc(ck_ready, 1)
                dve.wait_ge(rstd_ready, 2)
                opens(dve, ln_ready, ss_ready, qk_ready, qT_ready)
                with dve.Fori(0, NT // U) as i:
                    link.loop(i, U * 1)
                    for u in range(U):
                        t = i * U + u
                        dve.wait_ge(ln_tr, signals(i * U))
                        dve.tensor_scalar(ln[:, u, :], lat[:, t, :], mv[:, t, 0:1], rstd[:, bass.ds(t, 1)],
                                          ALU.subtract, ALU.mult).then_inc(ln_ready, 1)
                    for u in range(U):
                        t = i * U + u
                        dve.wait_ge(sq_ready, signals(t + 1))
                        dve.wait_ge(rn_ready, signals(i * U))
                        link(dve.tensor_reduce(ss[:, u, :], sq[:, u, :].rearrange("p (h d) -> p h d", h=2 * H), AXX, ALU.add))
                        dve.tensor_scalar(ss[:, u, :], ss[:, u, :], 1.0 / HD, 1e-16, ALU.mult, ALU.max).then_inc(ss_ready, 1)
                    for u in range(U):
                        t = i * U + u
                        dve.wait_ge(rn_ready, signals(t + 1))
                        dve.wait_ge(vl_ready, signals(t + 1))
                        dve.wait_ge(qk_tr, signals(i * U))
                        for j in range(2):
                            ins = dve.tensor_tensor(qk[:, u, j * D:(j + 1) * D].rearrange("p (h d) -> p h d", h=H),
                                                    ps[:, u, 1 + j, 0:D].rearrange("p (h d) -> p h d", h=H),
                                                    bc(rn[:, u, j * H:(j + 1) * H].unsqueeze(2), P, H, HD), ALU.mult)
                        ins.then_inc(qk_ready, 1)
                    for u in range(U):
                        t = i * U + u
                        dve.wait_ge(qk_tr, signals(t + 1))
                        for k in range(KT):
                            ins = dve.tensor_scalar(QT[:, k, tok(t)], ps[:, u, 0, k * P:(k + 1) * P], vec[:, 2, k:k + 1],
                                                    HD ** -0.5, ALU.mult, ALU.mult)
                        ins.then_inc(qT_ready, 1)
                link.end(NT // U)
        phase1_attention(nc, g, banks, dict(
            H=H, HD=HD, NK=NK, QT=QT, KE=KE, V3=V3, OT=OT, wkv=wkv, cvec=cvec, vec=vec,
            headmask=headmask, blockmask=blockmask, sel=sel, half=half, mask8=mask8))
        project_out(nc, g, "p1o", banks, OT, wo, vec[:, 4, :])


def phase1_attention(nc, g, banks, v):
    I = g.I
    BIG = 1e30
    H, HD, NK = v["H"], v["HD"], v["NK"]
    QT, KE, V3, OT, wkv, cvec, vec = (v[n] for n in ("QT", "KE", "V3", "OT", "wkv", "cvec", "vec"))
    headmask, blockmask, sel, half, mask8 = (v[n] for n in ("headmask", "blockmask", "sel", "half", "mask8"))
    with ExitStack() as ctx:
        s = Scope(nc, ctx, "s1b")
        sb = s.sb
        carry = sb("carry", [P, U])
        one = sb("one", [P, 1])
        cx = sb("cx", [P, U, 2, DC])
        cst, cmv = sb("cst", [P, U, 2, 6]), sb("cmv", [P, U, 2, 2])
        cve, crs = sb("cve", [P, U, 2]), sb("crs", [P, U, 2])
        cn = sb("cn", [P, U, 2, DC])
        cT = sb("cT", [DH, U, 2, 2 * P])
        sq = sb("sq", [P, U, 2, D])
        ss, rn = sb("ss", [P, U, 2 * H]), sb("rn", [P, U, 2 * H])
        kn = sb("kn", [P, U, 2, D])
        vv = sb("vv", [P, U, 2, D])
        kT = sb("kT", [P, U, KT, NK])
        qb = sb("qb", [P, U, KT, P])
        mb = sb("mb", [P, U, NK])
        sc = sb("sc", [P, U, NK])
        mx, nm = sb("mx", [P, U, 1]), sb("nm", [P, U, 1])
        pr = sb("pr", [P, U, NK])
        rs, ri = sb("rs", [P, U, 1]), sb("ri", [P, U, 1])
        pT = sb("pT", [P, U, 3, P])
        om = sb("om", [P, U, D])
        (cve_ready, crs_ready, cn_ready, c_tr, cT_ready, keys, values, sq_ready, vv_ready, ss_ready, rn_ready, kn_ready,
         k_tr, kT_ready, ke_ready, qb_ready, mb_zeroed, mb_ready, scores, sc_ready, pr_ready, p_tr, pT_ready, pv, om_ready, o_tr, oT_ready,
         one_ready, dve_link) = s.sems(
            "cve_ready crs_ready cn_ready c_tr cT_ready keys values sq_ready vv_ready ss_ready rn_ready kn_ready "
            "k_tr kT_ready ke_ready qb_ready mb_zeroed mb_ready scores sc_ready pr_ready p_tr pT_ready pv om_ready o_tr oT_ready "
            "one_ready dve_link")
        cx_loaded = [s.sem(f"cx_loaded{u}") for u in range(U)]
        K_BANK, V_BANK, TR_BANK, S_BANK, P_BANK, O_BANK = 0, 2, 4, 5, 6, 7
        LAG_TR, LAG_KV, LAG_KN, LAG_AT = range(4)
        block = ctx.enter_context(nc.Block())

        @block.sync
        def _(sp):
            def step(item):
                c = item(0)
                after(sp, cn_ready, c.b - 1)
                sp.dma_start(cx[:, c.u, :, :], I["ctx_768"][c.b, 0:2 * P, :].rearrange("(j p) c -> p j c", p=P)).then_inc(cx_loaded[c.u], 16)
            skewed(sp, B, 0, step)

        @block.gpsimd
        def _(pool):
            pool.memset(mb[:], 0.0).then_inc(mb_zeroed, 1)
            pool.memset(one[:], 1.0).then_inc(one_ready, 1)
            pool.wait_ge(one_ready, 1)

            def step(item):
                c = item(LAG_TR)
                if c:
                    pool.wait_ge(cve_ready, c.b + 1)
                    pool.tensor_tensor(crs[:, c.u, :], cve[:, c.u, :], bc(half[:], P, 2), ALU.pow).then_inc(crs_ready, 1)
                c = item(LAG_KN)
                if c:
                    after(pool, scores, c.b - 1)
                    pool.tensor_tensor(qb[:, c.u, :, :].rearrange("p k (h q) -> p k h q", h=H),
                                       bc(QT[:, :, bass.ts(c.b, S)].unsqueeze(2), P, KT, H, S),
                                       bc(headmask[:].unsqueeze(3), P, KT, H, S), ALU.mult).then_inc(qb_ready, 1)
                    pool.tensor_tensor(kT[:, c.u, :, 2 * P:NK], KE[:, :, c.b, :], bc(one[:].unsqueeze(1), P, KT, S + 1), ALU.mult).then_inc(ke_ready, 1)
                c = item(LAG_KV)
                if c:
                    pool.wait_ge(ss_ready, c.b + 1)
                    pool.tensor_tensor(rn[:, c.u, :], ss[:, c.u, :], bc(half[:], P, 2 * H), ALU.pow).then_inc(rn_ready, 1)
            skewed(pool, B, 3, step)

        @block.tensor
        def _(pe):
            def step(item):
                a, n, c, t = item(LAG_AT), item(LAG_KN), item(LAG_KV), item(LAG_TR)
                if a:
                    pe.wait_ge(kT_ready, a.b + 1)
                    pe.wait_ge(ke_ready, a.b + 1)
                    pe.wait_ge(qb_ready, a.b + 1)
                    after(pe, sc_ready, a.b)
                    for k in range(KT):
                        mm = pe.matmul(banks[:, S_BANK, 0:NK], lhsT=qb[:, a.u, k, :], rhs=kT[:, a.u, k, :], start=k == 0, stop=k == KT - 1)
                    mm.then_inc(scores, 1)
                if c:
                    pe.wait_ge(cT_ready, c.b + 1)
                    after(pe, kn_ready, c.b - 1)
                    for j in range(2):
                        for k in range(2):
                            mm = pe.matmul(banks[:, K_BANK + c.u, j * D:(j + 1) * D], lhsT=cT[:, c.u, k, tok(j)], rhs=wkv[:, k, 0:D], start=k == 0, stop=k == 1)
                    mm.then_inc(keys, 1)
                if a:
                    pe.wait_ge(pr_ready, a.b + 1)
                    after(pe, pT_ready, a.b)
                    for j in range(3):
                        w = min(P, NK - j * P)
                        mm = pe.transpose(banks[0:w, P_BANK, tok(j)], pr[:, a.u, j * P:j * P + w], g.ident[:])
                    mm.then_inc(p_tr, 1)
                if n:
                    pe.wait_ge(kn_ready, n.b + 1)
                    after(pe, cT_ready, n.b + 2 if t else B)
                    for k in range(KT):
                        for j in range(2):
                            mm = pe.transpose(banks[:, TR_BANK, tok(2 * k + j)], kn[:, n.u, j, tok(k)], g.ident[:])
                    mm.then_inc(k_tr, 1)
                if c:
                    after(pe, vv_ready, c.b - 1)
                    for j in range(2):
                        for k in range(2):
                            mm = pe.matmul(banks[:, V_BANK + c.u, j * D:(j + 1) * D], lhsT=cT[:, c.u, k, tok(j)], rhs=wkv[:, k, D:2 * D], start=k == 0, stop=k == 1)
                    mm.then_inc(values, 1)
                if a:
                    pe.wait_ge(pT_ready, a.b + 1)
                    pe.wait_ge(vv_ready, a.b + 1)
                    after(pe, oT_ready, a.b)
                    for j in range(2):
                        pe.matmul(banks[:, O_BANK, 0:D], lhsT=pT[:, a.u, j, :], rhs=vv[:, a.u, j, :], start=j == 0, stop=False)
                    pe.matmul(banks[:, O_BANK, 0:D], lhsT=pT[0:S + 1, a.u, 2, :], rhs=V3[:, a.b, :], start=False, stop=True).then_inc(pv, 1)
                if t:
                    pe.wait_ge(cn_ready, t.b + 1)
                    after(pe, kT_ready, t.b - 1)
                    for k in range(2):
                        for j in range(2):
                            mm = pe.transpose(banks[0:DH, TR_BANK, tok(2 * k + j)], cn[:, t.u, j, k * DH:(k + 1) * DH], g.ident[:])
                    mm.then_inc(c_tr, 1)
                if a:
                    pe.wait_ge(om_ready, a.b + 1)
                    for k in range(KT):
                        mm = pe.matmul(banks[:, O_BANK, D + k * S:D + (k + 1) * S], lhsT=om[:, a.u, tok(k)], rhs=sel[:], start=True, stop=True)
                    mm.then_inc(o_tr, 1)
            skewed(pe, B, 3, step)

        @block.scalar
        def _(act):
            def step(item):
                a, n, c, t = item(LAG_AT), item(LAG_KN), item(LAG_KV), item(LAG_TR)
                if a:
                    act.wait_ge(sc_ready, a.b + 1)
                    act.activation(pr[:, a.u, :], sc[:, a.u, :], ACT.Exp, bias=nm[:, a.u, :], accum_out=rs[:, a.u, :]).then_inc(pr_ready, 1)
                if c:
                    act.wait_ge(keys, c.b + 1)
                    act.activation(sq[:, c.u, :, :], banks[:, K_BANK + c.u, :].rearrange("p (j d) -> p j d", j=2), ACT.Square).then_inc(sq_ready, 1)
                if a:
                    act.wait_ge(p_tr, a.b + 1)
                    act.activation(pT[:, a.u, 0:2, :], banks[:, P_BANK, 0:2 * P].rearrange("p (j q) -> p j q", j=2), ACT.Copy)
                    act.activation(pT[0:S + 1, a.u, 2, :], banks[0:S + 1, P_BANK, 2 * P:3 * P], ACT.Copy).then_inc(pT_ready, 1)
                if n:
                    act.wait_ge(k_tr, n.b + 1)
                    for k in range(KT):
                        ins = act.activation(kT[:, n.u, k, 0:2 * P], banks[:, TR_BANK, 2 * k * P:2 * (k + 1) * P], ACT.Identity, scale=vec[:, 3, k:k + 1])
                    ins.then_inc(kT_ready, 1)
                    act.wait_ge(values, n.b + 1)
                    act.activation(vv[:, n.u, :, :], banks[:, V_BANK + n.u, :].rearrange("p (j d) -> p j d", j=2), ACT.Copy).then_inc(vv_ready, 1)
                if t:
                    act.wait_ge(c_tr, t.b + 1)
                    for k in range(2):
                        ins = act.activation(cT[:, t.u, k, :], banks[0:DH, TR_BANK, 2 * k * P:2 * (k + 1) * P], ACT.Identity,
                                             bias=cvec[:, 1, k:k + 1], scale=cvec[:, 0, k:k + 1])
                    ins.then_inc(cT_ready, 1)
                if a:
                    act.wait_ge(o_tr, a.b + 1)
                    act.activation(OT[:, :, bass.ts(a.b, S)], banks[:, O_BANK, D:D + KT * S].rearrange("p (k q) -> p k q", k=KT), ACT.Copy).then_inc(oT_ready, 1)
            skewed(act, B, 3, step)

        @block.vector
        def _(dve):
            link = Link(dve, dve_link)
            dve.wait_ge(mb_zeroed, 1)

            def step(item):
                a, n, c, t = item(LAG_AT), item(LAG_KN), item(LAG_KV), item(LAG_TR)
                if a:
                    dve.wait_ge(scores, a.b + 1)
                    dve.wait_ge(mb_ready, a.b + 1)
                    link(dve.tensor_tensor(sc[:, a.u, :], banks[:, S_BANK, 0:NK], mb[:, a.u, :], ALU.add))
                    link(dve.tensor_reduce(mx[:, a.u, :], sc[:, a.u, :], AXX, ALU.max))
                    dve.tensor_scalar(nm[:, a.u, :], mx[:, a.u, :], -1.0, None, ALU.mult).then_inc(sc_ready, 1)
                if n:
                    dve.wait_ge(rn_ready, n.b + 1)
                    dve.tensor_tensor(kn[:, n.u, :, :].rearrange("p j (h d) -> p (j h) d", h=H),
                                      banks[:, K_BANK + n.u, :].rearrange("p (j d) -> p j d", d=HD),
                                      bc(rn[:, n.u, :].unsqueeze(2), P, 2 * H, HD), ALU.mult).then_inc(kn_ready, 1)
                    dve.tensor_scalar(mb[:, n.u, 0:CTX], mask8[:, n.b, :], BIG, -BIG, ALU.mult, ALU.add).then_inc(mb_ready, 1)
                if t:
                    dve.wait_ge(cx_loaded[t.u], 16 * (t.turn + 1))
                    for j in range(2):
                        ins = dve.bn_stats(cst[:, t.u, j, :], cx[:, t.u, j, :])
                    link(ins)
                    dve.memset(carry[:, t.u:t.u + 1], 0.0)
                    for j in range(2):
                        ins = dve.bn_aggr(cmv[:, t.u, j, :], cst[:, t.u, j, :])
                    link(ins)
                    dve.tensor_scalar(cve[:, t.u, :], cmv[:, t.u, :, 1], LN_EPS, None, ALU.add).then_inc(cve_ready, 1)
                if c:
                    dve.wait_ge(sq_ready, c.b + 1)
                    link(dve.tensor_reduce(ss[:, c.u, :], sq[:, c.u, :, :].rearrange("p j (h d) -> p (j h) d", h=H), AXX, ALU.add))
                    dve.tensor_scalar(ss[:, c.u, :], ss[:, c.u, :], 1.0 / HD, 1e-16, ALU.mult, ALU.max).then_inc(ss_ready, 1)
                if t:
                    dve.wait_ge(crs_ready, t.b + 1)
                    for j in range(2):
                        ins = dve.tensor_scalar(cn[:, t.u, j, :], cx[:, t.u, j, :], cmv[:, t.u, j, 0:1], crs[:, t.u, j:j + 1], ALU.subtract, ALU.mult)
                    ins.then_inc(cn_ready, 1)
                if a:
                    dve.wait_ge(pr_ready, a.b + 1)
                    link(dve.reciprocal(ri[:, a.u, :], rs[:, a.u, :]))
                    dve.wait_ge(pv, a.b + 1)
                    dve.scalar_tensor_tensor(om[:, a.u, :], banks[:, O_BANK, 0:D], ri[:, a.u, :], blockmask[:], ALU.mult, ALU.mult).then_inc(om_ready, 1)
            skewed(dve, B, 3, step, link, 6)


def phase2(nc, g):
    I, X = g.I, g.X
    H, DK, DV = 16, 16, 64
    HK = P // DK
    QKV = H * (2 * DK + DV)
    VT = H * DV // P
    with ExitStack() as ctx:
        s = Scope(nc, ctx, "s2")
        sb, sem = s.sb, s.sem
        ps = s.psum()[:].rearrange("p (u n) c -> p u n c", u=U)
        w = sb("w", [P, KT, QKV])
        wo = sb("wo", [P, VT, D])
        headmask = sb("headmask", [P, HK])
        batchmask = sb("batchmask", [P, P])
        half = sb("half", [P, 1])
        stats, mv, var, rstd = sb("stats", [P, NT, 6]), sb("mv", [P, NT, 2]), sb("var", [P, NT]), sb("rstd", [P, NT])
        xn = sb("xn", [P, U, D])
        xT = sb("xT", [P, U, KT, P])
        sq = sb("sq", [P, U, QKV])
        ss, nrm, rn = sb("ss", [P, U, 3 * H]), sb("nrm", [P, U, 3 * H]), sb("rn", [P, U, 3 * H])
        qk = sb("qk", [P, U, 2 * D])
        vv = sb("vv", [P, U, H * DV])
        kT = sb("kT", [P, U, KT, P])
        qb = sb("qb", [P, U, KT, HK, P])
        at = sb("at", [P, U, H, P])
        so, no, th, fac = sb("so", [P, U, H]), sb("no", [P, U, H]), sb("th", [P, U, H]), sb("fac", [P, U, H])
        on = sb("on", [P, U, H * DV])
        oT = sb("oT", [P, U, VT, P])
        load, half_ready, stat_ready, rstd_ready, dve_link, act_link = s.sems(
            "load half_ready stat_ready rstd_ready dve_link act_link")
        (ln_ready, x_tr, xT_ready, proj, sq_ready, ss_ready, nrm_ready, qk_ready, qk_tr, kT_ready, qb_ready, scores, relu_ready,
         at_ready, o_ready, sqo_ready, so_ready, th_ready, on_ready, o_tr, oT_ready, y_ready, x_done) = s.sems(
            "ln_ready x_tr xT_ready proj sq_ready ss_ready nrm_ready qk_ready qk_tr kT_ready qb_ready scores relu_ready "
            "at_ready o_ready sqo_ready so_ready th_ready on_ready o_tr oT_ready y_ready x_done")
        G = NT // U
        NLOAD = 4
        block = ctx.enter_context(nc.Block())

        def heads(ap, n):
            return ap.rearrange("p (h d) -> p h d", h=n)

        @block.sync
        def _(sp):
            for dst, src in ((w, "p2_w"), (wo, "p2_wo"), (headmask, "headmask8"), (batchmask, "batchmask")):
                sp.dma_start(dst[:], I[src]).then_inc(load, 16)
            sp.wait_ge(load, 16 * NLOAD)

        @block.gpsimd
        def _(pool):
            pool.memset(half[:], -0.5).then_inc(half_ready, 1)
            pool.wait_ge(half_ready, 1)
            pool.wait_ge(stat_ready, 1)
            pool.tensor_tensor(rstd[:], var[:], bc(half[:], P, NT), ALU.pow).then_inc(rstd_ready, 1)

        @block.tensor
        def _(pe):
            opens(pe, x_tr, proj, qk_tr, scores, o_ready, o_tr, y_ready)
            pe.wait_ge(load, 16 * NLOAD)
            with pe.Fori(0, G) as i:
                for u in range(U):
                    t = i * U + u
                    pe.wait_ge(ln_ready, signals(t + 1))
                    pe.wait_ge(oT_ready, signals(i * U))
                    for k in range(KT):
                        mm = pe.transpose(ps[:, u, 3, tok(k)], xn[:, u, tok(k)], g.ident[:])
                    mm.then_inc(x_tr, 1)
                for u in range(U):
                    t = i * U + u
                    pe.wait_ge(xT_ready, signals(t + 1))
                    pe.wait_ge(x_done, signals(i * U))
                    for n in range(QKV // C):
                        for k in range(KT):
                            mm = pe.matmul(ps[:, u, n, :], lhsT=xT[:, u, k, :], rhs=w[:, k, n * C:(n + 1) * C], start=k == 0, stop=k == KT - 1)
                    mm.then_inc(proj, 1)
                for u in range(U):
                    t = i * U + u
                    pe.wait_ge(qk_ready, signals(t + 1))
                    for k in range(2 * KT):
                        mm = pe.transpose(ps[:, u, 3, tok(k)], qk[:, u, tok(k)], g.ident[:])
                    mm.then_inc(qk_tr, 1)
                for u in range(U):
                    t = i * U + u
                    pe.wait_ge(qb_ready, signals(t + 1))
                    for n in range(4):
                        k, h = divmod(4 * n, HK)
                        mm = pe.matmul(ps[:, u, n, :], lhsT=kT[:, u, k, :], rhs=qb[:, u, k, h:h + 4, :], start=True, stop=True)
                    mm.then_inc(scores, 1)
                for u in range(U):
                    t = i * U + u
                    pe.wait_ge(at_ready, signals(t + 1))
                    for h in range(H):
                        mm = pe.matmul(ps[:, u, h // 8, h % 8 * DV:(h % 8 + 1) * DV], lhsT=at[:, u, h, :], rhs=vv[:, u, h * DV:(h + 1) * DV],
                                       start=True, stop=True)
                    mm.then_inc(o_ready, 1)
                for u in range(U):
                    t = i * U + u
                    pe.wait_ge(on_ready, signals(t + 1))
                    for k in range(VT):
                        mm = pe.transpose(ps[:, u, 2 + k // 4, tok(k % 4)], on[:, u, tok(k)], g.ident[:])
                    mm.then_inc(o_tr, 1)
                for u in range(U):
                    t = i * U + u
                    pe.wait_ge(oT_ready, signals(t + 1))
                    for k in range(VT):
                        mm = pe.matmul(ps[:, u, 0, 0:D], lhsT=oT[:, u, k, :], rhs=wo[:, k, :], start=k == 0, stop=k == VT - 1)
                    mm.then_inc(y_ready, 1)

        @block.scalar
        def _(act):
            link = Link(act, act_link)
            opens(act, xT_ready, sq_ready, nrm_ready, kT_ready, at_ready, sqo_ready, th_ready, oT_ready)
            with act.Fori(0, G) as i:
                link.loop(i, U)
                for u in range(U):
                    t = i * U + u
                    act.wait_ge(x_tr, signals(t + 1))
                    act.activation(xT[:, u, :, :], ps[:, u, 3, 0:KT * P].rearrange("p (k q) -> p k q", k=KT), ACT.Copy).then_inc(xT_ready, 1)
                for u in range(U):
                    t = i * U + u
                    act.wait_ge(proj, signals(t + 1))
                    act.activation(sq[:, u, :], ps[:, u, 0:3, :].rearrange("p n c -> p (n c)"), ACT.Square).then_inc(sq_ready, 1)
                for u in range(U):
                    t = i * U + u
                    act.wait_ge(ss_ready, signals(t + 1))
                    act.activation(nrm[:, u, :], ss[:, u, :], ACT.Sqrt).then_inc(nrm_ready, 1)
                for u in range(U):
                    t = i * U + u
                    act.wait_ge(qk_tr, signals(t + 1))
                    act.activation(kT[:, u, :, :], ps[:, u, 3, KT * P:2 * KT * P].rearrange("p (k q) -> p k q", k=KT), ACT.Copy).then_inc(kT_ready, 1)
                for u in range(U):
                    t = i * U + u
                    act.wait_ge(relu_ready, signals(t + 1))
                    act.activation(at[:, u, :, :], at[:, u, :, :], ACT.Square).then_inc(at_ready, 1)
                for u in range(U):
                    t = i * U + u
                    act.wait_ge(o_ready, signals(t + 1))
                    act.activation(sq[:, u, 0:H * DV], ps[:, u, 0:2, :].rearrange("p n c -> p (n c)"), ACT.Square).then_inc(sqo_ready, 1)
                for u in range(U):
                    t = i * U + u
                    act.wait_ge(so_ready, signals(t + 1))
                    link(act.activation(no[:, u, :], so[:, u, :], ACT.Sqrt))
                for u in range(U):
                    act.activation(th[:, u, :], no[:, u, :], ACT.Tanh).then_inc(th_ready, 1)
                for u in range(U):
                    t = i * U + u
                    act.wait_ge(o_tr, signals(t + 1))
                    act.activation(oT[:, u, :, :], ps[:, u, 2:4, :].rearrange("p n (k q) -> p (n k) q", k=4), ACT.Copy).then_inc(oT_ready, 1)
            link.end(G)

        @block.vector
        def _(dve):
            link = Link(dve, dve_link)
            row_stats(dve, link, X, stats, mv, var, LN_EPS).then_inc(stat_ready, 1)
            dve.wait_ge(rstd_ready, 1)
            dve.wait_ge(load, 16 * NLOAD)
            opens(dve, ln_ready, ss_ready, qk_ready, qb_ready, relu_ready, so_ready, on_ready, x_done)
            with dve.Fori(0, G) as i:
                link.loop(i, 5 * U)
                for u in range(U):
                    t = i * U + u
                    dve.wait_ge(x_tr, signals(i * U))
                    dve.tensor_scalar(xn[:, u, :], X[:, t, :], mv[:, t, 0:1], rstd[:, bass.ds(t, 1)],
                                      ALU.subtract, ALU.mult).then_inc(ln_ready, 1)
                for u in range(U):
                    t = i * U + u
                    dve.wait_ge(sq_ready, signals(t + 1))
                    dve.tensor_reduce(ss[:, u, 0:2 * H], heads(sq[:, u, 0:2 * D], 2 * H), AXX, ALU.add)
                    link(dve.tensor_reduce(ss[:, u, 2 * H:3 * H], heads(sq[:, u, 2 * D:QKV], H), AXX, ALU.add))
                    dve.tensor_scalar(ss[:, u, :], ss[:, u, :], 1e-24, None, ALU.max).then_inc(ss_ready, 1)
                for u in range(U):
                    t = i * U + u
                    dve.wait_ge(nrm_ready, signals(t + 1))
                    link(dve.reciprocal(rn[:, u, :], nrm[:, u, :]))
                    dve.tensor_tensor(heads(vv[:, u, :], H), ps[:, u, 1:3, :].rearrange("p n (h d) -> p (n h) d", d=DV),
                                      bc(rn[:, u, 2 * H:3 * H].unsqueeze(2), P, H, DV), ALU.mult)
                    dve.tensor_tensor(heads(qk[:, u, :], 2 * H), heads(ps[:, u, 0, :], 2 * H),
                                      bc(rn[:, u, 0:2 * H].unsqueeze(2), P, 2 * H, DK), ALU.mult).then_inc(qk_ready, 1)
                for u in range(U):
                    t = i * U + u
                    dve.wait_ge(kT_ready, signals(t + 1))
                    for k in range(KT):
                        ins = dve.tensor_tensor(qb[:, u, k, :, :], bc(ps[:, u, 3, tok(k)].unsqueeze(1), P, HK, P),
                                                bc(headmask[:].unsqueeze(2), P, HK, P), ALU.mult)
                    ins.then_inc(qb_ready, 1)
                for u in range(U):
                    t = i * U + u
                    dve.wait_ge(scores, signals(t + 1))
                    dve.scalar_tensor_tensor(at[:, u, :, :], ps[:, u, :, :].rearrange("p n (h q) -> p (n h) q", q=P), 0.0,
                                             bc(batchmask[:].unsqueeze(1), P, H, P), ALU.max, ALU.mult).then_inc(relu_ready, 1)
                for u in range(U):
                    t = i * U + u
                    dve.wait_ge(sqo_ready, signals(t + 1))
                    dve.tensor_reduce(so[:, u, :], heads(sq[:, u, 0:H * DV], H), AXX, ALU.add).then_inc(so_ready, 1)
                for u in range(U):
                    t = i * U + u
                    dve.wait_ge(th_ready, signals(t + 1))
                    link(dve.tensor_scalar(no[:, u, :], no[:, u, :], 1e-12, None, ALU.max))
                    link(dve.reciprocal(fac[:, u, :], no[:, u, :]))
                    link(dve.tensor_tensor(fac[:, u, :], fac[:, u, :], th[:, u, :], ALU.mult))
                    dve.tensor_tensor(heads(on[:, u, :], H), ps[:, u, 0:2, :].rearrange("p n (h d) -> p (n h) d", d=DV),
                                      bc(fac[:, u, :].unsqueeze(2), P, H, DV), ALU.mult).then_inc(on_ready, 1)
                for u in range(U):
                    t = i * U + u
                    dve.wait_ge(y_ready, signals(t + 1))
                    dve.tensor_tensor(X[:, t, :], X[:, t, :], ps[:, u, 0, 0:D], ALU.add).then_inc(x_done, 1)
            link.end(G)


def phase3(nc, g):
    with ExitStack() as ctx:
        s = Scope(nc, ctx, "s3")
        banks = s.psum()
        n = Normed(s)
        pairs = s.sb("pairs", [P, KT, 1024])
        offset = s.sb("offset", [1, 1024])
        score_map(nc, g, banks, n, pairs, offset)
        retrieve(nc, g, banks, n, pairs, offset)


def score_map(nc, g, banks, n, pairs, offset):
    I, X = g.I, g.X
    PH, NK, BN_EPS = 16, 64, 1e-5
    with ExitStack() as ctx:
        s = Scope(nc, ctx, "s3s")
        sb = s.sb
        wq = sb("wq", [P, KT, PH * P])
        wqT = sb("wqT", [P, PH, D])
        keys = sb("keys", [P, PH, NK])
        gb = sb("gb", [P, 2, PH])
        xc = sb("xc", [P, NT, D])
        ones = sb("ones", [P, P])
        mean = sb("mean", [P, D])
        cov = sb("cov", [P, KT, D + 1])
        scrap = sb("scrap", [P, D])
        var, mq = sb("var", [P, PH]), sb("mq", [P, PH])
        rstd, gain, shift = sb("rstd", [P, PH]), sb("gain", [P, PH]), sb("shift", [P, PH])
        kg = sb("kg", [P, PH, NK])
        (loaded, set_up, stat_ready, rstd_ready, dve_link, xn_ready, summed, xc_ready, cov_summed, m_tr, cov_ready, spread, spread_read, var_ready,
         vr_ready, kg_ready, mapped, map_ready) = s.sems(
            "loaded set_up stat_ready rstd_ready dve_link xn_ready summed xc_ready cov_summed m_tr cov_ready spread spread_read var_ready "
            "vr_ready kg_ready mapped map_ready")
        NG = 4
        block = ctx.enter_context(nc.Block())

        @block.sync
        def _(sp):
            for dst, src in ((wq, "p3_wq"), (wqT, "p3_wqT"), (keys, "p3_keys"), (gb, "p3_gb")):
                sp.dma_start(dst[:], I[src]).then_inc(loaded, 16)

        @block.gpsimd
        def _(pool):
            pool.memset(ones[:], 1.0)
            pool.memset(n.half[:], -0.5).then_inc(set_up, 1)
            pool.wait_ge(set_up, 1)
            pool.wait_ge(stat_ready, 1)
            pool.tensor_tensor(n.rstd[:], n.var[:], bc(n.half[:], P, NT), ALU.pow).then_inc(rstd_ready, 1)
            pool.wait_ge(var_ready, 1)
            pool.tensor_tensor(rstd[:], var[:], bc(n.half[:], P, PH), ALU.pow).then_inc(vr_ready, 1)

        @block.tensor
        def _(pe):
            pe.wait_ge(set_up, 1)
            for t in range(NT):
                pe.wait_ge(xn_ready, t // NG + 1)
                mm = pe.matmul(banks[:, 0, 0:D], lhsT=ones[:], rhs=xc[:, t, :], start=t == 0, stop=t == NT - 1)
            mm.then_inc(summed, 1)
            for t in range(NT):
                pe.wait_ge(xc_ready, t // NG + 1)
                for k in range(KT):
                    mm = pe.matmul(banks[:, 1 + k, 0:D], lhsT=xc[:, t, tok(k)], rhs=xc[:, t, :], start=t == 0, stop=t == NT - 1)
            for k in range(KT):
                mm = pe.transpose(banks[:, 3, tok(k)], mean[:, tok(k)], g.ident[:])
            mm.then_inc(cov_summed, 1)
            pe.wait_ge(loaded, 64)
            pe.wait_ge(cov_ready, 1)
            for c in range(PH):
                if c == 8:
                    pe.wait_ge(spread_read, 1)
                for k in range(KT):
                    mm = pe.matmul(banks[:, c % 8, 0:D + 1], lhsT=wq[:, k, tok(c)], rhs=cov[:, k, :], start=k == 0, stop=k == KT - 1)
                mm.then_inc(spread, 1)
            pe.wait_ge(spread_read, 2)
            pe.wait_ge(kg_ready, 1)
            for c in range(PH):
                for k in range(KT):
                    pe.matmul(banks[:, 2 * k + c // 8, c % 8 * NK:(c % 8 + 1) * NK], lhsT=wqT[:, c, tok(k)], rhs=kg[:, c, :], start=True, stop=True)
                mm = pe.matmul(banks[0:1, 4 + c // 8, c % 8 * NK:(c % 8 + 1) * NK], lhsT=shift[:, c:c + 1], rhs=keys[:, c, :], start=True, stop=True)
            mm.then_inc(mapped, 1)

        @block.scalar
        def _(act):
            act.wait_ge(cov_summed, 1)
            act.activation(cov[:, :, 0:D], banks[:, 1:3, 0:D], ACT.Copy, scale=1.0 / T)
            act.activation(cov[:, :, D:D + 1], banks[:, 3, 0:KT * P].rearrange("p (k q) -> p k q", k=KT)[:, :, 0:1], ACT.Copy).then_inc(cov_ready, 1)
            act.wait_ge(mapped, 1)
            for k in range(KT):
                act.activation(pairs[:, k, :], banks[:, 2 * k:2 * k + 2, :].rearrange("p n c -> p (n c)"), ACT.Copy)
            act.activation(offset[:], banks[0:1, 4:6, :].rearrange("p n c -> p (n c)"), ACT.Copy).then_inc(map_ready, 1)
            act.wait_ge(map_ready, 1)

        @block.vector
        def _(dve):
            link = Link(dve, dve_link)
            row_stats(dve, link, X, n.stats, n.mv, n.var, LN_EPS).then_inc(stat_ready, 1)
            dve.wait_ge(rstd_ready, 1)
            for t in range(NT):
                ins = n.apply(dve, xc[:, t, :], X, t)
                if t % NG == NG - 1:
                    ins.then_inc(xn_ready, 1)
            dve.wait_ge(summed, 1)
            link(dve.tensor_scalar(mean[:], banks[:, 0, 0:D], 1.0 / T, None, ALU.mult))
            for i in range(NT // NG):
                ts = slice(i * NG, (i + 1) * NG)
                dve.tensor_tensor(xc[:, ts, :], xc[:, ts, :], bc(mean[:].unsqueeze(1), P, NG, D), ALU.subtract).then_inc(xc_ready, 1)
            dve.wait_ge(loaded, 64)
            for c in range(PH):
                dve.wait_ge(spread, c + 1)
                ins = dve.tensor_tensor_reduce(scrap[:], banks[:, c % 8, 0:D], wqT[:, c, :], 1.0, 0.0, ALU.mult, ALU.add, var[:, c:c + 1])
                link(ins)
                if c % 8 == 7:
                    dve.tensor_copy(mq[:, c - 7:c + 1], banks[:, :, D]).then_inc(spread_read, 1)
            link(dve.tensor_scalar(var[:], var[:], 0.0, BN_EPS, ALU.max, ALU.add))
            dve.sem_inc(var_ready, 1)
            dve.wait_ge(vr_ready, 1)
            dve.wait_ge(spread_read, 2)
            link(dve.tensor_tensor(gain[:], rstd[:], gb[:, 0, :], ALU.mult))
            link(dve.tensor_tensor(shift[:], mq[:], gain[:], ALU.mult))
            link(dve.tensor_tensor(shift[:], gb[:, 1, :], shift[:], ALU.subtract))
            dve.tensor_tensor(kg[:], keys[:], bc(gain[:].unsqueeze(2), P, PH, NK), ALU.mult).then_inc(kg_ready, 1)


def retrieve(nc, g, banks, n, pairs, offset):
    I, X = g.I, g.X
    H, K, NK = 8, 8, 64
    PH, M = 2 * H, H * K
    R = 4
    CHOOSE = 4
    with ExitStack() as ctx:
        s = Scope(nc, ctx, "s3e")
        sb = s.sb
        count, count_loaded = sb("count", [P, K]), s.sem("count_loaded")
        row1 = sb("row1", [1, P])
        xn = sb("xn", [P, U, D])
        xT = sb("xT", [P, KT, P])
        sim = sb("sim", [P, PH, NK])
        best, place = sb("best", [P, PH, K]), sb("place", [P, PH, K], U32)
        cand = sb("cand", [P, H, K * K])
        top, pos = sb("top", [P, H, K]), sb("pos", [P, H, K], U32)
        part, partf = sb("part", [P, 2, M], U32), sb("partf", [P, 2, M])
        keyf = sb("keyf", [P, 2, H, K])
        hit = sb("hit", [P, 2, H, K, K])
        key = sb("key", [P, 2, M])
        ex, den, rden = sb("ex", [P, H, K]), sb("den", [P, H]), sb("rden", [P, H])
        idf = sb("idf", [P, M])
        idx = sb("idx", [P, U, M], U32)
        wts = sb("wts", [P, U, H, K])
        carry = sb("carry", [P, 4])
        rows = sb("rows", [P, R, K, 2 * D])
        hd, hg, hw = sb("hd", [P, R, K]), sb("hg", [P, R, K]), sb("hw", [P, R, K])
        diag = sb("diag", [P, R, K, P])
        one = sb("one", [P, 2])
        gathered = [s.sem(f"gathered{r}") for r in range(R)]
        (set_up, carried, dve_link, xn_ready, x_tr, xT_ready, sims, sim_ready, diff_ready, ex_ready, idx_ready, dots, hg_ready, scaled, summed,
         added) = s.sems(
            "set_up carried dve_link xn_ready x_tr xT_ready sims sim_ready diff_ready ex_ready idx_ready dots hg_ready scaled summed added")
        T_BANK, S_BANK, Y_BANK = 0, 1, 4
        block = ctx.enter_context(nc.Block())

        def heads(t, h):
            return t.b * H + h + 1

        @block.sync
        def _(sp):
            sp.dma_start(count[:], I["count8"]).then_inc(count_loaded, 16)

        @block.gpsimd
        def _(pool):
            pool.memset(row1[:], 1.0).then_inc(set_up, 1)
            pool.memset(one[:], 1.0).then_inc(carried, 1)

            def step(item):
                t = item(0)
                pool.wait_ge(idx_ready, t.b + 1)
                for h in range(H):
                    r = h % R
                    after(pool, summed, heads(t, h) - R)
                    pool.wait_ge(carried, heads(t, h))
                    pool.tensor_tensor(one[:, 1:2], one[:, 0:1], one[:, 0:1], ALU.mult).then_inc(carried, 1)
                    for k in range(K):
                        m = h * K + k
                        pool.indirect_dma_start(rows[:, r, k, :], None, I["p3_table"],
                                                bass.IndirectOffsetOnAxis(idx[:, t.u, m:m + 1], 0)).then_inc(gathered[r], 16)
            skewed(pool, NT, 0, step)

        @block.tensor
        def _(pe):
            pe.wait_ge(set_up, 1)

            def step(item):
                c, t = item(0), item(1)
                if c:
                    pe.wait_ge(xn_ready, c.b + 1)
                    for k in range(KT):
                        mm = pe.transpose(banks[:, T_BANK, tok(k)], xn[:, c.u, tok(k)], g.ident[:])
                    mm.then_inc(x_tr, 1)
                    pe.wait_ge(xT_ready, c.b + 1)
                    after(pe, sim_ready, c.b)
                    for j in range(2):
                        cs = slice(j * C, (j + 1) * C)
                        for k in range(KT):
                            pe.matmul(banks[:, S_BANK + j, :], lhsT=xT[:, k, :], rhs=pairs[:, k, cs], start=k == 0, stop=False)
                        mm = pe.matmul(banks[:, S_BANK + j, :], lhsT=row1[:], rhs=offset[:, cs], start=False, stop=True)
                    mm.then_inc(sims, 1)
                if t:
                    after(pe, added, t.b - 1)
                    for h in range(H):
                        pe.wait_ge(scaled, heads(t, h))
                        for k in range(K):
                            mm = pe.matmul(banks[:, Y_BANK + t.u, 0:D], lhsT=diag[:, h % R, k, :], rhs=rows[:, h % R, k, D:2 * D],
                                           start=h == 0 and k == 0, stop=h == H - 1 and k == K - 1)
                        mm.then_inc(summed, 1)
            skewed(pe, NT, 1, step)

        @block.scalar
        def _(act):
            def step(item):
                c, t = item(0), item(1)
                if c:
                    act.wait_ge(x_tr, c.b + 1)
                    act.activation(xT[:], banks[:, T_BANK, 0:D].rearrange("p (k q) -> p k q", k=KT), ACT.Copy).then_inc(xT_ready, 1)
                    act.wait_ge(sims, c.b + 1)
                    act.activation(sim[:].rearrange("p c k -> p (c k)"), banks[:, S_BANK:S_BANK + 2, :].rearrange("p n c -> p (n c)"), ACT.Copy).then_inc(sim_ready, 1)

                def gelu(h):
                    act.wait_ge(dots, heads(t, h))
                    act.activation(hg[:, h % R, :], hd[:, h % R, :], ACT.Gelu_apprx_tanh).then_inc(hg_ready, 1)
                if t:
                    for h in range(CHOOSE + 1):
                        gelu(h)
                if c:
                    act.wait_ge(diff_ready, c.b + 1)
                    act.activation(ex[:], ex[:], ACT.Exp).then_inc(ex_ready, 1)
                if t:
                    for h in range(CHOOSE + 1, H):
                        gelu(h)
            skewed(act, NT, 1, step)

        @block.vector
        def _(dve):
            link = Link(dve, dve_link)
            dve.wait_ge(count_loaded, 16)

            def choose(c):
                dve.wait_ge(sim_ready, c.b + 1)
                dve.memset(carry[:, 0:1], 0.0)
                for q in range(PH):
                    ins = dve.max(best[:, q, :], sim[:, q, :])
                link(ins)
                dve.tensor_tensor(cand[:].rearrange("p h (a b) -> p h a b", a=K), bc(best[:, 0:H, :].unsqueeze(3), P, H, K, K),
                                  bc(best[:, H:PH, :].unsqueeze(2), P, H, K, K), ALU.add)
                for q in range(PH):
                    ins = dve.max_index(place[:, q, :], best[:, q, :], sim[:, q, :])
                link(ins)
                dve.memset(carry[:, 1:2], 0.0)
                for h in range(H):
                    ins = dve.max(top[:, h, :], cand[:, h, :])
                link(ins)
                dve.tensor_tensor(ex[:], top[:], bc(top[:, :, 0:1], P, H, K), ALU.subtract).then_inc(diff_ready, 1)
                for h in range(H):
                    ins = dve.max_index(pos[:, h, :], top[:, h, :], cand[:, h, :])
                link(ins)
                flat = pos[:].rearrange("p h k -> p (h k)")
                dve.tensor_scalar(part[:, 0, :], flat, 3, None, ALU.logical_shift_right)
                link(dve.tensor_scalar(part[:, 1, :], flat, K - 1, None, ALU.bitwise_and))
                dve.tensor_copy(partf[:], part[:])
                link(dve.tensor_copy(keyf[:].rearrange("p j h k -> p (j h) k"), place[:]))
                link(dve.tensor_tensor(hit[:].rearrange("p j h k a -> p (j h k) a"), bc(partf[:].rearrange("p j m -> p (j m)").unsqueeze(2), P, 2 * M, K),
                                       bc(count[:].unsqueeze(1), P, 2 * M, K), ALU.is_equal))
                wide = hit[:].rearrange("p j h k a -> p (j h) k a")
                link(dve.tensor_tensor(wide, wide, bc(keyf[:].rearrange("p j h a -> p (j h) a").unsqueeze(2), P, PH, K, K), ALU.mult))
                link(dve.tensor_reduce(key[:], hit[:].rearrange("p j h k a -> p j (h k) a"), AXX, ALU.add))
                link(dve.scalar_tensor_tensor(idf[:], key[:, 0, :], float(NK), key[:, 1, :], ALU.mult, ALU.add))
                dve.tensor_copy(idx[:, c.u, :], idf[:]).then_inc(idx_ready, 1)

            def soften(c):
                dve.wait_ge(ex_ready, c.b + 1)
                link(dve.tensor_reduce(den[:], ex[:], AXX, ALU.add))
                link(dve.reciprocal(rden[:], den[:]))
                link(dve.tensor_tensor(wts[:, c.u, :, :], ex[:], bc(rden[:].unsqueeze(2), P, H, K), ALU.mult))

            def step(item):
                c, t, y = item(0), item(1), item(2)

                def scale(h):
                    r = h % R
                    dve.wait_ge(hg_ready, heads(t, h))
                    link(dve.tensor_tensor(hw[:, r, :], hg[:, r, :], wts[:, t.u, h, :], ALU.mult))
                    after(dve, summed, heads(t, h) - R)
                    for k in range(K):
                        ins = dve.tensor_scalar(diag[:, r, k, :], g.ident[:], hw[:, r, k:k + 1], None, ALU.mult)
                    ins.then_inc(scaled, 1)
                if c:
                    n.apply(dve, xn[:, c.u, :], X, c.b).then_inc(xn_ready, 1)
                if t:
                    dve.wait_ge(xn_ready, t.b + 1)
                    for h in range(H):
                        r = h % R
                        dve.wait_ge(gathered[r], (t.b * (H // R) + h // R + 1) * (16 * K))
                        for k in range(K):
                            ins = dve.tensor_tensor_reduce(rows[:, r, k, 0:D], rows[:, r, k, 0:D], xn[:, t.u, :], 1.0, 0.0, ALU.mult, ALU.add, hd[:, r, k:k + 1])
                        ins.then_inc(dots, 1)
                        if h:
                            scale(h - 1)
                        if h == 1 and y:
                            add(y)
                        if h == CHOOSE and c:
                            choose(c)
                        if h == CHOOSE + 1 and c:
                            soften(c)
                    scale(H - 1)
                else:
                    if c:
                        choose(c)
                        soften(c)
                    if y:
                        add(y)

            def add(y):
                dve.wait_ge(summed, heads(y, H - 1))
                dve.tensor_tensor(X[:, y.b, :], X[:, y.b, :], banks[:, Y_BANK + y.u, 0:D], ALU.add).then_inc(added, 1)
            skewed(dve, NT, 2, step, link, 10 + 3 + H)


def phase4(nc, g):
    I, X = g.I, g.X
    H, HD = 16, 16
    HK = P // HD
    HG = P // S
    NG = H // HG
    GD = HG * HD
    CLAMP = 10000.0
    with ExitStack() as ctx:
        s = Scope(nc, ctx, "s4")
        sb, sem = s.sb, s.sem
        banks = s.psum()
        OT = sb("OT", [P, KT, T])
        wo = sb("wo", [P, KT, D])
        vec = sb("vec", [P, 4, KT])
        load = sem("load")
        NLOAD = 10
        with ExitStack() as actx:
            a = Scope(nc, actx, "s4a")
            sb = a.sb
            QT = sb("QT", [P, KT, T])
            wq = sb("wq", [P, KT, D])
            wk, wv = sb("wk", [DH, 2, D]), sb("wv", [DH, 2, D])
            headmask = sb("headmask", [P, HK])
            blockmask = sb("blockmask", [P, GD])
            sel = sb("sel", [P, S])
            VX = sb("VX", [1, B, D])
            csum = sb("csum", [DH, 2, B])
            sums = sb("sums", [P, B, NG])
            cx = sb("cx", [B, DC])
            cxT = sb("cxT", [DH, 2, B])
            vx = sb("vx", [B, D])
            with ExitStack() as nctx:
                q = Scope(nc, nctx, "s4q")
                n = Normed(q)
                xT = q.sb("xT", [P, KT, T])
                normed_transposed(nc, g, q, banks, n, xT)
                c_tr, cT_ready, c_proj, vx_ready, vx_loaded, q_ready, q_read = a.sems(
                    "c_tr cT_ready c_proj vx_ready vx_loaded q_ready q_read")
                block = nctx.enter_context(nc.Block())

                @block.sync
                def _(sp):
                    for dst, src in ((vec, "p4_vec"), (wq, "p4_wq"), (wk, "p4_wk"), (wv, "p4_wv"), (wo, "p4_wo"), (headmask, "headmask8"),
                                     (blockmask, "blockmask16"), (sel, "sel")):
                        sp.dma_start(dst[:], I[src]).then_inc(load, 16)
                    sp.dma_start(cx[:], I["ctx_768"][:, CTX - 1, :]).then_inc(load, 16)
                    sp.wait_ge(load, 16 * (NLOAD - 1))
                    sp.wait_ge(vx_ready, 1)
                    sp.dma_start(VX[:], vx[:]).then_inc(vx_loaded, 16)
                    sp.wait_ge(vx_loaded, 16)

                @block.tensor
                def _(pe):
                    pe.wait_ge(load, 16 * (NLOAD - 1))
                    opens(pe, q_ready)
                    for k in range(2):
                        mm = pe.transpose(banks[0:DH, 4, k * B:(k + 1) * B], cx[:, k * DH:(k + 1) * DH], g.ident[0:B, 0:B])
                    mm.then_inc(c_tr, 1)
                    pe.wait_ge(cT_ready, 1)
                    for k in range(2):
                        mm = pe.matmul(banks[0:B, 6, 0:D], lhsT=cxT[:, k, :], rhs=wv[:, k, :], start=k == 0, stop=k == 1)
                    mm.then_inc(c_proj, 1)
                    with pe.Fori(0, NC) as c:
                        pe.wait_ge(q_read, signals(c))
                        for m in range(KT):
                            for k in range(KT):
                                mm = pe.matmul(banks[:, m, :], lhsT=wq[:, k, tok(m)], rhs=xT[:, k, bass.ts(c, C)], start=k == 0, stop=k == KT - 1)
                        mm.then_inc(q_ready, 1)

                @block.scalar
                def _(act):
                    act.wait_ge(load, 16 * (NLOAD - 1))
                    act.wait_ge(c_tr, 1)
                    act.activation(cxT[:], banks[0:DH, 4, 0:2 * B].rearrange("p (k b) -> p k b", k=2), ACT.Copy).then_inc(cT_ready, 1)
                    act.wait_ge(c_proj, 1)
                    act.activation(vx[:], banks[0:B, 6, 0:D], ACT.Copy).then_inc(vx_ready, 1)

                @block.vector
                def _(dve):
                    dve.wait_ge(load, 16 * (NLOAD - 1))
                    opens(dve, q_read)
                    with dve.Fori(0, NC) as c:
                        dve.wait_ge(q_ready, signals(c + 1))
                        for m in range(KT):
                            ins = dve.tensor_scalar(QT[:, m, bass.ts(c, C)], banks[:, m, :], vec[:, 0, m:m + 1], HD ** -0.5, ALU.add, ALU.mult)
                        ins.then_inc(q_read, 1)

            attend(nc, g, banks, dict(
                HG=HG, NG=NG, GD=GD, HK=HK, CLAMP=CLAMP, QT=QT, OT=OT, wk=wk, wv=wv, vec=vec, cxT=cxT, VX=VX, csum=csum,
                sums=sums, headmask=headmask, blockmask=blockmask, sel=sel))
            guard(nc, g, banks, sums, csum, cxT, wv, vec, OT)
        project_out(nc, g, "s4o", banks, OT, wo, vec[:, 3, :])


def attend(nc, g, banks, v):
    I = g.I
    HG, NG, GD, HK, CLAMP = (v[n] for n in "HG NG GD HK CLAMP".split())
    QT, OT, wk, wv, vec, cxT, VX, csum, sums = (v[n] for n in "QT OT wk wv vec cxT VX csum sums".split())
    headmask, blockmask, sel = (v[n] for n in "headmask blockmask sel".split())
    NH = 2
    GH = NG // NH
    with ExitStack() as ctx:
        s = Scope(nc, ctx, "s4b")
        sb = s.sb
        cx = sb("cx", [P, U, 2, DC])
        cT = sb("cT", [DH, U, 2, CTX])
        kT = sb("kT", [P, U, KT, CTX])
        vv = sb("vv", [P, U, 2, D])
        qb = sb("qb", [P, U, KT, HK, S])
        sc = sb("sc", [P, U, NG, CTX])
        mx, nm, ri = sb("mx", [P, U, NG]), sb("nm", [P, U, NG]), sb("ri", [P, U, NG])
        pr = sb("pr", [P, U, NG, CTX])
        rs = sb("rs", [P, U, NG])
        pT = sb("pT", [P, U, NG, 2, P])
        pX = sb("pX", [1, U, NG, P])
        om = sb("om", [P, U, NG, GD])
        one = sb("one", [P, 1])
        cx_loaded = [s.sem(f"cx_loaded{u}") for u in range(U)]
        (c_tr, cT_ready, cl_ready, keys, values, kT_ready, vv_ready, qb_ready, scores, sc_ready, pr_ready, p_tr, pX_ready, pT_ready, pv, om_ready,
         o_tr, oT_ready, dve_link, one_ready) = s.sems(
            "c_tr cT_ready cl_ready keys values kT_ready vv_ready qb_ready scores sc_ready pr_ready p_tr pX_ready pT_ready pv om_ready "
            "o_tr oT_ready dve_link one_ready")
        T_BANK, K_BANK, V_BANK = 7, 4, 6
        PV_AT, O_AT = GH * P, GH * P + GH * GD
        block = ctx.enter_context(nc.Block())

        def half(c, h):
            return NH * c.b + h + 1

        @block.sync
        def _(sp):
            def step(item):
                c = item(0)
                after(sp, c_tr, c.b - 1)
                sp.dma_start(cx[:, c.u, :, :], I["ctx_768"][c.b, 0:2 * P, :].rearrange("(j p) c -> p j c", p=P)).then_inc(cx_loaded[c.u], 16)
            skewed(sp, B, 0, step)

        @block.gpsimd
        def _(pool):
            pool.memset(one[:], 1.0).then_inc(one_ready, 1)
            pool.wait_ge(one_ready, 1)

            def step(item):
                c = item(1)
                if c:
                    after(pool, scores, NH * (c.b - 1))
                    pool.tensor_tensor(qb[:, c.u, :, :, :], bc(QT[:, :, bass.ts(c.b, S)].unsqueeze(2), P, KT, HK, S),
                                       bc(headmask[:].unsqueeze(1).unsqueeze(3), P, KT, HK, S), ALU.mult).then_inc(qb_ready, 1)
                c = item(0)
                if c:
                    after(pool, values, c.b - 1)
                    pool.tensor_tensor(cT[:, c.u, :, 2 * P:CTX], cxT[:, :, bass.ds(c.b, 1)], bc(one[0:DH, :].unsqueeze(1), DH, 2, 1),
                                       ALU.mult).then_inc(cl_ready, 1)
            skewed(pool, B, 1, step)

        @block.tensor
        def _(pe):
            def step(item):
                c = item(2)
                if c:
                    pe.wait_ge(kT_ready, c.b + 1)
                    pe.wait_ge(qb_ready, c.b + 1)
                    for h in range(NH):
                        after(pe, oT_ready, half(c, h) - NH)
                        for n in range(GH):
                            k, head = divmod((h * GH + n) * HG, HK)
                            mm = pe.matmul(banks[:, 2 * h + n, 0:CTX], lhsT=qb[:, c.u, k, head:head + HG, :], rhs=kT[:, c.u, k, :], start=True, stop=True)
                        mm.then_inc(scores, 1)
                d = item(1)
                if d:
                    pe.wait_ge(cT_ready, d.b + 1)
                    pe.wait_ge(cl_ready, d.b + 1)
                    after(pe, kT_ready, d.b)
                    for m in range(KT):
                        for k in range(2):
                            mm = pe.matmul(banks[:, K_BANK + m, 0:CTX], lhsT=wk[:, k, tok(m)], rhs=cT[:, d.u, k, :], start=k == 0, stop=k == 1)
                    mm.then_inc(keys, 1)

                def p_transposed(h):
                    pe.wait_ge(pr_ready, half(c, h))
                    for n in range(GH):
                        m = h * GH + n
                        for j in range(2):
                            pe.transpose(banks[:, 2 * h, tok(2 * n + j)], pr[:, c.u, m, tok(j)], g.ident[:])
                        mm = pe.transpose(banks[0:1, 2 * h + 1, tok(n)], pr[:, c.u, m, 2 * P:CTX], g.ident[:])
                    mm.then_inc(p_tr, 1)
                if c:
                    p_transposed(0)
                if d:
                    after(pe, vv_ready, d.b)
                    for j in range(2):
                        for k in range(2):
                            mm = pe.matmul(banks[:, V_BANK, j * D:(j + 1) * D], lhsT=cT[:, d.u, k, tok(j)], rhs=wv[:, k, :], start=k == 0, stop=k == 1)
                    mm.then_inc(values, 1)
                if c:
                    p_transposed(1)
                    pe.wait_ge(vv_ready, c.b + 1)
                    for h in range(NH):
                        pe.wait_ge(pX_ready, half(c, h))
                        pe.wait_ge(pT_ready, half(c, h))
                        for n in range(GH):
                            m = h * GH + n
                            to = banks[:, 2 * h + 1, PV_AT + n * GD:PV_AT + (n + 1) * GD]
                            for j in range(2):
                                pe.matmul(to, lhsT=pT[:, c.u, m, j, :], rhs=vv[:, c.u, j, m * GD:(m + 1) * GD], start=j == 0, stop=False)
                            mm = pe.matmul(to, lhsT=pX[:, c.u, m, :], rhs=VX[:, c.b, m * GD:(m + 1) * GD], start=False, stop=True)
                        mm.then_inc(pv, 1)
                e = item(0)
                if e:
                    pe.wait_ge(cx_loaded[e.u], 16 * (e.turn + 1))
                    after(pe, cT_ready, e.b)
                    for k in range(2):
                        for j in range(2):
                            mm = pe.transpose(banks[0:DH, T_BANK, tok(2 * k + j)], cx[:, e.u, j, k * DH:(k + 1) * DH], g.ident[:])
                    mm.then_inc(c_tr, 1)
                if c:
                    for h in range(NH):
                        pe.wait_ge(om_ready, half(c, h))
                        pe.matmul(banks[:, 2 * h + 1, O_AT:O_AT + S], lhsT=om[:, c.u, h * GH:(h + 1) * GH, :], rhs=sel[:],
                                  start=True, stop=True).then_inc(o_tr, 1)
            skewed(pe, B, 2, step)

        @block.scalar
        def _(act):
            def step(item):
                c, d, e = item(2), item(1), item(0)
                if c:
                    for h in range(NH):
                        act.wait_ge(sc_ready, half(c, h))
                        for n in range(h * GH, (h + 1) * GH):
                            ins = act.activation(pr[:, c.u, n, :], sc[:, c.u, n, :], ACT.Exp, bias=nm[:, c.u, n:n + 1], accum_out=rs[:, c.u, n:n + 1])
                        ins.then_inc(pr_ready, 1)
                if d:
                    act.wait_ge(keys, d.b + 1)
                    for m in range(KT):
                        ins = act.activation(kT[:, d.u, m, :], banks[:, K_BANK + m, 0:CTX], ACT.Identity, bias=vec[:, 1, m:m + 1])
                    ins.then_inc(kT_ready, 1)
                if c:
                    for h in range(NH):
                        ns = slice(h * GH, (h + 1) * GH)
                        act.wait_ge(p_tr, half(c, h))
                        act.activation(pX[:, c.u, ns, :], banks[0:1, 2 * h + 1, 0:GH * P].rearrange("p (n q) -> p n q", n=GH), ACT.Copy).then_inc(pX_ready, 1)
                        act.activation(pT[:, c.u, ns, :, :], banks[:, 2 * h, :].rearrange("p (n j q) -> p n j q", n=GH, j=2), ACT.Copy).then_inc(pT_ready, 1)
                if e:
                    act.wait_ge(c_tr, e.b + 1)
                    for k in range(2):
                        ins = act.activation(cT[:, e.u, k, 0:2 * P], banks[0:DH, T_BANK, 2 * k * P:2 * (k + 1) * P], ACT.Copy,
                                             accum_out=csum[:, k, bass.ds(e.b, 1)])
                    ins.then_inc(cT_ready, 1)
                if c:
                    for h in range(NH):
                        act.wait_ge(o_tr, half(c, h))
                        act.activation(OT[:, h, bass.ts(c.b, S)], banks[:, 2 * h + 1, O_AT:O_AT + S], ACT.Identity, bias=vec[:, 2, h:h + 1]).then_inc(oT_ready, 1)
            skewed(act, B, 2, step)

        @block.vector
        def _(dve):
            link = Link(dve, dve_link)

            def step(item):
                c, d = item(2), item(1)
                if c:
                    for h in range(NH):
                        ns = slice(h * GH, (h + 1) * GH)
                        dve.wait_ge(scores, half(c, h))
                        link(dve.tensor_scalar(sc[:, c.u, ns, :], banks[:, 2 * h:2 * h + 2, 0:CTX], CLAMP, -CLAMP, ALU.min, ALU.max))
                        link(dve.tensor_reduce(mx[:, c.u, ns], sc[:, c.u, ns, :], AXX, ALU.max))
                        dve.tensor_scalar(nm[:, c.u, ns], mx[:, c.u, ns], -1.0, None, ALU.mult).then_inc(sc_ready, 1)
                if d:
                    dve.wait_ge(values, d.b + 1)
                    dve.tensor_copy(vv[:, d.u, :, :], banks[:, V_BANK, :].rearrange("p (j d) -> p j d", j=2)).then_inc(vv_ready, 1)
                if c:
                    dve.wait_ge(pr_ready, half(c, 1))
                    dve.tensor_copy(sums[:, c.b, :], rs[:, c.u, :])
                    link(dve.reciprocal(ri[:, c.u, :], rs[:, c.u, :]))
                    for h in range(NH):
                        ns = slice(h * GH, (h + 1) * GH)
                        dve.wait_ge(pv, half(c, h))
                        link(dve.tensor_tensor(om[:, c.u, ns, :], banks[:, 2 * h + 1, PV_AT:O_AT].rearrange("p (n c) -> p n c", n=GH),
                                               bc(ri[:, c.u, ns].unsqueeze(2), P, GH, GD), ALU.mult))
                        dve.tensor_tensor(om[:, c.u, ns, :], om[:, c.u, ns, :], bc(blockmask[:].unsqueeze(1), P, GH, GD), ALU.mult).then_inc(om_ready, 1)
            skewed(dve, B, 2, step, link, 2 * NH + 1 + NH)


def guard(nc, g, banks, sums, csum, cxT, wv, vec, OT):
    with ExitStack() as ctx:
        s = Scope(nc, ctx, "s4g")
        nan, any_p, any_all = s.sb("nan", [P, B * 4]), s.sb("any_p", [P, 1]), s.sb("any_all", [P, 1])
        flag = s.sb("flag", [P, 1], U32)
        mean = s.sb("mean", [P, KT, B])
        full = s.sb("full", [P, KT, T])
        flags = s.sb("flags", [P, T], U32)
        dve_link, any_ready, all_ready, total_ready, projected = s.sems("dve_link any_ready all_ready total_ready projected")
        block = ctx.enter_context(nc.Block())

        @block.gpsimd
        def _(pool):
            pool.wait_ge(any_ready, 1)
            pool.partition_all_reduce(any_all[:], any_p[:], P, bass.bass_isa.ReduceOp.max).then_inc(all_ready, 1)

        @block.tensor
        def _(pe):
            pe.wait_ge(total_ready, 1)
            for m in range(KT):
                for k in range(2):
                    mm = pe.matmul(banks[:, m, 0:B], lhsT=wv[:, k, tok(m)], rhs=csum[:, k, :], start=k == 0, stop=k == 1)
            mm.then_inc(projected, 1)

        @block.vector
        def _(dve):
            link = Link(dve, dve_link)
            flat = sums[:].rearrange("p b n -> p (b n)")
            dve.tensor_tensor(csum[:], csum[:], cxT[:], ALU.add).then_inc(total_ready, 1)
            link(dve.tensor_tensor(nan[:], flat, flat, ALU.not_equal))
            dve.tensor_reduce(any_p[:], nan[:], AXX, ALU.max).then_inc(any_ready, 1)
            dve.wait_ge(projected, 1)
            for k in range(KT):
                ins = dve.tensor_scalar(mean[:, k, :], banks[:, k, 0:B], 1.0 / CTX, vec[:, 2, k:k + 1], ALU.mult, ALU.add)
            link(ins)
            link(dve.tensor_copy(full[:].rearrange("p k (b q) -> p (k b) q", q=S), bc(mean[:].rearrange("p k b -> p (k b)").unsqueeze(2), P, KT * B, S)))
            dve.wait_ge(all_ready, 1)
            link(dve.tensor_copy(flag[:], any_all[:]))
            link(dve.tensor_copy(flags[:], bc(flag[:], P, T)))
            for k in range(KT):
                ins = dve.copy_predicated(OT[:, k, :], flags[:], full[:, k, :])
            link(ins)


def phase5(nc, g):
    I, X = g.I, g.X
    DI, DS, R, TAPS = 512, 16, 64, 4
    DT = DI // P
    with ExitStack() as ctx:
        s = Scope(nc, ctx, "s5")
        sb = s.sb
        banks = s.psum()
        xi = sb("xi", [P, DT, T])
        vec = sb("vec", [P, DT, TAPS + 3])
        zd = nc.dram_tensor("s5_silu_z", [DT, P, T], F32, kind="Internal").ap()
        vec_loaded = s.sem("vec_loaded")
        with ExitStack() as actx:
            a = Scope(nc, actx, "s5a")
            n = Normed(a)
            xT = a.sb("xT", [P, KT, T])
            normed_transposed(nc, g, a, banks, n, xT)
            project_in(nc, g, banks, xT, xi, vec, zd, vec_loaded)
        with ExitStack() as bctx:
            b = Scope(nc, bctx, "s5b")
            dt = b.sb("dt", [P, DT, T])
            bcs = b.sb("bcs", [P, T])
            step_sizes(nc, g, banks, xi, dt, bcs, vec)
            scan(nc, g, banks, xi, dt, bcs, vec)
        wo = sb("wo", [P, DT, D])
        gate(nc, g, xi, zd, wo)
        project_out(nc, g, "s5o", banks, xi, wo, None, kt=DT)


def project_in(nc, g, banks, xT, xi, vec, zd, vec_loaded):
    I = g.I
    DT, TAPS = 4, 4
    with ExitStack() as ctx:
        s = Scope(nc, ctx, "s5p")
        sb = s.sb
        w = sb("w", [P, U, KT, 2, P])
        conv = sb("conv", [P, U, B, S])
        sz = sb("sz", [P, U, T])
        w_loaded = [s.sem(f"w_loaded{u}") for u in range(U)]
        z_stored = [s.sem(f"z_stored{u}") for u in range(U)]
        x_ready, z_ready, conv_ready, xi_ready, sz_ready, dve_link = s.sems("x_ready z_ready conv_ready xi_ready sz_ready dve_link")
        G = DT // U
        xb = banks[:, 0:4, :].rearrange("p n (b t) -> p (n b) t", t=S)
        block = ctx.enter_context(nc.Block())

        @block.sync
        def _(sp):
            sp.dma_start(vec[:], I["p5_vec"]).then_inc(vec_loaded, 16)
            for q in z_stored:
                sp.sem_inc(q, 16)
            with sp.Fori(0, G) as i:
                for u in range(U):
                    d = i * U + u
                    sp.wait_ge(z_ready, signals(i * U))
                    sp.dma_start(w[:, u, :, :, :], I["p5_win"][d]).then_inc(w_loaded[u], 16)
                for u in range(U):
                    d = i * U + u
                    sp.wait_ge(sz_ready, signals(d + 1))
                    sp.dma_start(zd[d], sz[:, u, :]).then_inc(z_stored[u], 16)
            for q in z_stored:
                sp.wait_ge(q, dma_signals(G))

        @block.tensor
        def _(pe):
            opens(pe, x_ready, z_ready)
            with pe.Fori(0, G) as i:
                for u in range(U):
                    d = i * U + u
                    pe.wait_ge(w_loaded[u], 16 * (i + 1))
                    pe.wait_ge(conv_ready, signals(d))
                    pe.wait_ge(sz_ready, signals(d))
                    for half, done in ((0, x_ready), (1, z_ready)):
                        for n in range(NC):
                            for k in range(KT):
                                mm = pe.matmul(banks[:, 4 * half + n, :], lhsT=w[:, u, k, half, :], rhs=xT[:, k, n * C:(n + 1) * C],
                                               start=k == 0, stop=k == KT - 1)
                        mm.then_inc(done, 1)

        @block.scalar
        def _(act):
            opens(act, sz_ready, xi_ready)
            with act.Fori(0, G) as i:
                for u in range(U):
                    d = i * U + u
                    act.wait_ge(z_ready, signals(d + 1))
                    act.wait_ge(z_stored[u], dma_signals(i))
                    act.activation(sz[:, u, :], banks[:, 4:8, :].rearrange("p n c -> p (n c)"), ACT.Silu).then_inc(sz_ready, 1)
                    act.wait_ge(conv_ready, signals(d + 1))
                    act.activation(xi[:, d, :], conv[:, u, :, :].rearrange("p b t -> p (b t)"), ACT.Silu).then_inc(xi_ready, 1)

        @block.vector
        def _(dve):
            link = Link(dve, dve_link)
            opens(dve, conv_ready)
            dve.wait_ge(vec_loaded, 16)
            with dve.Fori(0, G) as i:
                link.loop(i, U * (TAPS - 1))
                for u in range(U):
                    d = i * U + u
                    dve.wait_ge(x_ready, signals(d + 1))
                    dve.wait_ge(xi_ready, signals(i * U))
                    link(dve.tensor_scalar(conv[:, u, :, :], xb, vec[:, bass.ds(d, 1), TAPS - 1], vec[:, bass.ds(d, 1), TAPS], ALU.mult, ALU.add))
                    for back in range(1, TAPS):
                        ins = dve.scalar_tensor_tensor(conv[:, u, :, back:S], xb[:, :, 0:S - back], vec[:, bass.ds(d, 1), TAPS - 1 - back],
                                                       conv[:, u, :, back:S], ALU.mult, ALU.add)
                        if back < TAPS - 1:
                            link(ins)
                    ins.then_inc(conv_ready, 1)
            link.end(G)


def step_sizes(nc, g, banks, xi, dt, bcs, vec):
    I = g.I
    DT, DS, R, TAPS = 4, 16, 64, 4
    with ExitStack() as ctx:
        s = Scope(nc, ctx, "s5s")
        sb = s.sb
        wx = sb("wx", [P, DT, R + 2 * DS])
        wdt = sb("wdt", [R, DT * P])
        dr = sb("dr", [R, C])
        mag, ex, pos = sb("mag", [P, DT, C]), sb("ex", [P, DT, C]), sb("pos", [P, DT, C])
        loaded, zeroed, dbc, dr_ready, v_ready, pos_ready, ln_ready, dt_ready, act_link = s.sems(
            "loaded zeroed dbc dr_ready v_ready pos_ready ln_ready dt_ready act_link")
        block = ctx.enter_context(nc.Block())

        @block.sync
        def _(sp):
            sp.dma_start(wx[:], I["p5_wx"]).then_inc(loaded, 16)
            sp.dma_start(wdt[:], I["p5_wdt"]).then_inc(loaded, 16)

        @block.gpsimd
        def _(pool):
            pool.memset(bcs[:], 0.0).then_inc(zeroed, 1)

        @block.tensor
        def _(pe):
            opens(pe, dbc, v_ready)
            pe.wait_ge(loaded, 32)
            with pe.Fori(0, NC) as c:
                pe.wait_ge(dr_ready, signals(c))
                for lo, hi, bank in ((0, R, 0), (R, R + 2 * DS, 1)):
                    for k in range(DT):
                        mm = pe.matmul(banks[0:hi - lo, bank, :], lhsT=wx[:, k, lo:hi], rhs=xi[:, k, bass.ts(c, C)], start=k == 0, stop=k == DT - 1)
                mm.then_inc(dbc, 1)
                pe.wait_ge(dr_ready, signals(c + 1))
                pe.wait_ge(ln_ready, signals(c))
                for m in range(DT):
                    mm = pe.matmul(banks[:, 2 + m, :], lhsT=wdt[:, tok(m)], rhs=dr[:], start=True, stop=True)
                mm.then_inc(v_ready, 1)

        @block.scalar
        def _(act):
            link = Link(act, act_link)
            opens(act, dr_ready, ln_ready)
            act.wait_ge(zeroed, 1)
            with act.Fori(0, NC) as c:
                link.loop(c, 2)
                act.wait_ge(dbc, signals(c + 1))
                act.wait_ge(v_ready, signals(c))
                act.activation(bcs[0:2 * DS, bass.ts(c, C)], banks[0:2 * DS, 1, :], ACT.Copy)
                act.activation(dr[:], banks[0:R, 0, :], ACT.Copy).then_inc(dr_ready, 1)
                act.wait_ge(pos_ready, signals(c + 1))
                act.wait_ge(dt_ready, signals(c))
                for m in range(DT):
                    ins = act.activation(mag[:, m, :], banks[:, 2 + m, :], ACT.Abs, bias=vec[:, m, TAPS + 1:TAPS + 2])
                link(ins)
                link(act.activation(ex[:], mag[:], ACT.Exp, scale=-1.0))
                act.activation(ex[:], ex[:], ACT.Ln, bias=1.0).then_inc(ln_ready, 1)

        @block.vector
        def _(dve):
            opens(dve, pos_ready, dt_ready)
            with dve.Fori(0, NC) as c:
                cs = bass.ts(c, C)
                dve.wait_ge(v_ready, signals(c + 1))
                dve.wait_ge(dt_ready, signals(c))
                for m in range(DT):
                    ins = dve.tensor_scalar(pos[:, m, :], banks[:, 2 + m, :], vec[:, m, TAPS + 1:TAPS + 2], 0.0, ALU.add, ALU.max)
                ins.then_inc(pos_ready, 1)
                dve.wait_ge(ln_ready, signals(c + 1))
                dve.tensor_tensor(dt[:, :, cs], pos[:], ex[:], ALU.add).then_inc(dt_ready, 1)


def scan(nc, g, banks, xi, dt, bcs, vec):
    DT, DS, TAPS = 4, 16, 4
    CLIP = 10.0
    KA = DT - 1
    with ExitStack() as ctx:
        s = Scope(nc, ctx, "s5c")
        sb = s.sb
        alog = sb("alog", [P, DT, DS])
        rate = sb("rate", [P, DT, DS])
        skip = sb("skip", [P, DT, P])
        dt_t = sb("dt_t", [P, U, DT, B])
        dtx = sb("dtx", [P, U, DT, B])
        decay = sb("decay", [P, U, DT, DS, B])
        inp = sb("inp", [P, U, DT, DS, B])
        state = sb("state", [P, DT, DS, B])
        prod = sb("prod", [P, DT, DS, B])
        b_all = sb("b_all", [P, U, DS, B])
        (loaded, rate_ready, neg_ready, skip_ready, zeroed, dt_ready, rise_ready, decay_ready, decay_used, dtx_ready, b_ready, b_read, inp_ready, inp_used,
         c_ready, prod_ready, y_ready, y_read, dve_link) = s.sems(
            "loaded rate_ready neg_ready skip_ready zeroed dt_ready rise_ready decay_ready decay_used dtx_ready b_ready b_read inp_ready inp_used "
            "c_ready prod_ready y_ready y_read dve_link")
        B_BANK, C_BANK, Y_BANK = 0, 2, 4

        def at(ap, t):
            return ap[:].rearrange("p k (b t) -> p k b t", t=S)[:, :, :, bass.ds(t, 1)].rearrange("p k b t -> p k (b t)")

        c_all = bc(banks[:, C_BANK:C_BANK + 2, :].rearrange("p n (m b) -> p (n m) b", b=B).unsqueeze(1), P, DT, DS, B)
        block = ctx.enter_context(nc.Block())

        @block.sync
        def _(sp):
            sp.dma_start(alog[:], g.I["p5_alog"]).then_inc(loaded, 16)

        @block.gpsimd
        def _(pool):
            pool.memset(state[:], 0.0).then_inc(zeroed, 1)
            pool.wait_ge(neg_ready, 1)

            def step(item):
                t = item(0)
                pool.wait_ge(dt_ready, t.b + 1)
                after(pool, decay_used, t.b - 1)
                pool.tensor_tensor(decay[:, t.u, KA, :, :], bc(rate[:, KA, :].unsqueeze(2), P, DS, B), bc(dt_t[:, t.u, KA, :].unsqueeze(1), P, DS, B),
                                   ALU.mult).then_inc(rise_ready, 1)
                pool.tensor_tensor(dtx[:, t.u, :, :], dt_t[:, t.u, :, :], at(xi, t.b), ALU.mult).then_inc(dtx_ready, 1)
                pool.wait_ge(dtx_ready, t.b + 1)
                pool.wait_ge(b_read, t.b + 1)
                after(pool, inp_used, t.b - 1)
                pool.tensor_tensor(inp[:, t.u, :, :, :], bc(dtx[:, t.u, :, :].unsqueeze(2), P, DT, DS, B), bc(b_all[:, t.u, :, :].unsqueeze(1), P, DT, DS, B), ALU.mult).then_inc(inp_ready, 1)
            skewed(pool, S, 0, step)

        @block.scalar
        def _(act):
            act.wait_ge(loaded, 16)
            act.activation(rate[:], alog[:], ACT.Exp).then_inc(rate_ready, 1)
            act.wait_ge(neg_ready, 1)

            def step(item):
                t = item(0)
                after(act, inp_ready, t.b - 1)
                act.activation(dt_t[:, t.u, :, :], at(dt, t.b), ACT.Copy).then_inc(dt_ready, 1)
                act.wait_ge(b_ready, t.b + 1)
                act.activation(b_all[:, t.u, :, :], banks[:, B_BANK:B_BANK + 2, :].rearrange("p n (m b) -> p (n m) b", b=B), ACT.Copy).then_inc(b_read, 1)
                act.wait_ge(dt_ready, t.b + 1)
                after(act, decay_used, t.b - 1)
                for k in range(KA):
                    for n in range(DS):
                        act.activation(decay[:, t.u, k, n, :], dt_t[:, t.u, k, :], ACT.Exp, scale=rate[:, k, n:n + 1])
                act.wait_ge(rise_ready, t.b + 1)
                act.activation(decay[:, t.u, KA, :, :], decay[:, t.u, KA, :, :], ACT.Exp).then_inc(decay_ready, 1)
            skewed(act, S, 0, step)

        @block.tensor
        def _(pe):
            pe.wait_ge(skip_ready, 1)
            bt = bcs[:].rearrange("n (b t) -> n b t", t=S)

            def picked(t, j, bank):
                for n in range(DS):
                    mm = pe.matmul(banks[:, bank + n // 8, n % 8 * B:(n % 8 + 1) * B], lhsT=bc(g.ident[:, j * DS + n:j * DS + n + 1], P, P),
                                   rhs=bt[:, :, bass.ds(t.b, 1)].rearrange("n b t -> n (b t)"), start=True, stop=True)
                return mm

            def step(item):
                t, c, y = item(0), item(1), item(2)
                if t:
                    after(pe, b_read, t.b)
                    picked(t, 0, B_BANK).then_inc(b_ready, 1)
                if y:
                    pe.wait_ge(prod_ready, y.b + 1)
                    after(pe, y_read, y.b - 1)
                    for n in range(DS):
                        pe.matmul(banks[:, Y_BANK + y.u, 0:DT * B], lhsT=g.ident[:], rhs=prod[:, :, n, :], start=n == 0, stop=False)
                    for k in range(DT):
                        mm = pe.matmul(banks[:, Y_BANK + y.u, k * B:(k + 1) * B], lhsT=skip[:, k, :],
                                       rhs=xi[:, k, :].rearrange("p (b t) -> p b t", t=S)[:, :, bass.ds(y.b, 1)].rearrange("p b t -> p (b t)"),
                                       start=False, stop=k == DT - 1)
                    mm.then_inc(y_ready, 1)
                if c:
                    after(pe, prod_ready, c.b)
                    picked(c, 1, C_BANK).then_inc(c_ready, 1)
            skewed(pe, S, 2, step)

        @block.vector
        def _(dve):
            link = Link(dve, dve_link)
            for k in range(DT):
                ins = dve.tensor_scalar(skip[:, k, :], g.ident[:], vec[:, k, TAPS + 2:TAPS + 3], None, ALU.mult)
            ins.then_inc(skip_ready, 1)
            dve.wait_ge(rate_ready, 1)
            dve.tensor_scalar(rate[:], rate[:], -1.0, None, ALU.mult).then_inc(neg_ready, 1)
            dve.wait_ge(zeroed, 1)
            floor = float(np.exp(-10.0))
            flat = state[:].rearrange("p k n b -> p (k n b)")

            def step(item):
                c, y = item(1), item(2)
                if c:
                    dve.wait_ge(decay_ready, c.b + 1)
                    ins = dve.scalar_tensor_tensor(flat, decay[:, c.u, :, :, :].rearrange("p k n b -> p (k n b)"), floor, flat, ALU.max, ALU.mult)
                    ins.then_inc(decay_used, 1)
                    dve.wait_ge(decay_used, c.b + 1)
                    dve.wait_ge(inp_ready, c.b + 1)
                    dve.tensor_tensor(state[:], state[:], inp[:, c.u, :, :, :], ALU.add).then_inc(inp_used, 1)
                    dve.wait_ge(inp_used, c.b + 1)
                    link(dve.tensor_scalar(flat, flat, -CLIP, CLIP, ALU.max, ALU.min))
                    dve.wait_ge(c_ready, c.b + 1)
                    after(dve, y_ready, c.b)
                    dve.tensor_tensor(prod[:], state[:], c_all, ALU.mult).then_inc(prod_ready, 1)
                if y:
                    dve.wait_ge(y_ready, y.b + 1)
                    dve.tensor_copy(at(xi, y.b), banks[:, Y_BANK + y.u, 0:DT * B].rearrange("p (k b) -> p k b", k=DT)).then_inc(y_read, 1)
            skewed(dve, S, 2, step, link, 1)


def gate(nc, g, xi, zd, wo):
    DT = 4
    with ExitStack() as ctx:
        s = Scope(nc, ctx, "s5g")
        sz = s.sb("sz", [P, DT, T])
        z_loaded = [s.sem(f"z_loaded{d}") for d in range(DT)]
        gated, wo_loaded = s.sems("gated wo_loaded")
        block = ctx.enter_context(nc.Block())

        @block.sync
        def _(sp):
            for d in range(DT):
                sp.dma_start(sz[:, d, :], zd[d]).then_inc(z_loaded[d], 16)
            sp.dma_start(wo[:], g.I["p5_wo"]).then_inc(wo_loaded, 16)
            sp.wait_ge(wo_loaded, 16)

        @block.vector
        def _(dve):
            for d in range(DT):
                dve.wait_ge(z_loaded[d], 16)
                dve.tensor_tensor(xi[:, d, :], xi[:, d, :], sz[:, d, :], ALU.mult).then_inc(gated, 1)
            dve.wait_ge(gated, DT)


def phase6(nc, g):
    E, FF = 8, 1024
    LISTED = 2 * T // P + E
    with ExitStack() as ctx:
        s = Scope(nc, ctx, "s6")
        banks = s.psum()
        w1, w2 = s.sb("w1", [P, E, KT, FF]), s.sb("w2", [P, E, FF // P, D])
        b1, b2 = s.sb("b1", [P, E, FF // P]), s.sb("b2", [1, E, D])
        w_loaded = s.sem("w_loaded")
        slots = s.sb("slots", [P, 2, NT], U32)
        gates = s.sb("gates", [P, 2, NT])
        listed = s.sb("listed", [P, LISTED], U32)
        owner = s.sb("owner", [1, LISTED], U32)
        rows = nc.dram_tensor("s6_rows", [T, D], F32, kind="Internal").ap()
        tokens = nc.dram_tensor("s6_tokens", [P * LISTED, 1], U32, kind="Internal").ap()
        results = nc.dram_tensor("s6_results", [LISTED * P, D], F32, kind="Internal").ap()
        route(nc, g, banks, dict(E=E, LISTED=LISTED, w1=w1, w2=w2, b1=b1, b2=b2, w_loaded=w_loaded, slots=slots, gates=gates, listed=listed,
                                 owner=owner, rows=rows, tokens=tokens))
        experts(nc, g, banks, dict(LISTED=LISTED, FF=FF, w1=w1, w2=w2, b1=b1, b2=b2, w_loaded=w_loaded, listed=listed, owner=owner,
                                   rows=rows, results=results))
        combine(nc, g, slots, gates, results)


def route(nc, g, banks, v):
    I, X = g.I, g.X
    E, LISTED = v["E"], v["LISTED"]
    slots, gates, listed, owner, rows, tokens = (v[n] for n in "slots gates listed owner rows tokens".split())
    SHIFT = P.bit_length() - 1
    with ExitStack() as ctx:
        s = Scope(nc, ctx, "s6r")
        sb = s.sb
        n = Normed(s)
        xn = sb("xn", [P, NT, D])
        xT = sb("xT", [P, U, KT, P])
        rw, rb = sb("rw", [P, KT, E]), sb("rb", [P, E])
        count, below = sb("count", [P, E]), sb("below", [P, E, E])
        earlier = sb("earlier", [P, P])
        tile_before = sb("tile_before", [P, P + E])
        tile_no, token = sb("tile_no", [P, LISTED]), sb("token", [P, NT], U32)
        empty = sb("empty", [P, LISTED], U32)
        ones = sb("ones", [P, 1])
        lg = sb("lg", [P, NT, E])
        best, best_at = sb("best", [P, NT, E]), sb("best_at", [P, NT, E], U32)
        at = sb("at", [P, 2, NT])
        diff, ex = sb("diff", [P, NT]), sb("ex", [P, NT])
        hit = sb("hit", [P, 2, E, NT])
        mask = sb("mask", [P, E, NT])
        counts = sb("counts", [P, P])
        size, sizeu, tiles = sb("size", [P, E]), sb("sizeu", [P, E], U32), sb("tiles", [P, E])
        upto, start = sb("upto", [P, E, E]), sb("start", [P, E])
        place = sb("place", [P, E, NT])
        picked, slotf = sb("picked", [P, 2, E, NT]), sb("slotf", [P, 2, NT])
        row_of, tile_of = sb("row_of", [P, 2, NT], U32), sb("tile_of", [P, 2, NT], U32)
        row_f, tile_f, addr = sb("row_f", [P, 2, NT]), sb("tile_f", [P, 2, NT]), sb("addr", [P, 2, NT], U32)
        begun, owned = sb("begun", [P, LISTED, E]), sb("owned", [P, LISTED])
        NCONST = 8
        NG = 4
        (loaded, set_up, stat_ready, rstd_ready, dve_link, xn_ready, xn_stored, emptied, x_tr, xT_ready, logits, diff_ready, ex_ready, mask_ready,
         counted, counts_ready, ranked, addr_ready, scattered, list_loaded) = s.sems(
            "loaded set_up stat_ready rstd_ready dve_link xn_ready xn_stored emptied x_tr xT_ready logits diff_ready ex_ready mask_ready "
            "counted counts_ready ranked addr_ready scattered list_loaded")
        block = ctx.enter_context(nc.Block())

        @block.sync
        def _(sp):
            for dst, src in ((rw, "p6_rw"), (rb, "p6_rb"), (count, "count8"), (below, "below8"), (earlier, "earlier"), (tile_before, "tile_before"),
                             (tile_no, "tile_no"), (token, "token")):
                sp.dma_start(dst[:], I[src]).then_inc(loaded, 16)
            sp.wait_ge(set_up, 1)
            sp.dma_start(tokens.rearrange("(p i) o -> p (i o)", p=P), empty[:]).then_inc(emptied, 16)
            for i in range(NT // NG):
                sp.wait_ge(xn_ready, i + 1)
                sp.dma_start(rows.rearrange("(t p) d -> p t d", p=P)[:, i * NG:(i + 1) * NG, :], xn[:, i * NG:(i + 1) * NG, :]).then_inc(xn_stored, 16)
            sp.dma_start(v["b1"][:], I["p6_b1"]).then_inc(v["w_loaded"], 16)
            sp.dma_start(v["b2"][:], I["p6_b2"]).then_inc(v["w_loaded"], 16)
            for e in range(E):
                sp.dma_start(v["w1"][:, e, :, :], I["p6_w1"][e]).then_inc(v["w_loaded"], 16)
                sp.dma_start(v["w2"][:, e, :, :], I["p6_w2"][e]).then_inc(v["w_loaded"], 16)
            sp.wait_ge(scattered, 16 * 2 * NT)
            sp.dma_start(listed[:], tokens.rearrange("(p i) o -> p (i o)", p=P)).then_inc(list_loaded, 16)
            sp.wait_ge(list_loaded, 16)
            sp.wait_ge(xn_stored, 16 * NG)

        @block.gpsimd
        def _(pool):
            pool.memset(ones[:], 1.0)
            pool.memset(n.half[:], -0.5)
            pool.memset(empty[:], 0).then_inc(set_up, 1)
            pool.wait_ge(set_up, 1)
            pool.wait_ge(stat_ready, 1)
            pool.tensor_tensor(n.rstd[:], n.var[:], bc(n.half[:], P, NT), ALU.pow).then_inc(rstd_ready, 1)
            pool.wait_ge(loaded, 16 * NCONST)
            pool.wait_ge(emptied, 16)
            pool.wait_ge(addr_ready, 1)
            for t in range(NT):
                for j in range(2):
                    pool.indirect_dma_start(tokens, bass.IndirectOffsetOnAxis(addr[:, j, t:t + 1], 0), token[:, t:t + 1], None).then_inc(scattered, 16)

        @block.tensor
        def _(pe):
            pe.wait_ge(loaded, 16 * NCONST)
            for t in range(NT + 1):
                if t < NT:
                    pe.wait_ge(xn_ready, t // NG + 1)
                    after(pe, xT_ready, t - 1)
                    for k in range(KT):
                        mm = pe.transpose(banks[:, t % U, tok(k)], xn[:, t, tok(k)], g.ident[:])
                    mm.then_inc(x_tr, 1)
                if t:
                    pe.wait_ge(xT_ready, t)
                    for k in range(KT):
                        mm = pe.matmul(banks[:, 2, (t - 1) * E:t * E], lhsT=xT[:, (t - 1) % U, k, :], rhs=rw[:, k, :], start=k == 0, stop=k == KT - 1)
                    mm.then_inc(logits, 1)
            pe.wait_ge(mask_ready, 1)
            flat = mask[:].rearrange("p e t -> p (e t)")
            pe.matmul(banks[:, 3, 0:1], lhsT=flat, rhs=ones[:], start=True, stop=True).then_inc(counted, 1)
            pe.matmul(banks[:, 4, 0:P], lhsT=earlier[:], rhs=flat, start=True, stop=False)
            pe.wait_ge(counts_ready, 1)
            pe.matmul(banks[:, 4, 0:P], lhsT=counts[:], rhs=tile_before[:, 0:P], start=False, stop=True)
            pe.matmul(banks[:, 5, 0:E], lhsT=counts[:], rhs=tile_before[:, P:P + E], start=True, stop=True).then_inc(ranked, 1)

        @block.scalar
        def _(act):
            for t in range(NT):
                act.wait_ge(x_tr, t + 1)
                after(act, logits, t - 1)
                act.activation(xT[:, t % U, :, :], banks[:, t % U, 0:D].rearrange("p (k q) -> p k q", k=KT), ACT.Copy).then_inc(xT_ready, 1)
            act.wait_ge(diff_ready, 1)
            act.activation(ex[:], diff[:], ACT.Exp).then_inc(ex_ready, 1)

        @block.vector
        def _(dve):
            link = Link(dve, dve_link)
            row_stats(dve, link, X, n.stats, n.mv, n.var, LN_EPS).then_inc(stat_ready, 1)
            dve.wait_ge(rstd_ready, 1)
            for t in range(NT):
                ins = n.apply(dve, xn[:, t, :], X, t)
                if t % NG == NG - 1:
                    ins.then_inc(xn_ready, 1)
            dve.wait_ge(loaded, 16 * NCONST)
            dve.wait_ge(logits, NT)
            link(dve.tensor_tensor(lg[:], banks[:, 2, 0:NT * E].rearrange("p (t e) -> p t e", e=E), bc(rb[:].unsqueeze(1), P, NT, E), ALU.add))
            for t in range(NT):
                ins = dve.max(best[:, t, :], lg[:, t, :])
            link(ins)
            dve.tensor_tensor(diff[:], best[:, :, 1], best[:, :, 0], ALU.subtract).then_inc(diff_ready, 1)
            for t in range(NT):
                ins = dve.max_index(best_at[:, t, :], best[:, t, :], lg[:, t, :])
            link(ins)
            link(dve.tensor_copy(at[:], best_at[:, :, 0:2].rearrange("p t n -> p n t")))
            for j in range(2):
                ins = dve.tensor_tensor(hit[:, j, :, :], bc(count[:].unsqueeze(2), P, E, NT), bc(at[:, j, :].unsqueeze(1), P, E, NT), ALU.is_equal)
            link(ins)
            dve.tensor_tensor(mask[:], hit[:, 0, :, :], hit[:, 1, :, :], ALU.add).then_inc(mask_ready, 1)
            dve.wait_ge(counted, 1)
            dve.tensor_copy(counts[:], bc(banks[:, 3, 0:1], P, P)).then_inc(counts_ready, 1)
            dve.wait_ge(ex_ready, 1)
            link(dve.tensor_scalar(diff[:], ex[:], 1.0, None, ALU.add))
            link(dve.reciprocal(gates[:, 0, :], diff[:]))
            dve.tensor_tensor(gates[:, 1, :], gates[:, 0, :], ex[:], ALU.mult)
            dve.wait_ge(ranked, 1)
            link(dve.tensor_scalar(size[:], banks[:, 5, 0:E], float(P - 1), None, ALU.add))
            link(dve.tensor_copy(sizeu[:], size[:]))
            link(dve.tensor_scalar(sizeu[:], sizeu[:], SHIFT, None, ALU.logical_shift_right))
            link(dve.tensor_copy(tiles[:], sizeu[:]))
            link(dve.tensor_tensor(upto[:], bc(tiles[:].unsqueeze(1), P, E, E), below[:], ALU.mult))
            link(dve.tensor_reduce(start[:], upto[:], AXX, ALU.add))
            link(dve.scalar_tensor_tensor(place[:], bc(start[:].unsqueeze(2), P, E, NT), float(P), banks[:, 4, 0:P].rearrange("p (e t) -> p e t", e=E),
                                          ALU.mult, ALU.add))
            for j in range(2):
                ins = dve.tensor_tensor(picked[:, j, :, :], hit[:, j, :, :], place[:], ALU.mult)
            link(ins)
            link(dve.tensor_reduce(slotf[:], picked[:].rearrange("p j e t -> p j t e"), AXX, ALU.add))
            link(dve.tensor_copy(slots[:], slotf[:]))
            dve.tensor_scalar(row_of[:], slots[:], P - 1, None, ALU.bitwise_and)
            link(dve.tensor_scalar(tile_of[:], slots[:], SHIFT, None, ALU.logical_shift_right))
            dve.tensor_copy(row_f[:], row_of[:])
            link(dve.tensor_copy(tile_f[:], tile_of[:]))
            link(dve.scalar_tensor_tensor(row_f[:], row_f[:], float(LISTED), tile_f[:], ALU.mult, ALU.add))
            dve.tensor_copy(addr[:], row_f[:]).then_inc(addr_ready, 1)
            link(dve.tensor_tensor(begun[:], bc(tile_no[:].unsqueeze(2), P, LISTED, E), bc(start[:].unsqueeze(1), P, LISTED, E), ALU.is_ge))
            link(dve.tensor_reduce(owned[:], begun[:], AXX, ALU.add))
            link(dve.tensor_scalar(owned[:], owned[:], -1.0, None, ALU.add))
            link(dve.tensor_copy(owner[:], owned[0:1, :]))


def experts(nc, g, banks, v):
    LISTED, FF = v["LISTED"], v["FF"]
    FT = FF // P
    w1, w2, b1, b2, w_loaded, listed, owner, rows, results = (v[n] for n in "w1 w2 b1 b2 w_loaded listed owner rows results".split())
    E = 8
    with ExitStack() as ctx:
        s = Scope(nc, ctx, "s6e")
        sb = s.sb
        idx = sb("idx", [P, U, 1], U32)
        one, row1 = sb("one", [P, 2]), sb("row1", [1, P])
        xg = sb("xg", [P, U, D])
        xT = sb("xT", [P, U, KT, P])
        h = sb("h", [P, U, FF])
        hT = sb("hT", [P, U, FT, P])
        y = sb("y", [P, U, D])
        gathered = [s.sem(f"gathered{u}") for u in range(U)]
        stored = [s.sem(f"stored{u}") for u in range(U)]
        set_up, carried, idx_ready, x_tr, xT_ready, hidden, h_ready, h_tr, hT_ready, product, y_ready = s.sems(
            "set_up carried idx_ready x_tr xT_ready hidden h_ready h_tr hT_ready product y_ready")
        X_BANK, H_BANK, HT_BANK, Y_BANK = 0, 1, 3, 5
        WEIGHTS = 16 * (2 + 2 * E)
        block = ctx.enter_context(nc.Block())

        def expert(engine, t):
            return nc.values_load(owner[0:1, bass.ds(t.b, 1)], engines=[engine], min_val=0, max_val=E - 1,
                                  skip_runtime_bounds_check_because="a count of the eight experts, less one for the first, which always starts at 0")

        @block.sync
        def _(sp):
            def step(item):
                t = item(0)
                sp.wait_ge(y_ready, t.b + 1)
                sp.dma_start(results[bass.ts(t.b, P), :], y[:, t.u, :]).then_inc(stored[t.u], 16)
            skewed(sp, LISTED, 0, step)
            for q in stored:
                sp.wait_ge(q, 16 * (LISTED // U))

        @block.gpsimd
        def _(pool):
            pool.memset(row1[:], 1.0).then_inc(set_up, 1)
            pool.memset(one[:], 1.0).then_inc(carried, 1)

            def step(item):
                t = item(0)
                pool.wait_ge(idx_ready, t.b + 1)
                after(pool, x_tr, t.b - 1)
                pool.wait_ge(carried, t.b + 1)
                pool.tensor_tensor(one[:, 1:2], one[:, 0:1], one[:, 0:1], ALU.mult).then_inc(carried, 1)
                pool.indirect_dma_start(xg[:, t.u, :], None, rows, bass.IndirectOffsetOnAxis(idx[:, t.u, :], 0)).then_inc(gathered[t.u], 16)
            skewed(pool, LISTED, 0, step)

        @block.tensor
        def _(pe):
            pe.wait_ge(set_up, 1)
            pe.wait_ge(w_loaded, WEIGHTS)

            def step(item):
                x, m, o = item(0), item(1), item(2)
                if o:
                    pe.wait_ge(h_ready, o.b + 1)
                    after(pe, hT_ready, FT * o.b)
                    for f in range(FT):
                        mm = pe.transpose(banks[:, HT_BANK + f // 4, tok(f % 4)], h[:, o.u, tok(f)], g.ident[:])
                    mm.then_inc(h_tr, 1)
                if m:
                    e = expert(mybir.EngineType.PE, m)
                    pe.wait_ge(xT_ready, m.b + 1)
                    for j in range(FF // C):
                        for k in range(KT):
                            mm = pe.matmul(banks[:, H_BANK + j, :], lhsT=xT[:, m.u, k, :], rhs=w1[:, bass.ds(e, 1), k, j * C:(j + 1) * C],
                                           start=k == 0, stop=k == KT - 1)
                    mm.then_inc(hidden, 1)
                if o:
                    e = expert(mybir.EngineType.PE, o)
                    pe.wait_ge(hT_ready, FT * (o.b + 1))
                    after(pe, y_ready, o.b)
                    for f in range(FT):
                        pe.matmul(banks[:, Y_BANK, 0:D], lhsT=hT[:, o.u, f, :], rhs=w2[:, bass.ds(e, 1), f, :], start=f == 0, stop=False)
                    pe.matmul(banks[:, Y_BANK, 0:D], lhsT=row1[:], rhs=b2[:, bass.ds(e, 1), :], start=False, stop=True).then_inc(product, 1)
                if x:
                    pe.wait_ge(gathered[x.u], 16 * (x.turn + 1))
                    after(pe, xT_ready, x.b)
                    for k in range(KT):
                        mm = pe.transpose(banks[:, X_BANK, tok(k)], xg[:, x.u, tok(k)], g.ident[:])
                    mm.then_inc(x_tr, 1)
            skewed(pe, LISTED, 2, step)

        @block.scalar
        def _(act):
            act.wait_ge(w_loaded, WEIGHTS)

            def step(item):
                x, o = item(0), item(2)
                if o:
                    e = expert(mybir.EngineType.Activation, o)
                    act.wait_ge(h_tr, o.b + 1)
                    for f in range(FT):
                        act.activation(hT[:, o.u, f, :], banks[:, HT_BANK + f // 4, tok(f % 4)], ACT.Relu,
                                       bias=b1[:, bass.ds(e, 1), f]).then_inc(hT_ready, 1)
                if x:
                    act.wait_ge(x_tr, x.b + 1)
                    act.activation(xT[:, x.u, :, :], banks[:, X_BANK, 0:D].rearrange("p (k q) -> p k q", k=KT), ACT.Copy).then_inc(xT_ready, 1)
            skewed(act, LISTED, 2, step)

        @block.vector
        def _(dve):
            def step(item):
                x, m, o = item(0), item(2), item(3)
                if x:
                    after(dve, x_tr, x.b - 1)
                    dve.tensor_copy(idx[:, x.u, :], listed[:, bass.ds(x.b, 1)]).then_inc(idx_ready, 1)
                if m:
                    dve.wait_ge(hidden, m.b + 1)
                    dve.tensor_copy(h[:, m.u, :], banks[:, H_BANK:H_BANK + 2, :].rearrange("p n c -> p (n c)")).then_inc(h_ready, 1)
                if o:
                    dve.wait_ge(product, o.b + 1)
                    after(dve, stored[o.u], 16 * o.turn)
                    dve.tensor_copy(y[:, o.u, :], banks[:, Y_BANK, 0:D]).then_inc(y_ready, 1)
            skewed(dve, LISTED, 3, step)


def combine(nc, g, slots, gates, results):
    X = g.X
    R = 4
    with ExitStack() as ctx:
        s = Scope(nc, ctx, "s6c")
        got = s.sb("got", [P, R, 2, D])
        one = s.sb("one", [P, 2])
        gathered = [s.sem(f"gathered{r}") for r in range(R)]
        carried, dve_link, added = s.sems("carried dve_link added")
        block = ctx.enter_context(nc.Block())

        @block.gpsimd
        def _(pool):
            pool.memset(one[:], 1.0).then_inc(carried, 1)
            for t in range(NT):
                after(pool, added, t - R + 1)
                pool.wait_ge(carried, t + 1)
                pool.tensor_tensor(one[:, 1:2], one[:, 0:1], one[:, 0:1], ALU.mult).then_inc(carried, 1)
                for j in range(2):
                    pool.indirect_dma_start(got[:, t % R, j, :], None, results, bass.IndirectOffsetOnAxis(slots[:, j, t:t + 1], 0)).then_inc(gathered[t % R], 16)

        @block.vector
        def _(dve):
            link = Link(dve, dve_link)
            for t in range(NT):
                dve.wait_ge(gathered[t % R], 32 * (t // R + 1))
                for j in range(2):
                    ins = dve.scalar_tensor_tensor(X[:, t, :], got[:, t % R, j, :], gates[:, j, t:t + 1], X[:, t, :], ALU.mult, ALU.add)
                    if not j:
                        link(ins)
                ins.then_inc(added, 1)
            dve.wait_ge(added, NT)


class Env:

    def __init__(self, inputs, x, ident):
        self.I, self.X, self.ident = inputs, x, ident


def layers(nc, out, inputs):
    with ExitStack() as ctx:
        s = Scope(nc, ctx, "x")
        g = Env(inputs, s.sb("rows", [P, NT, D]), s.sb("ident", [P, P]))
        loaded, stored = s.sems("loaded stored")
        with nc.Block() as block:
            @block.sync
            def _(sp):
                sp.dma_start(g.X[:], inputs["x"]).then_inc(loaded, 16)
                sp.dma_start(g.ident[:], inputs["ident"]).then_inc(loaded, 16)
                sp.wait_ge(loaded, 32)
        for phase in (phase1, phase2, phase3, phase4, phase5, phase6):
            before = nc.snapshot_sems()
            phase(nc, g)
            nc.clear_and_free_semaphores(nc.allocated_since(before))
            nc.all_engine_barrier()
        with nc.Block() as block:
            @block.sync
            def _(sp):
                sp.dma_start(out.rearrange("(t p) d -> p t d", p=P), g.X[:]).then_inc(stored, 16)
                sp.wait_ge(stored, 16)


def layout(a):
    import numpy as np
    c = np.ascontiguousarray
    P, H1, HD1 = 128, 4, 64
    kp = lambda w, p=P: c(w.reshape(w.shape[0] // p, p, -1).transpose(1, 0, 2))
    col = lambda v, p=P: v.reshape(-1, p).T
    r = {}
    r["x"] = c(a["x"].reshape(16, P, 256).transpose(1, 0, 2))
    r["ctx_768"] = c(a["ctx_768"])
    r["mask_BxS2_bk0"] = c(a["mask_BxS2_bk0"])
    r["ident"] = np.eye(P, dtype=np.float32)
    ch, row = np.arange(256), np.arange(P)
    r["headmask4"] = c((ch[:, None] // HD1 == np.arange(H1)).astype(np.float32).reshape(2, P, H1).transpose(1, 0, 2))
    r["blockmask4"] = (row[:, None] // 32 == ch // HD1).astype(np.float32)
    r["sel"] = (row[:, None] % 32 == np.arange(32)).astype(np.float32)
    p = "L0_xattn_"
    two = lambda v: np.concatenate([v, v])
    r["p1_vec"] = c(np.stack([col(a[p + "ln_l_g"]), col(a[p + "ln_l_b"]), col(np.tile(a[p + "qn_g"], 4)),
                              col(np.tile(a[p + "kn_g"], 4)), col(a[p + "bo"])], axis=1))
    r["p1_cvec"] = c(np.stack([col(a[p + "ln_x_g"], 96), col(a[p + "ln_x_b"], 96)], axis=1))
    r["p1_wq"], r["p1_wlkv"], r["p1_wo"] = (kp(a[p + n].T) for n in ("Wq", "Wlkv", "Wo"))
    r["p1_wkv"] = kp(a[p + "Wkv"].T, 96)
    r["p2_w"] = kp(np.concatenate([a["L0_attn_Wq"], *(a["L0_attn_Wkv"].reshape(256, 16, 80)[:, :, lo:hi].reshape(256, -1)
                                                     for lo, hi in ((0, 16), (16, 80)))], axis=1))
    r["p2_wo"] = kp(a["L0_attn_Wout"])
    r["headmask8"] = (row[:, None] // 16 == np.arange(8)).astype(np.float32)
    r["batchmask"] = (row[:, None] // 32 == row // 32).astype(np.float32)
    p = "L0_ffn_"
    r["p3_wq"], r["p3_wqT"] = kp(a[p + "w_q"]), kp(c(a[p + "w_q"].T))
    r["p3_gb"] = c(np.stack([col(a[p + "bn_gamma"]), col(a[p + "bn_beta"])], axis=1))
    r["p3_keys"] = c(a[p + "keys"].transpose(3, 2, 0, 1).reshape(P, 16, 64))
    r["p3_table"] = np.concatenate([a[p + "down_embed"], a[p + "up_embed"]], axis=1)
    r["count8"] = np.tile(np.arange(8, dtype=np.float32), (P, 1))
    p = "L1_xattn_"
    r["p4_vec"] = c(np.stack([col(a[p + n]) for n in ("bq", "bk", "bv", "bo")], axis=1))
    r["p4_wq"], r["p4_wo"] = kp(a[p + "Wq"]), kp(a[p + "Wo"])
    r["p4_wk"], r["p4_wv"] = kp(a[p + "Wk"], 96), kp(a[p + "Wv"], 96)
    r["blockmask16"] = (row[:, None] // 32 == np.arange(64) // 16).astype(np.float32)
    p = "L1_attn_"
    r["p5_vec"] = c(np.stack([col(v) for v in (*a[p + "W_conv"], a[p + "b_conv"], a[p + "b_dt"], a[p + "D"])], axis=2))
    r["p5_win"] = c(a[p + "W_in"].reshape(2, P, 2, 4, P).transpose(3, 1, 0, 2, 4))
    r["p5_wo"], r["p5_wx"], r["p5_wdt"] = kp(a[p + "W_out"]), kp(a[p + "W_xproj"]), c(a[p + "W_dt"])
    r["p5_alog"] = kp(a[p + "A_log"])
    r["p6_rw"], r["p6_rb"] = kp(a["L1_ffn_router_w"]), np.tile(a["L1_ffn_router_b"], (P, 1))
    r["p6_b2"] = c(a["L1_ffn_b2"].reshape(1, 8, 256))
    r["below8"] = np.tile(np.tril(np.ones((8, 8), np.float32), -1), (P, 1, 1))
    r["earlier"] = np.triu(np.ones((P, P), np.float32), 1)
    same, before = row[:, None] // 16 == row // 16, row[:, None] % 16 < row % 16
    r["tile_before"] = np.concatenate([same & before, row[:, None] // 16 == np.arange(8)], axis=1).astype(np.float32)
    r["tile_no"] = np.tile(np.arange(40, dtype=np.float32), (P, 1))
    r["token"] = c(np.arange(2048, dtype=np.uint32).reshape(16, P).T)
    r["p6_w1"] = c(a["L1_ffn_W1"].reshape(8, 2, P, 1024).transpose(0, 2, 1, 3))
    r["p6_w2"] = c(a["L1_ffn_W2"].reshape(8, 8, P, 256).transpose(0, 2, 1, 3))
    r["p6_b1"] = c(a["L1_ffn_b1"].reshape(8, 8, P).transpose(2, 0, 1))
    return r


def kernel(**inputs):
    import numpy as _np
    import concourse.bacc as _bacc
    from concourse import mybir as _mybir
    from concourse.bass_utils import run_bass_kernel_spmd as _run

    nc = _bacc.Bacc("TRN2", target_bir_lowering=False, num_devices=1)
    arrays = layout({name: _np.asarray(a) for name, a in inputs.items()})
    aps = {name: nc.dram_tensor(name, a.shape, _mybir.dt.from_np(a.dtype), kind="ExternalInput").ap() for name, a in arrays.items()}
    out = nc.dram_tensor("out", (T, D), _mybir.dt.float32, kind="ExternalOutput").ap()
    layers(nc, out, aps)
    r = _run(nc, [arrays], core_ids=[0])
    return _np.asarray(r.results[0]["out"]).reshape(B, S, D)
```

```python
from contextlib import ExitStack

import numpy as np
import concourse.bass as bass
from concourse import mybir

ALU = mybir.AluOpType
ACT = mybir.ActivationFunctionType
AXX = mybir.AxisListType.X
F32 = mybir.dt.float32
U32 = mybir.dt.uint32
U8 = mybir.dt.uint8

P = 128
B, S, D = 64, 32, 256
T = B * S
NT = T // P
BT = P // S
KT = D // P
CTX, DC = 257, 192
DH = DC // 2
C = 512
NC = T // C
LN_EPS = 1e-5
U = 2


class Link:

    def __init__(self, eng, sem):
        self.eng, self.sem, self.base, self.n = eng, sem, 0, 0

    def __call__(self, ins):
        self.n += 1
        ins.then_inc(self.sem, 1)
        self.eng.wait_ge(self.sem, self.base + self.n)

    def loop(self, i, per):
        self.start, self.per = self.n, per
        self.base, self.n = i * per + self.start, 0

    def end(self, trips):
        assert self.n == self.per, (self.n, self.per)
        self.base, self.n = 0, self.start + trips * self.per


def signals(n):
    return n + 1


def dma_signals(n):
    return 16 * (n + 1)


def opens(eng, *sems):
    for s in sems:
        eng.sem_inc(s, 1)


def bc(ap, *shape):
    return ap.broadcast_to(list(shape))


def tok(t):
    return bass.ts(t, P)


class Scope:

    def __init__(self, nc, ctx, name):
        self.nc, self.ctx, self.name = nc, ctx, name

    def sb(self, name, shape, dt=F32):
        return self.ctx.enter_context(self.nc.sbuf_tensor(f"{self.name}_{name}", shape, dt))

    def sem(self, name):
        return self.nc.alloc_semaphore(f"{self.name}_{name}")

    def sems(self, names):
        return [self.sem(n) for n in names.split()]

    def psum(self):
        return self.ctx.enter_context(self.nc.psum_tensor(f"{self.name}_ps", [P, 8, 512], F32))


def row_stats(dve, link, stats, mv, var, eps, x=None, loaded=()):
    if x is not None:
        for t in range(NT):
            if loaded and t % (NT // len(loaded)) == 0:
                dve.wait_ge(loaded[t // (NT // len(loaded))], 16)
            last = dve.bn_stats(stats[:, t, :], x[:, t, :])
        link(last)
    for t in range(NT):
        last = dve.bn_aggr(mv[:, t, :], stats[:, t, :])
    link(last)
    return dve.tensor_scalar(var[:, :], mv[:, :, 1], eps, None, ALU.add)


def project_out(nc, g, name, banks, OT, wo, bias=None, kt=KT, gate=None):
    X = g.X
    CT = C // P
    with ExitStack() as ctx:
        s = Scope(nc, ctx, name)
        product, added, gated, biased = s.sems("product added gated biased")
        if gate is not None:
            gt = s.sb("gate", [P, NC, kt, C])
            gate_loaded = [s.sem(f"gate_loaded{c}") for c in range(NC)]
        block = ctx.enter_context(nc.Block())

        if gate is not None:
            @block.sync
            def _(sp):
                for c in range(NC):
                    sp.dma_start(gt[:, c, :, :], gate.rearrange("k p t -> p k t")[:, :, c * C:(c + 1) * C]).then_inc(gate_loaded[c], 16)

        @block.tensor
        def _(pe):
            for t in range(NT):
                if gate is not None:
                    pe.wait_ge(gated, t // CT + 1)
                after(pe, added, t - 7)
                for k in range(kt):
                    mm = pe.matmul(banks[:, t % 8, 0:D], lhsT=OT[:, k, tok(t)], rhs=wo[:, k, :], start=k == 0, stop=k == kt - 1)
                mm.then_inc(product, 1)

        @block.vector
        def _(dve):
            def gate_chunk(c):
                cs = slice(c * C, (c + 1) * C)
                dve.wait_ge(gate_loaded[c], 16)
                dve.tensor_tensor(OT[:, :, cs], OT[:, :, cs], gt[:, c, :, :], ALU.mult).then_inc(gated, 1)
            if gate is not None:
                gate_chunk(0)
            if bias is not None:
                dve.tensor_tensor(X[:], X[:], bc(bias[:].unsqueeze(1), P, NT, D), ALU.add).then_inc(biased, 1)
                dve.wait_ge(biased, 1)
            for t in range(NT):
                if gate is not None and t % CT == 0 and t // CT + 1 < NC:
                    gate_chunk(t // CT + 1)
                dve.wait_ge(product, t + 1)
                dve.tensor_tensor(X[:, t, :], X[:, t, :], banks[:, t % 8, 0:D], ALU.add).then_inc(added, 1)
                if t:
                    dve.wait_ge(added, t)
                    dve.bn_stats(g.stats[:, t - 1, :], X[:, t - 1, :])
            dve.wait_ge(added, NT)
            dve.bn_stats(g.stats[:, NT - 1, :], X[:, NT - 1, :])


class Normed:

    def __init__(self, s):
        self.mv = s.sb("mv", [P, NT, 2])
        self.var, self.rstd, self.half = s.sb("var", [P, NT]), s.sb("rstd", [P, NT]), s.sb("half", [P, 1])

    def apply(self, dve, out, X, t):
        return dve.tensor_scalar(out, X[:, t, :], self.mv[:, t, 0:1], self.rstd[:, bass.ds(t, 1)], ALU.subtract, ALU.mult)


def normed_transposed(nc, g, s, banks, n, xT, loads=(), loaded=None, beside=None):
    X = g.X
    W = 2 * P
    with ExitStack() as ctx:
        a = Scope(nc, ctx, s.name + "n")
        xn = a.sb("xn", [P, U, 2, D])
        half_ready, stat_ready, rstd_ready, dve_link, ln_ready, x_tr, xT_ready = a.sems(
            "half_ready stat_ready rstd_ready dve_link ln_ready x_tr xT_ready")
        block = ctx.enter_context(nc.Block())

        @block.sync
        def _(sp):
            for dst, src in loads:
                sp.dma_start(dst[:], g.I[src]).then_inc(loaded, 16)
            if beside:
                beside["sync"](sp)

        @block.gpsimd
        def _(pool):
            pool.memset(n.half[:], -0.5).then_inc(half_ready, 1)
            pool.wait_ge(half_ready, 1)
            pool.wait_ge(stat_ready, 1)
            pool.tensor_tensor(n.rstd[:], n.var[:], bc(n.half[:], P, NT), ALU.pow).then_inc(rstd_ready, 1)

        @block.vector
        def _(dve):
            link = Link(dve, dve_link)
            row_stats(dve, link, g.stats, n.mv, n.var, LN_EPS).then_inc(stat_ready, 1)
            dve.wait_ge(rstd_ready, 1)

            def step(item):
                c = item(0)
                after(dve, x_tr, c.b - 1)
                for j in range(2):
                    ins = n.apply(dve, xn[:, c.u, j, :], X, c.b * 2 + j)
                ins.then_inc(ln_ready, 1)
            skewed(dve, NT // 2, 0, step)

        @block.tensor
        def _(pe):
            def step(item):
                c = item(0)
                pe.wait_ge(ln_ready, c.b + 1)
                after(pe, xT_ready, c.b - 1)
                for k in range(KT):
                    for j in range(2):
                        mm = pe.transpose(banks[:, c.u, k * W + j * P:k * W + (j + 1) * P], xn[:, c.u, j, tok(k)], g.ident[:])
                mm.then_inc(x_tr, 1)
            if beside:
                beside["tensor"](pe)
            skewed(pe, NT // 2, 0, step)

        @block.scalar
        def _(act):
            def step(item):
                c = item(0)
                act.wait_ge(x_tr, c.b + 1)
                act.activation(xT[:, :, bass.ts(c.b, W)], banks[:, c.u, :].rearrange("p (k q) -> p k q", k=KT), ACT.Copy).then_inc(xT_ready, 1)
            if beside:
                beside["scalar"](act)
            skewed(act, NT // 2, 0, step)


class Item:

    def __init__(self, i, offset):
        self.b, self.u, self.turn = i * 2 + offset, offset % 2, i + offset // 2


def skewed(eng, n, depth, step, link=None, links=0):
    lead = depth + 2 + depth % 2

    def lone(v):
        step(lambda s: Item(0, v - s) if 0 <= v - s < n else None)
    for v in range(lead):
        lone(v)
    trips = (n - lead) // 2
    with eng.Fori(0, trips) as i:
        if link:
            link.loop(i, 2 * links)
        for u in range(2):
            step(lambda s: Item(i, lead + u - s))
    if link:
        link.end(trips)
    for v in range(lead + 2 * trips, n + depth):
        lone(v)


def after(eng, sem, n):
    if not (isinstance(n, int) and n <= 0):
        eng.wait_ge(sem, n)


def phase1(nc, g):
    I, X, ident = g.I, g.X, g.ident
    H, HD = 4, 64
    NK = CTX + S
    with ExitStack() as ctx:
        def sb(name, shape, dt=F32):
            return ctx.enter_context(nc.sbuf_tensor("s1_" + name, shape, dt))

        def sem(name):
            return nc.alloc_semaphore("p1_" + name)

        banks = ctx.enter_context(nc.psum_tensor("p1_ps", [P, 8, 512], F32))
        ps = banks[:].rearrange("p (u n) c -> p u n c", u=U)
        QT = sb("QT", [P, KT, B * S])
        KE = sb("KE", [P, KT, B, S + 1])
        V3 = sb("V3", [S + 1, B, D])
        OT = sb("OT", [P, KT, B * S])
        wq = sb("wq", [P, KT, D])
        wlkv = sb("wlkv", [P, KT, 2 * D])
        wkv = sb("wkv", [DH, 2, 2 * D])
        wc = sb("wc", [DH, 2, 2 * D])
        bias = sb("bias", [P, 2 * D])
        wo = sb("wo", [P, KT, D])
        vec = sb("vec", [P, 4, KT])
        bo = sb("bo", [P, D])
        cvec = sb("cvec", [DH, 2, 2])
        headmask = sb("headmask", [P, KT, H])
        blockmask = sb("blockmask", [P, D])
        sel = sb("sel", [P, S])
        half = sb("half", [P, 1])
        mask8 = sb("mask8", [P, B, CTX], U8)

        load, load_late = sem("load"), sem("load_late")
        dve_link = sem("dve_link")

        with ExitStack() as actx:
            def sa(name, shape, dt=F32):
                return actx.enter_context(nc.sbuf_tensor("p1a_" + name, shape, dt))

            stats = sa("stats", [P, NT, 6])
            mv = sa("mv", [P, NT, 2])
            var = sa("var", [P, NT])
            rstd = sa("rstd", [P, NT])
            lat = sa("lat", [P, NT, D])
            ln = sa("ln", [P, U, D])
            lnT = sa("lnT", [P, U, KT, P])
            sq = sa("sq", [P, U, 2 * D])
            ss = sa("ss", [P, U, 8])
            rn = sa("rn", [P, U, 8])
            qk = sa("qk", [P, U, 2 * D])
            vl = sa("vl", [P, U, D])
            cx = sa("cx", [B, DC])
            cst = sa("cst", [B, 6])
            cmv = sa("cmv", [B, 2])
            cve = sa("cve", [B, 1])
            crs = sa("crs", [B, 1])
            cn = sa("cn", [B, DC])
            cT = sa("cT", [DH, 2, B])
            csq = sa("csq", [B, D])
            css = sa("css", [B, 4])
            crn = sa("crn", [B, 4])
            ck = sa("ck", [B, D])
            cv = sa("cv", [B, D])
            stat_ready, rstd_ready = sem("stat_ready"), sem("rstd_ready")
            half_ready, wg_ready, w_summed = sem("half_ready"), sem("wg_ready"), sem("w_summed")
            cstat_ready, crstd_ready, cn_ready = sem("cstat_ready"), sem("crstd_ready"), sem("cn_ready")
            c_tr, cT_ready, c_proj, csq_ready = sem("c_tr"), sem("cT_ready"), sem("c_proj"), sem("csq_ready")
            css_ready, crn_ready, ck_ready, c_tr2 = sem("css_ready"), sem("crn_ready"), sem("ck_ready"), sem("c_tr2")
            cv_ready, kx_ready, cv_loaded = sem("cv_ready"), sem("kx_ready"), sem("cv_loaded")
            v3_loaded = [sem(f"v3_loaded{u}") for u in range(U)]
            ln_ready, ln_tr, lnT_ready, proj = sem("ln_ready"), sem("ln_tr"), sem("lnT_ready"), sem("proj")
            sq_ready, ss_ready, rn_ready, qk_ready = sem("sq_ready"), sem("ss_ready"), sem("rn_ready"), sem("qk_ready")
            qk_tr, qT_ready, kT_ready, vl_ready = sem("qk_tr"), sem("qT_ready"), sem("kT_ready"), sem("vl_ready")
            NLOAD = 6
            T_BANK, Q_BANK, KV_BANK, QK_BANK = 0, 1, 3, 5
            block = actx.enter_context(nc.Block())

            @block.sync
            def _(sp):
                sp.dma_start(cx[:], I["ctx_768"][:, CTX - 1, :]).then_inc(load, 16)
                for dst, src in ((cvec, "p1_cvec"), (wkv, "p1_wkv"), (vec, "p1_vec"), (wq, "p1_wq"), (wlkv, "p1_wlkv")):
                    sp.dma_start(dst[:], I[src]).then_inc(load, 16)
                for dst, src in ((headmask, "headmask4"), (blockmask, "blockmask4"), (sel, "sel"), (wo, "p1_wo"), (bo, "p1_bo")):
                    sp.dma_start(dst[:], I[src]).then_inc(load_late, 16)
                sp.dma_start(mask8[:].rearrange("p b k -> p (b k)"),
                             I["mask_BxS2_bk0"].rearrange("b k -> (b k)").unsqueeze(0).broadcast_to([P, B * CTX])).then_inc(load_late, 16)
                sp.wait_ge(cv_ready, 1)
                sp.dma_start(V3[0:1, :, :], cv[:]).then_inc(cv_loaded, 16)

                def step(item):
                    c = item(0)
                    sp.wait_ge(vl_ready, c.b + 1)
                    for b in range(BT):
                        sp.dma_start(V3[1:S + 1, c.b * BT + b, :], vl[b * S:b * S + S, c.u, :]).then_inc(v3_loaded[c.u], 16)
                skewed(sp, NT, 0, step)
                sp.wait_ge(cv_loaded, 16)
                sp.wait_ge(load_late, 16 * 6)
                for q in v3_loaded:
                    sp.wait_ge(q, 16 * BT * NT // U)

            @block.gpsimd
            def _(pool):
                pool.memset(half[:], -0.5).then_inc(half_ready, 1)
                pool.wait_ge(half_ready, 1)
                for n in range(2):
                    pool.wait_ge(stat_ready, n + 1)
                    pool.tensor_tensor(rstd[:], var[:], bc(half[:], P, NT), ALU.pow).then_inc(rstd_ready, 1)
                    if n == 0:
                        pool.wait_ge(cstat_ready, 1)
                        pool.tensor_tensor(crs[:], cve[:], half[0:B, :], ALU.pow).then_inc(crstd_ready, 1)
                pool.wait_ge(css_ready, 1)
                pool.tensor_tensor(crn[:], css[:], bc(half[0:B, :], B, 4), ALU.pow).then_inc(crn_ready, 1)

                def step(item):
                    c = item(0)
                    pool.wait_ge(ss_ready, c.b + 1)
                    pool.tensor_tensor(rn[:, c.u, :], ss[:, c.u, :], bc(half[:], P, 8), ALU.pow).then_inc(rn_ready, 1)
                skewed(pool, NT, 0, step)

            @block.tensor
            def _(pe):
                pe.wait_ge(load, 16 * NLOAD)
                pe.wait_ge(half_ready, 1)
                for k in range(2):
                    pe.matmul(banks[:, 6, :], lhsT=bc(cvec[:, 1, k:k + 1], DH, P), rhs=wkv[:, k, :], start=k == 0, stop=k == 1)
                pe.wait_ge(wg_ready, 1)
                for k in range(2):
                    mm = pe.matmul(banks[0:DH, 7, :], lhsT=bc(half[0:DH, :], DH, DH), rhs=wc[:, k, :], start=k == 0, stop=k == 1)
                mm.then_inc(w_summed, 1)
                pe.wait_ge(cn_ready, 1)
                for k in range(2):
                    mm = pe.transpose(ps[0:DH, 0, 0, k * B:(k + 1) * B], cn[:, k * DH:(k + 1) * DH], g.ident[0:B, 0:B])
                mm.then_inc(c_tr, 1)
                pe.wait_ge(cT_ready, 1)
                for k in range(2):
                    mm = pe.matmul(ps[0:B, 0, 1, :], lhsT=cT[:, k, :], rhs=wkv[:, k, :], start=k == 0, stop=k == 1)
                mm.then_inc(c_proj, 1)
                pe.wait_ge(ck_ready, 1)
                for k in range(KT):
                    mm = pe.transpose(ps[:, 0, 2, k * B:(k + 1) * B], ck[:, k * P:(k + 1) * P], g.ident[0:B, 0:B])
                mm.then_inc(c_tr2, 1)
                pe.wait_ge(kx_ready, 1)

                def step(item):
                    t, c, n = item(1), item(2), item(4)
                    if t:
                        pe.wait_ge(ln_ready, t.b + 1)
                        after(pe, lnT_ready, t.b)
                        for k in range(KT):
                            mm = pe.transpose(banks[:, T_BANK, tok(k)], ln[:, t.u, tok(k)], g.ident[:])
                        mm.then_inc(ln_tr, 1)
                    if c:
                        pe.wait_ge(lnT_ready, c.b + 1)
                        after(pe, qk_ready, c.b - 1)
                        for k in range(KT):
                            pe.matmul(banks[:, Q_BANK + c.u, 0:D], lhsT=lnT[:, c.u, k, :], rhs=wq[:, k, :], start=k == 0, stop=k == KT - 1)
                        for k in range(KT):
                            mm = pe.matmul(banks[:, KV_BANK + c.u, :], lhsT=lnT[:, c.u, k, :], rhs=wlkv[:, k, :], start=k == 0, stop=k == KT - 1)
                        mm.then_inc(proj, 1)
                    if n:
                        pe.wait_ge(qk_ready, n.b + 1)
                        after(pe, kT_ready, n.b)
                        for k in range(2 * KT):
                            mm = pe.transpose(banks[:, QK_BANK, tok(k)], qk[:, n.u, tok(k)], g.ident[:])
                        mm.then_inc(qk_tr, 1)
                skewed(pe, NT, 4, step)

            @block.scalar
            def _(act):
                act.wait_ge(load, 16 * NLOAD)
                act.wait_ge(c_tr, 1)
                for k in range(2):
                    ins = act.activation(cT[:, k, :], ps[0:DH, 0, 0, k * B:(k + 1) * B], ACT.Identity,
                                         bias=cvec[:, 1, k:k + 1], scale=cvec[:, 0, k:k + 1])
                ins.then_inc(cT_ready, 1)
                act.wait_ge(c_proj, 1)
                act.activation(csq[:], ps[0:B, 0, 1, 0:D], ACT.Square).then_inc(csq_ready, 1)
                act.activation(cv[:], ps[0:B, 0, 1, D:2 * D], ACT.Copy).then_inc(cv_ready, 1)
                act.wait_ge(c_tr2, 1)
                for k in range(KT):
                    ins = act.activation(KE[:, k, :, 0:1], ps[:, 0, 2, k * B:(k + 1) * B].unsqueeze(2), ACT.Identity, scale=vec[:, 3, k:k + 1])
                ins.then_inc(kx_ready, 1)

                def step(item):
                    t, c, n = item(1), item(2), item(4)
                    if t:
                        act.wait_ge(ln_tr, t.b + 1)
                        for k in range(KT):
                            ins = act.activation(lnT[:, t.u, k, :], banks[:, T_BANK, tok(k)], ACT.Identity,
                                                 bias=vec[:, 1, k:k + 1], scale=vec[:, 0, k:k + 1])
                        ins.then_inc(lnT_ready, 1)
                    if c:
                        act.wait_ge(proj, c.b + 1)
                        act.activation(sq[:, c.u, 0:D], banks[:, Q_BANK + c.u, 0:D], ACT.Square)
                        act.activation(sq[:, c.u, D:2 * D], banks[:, KV_BANK + c.u, 0:D], ACT.Square).then_inc(sq_ready, 1)
                        after(act, v3_loaded[c.u], 16 * BT * c.turn)
                        act.activation(vl[:, c.u, :], banks[:, KV_BANK + c.u, D:2 * D], ACT.Copy).then_inc(vl_ready, 1)
                    if n:
                        act.wait_ge(qk_tr, n.b + 1)
                        act.wait_ge(qT_ready, n.b + 1)
                        for k in range(KT):
                            ins = act.activation(KE[:, k, bass.ts(n.b, BT), 1:S + 1], banks[:, QK_BANK, tok(KT + k)].rearrange("p (b q) -> p b q", q=S),
                                                 ACT.Identity, scale=vec[:, 3, k:k + 1])
                        ins.then_inc(kT_ready, 1)
                skewed(act, NT, 4, step)

            @block.vector
            def _(dve):
                link = Link(dve, dve_link)
                row_stats(dve, link, stats, mv, var, LN_EPS, X, g.x_loaded).then_inc(stat_ready, 1)
                dve.wait_ge(load, 16 * NLOAD)
                for k in range(2):
                    ins = dve.tensor_scalar(wc[:, k, :], wkv[:, k, :], cvec[:, 0, k:k + 1], None, ALU.mult)
                ins.then_inc(wg_ready, 1)
                link(dve.bn_stats(cst[:], cx[:]))
                link(dve.bn_aggr(cmv[:], cst[:]))
                dve.tensor_scalar(cve[:], cmv[:, 1:2], LN_EPS, None, ALU.add).then_inc(cstat_ready, 1)
                dve.wait_ge(rstd_ready, 1)
                for t in range(NT):
                    ins = dve.tensor_scalar(lat[:, t, :], X[:, t, :], mv[:, t, 0:1], rstd[:, t:t + 1], ALU.subtract, ALU.mult)
                dve.wait_ge(crstd_ready, 1)
                dve.tensor_scalar(cn[:], cx[:], cmv[:, 0:1], crs[:], ALU.subtract, ALU.mult).then_inc(cn_ready, 1)
                link(ins)
                row_stats(dve, link, stats, mv, var, LN_EPS, lat).then_inc(stat_ready, 1)
                dve.wait_ge(w_summed, 1)
                dve.wait_ge(wg_ready, 1)
                dve.tensor_copy(bias[:], banks[:, 6, :])
                for k in range(2):
                    ins = dve.scalar_tensor_tensor(wc[:, k, :], banks[0:DH, 7, :], 2.0 / DC, wc[:, k, :], ALU.mult, ALU.add)
                link(ins)
                dve.wait_ge(csq_ready, 1)
                link(dve.tensor_reduce(css[:], csq[:].rearrange("p (h d) -> p h d", h=H), AXX, ALU.add))
                dve.tensor_scalar(css[:], css[:], 1.0 / HD, 1e-16, ALU.mult, ALU.max).then_inc(css_ready, 1)
                dve.wait_ge(crn_ready, 1)
                dve.wait_ge(cv_ready, 1)
                dve.tensor_tensor(ck[:].rearrange("p (h d) -> p h d", h=H), ps[0:B, 0, 1, 0:D].rearrange("p (h d) -> p h d", h=H),
                                  bc(crn[:].unsqueeze(2), B, H, HD), ALU.mult).then_inc(ck_ready, 1)
                dve.wait_ge(rstd_ready, 2)

                def step(item):
                    t, c, n, m = item(0), item(2), item(3), item(4)
                    if t:
                        after(dve, ln_tr, t.b - 1)
                        dve.tensor_scalar(ln[:, t.u, :], lat[:, t.b, :], mv[:, t.b, 0:1], rstd[:, bass.ds(t.b, 1)],
                                          ALU.subtract, ALU.mult).then_inc(ln_ready, 1)
                    if n:
                        dve.wait_ge(rn_ready, n.b + 1)
                        dve.wait_ge(vl_ready, n.b + 1)
                        after(dve, qk_tr, n.b - 1)
                        for j, bank in enumerate((Q_BANK, KV_BANK)):
                            ins = dve.tensor_tensor(qk[:, n.u, j * D:(j + 1) * D].rearrange("p (h d) -> p h d", h=H),
                                                    banks[:, bank + n.u, 0:D].rearrange("p (h d) -> p h d", h=H),
                                                    bc(rn[:, n.u, j * H:(j + 1) * H].unsqueeze(2), P, H, HD), ALU.mult)
                        ins.then_inc(qk_ready, 1)
                    if c:
                        dve.wait_ge(sq_ready, c.b + 1)
                        link(dve.tensor_reduce(ss[:, c.u, :], sq[:, c.u, :].rearrange("p (h d) -> p h d", h=2 * H), AXX, ALU.add))
                        dve.tensor_scalar(ss[:, c.u, :], ss[:, c.u, :], 1.0 / HD, 1e-16, ALU.mult, ALU.max).then_inc(ss_ready, 1)
                    if m:
                        dve.wait_ge(qk_tr, m.b + 1)
                        for k in range(KT):
                            ins = dve.tensor_scalar(QT[:, k, tok(m.b)], banks[:, QK_BANK, tok(k)], vec[:, 2, k:k + 1],
                                                    HD ** -0.5, ALU.mult, ALU.mult)
                        ins.then_inc(qT_ready, 1)
                skewed(dve, NT, 4, step, link, 1)
        phase1_attention(nc, g, banks, dict(
            H=H, HD=HD, NK=NK, QT=QT, KE=KE, V3=V3, OT=OT, vec=vec,
            headmask=headmask, blockmask=blockmask, sel=sel, half=half, mask8=mask8, wc=wc, bias=bias))
        project_out(nc, g, "s1o", banks, OT, wo, bo)


def phase1_attention(nc, g, banks, v):
    I = g.I
    BIG = 1e30
    H, HD, NK = v["H"], v["HD"], v["NK"]
    QT, KE, V3, OT, wc, bias, vec = (v[n] for n in ("QT", "KE", "V3", "OT", "wc", "bias", "vec"))
    headmask, blockmask, sel, half, mask8 = (v[n] for n in ("headmask", "blockmask", "sel", "half", "mask8"))
    with ExitStack() as ctx:
        s = Scope(nc, ctx, "s1b")
        sb = s.sb
        carry = sb("carry", [P, U])
        one = sb("one", [P, 1])
        cx = sb("cx", [P, U, 2, DC])
        cst, cmv = sb("cst", [P, U, 2, 6]), sb("cmv", [P, U, 2, 2])
        cve, crs = sb("cve", [P, U, 2]), sb("crs", [P, U, 2])
        cT = sb("cT", [DH, U, 2, 2 * P])
        sq = sb("sq", [P, U, 2, D])
        ss, rn = sb("ss", [P, U, 2 * H]), sb("rn", [P, U, 2 * H])
        kn = sb("kn", [P, U, 2, D])
        vv = sb("vv", [P, U, 2, D])
        kT = sb("kT", [P, U, KT, NK])
        qb = sb("qb", [P, U, KT, P])
        mb = sb("mb", [P, U, NK])
        sc = sb("sc", [P, U, NK])
        mx, nm = sb("mx", [P, U, 1]), sb("nm", [P, U, 1])
        pr = sb("pr", [P, U, NK])
        rs, ri = sb("rs", [P, U, 1]), sb("ri", [P, U, 1])
        pT = sb("pT", [P, U, 3, P])
        om = sb("om", [P, U, D])
        (cve_ready, crs_ready, kr_ready, keys, values, sq_ready, vv_ready, ss_ready, rn_ready, kn_ready,
         k_tr, kT_ready, ke_ready, qb_ready, mb_zeroed, mb_ready, scores, sc_ready, pr_ready, p_tr, pT_ready, pv, om_ready, o_tr, oT_ready,
         one_ready, dve_link) = s.sems(
            "cve_ready crs_ready kr_ready keys values sq_ready vv_ready ss_ready rn_ready kn_ready "
            "k_tr kT_ready ke_ready qb_ready mb_zeroed mb_ready scores sc_ready pr_ready p_tr pT_ready pv om_ready o_tr oT_ready "
            "one_ready dve_link")
        cx_loaded = [s.sem(f"cx_loaded{u}") for u in range(U)]
        c_loaded = [s.sem(f"c_loaded{u}") for u in range(U)]
        K_BANK, V_BANK, TR_BANK, S_BANK, P_BANK, O_BANK = 0, 2, 4, 5, 6, 7
        LAG_TR, LAG_KV, LAG_KN, LAG_AT, LAG_OUT = range(5)
        block = ctx.enter_context(nc.Block())

        @block.sync
        def _(sp):
            def step(item):
                c = item(0)
                after(sp, cve_ready, c.b - 1)
                sp.dma_start(cx[:, c.u, :, :], I["ctx_768"][c.b, 0:2 * P, :].rearrange("(j p) c -> p j c", p=P)).then_inc(cx_loaded[c.u], 16)
                after(sp, values, c.b - 1)
                sp.dma_start(cT[:, c.u, :, :], I["ctxT"][c.b, :, :, 0:2 * P]).then_inc(c_loaded[c.u], 16)
            skewed(sp, B, 0, step)

        @block.gpsimd
        def _(pool):
            pool.memset(mb[:], 0.0).then_inc(mb_zeroed, 1)
            pool.memset(one[:], 1.0).then_inc(one_ready, 1)
            pool.wait_ge(one_ready, 1)

            def step(item):
                c = item(LAG_KN)
                if c:
                    after(pool, scores, c.b - 1)
                    pool.tensor_tensor(qb[:, c.u, :, :].rearrange("p k (h q) -> p k h q", h=H),
                                       bc(QT[:, :, bass.ts(c.b, S)].unsqueeze(2), P, KT, H, S),
                                       bc(headmask[:].unsqueeze(3), P, KT, H, S), ALU.mult).then_inc(qb_ready, 1)
                    pool.tensor_tensor(kT[:, c.u, :, 2 * P:NK], KE[:, :, c.b, :], bc(one[:].unsqueeze(1), P, KT, S + 1), ALU.mult).then_inc(ke_ready, 1)
                c = item(LAG_TR)
                if c:
                    pool.wait_ge(cve_ready, c.b + 1)
                    after(pool, vv_ready, c.b - 1)
                    pool.tensor_tensor(crs[:, c.u, :], cve[:, c.u, :], bc(half[:], P, 2), ALU.pow).then_inc(crs_ready, 1)
                c = item(LAG_KV)
                if c:
                    pool.wait_ge(ss_ready, c.b + 1)
                    pool.tensor_tensor(rn[:, c.u, :], ss[:, c.u, :], bc(half[:], P, 2 * H), ALU.pow).then_inc(rn_ready, 1)
            skewed(pool, B, 3, step)

        @block.tensor
        def _(pe):
            def step(item):
                a, n, c = item(LAG_AT), item(LAG_KN), item(LAG_KV)
                if a:
                    pe.wait_ge(kT_ready, a.b + 1)
                    pe.wait_ge(ke_ready, a.b + 1)
                    pe.wait_ge(qb_ready, a.b + 1)
                    after(pe, sc_ready, a.b)
                    for k in range(KT):
                        mm = pe.matmul(banks[:, S_BANK, 0:NK], lhsT=qb[:, a.u, k, :], rhs=kT[:, a.u, k, :], start=k == 0, stop=k == KT - 1)
                    mm.then_inc(scores, 1)
                o = item(LAG_OUT)
                if o:
                    pe.wait_ge(om_ready, o.b + 1)
                    for k in range(KT):
                        mm = pe.matmul(banks[:, O_BANK, D + k * S:D + (k + 1) * S], lhsT=om[:, o.u, tok(k)], rhs=sel[:], start=True, stop=True)
                    mm.then_inc(o_tr, 1)
                if c:
                    pe.wait_ge(c_loaded[c.u], 16 * (c.turn + 1))
                    after(pe, kr_ready, c.b - 1)
                    for j in range(2):
                        for k in range(2):
                            mm = pe.matmul(banks[:, K_BANK + c.u, j * D:(j + 1) * D], lhsT=cT[:, c.u, k, tok(j)], rhs=wc[:, k, 0:D], start=k == 0, stop=k == 1)
                    mm.then_inc(keys, 1)
                if a:
                    pe.wait_ge(pr_ready, a.b + 1)
                    after(pe, pT_ready, a.b)
                    for j in range(3):
                        w = min(P, NK - j * P)
                        mm = pe.transpose(banks[0:w, P_BANK, tok(j)], pr[:, a.u, j * P:j * P + w], g.ident[:])
                    mm.then_inc(p_tr, 1)
                if n:
                    pe.wait_ge(kn_ready, n.b + 1)
                    after(pe, kT_ready, n.b)
                    for k in range(KT):
                        for j in range(2):
                            mm = pe.transpose(banks[:, TR_BANK, tok(2 * k + j)], kn[:, n.u, j, tok(k)], g.ident[:])
                    mm.then_inc(k_tr, 1)
                if c:
                    after(pe, vv_ready, c.b - 1)
                    for j in range(2):
                        for k in range(2):
                            mm = pe.matmul(banks[:, V_BANK + c.u, j * D:(j + 1) * D], lhsT=cT[:, c.u, k, tok(j)], rhs=wc[:, k, D:2 * D], start=k == 0, stop=k == 1)
                    mm.then_inc(values, 1)
                if a:
                    pe.wait_ge(pT_ready, a.b + 1)
                    pe.wait_ge(vv_ready, a.b + 1)
                    after(pe, oT_ready, a.b)
                    for j in range(2):
                        pe.matmul(banks[:, O_BANK, 0:D], lhsT=pT[:, a.u, j, :], rhs=vv[:, a.u, j, :], start=j == 0, stop=False)
                    pe.matmul(banks[:, O_BANK, 0:D], lhsT=pT[0:S + 1, a.u, 2, :], rhs=V3[:, a.b, :], start=False, stop=True).then_inc(pv, 1)
            skewed(pe, B, 4, step)

        @block.scalar
        def _(act):
            def step(item):
                a, n, c = item(LAG_AT), item(LAG_KN), item(LAG_KV)
                o = item(LAG_OUT)
                if o:
                    act.wait_ge(o_tr, o.b + 1)
                    act.activation(OT[:, :, bass.ts(o.b, S)], banks[:, O_BANK, D:D + KT * S].rearrange("p (k q) -> p k q", k=KT), ACT.Copy).then_inc(oT_ready, 1)
                if a:
                    act.wait_ge(sc_ready, a.b + 1)
                    act.activation(pr[:, a.u, :], sc[:, a.u, :], ACT.Exp, bias=nm[:, a.u, :], accum_out=rs[:, a.u, :]).then_inc(pr_ready, 1)
                if c:
                    act.wait_ge(kr_ready, c.b + 1)
                    act.activation(sq[:, c.u, :, :], kn[:, c.u, :, :], ACT.Square).then_inc(sq_ready, 1)
                if a:
                    act.wait_ge(p_tr, a.b + 1)
                    act.activation(pT[:, a.u, 0:2, :], banks[:, P_BANK, 0:2 * P].rearrange("p (j q) -> p j q", j=2), ACT.Copy)
                    act.activation(pT[0:S + 1, a.u, 2, :], banks[0:S + 1, P_BANK, 2 * P:3 * P], ACT.Copy).then_inc(pT_ready, 1)
                if n:
                    act.wait_ge(k_tr, n.b + 1)
                    for k in range(KT):
                        ins = act.activation(kT[:, n.u, k, 0:2 * P], banks[:, TR_BANK, 2 * k * P:2 * (k + 1) * P], ACT.Identity, scale=vec[:, 3, k:k + 1])
                    ins.then_inc(kT_ready, 1)
            skewed(act, B, 4, step)

        @block.vector
        def _(dve):
            link = Link(dve, dve_link)
            dve.wait_ge(mb_zeroed, 1)

            def scaled(to, bank, c, cols):
                for j in range(2):
                    ins = dve.scalar_tensor_tensor(to[:, c.u, j, :], banks[:, bank + c.u, j * D:(j + 1) * D], crs[:, c.u, j:j + 1], bias[:, cols], ALU.mult, ALU.add)
                return ins

            def step(item):
                a, n, c, t = item(LAG_AT), item(LAG_KN), item(LAG_KV), item(LAG_TR)
                if a:
                    dve.wait_ge(scores, a.b + 1)
                    dve.wait_ge(mb_ready, a.b + 1)
                    link(dve.tensor_tensor(sc[:, a.u, :], banks[:, S_BANK, 0:NK], mb[:, a.u, :], ALU.add))
                    link(dve.tensor_reduce(mx[:, a.u, :], sc[:, a.u, :], AXX, ALU.max))
                    dve.tensor_scalar(nm[:, a.u, :], mx[:, a.u, :], -1.0, None, ALU.mult).then_inc(sc_ready, 1)
                if n:
                    dve.wait_ge(rn_ready, n.b + 1)
                    dve.tensor_tensor(kn[:, n.u, :, :].rearrange("p j (h d) -> p (j h) d", h=H),
                                      kn[:, n.u, :, :].rearrange("p j (h d) -> p (j h) d", d=HD),
                                      bc(rn[:, n.u, :].unsqueeze(2), P, 2 * H, HD), ALU.mult).then_inc(kn_ready, 1)
                    dve.tensor_scalar(mb[:, n.u, 0:CTX], mask8[:, n.b, :], BIG, -BIG, ALU.mult, ALU.add).then_inc(mb_ready, 1)
                if c:
                    dve.wait_ge(keys, c.b + 1)
                    dve.wait_ge(crs_ready, c.b + 1)
                    after(dve, k_tr, c.b - 1)
                    scaled(kn, K_BANK, c, slice(0, D)).then_inc(kr_ready, 1)
                if n:
                    dve.wait_ge(values, n.b + 1)
                    scaled(vv, V_BANK, n, slice(D, 2 * D)).then_inc(vv_ready, 1)
                if t:
                    dve.wait_ge(cx_loaded[t.u], 16 * (t.turn + 1))
                    for j in range(2):
                        ins = dve.bn_stats(cst[:, t.u, j, :], cx[:, t.u, j, :])
                    link(ins)
                    dve.memset(carry[:, t.u:t.u + 1], 0.0)
                    for j in range(2):
                        ins = dve.bn_aggr(cmv[:, t.u, j, :], cst[:, t.u, j, :])
                    link(ins)
                    dve.tensor_scalar(cve[:, t.u, :], cmv[:, t.u, :, 1], LN_EPS, None, ALU.add).then_inc(cve_ready, 1)
                if c:
                    dve.wait_ge(sq_ready, c.b + 1)
                    link(dve.tensor_reduce(ss[:, c.u, :], sq[:, c.u, :, :].rearrange("p j (h d) -> p (j h) d", h=H), AXX, ALU.add))
                    dve.tensor_scalar(ss[:, c.u, :], ss[:, c.u, :], 1.0 / HD, 1e-16, ALU.mult, ALU.max).then_inc(ss_ready, 1)
                if a:
                    dve.wait_ge(pr_ready, a.b + 1)
                    link(dve.reciprocal(ri[:, a.u, :], rs[:, a.u, :]))
                    dve.wait_ge(pv, a.b + 1)
                    dve.scalar_tensor_tensor(om[:, a.u, :], banks[:, O_BANK, 0:D], ri[:, a.u, :], blockmask[:], ALU.mult, ALU.mult).then_inc(om_ready, 1)
            skewed(dve, B, 3, step, link, 6)


def phase2(nc, g):
    I, X = g.I, g.X
    H, DK, DV = 16, 16, 64
    HK = P // DK
    QKV = H * (2 * DK + DV)
    VT = H * DV // P
    with ExitStack() as ctx:
        s = Scope(nc, ctx, "s2")
        sb, sem = s.sb, s.sem
        banks = s.psum()
        w = sb("w", [P, KT, QKV])
        wo = sb("wo", [P, VT, D])
        headmask = sb("headmask", [P, HK])
        batchmask = sb("batchmask", [P, P])
        half = sb("half", [P, 1])
        mv, var, rstd = sb("mv", [P, NT, 2]), sb("var", [P, NT]), sb("rstd", [P, NT])
        xn = sb("xn", [P, U, D])
        xT = sb("xT", [P, U, KT, P])
        sq = sb("sq", [P, U, QKV])
        ss, nrm, rn = sb("ss", [P, U, 3 * H]), sb("nrm", [P, U, 3 * H]), sb("rn", [P, U, 3 * H])
        qk = sb("qk", [P, U, 2 * D])
        vv = sb("vv", [P, U, H * DV])
        qkT = sb("qkT", [P, U, 2 * KT, P])
        qb = sb("qb", [P, U, KT, HK, P])
        at = sb("at", [P, U, H, P])
        sqo = sb("sqo", [P, H * DV])
        so, no, th, fac = sb("so", [P, U, H]), sb("no", [P, U, H]), sb("th", [P, U, H]), sb("fac", [P, U, H])
        on = sb("on", [P, U, H * DV])
        oT = sb("oT", [P, U, VT, P])
        (load, half_ready, stat_ready, rstd_ready, dve_link, ln_ready, x_tr, xT_ready, qk_proj, v_proj, sqk_ready, sqv_ready, ssk_ready, ssv_ready,
         nk_ready, nv_ready, qk_ready, vv_ready, qk_tr, kT_ready, qb_ready, scores, relu_ready, at_ready, o_ready, sqo_ready, so_ready, no_ready,
         th_ready, on_ready, o_tr, oT_ready, y_ready, x_done) = s.sems(
            "load half_ready stat_ready rstd_ready dve_link ln_ready x_tr xT_ready qk_proj v_proj sqk_ready sqv_ready ssk_ready ssv_ready "
            "nk_ready nv_ready qk_ready vv_ready qk_tr kT_ready qb_ready scores relu_ready at_ready o_ready sqo_ready so_ready no_ready "
            "th_ready on_ready o_tr oT_ready y_ready x_done")
        NLOAD = 4
        TR_BANK, QK_BANK, V_BANK, S_BANK, O_BANK = 0, 1, 2, 4, 6
        Y_BANK = QK_BANK
        NH, HH = 2, H // 2
        LAG_TR, LAG_QKV, LAG_AT, LAG_OUT, LAG_ADD = range(5)
        QK, V = slice(0, 2 * H), slice(2 * H, 3 * H)
        block = ctx.enter_context(nc.Block())

        def heads(ap, n):
            return ap.rearrange("p (h d) -> p h d", h=n)

        def half_of(c, h):
            return NH * c.b + h + 1

        @block.sync
        def _(sp):
            for dst, src in ((w, "p2_w"), (wo, "p2_wo"), (headmask, "headmask8"), (batchmask, "batchmask")):
                sp.dma_start(dst[:], I[src]).then_inc(load, 16)
            sp.wait_ge(load, 16 * NLOAD)

        @block.gpsimd
        def _(pool):
            pool.memset(half[:], -0.5).then_inc(half_ready, 1)
            pool.wait_ge(half_ready, 1)
            pool.wait_ge(stat_ready, 1)
            pool.tensor_tensor(rstd[:], var[:], bc(half[:], P, NT), ALU.pow).then_inc(rstd_ready, 1)
            pool.wait_ge(load, 16 * NLOAD)

            def step(item):
                c = item(LAG_QKV)
                if c:
                    pool.wait_ge(kT_ready, c.b + 1)
                    after(pool, scores, NH * (c.b - 1))
                    for k in range(KT):
                        pool.tensor_tensor(qb[:, c.u, k, :, :], bc(qkT[:, c.u, k, :].unsqueeze(1), P, HK, P),
                                           bc(headmask[:].unsqueeze(2), P, HK, P), ALU.mult).then_inc(qb_ready, 1)
            skewed(pool, NT, 1, step)

        @block.tensor
        def _(pe):
            pe.wait_ge(load, 16 * NLOAD)

            def step(item):
                x, c, t, o = item(LAG_TR), item(LAG_QKV), item(LAG_AT), item(LAG_OUT)

                def score(h):
                    if h:
                        pe.wait_ge(relu_ready, half_of(t, 0))
                    else:
                        after(pe, relu_ready, half_of(t, 1) - NH)
                    pe.wait_ge(qb_ready, half_of(t, h))
                    for n in range(2):
                        k, head = divmod(h * HH + 4 * n, HK)
                        mm = pe.matmul(banks[:, S_BANK + n, :], lhsT=qkT[:, t.u, KT + k, :], rhs=qb[:, t.u, k, head:head + 4, :], start=True, stop=True)
                    mm.then_inc(scores, 1)

                def project(n, bank):
                    for k in range(KT):
                        mm = pe.matmul(banks[:, bank, :], lhsT=xT[:, c.u, k, :], rhs=w[:, k, n * C:(n + 1) * C], start=k == 0, stop=k == KT - 1)
                    return mm

                def out_transposed(h):
                    if h:
                        pe.wait_ge(oT_ready, half_of(o, 0))
                    else:
                        pe.wait_ge(on_ready, o.b + 1)
                        if t:
                            pe.wait_ge(kT_ready, t.b + 1)
                    for n in range(4):
                        mm = pe.transpose(banks[:, TR_BANK, tok(n)], on[:, o.u, tok(4 * h + n)], g.ident[:])
                    mm.then_inc(o_tr, 1)

                def sums(h):
                    pe.wait_ge(at_ready, half_of(t, h))
                    pe.wait_ge(vv_ready, t.b + 1)
                    after(pe, on_ready, t.b)
                    for n in range(HH):
                        m = h * HH + n
                        mm = pe.matmul(banks[:, O_BANK + h, n * DV:(n + 1) * DV], lhsT=at[:, t.u, m, :], rhs=vv[:, t.u, m * DV:(m + 1) * DV],
                                       start=True, stop=True)
                    mm.then_inc(o_ready, 1)
                if t:
                    score(0)
                if c:
                    pe.wait_ge(xT_ready, c.b + 1)
                    after(pe, x_done, c.b - 2)
                    project(0, QK_BANK).then_inc(qk_proj, 1)
                if t:
                    score(1)
                if o:
                    out_transposed(0)
                if c:
                    after(pe, vv_ready, c.b)
                    project(1, V_BANK)
                    project(2, V_BANK + 1).then_inc(v_proj, 1)
                if o:
                    out_transposed(1)
                if t:
                    sums(0)
                if x:
                    pe.wait_ge(ln_ready, x.b + 1)
                    after(pe, kT_ready, x.b - 1)
                    if o:
                        pe.wait_ge(oT_ready, half_of(o, 1))
                    for k in range(KT):
                        mm = pe.transpose(banks[:, TR_BANK, tok(k)], xn[:, x.u, tok(k)], g.ident[:])
                    mm.then_inc(x_tr, 1)
                if t:
                    sums(1)
                if c:
                    pe.wait_ge(qk_ready, c.b + 1)
                    after(pe, xT_ready, c.b + 2 if x else NT)
                    if o:
                        pe.wait_ge(oT_ready, half_of(o, 1))
                    for k in range(2 * KT):
                        mm = pe.transpose(banks[:, TR_BANK, tok(k)], qk[:, c.u, tok(k)], g.ident[:])
                    mm.then_inc(qk_tr, 1)
                if o:
                    pe.wait_ge(oT_ready, half_of(o, 1))
                    pe.wait_ge(qk_ready, o.b + 3 if c else NT)
                    after(pe, x_done, o.b)
                    for k in range(VT):
                        mm = pe.matmul(banks[:, Y_BANK, 0:D], lhsT=oT[:, o.u, k, :], rhs=wo[:, k, :], start=k == 0, stop=k == VT - 1)
                    mm.then_inc(y_ready, 1)
            skewed(pe, NT, 3, step)

        @block.scalar
        def _(act):
            def step(item):
                x, c, t, o = item(LAG_TR), item(LAG_QKV), item(LAG_AT), item(LAG_OUT)

                def squared(h):
                    hs = slice(h * HH, (h + 1) * HH)
                    act.wait_ge(relu_ready, half_of(t, h))
                    act.activation(at[:, t.u, hs, :], at[:, t.u, hs, :], ACT.Square).then_inc(at_ready, 1)

                def out_transposed(h):
                    act.wait_ge(o_tr, half_of(o, h))
                    act.activation(oT[:, o.u, 4 * h:4 * h + 4, :], heads(banks[:, TR_BANK, :], 4), ACT.Copy).then_inc(oT_ready, 1)
                if t:
                    squared(0)
                if c:
                    act.wait_ge(qk_proj, c.b + 1)
                    act.activation(sq[:, c.u, 0:2 * D], banks[:, QK_BANK, :], ACT.Square).then_inc(sqk_ready, 1)
                if t:
                    squared(1)
                if o:
                    out_transposed(0)
                if c:
                    act.wait_ge(ssk_ready, c.b + 1)
                    act.activation(nrm[:, c.u, QK], ss[:, c.u, QK], ACT.Sqrt).then_inc(nk_ready, 1)
                    act.wait_ge(v_proj, c.b + 1)
                    act.activation(sq[:, c.u, 2 * D:QKV], banks[:, V_BANK:V_BANK + 2, :].rearrange("p n c -> p (n c)"), ACT.Square).then_inc(sqv_ready, 1)
                if o:
                    out_transposed(1)
                if c:
                    act.wait_ge(ssv_ready, c.b + 1)
                    act.activation(nrm[:, c.u, V], ss[:, c.u, V], ACT.Sqrt).then_inc(nv_ready, 1)
                if x:
                    act.wait_ge(x_tr, x.b + 1)
                    act.activation(xT[:, x.u, :, :], heads(banks[:, TR_BANK, 0:KT * P], KT), ACT.Copy).then_inc(xT_ready, 1)
                if t:
                    act.wait_ge(o_ready, half_of(t, 1))
                    after(act, so_ready, t.b)
                    act.activation(sqo[:], banks[:, O_BANK:O_BANK + 2, :].rearrange("p n c -> p (n c)"), ACT.Square).then_inc(sqo_ready, 1)
                if c:
                    act.wait_ge(qk_tr, c.b + 1)
                    after(act, qb_ready, NH * (c.b - 1))
                    act.activation(qkT[:, c.u, :, :], heads(banks[:, TR_BANK, :], 2 * KT), ACT.Copy).then_inc(kT_ready, 1)
                if t:
                    act.wait_ge(so_ready, t.b + 1)
                    act.activation(no[:, t.u, :], so[:, t.u, :], ACT.Sqrt).then_inc(no_ready, 1)
                    act.wait_ge(no_ready, t.b + 1)
                    act.activation(th[:, t.u, :], no[:, t.u, :], ACT.Tanh).then_inc(th_ready, 1)
            skewed(act, NT, 3, step)

        @block.vector
        def _(dve):
            link = Link(dve, dve_link)
            row_stats(dve, link, g.stats, mv, var, LN_EPS).then_inc(stat_ready, 1)
            dve.wait_ge(rstd_ready, 1)
            dve.wait_ge(load, 16 * NLOAD)

            def step(item):
                x, c, t, o, y = item(LAG_TR), item(LAG_QKV), item(LAG_AT), item(LAG_OUT), item(LAG_ADD)

                def masked(h):
                    dve.wait_ge(scores, half_of(t, h))
                    dve.scalar_tensor_tensor(at[:, t.u, h * HH:(h + 1) * HH, :], banks[:, S_BANK:S_BANK + 2, :].rearrange("p n (h q) -> p (n h) q", q=P), 0.0,
                                             bc(batchmask[:].unsqueeze(1), P, HH, P), ALU.max, ALU.mult).then_inc(relu_ready, 1)

                def root_at_least(cols, ready):
                    dve.tensor_scalar(ss[:, c.u, cols], ss[:, c.u, cols], 1e-24, None, ALU.max).then_inc(ready, 1)
                if y:
                    dve.wait_ge(y_ready, y.b + 1)
                    dve.tensor_tensor(X[:, y.b, :], X[:, y.b, :], banks[:, Y_BANK, 0:D], ALU.add).then_inc(x_done, 1)
                if t:
                    masked(0)
                if o:
                    dve.wait_ge(th_ready, o.b + 1)
                    link(dve.tensor_scalar(no[:, o.u, :], no[:, o.u, :], 1e-12, None, ALU.max))
                    link(dve.reciprocal(fac[:, o.u, :], no[:, o.u, :]))
                    link(dve.tensor_tensor(fac[:, o.u, :], fac[:, o.u, :], th[:, o.u, :], ALU.mult))
                    dve.tensor_tensor(heads(on[:, o.u, :], H), banks[:, O_BANK:O_BANK + 2, :].rearrange("p n (h d) -> p (n h) d", d=DV),
                                      bc(fac[:, o.u, :].unsqueeze(2), P, H, DV), ALU.mult).then_inc(on_ready, 1)
                if c:
                    dve.wait_ge(sqk_ready, c.b + 1)
                    link(dve.tensor_reduce(ss[:, c.u, QK], heads(sq[:, c.u, 0:2 * D], 2 * H), AXX, ALU.add))
                    root_at_least(QK, ssk_ready)
                if t:
                    masked(1)
                if x:
                    after(dve, x_tr, x.b - 1)
                    dve.tensor_scalar(xn[:, x.u, :], X[:, x.b, :], mv[:, x.b, 0:1], rstd[:, bass.ds(x.b, 1)],
                                      ALU.subtract, ALU.mult).then_inc(ln_ready, 1)
                if c:
                    dve.wait_ge(nk_ready, c.b + 1)
                    link(dve.reciprocal(rn[:, c.u, QK], nrm[:, c.u, QK]))
                    dve.tensor_tensor(heads(qk[:, c.u, :], 2 * H), heads(banks[:, QK_BANK, :], 2 * H),
                                      bc(rn[:, c.u, QK].unsqueeze(2), P, 2 * H, DK), ALU.mult).then_inc(qk_ready, 1)
                    dve.wait_ge(sqv_ready, c.b + 1)
                    link(dve.tensor_reduce(ss[:, c.u, V], heads(sq[:, c.u, 2 * D:QKV], H), AXX, ALU.add))
                    root_at_least(V, ssv_ready)
                    dve.wait_ge(nv_ready, c.b + 1)
                    link(dve.reciprocal(rn[:, c.u, V], nrm[:, c.u, V]))
                    dve.tensor_tensor(heads(vv[:, c.u, :], H), banks[:, V_BANK:V_BANK + 2, :].rearrange("p n (h d) -> p (n h) d", d=DV),
                                      bc(rn[:, c.u, V].unsqueeze(2), P, H, DV), ALU.mult).then_inc(vv_ready, 1)
                if y:
                    dve.wait_ge(x_done, y.b + 1)
                    dve.bn_stats(g.stats[:, y.b, :], X[:, y.b, :])
                if t:
                    dve.wait_ge(sqo_ready, t.b + 1)
                    dve.tensor_reduce(so[:, t.u, :], heads(sqo[:], H), AXX, ALU.add).then_inc(so_ready, 1)
            skewed(dve, NT, 4, step, link, 7)


def phase3(nc, g):
    with ExitStack() as ctx:
        s = Scope(nc, ctx, "s3")
        banks = s.psum()
        n = Normed(s)
        pairs = s.sb("pairs", [P, KT, 1024])
        offset = s.sb("offset", [1, 1024])
        score_map(nc, g, banks, n, pairs, offset)
        retrieve(nc, g, banks, n, pairs, offset)


def score_map(nc, g, banks, n, pairs, offset):
    I, X = g.I, g.X
    PH, NK, BN_EPS = 16, 64, 1e-5
    with ExitStack() as ctx:
        s = Scope(nc, ctx, "s3s")
        sb = s.sb
        wq = sb("wq", [P, KT, PH * P])
        wqT = sb("wqT", [P, PH, D])
        keys = sb("keys", [P, PH, NK])
        gb = sb("gb", [P, 2, PH])
        xc = sb("xc", [P, NT, D])
        ones = sb("ones", [P, P])
        mean = sb("mean", [P, D])
        cov = sb("cov", [P, KT, D + 1])
        scrap = sb("scrap", [P, D])
        var, mq = sb("var", [P, PH]), sb("mq", [P, PH])
        rstd, gain, shift = sb("rstd", [P, PH]), sb("gain", [P, PH]), sb("shift", [P, PH])
        kg, ks = sb("kg", [P, PH, NK]), sb("ks", [P, PH, NK])
        (loaded, set_up, stat_ready, rstd_ready, dve_link, xn_ready, summed, xc_ready, cov_summed, m_tr, cov_ready, spread, spread_read, var_ready,
         vr_ready, kg_ready, ks_ready, mapped, map_ready) = s.sems(
            "loaded set_up stat_ready rstd_ready dve_link xn_ready summed xc_ready cov_summed m_tr cov_ready spread spread_read var_ready "
            "vr_ready kg_ready ks_ready mapped map_ready")
        NG = 4
        block = ctx.enter_context(nc.Block())

        @block.sync
        def _(sp):
            for dst, src in ((wq, "p3_wq"), (wqT, "p3_wqT"), (keys, "p3_keys"), (gb, "p3_gb")):
                sp.dma_start(dst[:], I[src]).then_inc(loaded, 16)

        @block.gpsimd
        def _(pool):
            pool.memset(ones[:], 1.0)
            pool.memset(n.half[:], -0.5).then_inc(set_up, 1)
            pool.wait_ge(set_up, 1)
            pool.wait_ge(stat_ready, 1)
            pool.tensor_tensor(n.rstd[:], n.var[:], bc(n.half[:], P, NT), ALU.pow).then_inc(rstd_ready, 1)
            pool.wait_ge(var_ready, 1)
            pool.tensor_tensor(rstd[:], var[:], bc(n.half[:], P, PH), ALU.pow).then_inc(vr_ready, 1)

        @block.tensor
        def _(pe):
            pe.wait_ge(set_up, 1)
            for t in range(NT):
                pe.wait_ge(xn_ready, t // NG + 1)
                mm = pe.matmul(banks[:, 0, 0:D], lhsT=ones[:], rhs=xc[:, t, :], start=t == 0, stop=t == NT - 1)
            mm.then_inc(summed, 1)
            for t in range(NT):
                pe.wait_ge(xc_ready, t // NG + 1)
                for k in range(KT):
                    mm = pe.matmul(banks[:, 1 + k, 0:D], lhsT=xc[:, t, tok(k)], rhs=xc[:, t, :], start=t == 0, stop=t == NT - 1)
            for k in range(KT):
                mm = pe.transpose(banks[:, 3, tok(k)], mean[:, tok(k)], g.ident[:])
            mm.then_inc(cov_summed, 1)
            pe.wait_ge(loaded, 64)
            pe.wait_ge(cov_ready, 1)
            for c in range(PH):
                if c == 8:
                    pe.wait_ge(spread_read, 1)
                for k in range(KT):
                    mm = pe.matmul(banks[:, c % 8, 0:D + 1], lhsT=wq[:, k, tok(c)], rhs=cov[:, k, :], start=k == 0, stop=k == KT - 1)
                mm.then_inc(spread, 1)
            pe.wait_ge(spread_read, 2)
            pe.wait_ge(kg_ready, 1)
            for k in range(KT):
                for n in range(2):
                    for c in range(8):
                        mm = pe.matmul(banks[:, 2 * k + n, c * NK:(c + 1) * NK], lhsT=wqT[:, 8 * n + c, tok(k)], rhs=kg[:, 8 * n + c, :], start=True, stop=True)
                    mm.then_inc(mapped, 1)
            pe.wait_ge(ks_ready, 1)
            for n in range(2):
                mm = pe.matmul(banks[0:1, 4 + n, :], lhsT=ones[:, 0:1], rhs=ks[:, 8 * n:8 * n + 8, :].rearrange("p c k -> p (c k)"), start=True, stop=True)
            mm.then_inc(mapped, 1)

        @block.scalar
        def _(act):
            act.wait_ge(cov_summed, 1)
            act.activation(cov[:, :, 0:D], banks[:, 1:3, 0:D], ACT.Copy, scale=1.0 / T)
            act.activation(cov[:, :, D:D + 1], banks[:, 3, 0:KT * P].rearrange("p (k q) -> p k q", k=KT)[:, :, 0:1], ACT.Copy).then_inc(cov_ready, 1)
            for k in range(KT):
                for n in range(2):
                    act.wait_ge(mapped, 2 * k + n + 1)
                    act.activation(pairs[:, k, n * C:(n + 1) * C], banks[:, 2 * k + n, :], ACT.Copy)
            act.wait_ge(mapped, 2 * KT + 1)
            act.activation(offset[:], banks[0:1, 4:6, :].rearrange("p n c -> p (n c)"), ACT.Copy).then_inc(map_ready, 1)
            act.wait_ge(map_ready, 1)

        @block.vector
        def _(dve):
            link = Link(dve, dve_link)
            row_stats(dve, link, g.stats, n.mv, n.var, LN_EPS).then_inc(stat_ready, 1)
            dve.wait_ge(rstd_ready, 1)
            for t in range(NT):
                ins = n.apply(dve, xc[:, t, :], X, t)
                if t % NG == NG - 1:
                    ins.then_inc(xn_ready, 1)
            dve.wait_ge(summed, 1)
            link(dve.tensor_scalar(mean[:], banks[:, 0, 0:D], 1.0 / T, None, ALU.mult))
            for i in range(NT // NG):
                ts = slice(i * NG, (i + 1) * NG)
                dve.tensor_tensor(xc[:, ts, :], xc[:, ts, :], bc(mean[:].unsqueeze(1), P, NG, D), ALU.subtract).then_inc(xc_ready, 1)
            dve.wait_ge(loaded, 64)
            for c in range(PH):
                dve.wait_ge(spread, c + 1)
                ins = dve.tensor_tensor_reduce(scrap[:], banks[:, c % 8, 0:D], wqT[:, c, :], 1.0, 0.0, ALU.mult, ALU.add, var[:, c:c + 1])
                link(ins)
                if c % 8 == 7:
                    dve.tensor_copy(mq[:, c - 7:c + 1], banks[:, :, D]).then_inc(spread_read, 1)
            link(dve.tensor_scalar(var[:], var[:], 0.0, BN_EPS, ALU.max, ALU.add))
            dve.sem_inc(var_ready, 1)
            dve.wait_ge(vr_ready, 1)
            dve.wait_ge(spread_read, 2)
            link(dve.tensor_tensor(gain[:], rstd[:], gb[:, 0, :], ALU.mult))
            link(dve.tensor_tensor(shift[:], mq[:], gain[:], ALU.mult))
            link(dve.tensor_tensor(shift[:], gb[:, 1, :], shift[:], ALU.subtract))
            dve.tensor_tensor(kg[:], keys[:], bc(gain[:].unsqueeze(2), P, PH, NK), ALU.mult).then_inc(kg_ready, 1)
            dve.tensor_tensor(ks[:], keys[:], bc(shift[:].unsqueeze(2), P, PH, NK), ALU.mult).then_inc(ks_ready, 1)


def retrieve(nc, g, banks, n, pairs, offset):
    I, X = g.I, g.X
    H, K, NK = 8, 8, 64
    PH, M = 2 * H, H * K
    R = 8
    RP = 4
    RD = 4
    CHOOSE = 4
    with ExitStack() as ctx:
        s = Scope(nc, ctx, "s3e")
        sb = s.sb
        count, count_loaded = sb("count", [P, K]), s.sem("count_loaded")
        row1 = sb("row1", [1, P])
        xn = sb("xn", [P, U, D])
        xT = sb("xT", [P, KT, P])
        sim = sb("sim", [P, PH, NK])
        best, place = sb("best", [P, PH, K]), sb("place", [P, PH, K], U32)
        cand = sb("cand", [P, H, K * K])
        top, pos = sb("top", [P, H, K]), sb("pos", [P, H, K], U32)
        part, partf = sb("part", [P, 2, M], U32), sb("partf", [P, 2, M])
        keyf = sb("keyf", [P, 2, H, K])
        hit = sb("hit", [P, 2, H, K, K])
        key = sb("key", [P, 2, M])
        ex, den, rden = sb("ex", [P, H, K]), sb("den", [P, H]), sb("rden", [P, H])
        idf = sb("idf", [P, M])
        idx = sb("idx", [P, U, M], U32)
        wts = sb("wts", [P, U, H, K])
        carry = sb("carry", [P, 4])
        rows = sb("rows", [P, R, K, 2 * D])
        hd, hg, hw = sb("hd", [P, R, K]), sb("hg", [P, R, K]), sb("hw", [P, R, K])
        diag = sb("diag", [P, RD, K, P])
        one = sb("one", [P, 2])
        gathered = [s.sem(f"gathered{r}") for r in range(R)]
        (set_up, carried, dve_link, xn_ready, x_tr, xT_ready, sims, sim_ready, diff_ready, ex_ready, idx_ready, dots, hg_ready, hw_ready, scaled, summed,
         added) = s.sems(
            "set_up carried dve_link xn_ready x_tr xT_ready sims sim_ready diff_ready ex_ready idx_ready dots hg_ready hw_ready scaled summed added")
        T_BANK, S_BANK, Y_BANK = 0, 1, 4
        block = ctx.enter_context(nc.Block())

        def heads(t, h):
            return t.b * H + h + 1

        @block.sync
        def _(sp):
            sp.dma_start(count[:], I["count8"]).then_inc(count_loaded, 16)

        @block.gpsimd
        def _(pool):
            pool.memset(row1[:], 1.0).then_inc(set_up, 1)
            pool.memset(one[:], 1.0).then_inc(carried, 1)

            def step(item):
                t = item(0)
                pool.wait_ge(idx_ready, t.b + 1)
                for h in range(H):
                    r = h % R
                    if h % RP == 0:
                        after(pool, summed, heads(t, h + RP - 1) - R)
                        pool.wait_ge(carried, t.b * (H // RP) + h // RP + 1)
                        pool.tensor_tensor(one[:, 1:2], one[:, 0:1], one[:, 0:1], ALU.mult).then_inc(carried, 1)
                    for k in range(K):
                        m = h * K + k
                        pool.indirect_dma_start(rows[:, r, k, :], None, I["p3_table"],
                                                bass.IndirectOffsetOnAxis(idx[:, t.u, m:m + 1], 0)).then_inc(gathered[r], 16)
            skewed(pool, NT, 0, step)

        @block.tensor
        def _(pe):
            pe.wait_ge(set_up, 1)

            def step(item):
                c, t = item(0), item(1)
                if c:
                    pe.wait_ge(xn_ready, c.b + 1)
                    for k in range(KT):
                        mm = pe.transpose(banks[:, T_BANK, tok(k)], xn[:, c.u, tok(k)], g.ident[:])
                    mm.then_inc(x_tr, 1)
                    pe.wait_ge(xT_ready, c.b + 1)
                    after(pe, sim_ready, c.b)
                    for j in range(2):
                        cs = slice(j * C, (j + 1) * C)
                        for k in range(KT):
                            pe.matmul(banks[:, S_BANK + j, :], lhsT=xT[:, k, :], rhs=pairs[:, k, cs], start=k == 0, stop=False)
                        mm = pe.matmul(banks[:, S_BANK + j, :], lhsT=row1[:], rhs=offset[:, cs], start=False, stop=True)
                    mm.then_inc(sims, 1)
                if t:
                    after(pe, added, t.b - 1)
                    for h in range(H):
                        pe.wait_ge(scaled, heads(t, h))
                        for k in range(K):
                            mm = pe.matmul(banks[:, Y_BANK + t.u, 0:D], lhsT=diag[:, h % RD, k, :], rhs=rows[:, h % R, k, D:2 * D],
                                           start=h == 0 and k == 0, stop=h == H - 1 and k == K - 1)
                        mm.then_inc(summed, 1)
            skewed(pe, NT, 1, step)

        @block.scalar
        def _(act):
            def step(item):
                c, t = item(0), item(1)
                if c:
                    act.wait_ge(x_tr, c.b + 1)
                    act.activation(xT[:], banks[:, T_BANK, 0:D].rearrange("p (k q) -> p k q", k=KT), ACT.Copy).then_inc(xT_ready, 1)
                    act.wait_ge(sims, c.b + 1)
                    act.activation(sim[:].rearrange("p c k -> p (c k)"), banks[:, S_BANK:S_BANK + 2, :].rearrange("p n c -> p (n c)"), ACT.Copy).then_inc(sim_ready, 1)

                def gelu(h):
                    act.wait_ge(dots, heads(t, h))
                    act.activation(hg[:, h % R, :], hd[:, h % R, :], ACT.Gelu_apprx_tanh).then_inc(hg_ready, 1)

                def spread(h):
                    act.wait_ge(hw_ready, heads(t, h))
                    after(act, summed, heads(t, h) - RD)
                    for k in range(K):
                        ins = act.activation(diag[:, h % RD, k, :], g.ident[:], ACT.Copy, scale=hw[:, h % R, k:k + 1])
                    ins.then_inc(scaled, 1)
                if t:
                    for h in range(CHOOSE + 1):
                        gelu(h)
                        if h:
                            spread(h - 1)
                if c:
                    act.wait_ge(diff_ready, c.b + 1)
                    act.activation(ex[:], ex[:], ACT.Exp).then_inc(ex_ready, 1)
                if t:
                    for h in range(CHOOSE + 1, H):
                        gelu(h)
                        spread(h - 1)
                    spread(H - 1)
            skewed(act, NT, 1, step)

        @block.vector
        def _(dve):
            link = Link(dve, dve_link)
            dve.wait_ge(count_loaded, 16)

            def choose(c):
                dve.wait_ge(sim_ready, c.b + 1)
                dve.memset(carry[:, 0:1], 0.0)
                for q in range(PH):
                    ins = dve.max(best[:, q, :], sim[:, q, :])
                link(ins)
                dve.tensor_tensor(cand[:].rearrange("p h (a b) -> p h a b", a=K), bc(best[:, 0:H, :].unsqueeze(3), P, H, K, K),
                                  bc(best[:, H:PH, :].unsqueeze(2), P, H, K, K), ALU.add)
                for q in range(PH):
                    ins = dve.max_index(place[:, q, :], best[:, q, :], sim[:, q, :])
                link(ins)
                dve.memset(carry[:, 1:2], 0.0)
                for h in range(H):
                    ins = dve.max(top[:, h, :], cand[:, h, :])
                link(ins)
                dve.tensor_tensor(ex[:], top[:], bc(top[:, :, 0:1], P, H, K), ALU.subtract).then_inc(diff_ready, 1)
                for h in range(H):
                    ins = dve.max_index(pos[:, h, :], top[:, h, :], cand[:, h, :])
                link(ins)
                flat = pos[:].rearrange("p h k -> p (h k)")
                dve.tensor_scalar(part[:, 0, :], flat, 3, None, ALU.logical_shift_right)
                link(dve.tensor_scalar(part[:, 1, :], flat, K - 1, None, ALU.bitwise_and))
                dve.tensor_copy(partf[:], part[:])
                link(dve.tensor_copy(keyf[:].rearrange("p j h k -> p (j h) k"), place[:]))
                link(dve.tensor_tensor(hit[:].rearrange("p j h k a -> p (j h k) a"), bc(partf[:].rearrange("p j m -> p (j m)").unsqueeze(2), P, 2 * M, K),
                                       bc(count[:].unsqueeze(1), P, 2 * M, K), ALU.is_equal))
                wide = hit[:].rearrange("p j h k a -> p (j h) k a")
                link(dve.tensor_tensor(wide, wide, bc(keyf[:].rearrange("p j h a -> p (j h) a").unsqueeze(2), P, PH, K, K), ALU.mult))
                link(dve.tensor_reduce(key[:], hit[:].rearrange("p j h k a -> p j (h k) a"), AXX, ALU.add))
                link(dve.scalar_tensor_tensor(idf[:], key[:, 0, :], float(NK), key[:, 1, :], ALU.mult, ALU.add))
                dve.tensor_copy(idx[:, c.u, :], idf[:]).then_inc(idx_ready, 1)

            def soften(c):
                dve.wait_ge(ex_ready, c.b + 1)
                link(dve.tensor_reduce(den[:], ex[:], AXX, ALU.add))
                link(dve.reciprocal(rden[:], den[:]))
                link(dve.tensor_tensor(wts[:, c.u, :, :], ex[:], bc(rden[:].unsqueeze(2), P, H, K), ALU.mult))

            def step(item):
                c, t, y = item(0), item(1), item(2)

                def scale(h):
                    r = h % R
                    dve.wait_ge(hg_ready, heads(t, h))
                    dve.tensor_tensor(hw[:, r, :], hg[:, r, :], wts[:, t.u, h, :], ALU.mult).then_inc(hw_ready, 1)
                if c:
                    n.apply(dve, xn[:, c.u, :], X, c.b).then_inc(xn_ready, 1)
                if t:
                    dve.wait_ge(xn_ready, t.b + 1)
                    for h in range(H):
                        r = h % R
                        dve.wait_ge(gathered[r], (t.b * (H // R) + h // R + 1) * (16 * K))
                        for k in range(K):
                            ins = dve.tensor_tensor_reduce(rows[:, r, k, 0:D], rows[:, r, k, 0:D], xn[:, t.u, :], 1.0, 0.0, ALU.mult, ALU.add, hd[:, r, k:k + 1])
                        ins.then_inc(dots, 1)
                        if h:
                            scale(h - 1)
                        if h == 1 and y:
                            add(y)
                        if h == 2 and y:
                            sums(y)
                        if h == CHOOSE and c:
                            choose(c)
                        if h == CHOOSE + 1 and c:
                            soften(c)
                    scale(H - 1)
                else:
                    if c:
                        choose(c)
                        soften(c)
                    if y:
                        add(y)
                        sums(y)

            def add(y):
                dve.wait_ge(summed, heads(y, H - 1))
                dve.tensor_tensor(X[:, y.b, :], X[:, y.b, :], banks[:, Y_BANK + y.u, 0:D], ALU.add).then_inc(added, 1)

            def sums(y):
                dve.wait_ge(added, y.b + 1)
                dve.bn_stats(g.stats[:, y.b, :], X[:, y.b, :])
            skewed(dve, NT, 2, step, link, 10 + 3)


def phase4(nc, g):
    I, X = g.I, g.X
    H, HD = 16, 16
    HK = P // HD
    HG = P // S
    NG = H // HG
    GD = HG * HD
    CLAMP = 10000.0
    with ExitStack() as ctx:
        s = Scope(nc, ctx, "s4")
        sb, sem = s.sb, s.sem
        banks = s.psum()
        OT = sb("OT", [P, KT, T])
        wo = sb("wo", [P, KT, D])
        vec = sb("vec", [P, 3, KT])
        bo = sb("bo", [P, D])
        load = sem("load")
        NLOAD = 10
        with ExitStack() as actx:
            a = Scope(nc, actx, "s4a")
            sb = a.sb
            QT = sb("QT", [P, KT, T])
            wq = sb("wq", [P, KT, D])
            wk, wv = sb("wk", [DH, 2, D]), sb("wv", [DH, 2, D])
            headmask = sb("headmask", [P, HK])
            blockmask = sb("blockmask", [P, GD])
            sel = sb("sel", [P, S])
            VX = sb("VX", [P, B, D])
            csum = sb("csum", [DH, 2, B])
            sums = sb("sums", [P, B, NG])
            cxT = sb("cxT", [DH, 2, B])
            vx = sb("vx", [B, D])
            last = nc.dram_tensor("s4_last", [B, D], F32, kind="Internal").ap()
            with ExitStack() as nctx:
                q = Scope(nc, nctx, "s4q")
                n = Normed(q)
                xT = q.sb("xT", [P, KT, T])
                c_proj, vx_ready, vx_loaded, q_ready, q_read = a.sems("c_proj vx_ready vx_loaded q_ready q_read")

                def last_loads(sp):
                    sp.wait_ge(vx_ready, 1)
                    sp.dma_start(last[:], vx[:]).then_inc(vx_loaded, 16)
                    sp.wait_ge(vx_loaded, 16)
                    sp.dma_start(VX[:].rearrange("p b d -> p (b d)"), last.rearrange("b d -> (b d)").unsqueeze(0).broadcast_to([P, B * D])).then_inc(vx_loaded, 16)

                def last_projected(pe):
                    pe.wait_ge(load, 16 * NLOAD)
                    for k in range(2):
                        mm = pe.matmul(banks[0:B, 6, 0:D], lhsT=cxT[:, k, :], rhs=wv[:, k, :], start=k == 0, stop=k == 1)
                    mm.then_inc(c_proj, 1)

                def last_read(act):
                    act.wait_ge(c_proj, 1)
                    act.activation(vx[:], banks[0:B, 6, 0:D], ACT.Copy).then_inc(vx_ready, 1)
                normed_transposed(nc, g, q, banks, n, xT, (
                    (vec, "p4_vec"), (wq, "p4_wq"), (wk, "p4_wk"), (wv, "p4_wv"), (wo, "p4_wo"), (bo, "p4_bo"), (headmask, "headmask8"),
                    (blockmask, "blockmask16"), (sel, "sel"), (cxT, "p4_lastT")), load, dict(sync=last_loads, tensor=last_projected, scalar=last_read))
                block = nctx.enter_context(nc.Block())

                @block.tensor
                def _(pe):
                    pe.wait_ge(load, 16 * NLOAD)
                    opens(pe, q_ready)
                    with pe.Fori(0, NC) as c:
                        pe.wait_ge(q_read, signals(c))
                        for m in range(KT):
                            for k in range(KT):
                                mm = pe.matmul(banks[:, m, :], lhsT=wq[:, k, tok(m)], rhs=xT[:, k, bass.ts(c, C)], start=k == 0, stop=k == KT - 1)
                        mm.then_inc(q_ready, 1)

                @block.vector
                def _(dve):
                    dve.wait_ge(load, 16 * NLOAD)
                    opens(dve, q_read)
                    with dve.Fori(0, NC) as c:
                        dve.wait_ge(q_ready, signals(c + 1))
                        for m in range(KT):
                            ins = dve.tensor_scalar(QT[:, m, bass.ts(c, C)], banks[:, m, :], vec[:, 0, m:m + 1], HD ** -0.5, ALU.add, ALU.mult)
                        ins.then_inc(q_read, 1)

            attend(nc, g, banks, vx_loaded, dict(
                HG=HG, NG=NG, GD=GD, HK=HK, CLAMP=CLAMP, QT=QT, OT=OT, wk=wk, wv=wv, vec=vec, VX=VX, csum=csum,
                sums=sums, headmask=headmask, blockmask=blockmask, sel=sel))
            guard(nc, g, banks, sums, csum, wv, vec, OT)
        project_out(nc, g, "s4o", banks, OT, wo, bo)


def attend(nc, g, banks, vx_loaded, v):
    I = g.I
    HG, NG, GD, HK, CLAMP = (v[n] for n in "HG NG GD HK CLAMP".split())
    QT, OT, wk, wv, vec, VX, csum, sums = (v[n] for n in "QT OT wk wv vec VX csum sums".split())
    headmask, blockmask, sel = (v[n] for n in "headmask blockmask sel".split())
    NH = 2
    GH = NG // NH
    with ExitStack() as ctx:
        s = Scope(nc, ctx, "s4b")
        sb = s.sb
        cT = sb("cT", [DH, U, 2, CTX])
        scrap = sb("scrap", [DH, U, 2, CTX])
        kT = sb("kT", [P, U, KT, CTX])
        vv = sb("vv", [P, U, 2, D])
        qb = sb("qb", [P, U, KT, HK, S])
        sc = sb("sc", [P, U, NG, CTX])
        mx, nm, ri = sb("mx", [P, U, NG]), sb("nm", [P, U, NG]), sb("ri", [P, U, NG])
        pr = sb("pr", [P, U, NG, CTX])
        rs = sb("rs", [P, U, NG])
        pT = sb("pT", [P, U, NG, 2, P])
        om = sb("om", [P, U, NG, GD])
        c_loaded = [s.sem(f"c_loaded{u}") for u in range(U)]
        (c_summed, keys, values, kT_ready, vv_ready, qb_ready, scores, sc_ready, pr_ready, p_tr, pT_ready, pv, om_ready,
         o_tr, oT_ready, dve_link) = s.sems(
            "c_summed keys values kT_ready vv_ready qb_ready scores sc_ready pr_ready p_tr pT_ready pv om_ready "
            "o_tr oT_ready dve_link")
        K_BANK, V_BANK, O_BANK = 4, 6, 7
        O_AT = NG * GD
        block = ctx.enter_context(nc.Block())

        def half(c, h):
            return NH * c.b + h + 1

        @block.sync
        def _(sp):
            def step(item):
                c = item(0)
                after(sp, values, c.b - 1)
                after(sp, c_summed, c.b - 1)
                sp.dma_start(cT[:, c.u, :, :], I["ctxT"][c.b]).then_inc(c_loaded[c.u], 16)
            skewed(sp, B, 0, step)

        @block.gpsimd
        def _(pool):
            def step(item):
                c = item(1)
                if c:
                    after(pool, scores, NH * (c.b - 1))
                    pool.tensor_tensor(qb[:, c.u, :, :, :], bc(QT[:, :, bass.ts(c.b, S)].unsqueeze(2), P, KT, HK, S),
                                       bc(headmask[:].unsqueeze(1).unsqueeze(3), P, KT, HK, S), ALU.mult).then_inc(qb_ready, 1)
            skewed(pool, B, 1, step)

        @block.tensor
        def _(pe):
            def step(item):
                d, c, o = item(1), item(2), item(3)

                def p_transposed(h):
                    pe.wait_ge(pr_ready, half(c, h))
                    for n in range(GH):
                        m = h * GH + n
                        for j in range(2):
                            mm = pe.transpose(banks[:, 2 * h, tok(2 * n + j)], pr[:, c.u, m, tok(j)], g.ident[:])
                    mm.then_inc(p_tr, 1)

                def scored(h):
                    after(pe, pT_ready, half(d, h) - NH)
                    for n in range(GH):
                        k, head = divmod((h * GH + n) * HG, HK)
                        mm = pe.matmul(banks[:, 2 * h + n, 0:CTX], lhsT=qb[:, d.u, k, head:head + HG, :], rhs=kT[:, d.u, k, :], start=True, stop=True)
                    mm.then_inc(scores, 1)

                def summed(h):
                    pe.wait_ge(pT_ready, half(c, h))
                    for n in range(GH):
                        m = h * GH + n
                        for j in range(2):
                            mm = pe.matmul(banks[:, O_BANK, m * GD:(m + 1) * GD], lhsT=pT[:, c.u, m, j, :], rhs=vv[:, c.u, j, m * GD:(m + 1) * GD],
                                           start=j == 0, stop=j == 1)
                    mm.then_inc(pv, 1)
                if d:
                    pe.wait_ge(c_loaded[d.u], 16 * (d.turn + 1))
                    after(pe, kT_ready, d.b)
                    for m in range(KT):
                        for k in range(2):
                            mm = pe.matmul(banks[:, K_BANK + m, 0:CTX], lhsT=wk[:, k, tok(m)], rhs=cT[:, d.u, k, :], start=k == 0, stop=k == 1)
                    mm.then_inc(keys, 1)
                if c:
                    p_transposed(0)
                if d:
                    after(pe, vv_ready, d.b)
                    for j in range(2):
                        for k in range(2):
                            mm = pe.matmul(banks[:, V_BANK, j * D:(j + 1) * D], lhsT=cT[:, d.u, k, tok(j)], rhs=wv[:, k, :], start=k == 0, stop=k == 1)
                    mm.then_inc(values, 1)
                if o:
                    pe.wait_ge(om_ready, half(o, NH - 1))
                    for h in range(NH):
                        mm = pe.matmul(banks[:, O_BANK, O_AT + h * S:O_AT + (h + 1) * S], lhsT=om[:, o.u, h * GH:(h + 1) * GH, :], rhs=sel[:],
                                       start=True, stop=True)
                    mm.then_inc(o_tr, 1)
                if c:
                    p_transposed(1)
                if d:
                    pe.wait_ge(kT_ready, d.b + 1)
                    pe.wait_ge(qb_ready, d.b + 1)
                    scored(0)
                if c:
                    pe.wait_ge(vv_ready, c.b + 1)
                    if o:
                        pe.wait_ge(oT_ready, o.b + 1)
                    summed(0)
                if d:
                    scored(1)
                if c:
                    summed(1)
            skewed(pe, B, 3, step)

        @block.scalar
        def _(act):
            def step(item):
                d, c, o = item(1), item(2), item(3)

                def p_moved(h):
                    ns = slice(h * GH, (h + 1) * GH)
                    act.wait_ge(p_tr, half(c, h))
                    act.activation(pT[:, c.u, ns, :, :], banks[:, 2 * h, :].rearrange("p (n j q) -> p n j q", n=GH, j=2), ACT.Copy).then_inc(pT_ready, 1)
                if c:
                    for h in range(NH):
                        act.wait_ge(sc_ready, half(c, h))
                        for n in range(h * GH, (h + 1) * GH):
                            ins = act.activation(pr[:, c.u, n, :], sc[:, c.u, n, :], ACT.Exp, bias=nm[:, c.u, n:n + 1], accum_out=rs[:, c.u, n:n + 1])
                        ins.then_inc(pr_ready, 1)
                if d:
                    act.wait_ge(keys, d.b + 1)
                    for m in range(KT):
                        ins = act.activation(kT[:, d.u, m, :], banks[:, K_BANK + m, 0:CTX], ACT.Identity, bias=vec[:, 1, m:m + 1])
                    ins.then_inc(kT_ready, 1)
                if c:
                    p_moved(0)
                if o:
                    act.wait_ge(o_tr, o.b + 1)
                    for h in range(NH):
                        ins = act.activation(OT[:, h, bass.ts(o.b, S)], banks[:, O_BANK, O_AT + h * S:O_AT + (h + 1) * S], ACT.Identity, bias=vec[:, 2, h:h + 1])
                    ins.then_inc(oT_ready, 1)
                if c:
                    p_moved(1)
                if d:
                    act.wait_ge(c_loaded[d.u], 16 * (d.turn + 1))
                    after(act, c_summed, d.b - 1)
                    for k in range(2):
                        ins = act.activation(scrap[:, d.u, k, :], cT[:, d.u, k, :], ACT.Copy, accum_out=csum[:, k, bass.ds(d.b, 1)])
                    ins.then_inc(c_summed, 1)
            skewed(act, B, 3, step)

        @block.vector
        def _(dve):
            link = Link(dve, dve_link)
            dve.wait_ge(vx_loaded, 32)

            def step(item):
                d, c = item(1), item(2)
                if d:
                    dve.wait_ge(values, d.b + 1)
                    dve.tensor_copy(vv[:, d.u, :, :], banks[:, V_BANK, :].rearrange("p (j d) -> p j d", j=2)).then_inc(vv_ready, 1)
                    for h in range(NH):
                        ns = slice(h * GH, (h + 1) * GH)
                        dve.wait_ge(scores, half(d, h))
                        link(dve.tensor_scalar(sc[:, d.u, ns, :], banks[:, 2 * h:2 * h + 2, 0:CTX], CLAMP, -CLAMP, ALU.min, ALU.max))
                        link(dve.tensor_reduce(mx[:, d.u, ns], sc[:, d.u, ns, :], AXX, ALU.max))
                        dve.tensor_scalar(nm[:, d.u, ns], mx[:, d.u, ns], -1.0, None, ALU.mult).then_inc(sc_ready, 1)
                if c:
                    dve.wait_ge(pr_ready, half(c, 1))
                    dve.tensor_copy(sums[:, c.b, :], rs[:, c.u, :])
                    link(dve.reciprocal(ri[:, c.u, :], rs[:, c.u, :]))
                    for h in range(NH):
                        ns = slice(h * GH, (h + 1) * GH)
                        dve.wait_ge(pv, half(c, NH - 1))
                        for n in range(GH):
                            m = h * GH + n
                            ins = dve.scalar_tensor_tensor(om[:, c.u, m, :], VX[:, c.b, m * GD:(m + 1) * GD], pr[:, c.u, m, 2 * P:CTX],
                                                           banks[:, O_BANK, m * GD:(m + 1) * GD], ALU.mult, ALU.add)
                        link(ins)
                        link(dve.tensor_tensor(om[:, c.u, ns, :], om[:, c.u, ns, :], bc(ri[:, c.u, ns].unsqueeze(2), P, GH, GD), ALU.mult))
                        dve.tensor_tensor(om[:, c.u, ns, :], om[:, c.u, ns, :], bc(blockmask[:].unsqueeze(1), P, GH, GD), ALU.mult).then_inc(om_ready, 1)
            skewed(dve, B, 2, step, link, 2 * NH + 1 + 2 * NH)


def guard(nc, g, banks, sums, csum, wv, vec, OT):
    with ExitStack() as ctx:
        s = Scope(nc, ctx, "s4g")
        nan, any_p, any_all = s.sb("nan", [P, B * 4]), s.sb("any_p", [P, 1]), s.sb("any_all", [P, 1])
        flag = s.sb("flag", [P, 1], U32)
        mean = s.sb("mean", [P, KT, B])
        full = s.sb("full", [P, KT, T])
        flags = s.sb("flags", [P, T], U32)
        dve_link, any_ready, all_ready, projected = s.sems("dve_link any_ready all_ready projected")
        block = ctx.enter_context(nc.Block())

        @block.gpsimd
        def _(pool):
            pool.wait_ge(any_ready, 1)
            pool.partition_all_reduce(any_all[:], any_p[:], P, bass.bass_isa.ReduceOp.max).then_inc(all_ready, 1)

        @block.tensor
        def _(pe):
            for m in range(KT):
                for k in range(2):
                    mm = pe.matmul(banks[:, m, 0:B], lhsT=wv[:, k, tok(m)], rhs=csum[:, k, :], start=k == 0, stop=k == 1)
            mm.then_inc(projected, 1)

        @block.vector
        def _(dve):
            link = Link(dve, dve_link)
            flat = sums[:].rearrange("p b n -> p (b n)")
            link(dve.tensor_tensor(nan[:], flat, flat, ALU.not_equal))
            dve.tensor_reduce(any_p[:], nan[:], AXX, ALU.max).then_inc(any_ready, 1)
            dve.wait_ge(projected, 1)
            for k in range(KT):
                ins = dve.tensor_scalar(mean[:, k, :], banks[:, k, 0:B], 1.0 / CTX, vec[:, 2, k:k + 1], ALU.mult, ALU.add)
            link(ins)
            link(dve.tensor_copy(full[:].rearrange("p k (b q) -> p (k b) q", q=S), bc(mean[:].rearrange("p k b -> p (k b)").unsqueeze(2), P, KT * B, S)))
            dve.wait_ge(all_ready, 1)
            link(dve.tensor_copy(flag[:], any_all[:]))
            link(dve.tensor_copy(flags[:], bc(flag[:], P, T)))
            for k in range(KT):
                ins = dve.copy_predicated(OT[:, k, :], flags[:], full[:, k, :])
            link(ins)


def phase5(nc, g):
    I, X = g.I, g.X
    DI, DS, R, TAPS = 512, 16, 64, 4
    DT = DI // P
    with ExitStack() as ctx:
        s = Scope(nc, ctx, "s5")
        sb = s.sb
        banks = s.psum()
        xi = sb("xi", [P, DT, T])
        vec = sb("vec", [P, DT, TAPS + 3])
        zd = nc.dram_tensor("s5_silu_z", [DT, P, T], F32, kind="Internal").ap()
        wx = sb("wx", [P, DT, R + 2 * DS])
        wdt = sb("wdt", [R, DI])
        wo = sb("wo", [P, DT, D])
        rate = sb("rate", [P, DT, DS])
        loaded = s.sem("loaded")
        with ExitStack() as actx:
            a = Scope(nc, actx, "s5a")
            n = Normed(a)
            xT = a.sb("xT", [P, KT, T])
            w = a.sb("w", [P, DT, KT, 2, P])
            normed_transposed(nc, g, a, banks, n, xT, ((w, "p5_win"), (vec, "p5_vec"), (wx, "p5_wx"), (wdt, "p5_wdt"), (wo, "p5_wo"), (rate, "p5_alog")), loaded)
            project_in(nc, g, banks, xT, xi, vec, w, zd, loaded)
        with ExitStack() as bctx:
            b = Scope(nc, bctx, "s5b")
            dt = b.sb("dt", [P, DT, T])
            bcs = b.sb("bcs", [P, T])
            state = b.sb("state", [P, DT, DS, B])
            skip = b.sb("skip", [P, DT, P])
            step_sizes(nc, g, banks, xi, dt, bcs, vec, wx, wdt, rate, state, skip)
            scan(nc, g, banks, xi, dt, bcs, rate, state, skip)
        project_out(nc, g, "s5o", banks, xi, wo, kt=DT, gate=zd)


def project_in(nc, g, banks, xT, xi, vec, w, zd, loaded):
    DT, TAPS = 4, 4
    NH = 2
    HB = NC // NH
    with ExitStack() as ctx:
        s = Scope(nc, ctx, "s5p")
        sb = s.sb
        conv = sb("conv", [P, U, NH, B // NH, S])
        sz = sb("sz", [P, U, T])
        z_stored = [s.sem(f"z_stored{u}") for u in range(U)]
        x_ready, z_ready, conv_ready, xi_ready, sz_ready, dve_link = s.sems("x_ready z_ready conv_ready xi_ready sz_ready dve_link")
        block = ctx.enter_context(nc.Block())

        @block.sync
        def _(sp):
            for d in range(DT):
                sp.wait_ge(sz_ready, d + 1)
                sp.dma_start(zd[d], sz[:, d % U, :]).then_inc(z_stored[d % U], 16)
            for q in z_stored:
                sp.wait_ge(q, 16 * (DT // U))

        @block.tensor
        def _(pe):
            pe.wait_ge(loaded, 96)
            for d in range(DT):
                after(pe, sz_ready, d)
                for n in range(NC):
                    for k in range(KT):
                        mm = pe.matmul(banks[:, NC + n, :], lhsT=w[:, d, k, 1, :], rhs=xT[:, k, n * C:(n + 1) * C], start=k == 0, stop=k == KT - 1)
                mm.then_inc(z_ready, 1)
                for n in range(NC):
                    after(pe, conv_ready, NH * (d - 1) + n // HB + 1)
                    for k in range(KT):
                        mm = pe.matmul(banks[:, n, :], lhsT=w[:, d, k, 0, :], rhs=xT[:, k, n * C:(n + 1) * C], start=k == 0, stop=k == KT - 1)
                    if n % HB == HB - 1:
                        mm.then_inc(x_ready, 1)

        @block.scalar
        def _(act):
            for d in range(DT):
                act.wait_ge(z_ready, d + 1)
                after(act, z_stored[d % U], 16 * (d // U))
                act.activation(sz[:, d % U, :], banks[:, NC:2 * NC, :].rearrange("p n c -> p (n c)"), ACT.Silu).then_inc(sz_ready, 1)
                act.wait_ge(conv_ready, NH * (d + 1))
                act.activation(xi[:, d, :], conv[:, d % U, :, :, :].rearrange("p h b t -> p (h b t)"), ACT.Silu).then_inc(xi_ready, 1)
            act.wait_ge(xi_ready, DT)

        @block.vector
        def _(dve):
            link = Link(dve, dve_link)
            dve.wait_ge(loaded, 96)
            for d in range(DT):
                after(dve, xi_ready, d - 1)
                for h in range(NH):
                    xb = banks[:, h * HB:(h + 1) * HB, :].rearrange("p n (b t) -> p (n b) t", t=S)
                    out = conv[:, d % U, h, :, :]
                    dve.wait_ge(x_ready, NH * d + h + 1)
                    link(dve.tensor_scalar(out, xb, vec[:, d, TAPS - 1:TAPS], vec[:, d, TAPS:TAPS + 1], ALU.mult, ALU.add))
                    for back in range(1, TAPS):
                        ins = dve.scalar_tensor_tensor(out[:, :, back:S], xb[:, :, 0:S - back], vec[:, d, TAPS - 1 - back:TAPS - back], out[:, :, back:S],
                                                       ALU.mult, ALU.add)
                        if back < TAPS - 1:
                            link(ins)
                    ins.then_inc(conv_ready, 1)


def step_sizes(nc, g, banks, xi, dt, bcs, vec, wx, wdt, rate, state, skip):
    DT, DS, R, TAPS = 4, 16, 64, 4
    RB = R + 2 * DS
    with ExitStack() as ctx:
        s = Scope(nc, ctx, "s5s")
        sb = s.sb
        dr = sb("dr", [R, U, C])
        mag, pos = sb("mag", [P, U, DT, C]), sb("pos", [P, NC, DT, C])
        zeroed, dbc, dr_ready, v_ready, pos_ready, abs_ready, ex_ready, ln_ready, dt_ready, rate_ready = s.sems(
            "zeroed dbc dr_ready v_ready pos_ready abs_ready ex_ready ln_ready dt_ready rate_ready")
        R_BANK, V_BANK = 0, 4
        block = ctx.enter_context(nc.Block())

        def of_chunk(c):
            return dt[:, :, c * C:(c + 1) * C]

        @block.gpsimd
        def _(pool):
            pool.memset(bcs[:], 0.0).then_inc(zeroed, 1)
            pool.memset(state[:], 0.0)

        @block.tensor
        def _(pe):
            for c in range(NC + 1):
                if c < NC:
                    after(pe, dr_ready, c - 1)
                    for k in range(DT):
                        mm = pe.matmul(banks[0:RB, R_BANK + c % U, :], lhsT=wx[:, k, :], rhs=xi[:, k, c * C:(c + 1) * C], start=k == 0, stop=k == DT - 1)
                    mm.then_inc(dbc, 1)
                if c:
                    pe.wait_ge(dr_ready, c)
                    after(pe, abs_ready, c - 1)
                    after(pe, pos_ready, c - 1)
                    for m in range(DT):
                        mm = pe.matmul(banks[:, V_BANK + m, :], lhsT=wdt[:, tok(m)], rhs=dr[:, (c - 1) % U, :], start=True, stop=True)
                    mm.then_inc(v_ready, 1)

        @block.scalar
        def _(act):
            act.activation(rate[:], rate[:], ACT.Exp).then_inc(rate_ready, 1)
            act.wait_ge(zeroed, 1)

            def ranks(c):
                act.wait_ge(dbc, c + 1)
                after(act, v_ready, c - 1)
                act.activation(bcs[R:RB, c * C:(c + 1) * C], banks[R:RB, R_BANK + c % U, :], ACT.Copy)
                act.activation(dr[:, c % U, :], banks[0:R, R_BANK + c % U, :], ACT.Copy).then_inc(dr_ready, 1)

            def logs(c):
                act.wait_ge(ex_ready, c + 1)
                act.activation(of_chunk(c), of_chunk(c), ACT.Ln, bias=1.0).then_inc(ln_ready, 1)
            ranks(0)
            for c in range(NC):
                if c + 1 < NC:
                    ranks(c + 1)
                else:
                    for early in range(c):
                        logs(early)
                act.wait_ge(pos_ready, c + 1)
                after(act, ex_ready, c - 1)
                for m in range(DT):
                    ins = act.activation(mag[:, c % U, m, :], banks[:, V_BANK + m, :], ACT.Abs, bias=vec[:, m, TAPS + 1:TAPS + 2])
                ins.then_inc(abs_ready, 1)
                act.wait_ge(abs_ready, c + 1)
                act.activation(of_chunk(c), mag[:, c % U, :, :], ACT.Exp, scale=-1.0).then_inc(ex_ready, 1)
            logs(NC - 1)

        @block.vector
        def _(dve):
            for k in range(DT):
                dve.tensor_scalar(skip[:, k, :], g.ident[:], vec[:, k, TAPS + 2:TAPS + 3], None, ALU.mult)
            dve.wait_ge(rate_ready, 1)
            dve.tensor_scalar(rate[:], rate[:], -1.0, None, ALU.mult)
            for c in range(NC):
                dve.wait_ge(v_ready, c + 1)
                for m in range(DT):
                    ins = dve.tensor_scalar(pos[:, c, m, :], banks[:, V_BANK + m, :], vec[:, m, TAPS + 1:TAPS + 2], 0.0, ALU.add, ALU.max)
                ins.then_inc(pos_ready, 1)
            for c in range(NC):
                dve.wait_ge(pos_ready, c + 1)
                dve.wait_ge(ln_ready, c + 1)
                dve.tensor_tensor(of_chunk(c), pos[:, c, :, :], of_chunk(c), ALU.add).then_inc(dt_ready, 1)
            dve.wait_ge(dt_ready, NC)


def scan(nc, g, banks, xi, dt, bcs, rate, state, skip):
    DT, DS, R = 4, 16, 64
    CLIP = 10.0
    KA = DT - 1
    with ExitStack() as ctx:
        s = Scope(nc, ctx, "s5c")
        sb = s.sb
        dt_t = sb("dt_t", [P, U, DT, B])
        dtx = sb("dtx", [P, U, DT, B])
        decay = sb("decay", [P, U, DT, DS, B])
        inp = sb("inp", [P, U, DT, DS, B])
        prod = sb("prod", [P, DT, DS, B])
        b_all = sb("b_all", [P, U, DS, B])
        (dt_ready, rise_ready, decay_ready, decay_used, dtx_ready, b_ready, b_read, inp_ready, inp_used, last_decayed, last_added,
         c_ready, prod_ready, y_ready, y_read, dve_link) = s.sems(
            "dt_ready rise_ready decay_ready decay_used dtx_ready b_ready b_read inp_ready inp_used last_decayed last_added "
            "c_ready prod_ready y_ready y_read dve_link")
        B_BANK, C_BANK, Y_BANK = 0, 2, 4

        def at(ap, t):
            return ap[:].rearrange("p k (b t) -> p k b t", t=S)[:, :, :, bass.ds(t, 1)].rearrange("p k b t -> p k (b t)")

        c_all = bc(banks[:, C_BANK:C_BANK + 2, :].rearrange("p n (m b) -> p (n m) b", b=B).unsqueeze(1), P, DT, DS, B)
        block = ctx.enter_context(nc.Block())

        @block.gpsimd
        def _(pool):
            def step(item):
                t, c = item(0), item(1)
                if c:
                    pool.wait_ge(last_decayed, c.b + 1)
                    pool.wait_ge(inp_ready, c.b + 1)
                    pool.tensor_tensor(state[:, KA, :, :], state[:, KA, :, :], inp[:, c.u, KA, :, :], ALU.add).then_inc(last_added, 1)
                if not t:
                    return
                pool.wait_ge(dt_ready, t.b + 1)
                after(pool, decay_used, t.b - 1)
                pool.tensor_tensor(decay[:, t.u, KA, :, :], bc(rate[:, KA, :].unsqueeze(2), P, DS, B), bc(dt_t[:, t.u, KA, :].unsqueeze(1), P, DS, B),
                                   ALU.mult).then_inc(rise_ready, 1)
                pool.tensor_tensor(dtx[:, t.u, :, :], dt_t[:, t.u, :, :], at(xi, t.b), ALU.mult).then_inc(dtx_ready, 1)
                pool.wait_ge(dtx_ready, t.b + 1)
                pool.wait_ge(b_read, t.b + 1)
                after(pool, inp_used, t.b - 1)
                after(pool, last_added, t.b - 1)
                pool.tensor_tensor(inp[:, t.u, :, :, :], bc(dtx[:, t.u, :, :].unsqueeze(2), P, DT, DS, B), bc(b_all[:, t.u, :, :].unsqueeze(1), P, DT, DS, B), ALU.mult).then_inc(inp_ready, 1)
            skewed(pool, S, 1, step)

        @block.scalar
        def _(act):
            def step(item):
                t = item(0)
                after(act, inp_ready, t.b - 1)
                act.activation(dt_t[:, t.u, :, :], at(dt, t.b), ACT.Copy).then_inc(dt_ready, 1)
                act.wait_ge(dt_ready, t.b + 1)
                after(act, decay_used, t.b - 1)
                for k in range(KA):
                    if k == 2:
                        act.wait_ge(b_ready, t.b + 1)
                        act.activation(b_all[:, t.u, :, :], banks[:, B_BANK:B_BANK + 2, :].rearrange("p n (m b) -> p (n m) b", b=B), ACT.Copy).then_inc(b_read, 1)
                    for n in range(DS):
                        act.activation(decay[:, t.u, k, n, :], dt_t[:, t.u, k, :], ACT.Exp, scale=rate[:, k, n:n + 1])
                act.wait_ge(rise_ready, t.b + 1)
                act.activation(decay[:, t.u, KA, :, :], decay[:, t.u, KA, :, :], ACT.Exp).then_inc(decay_ready, 1)
            skewed(act, S, 0, step)

        @block.tensor
        def _(pe):
            bt = bcs[:].rearrange("n (b t) -> n b t", t=S)

            def picked(t, j, bank):
                for n in range(DS):
                    mm = pe.matmul(banks[:, bank + n // 8, n % 8 * B:(n % 8 + 1) * B], lhsT=bc(g.ident[:, R + j * DS + n:R + j * DS + n + 1], P, P),
                                   rhs=bt[:, :, bass.ds(t.b, 1)].rearrange("n b t -> n (b t)"), start=True, stop=True)
                return mm

            def step(item):
                t, c, y = item(0), item(1), item(2)
                if t:
                    after(pe, b_read, t.b)
                    picked(t, 0, B_BANK).then_inc(b_ready, 1)
                if y:
                    after(pe, y_read, y.b - 1)
                    for k in range(DT):
                        pe.matmul(banks[:, Y_BANK + y.u, k * B:(k + 1) * B], lhsT=skip[:, k, :],
                                  rhs=xi[:, k, :].rearrange("p (b t) -> p b t", t=S)[:, :, bass.ds(y.b, 1)].rearrange("p b t -> p (b t)"),
                                  start=k == 0, stop=False)
                    pe.wait_ge(prod_ready, y.b + 1)
                    for n in range(DS):
                        mm = pe.matmul(banks[:, Y_BANK + y.u, 0:DT * B], lhsT=g.ident[:], rhs=prod[:, :, n, :], start=False, stop=n == DS - 1)
                    mm.then_inc(y_ready, 1)
                if c:
                    after(pe, prod_ready, c.b)
                    picked(c, 1, C_BANK).then_inc(c_ready, 1)
            skewed(pe, S, 2, step)

        @block.vector
        def _(dve):
            link = Link(dve, dve_link)
            floor = float(np.exp(-10.0))
            flat = state[:].rearrange("p k n b -> p (k n b)")

            def step(item):
                c, y = item(1), item(2)
                if c:
                    dve.wait_ge(decay_ready, c.b + 1)
                    after(dve, prod_ready, c.b)
                    for ks, ready in ((slice(KA, DT), last_decayed), (slice(0, KA), decay_used)):
                        part = state[:, ks, :, :].rearrange("p k n b -> p (k n b)")
                        dve.scalar_tensor_tensor(part, decay[:, c.u, ks, :, :].rearrange("p k n b -> p (k n b)"), floor, part,
                                                 ALU.max, ALU.mult).then_inc(ready, 1)
                    dve.wait_ge(decay_used, c.b + 1)
                    dve.wait_ge(inp_ready, c.b + 1)
                    dve.tensor_tensor(state[:, 0:KA, :, :], state[:, 0:KA, :, :], inp[:, c.u, 0:KA, :, :], ALU.add).then_inc(inp_used, 1)
                    dve.wait_ge(inp_used, c.b + 1)
                    dve.wait_ge(last_added, c.b + 1)
                    link(dve.tensor_scalar(flat, flat, -CLIP, CLIP, ALU.max, ALU.min))
                    dve.wait_ge(c_ready, c.b + 1)
                    after(dve, y_ready, c.b)
                    dve.tensor_tensor(prod[:], state[:], c_all, ALU.mult).then_inc(prod_ready, 1)
                if y:
                    dve.wait_ge(y_ready, y.b + 1)
                    dve.tensor_copy(at(xi, y.b), banks[:, Y_BANK + y.u, 0:DT * B].rearrange("p (k b) -> p k b", k=DT)).then_inc(y_read, 1)
            skewed(dve, S, 2, step, link, 1)


def phase6(nc, g):
    E, FF = 8, 1024
    LISTED = 2 * T // P + E - 1
    with ExitStack() as ctx:
        s = Scope(nc, ctx, "s6")
        banks = s.psum()
        w1, w2 = s.sb("w1", [P, E, KT, FF]), s.sb("w2", [P, E, FF // P, D])
        b1, b2 = s.sb("b1", [P, E, FF // P]), s.sb("b2", [1, E, D])
        w_loaded = s.sem("w_loaded")
        slots = s.sb("slots", [P, 2, NT], U32)
        gates = s.sb("gates", [P, 2, NT])
        listed = s.sb("listed", [P, LISTED], U32)
        owner = s.sb("owner", [1, LISTED], U32)
        rows = nc.dram_tensor("s6_rows", [T, D], F32, kind="Internal").ap()
        results = nc.dram_tensor("s6_results", [LISTED * P, D], F32, kind="Internal").ap()
        route(nc, g, banks, dict(E=E, LISTED=LISTED, w1=w1, w2=w2, b1=b1, b2=b2, w_loaded=w_loaded, slots=slots, gates=gates, listed=listed,
                                 owner=owner, rows=rows))
        experts(nc, g, banks, dict(LISTED=LISTED, FF=FF, w1=w1, w2=w2, b1=b1, b2=b2, w_loaded=w_loaded, listed=listed, owner=owner,
                                   rows=rows, results=results))
        combine(nc, g, slots, gates, results)


def route(nc, g, banks, v):
    I, X = g.I, g.X
    E, LISTED = v["E"], v["LISTED"]
    slots, gates, listed, owner, rows = (v[n] for n in "slots gates listed owner rows".split())
    SHIFT = P.bit_length() - 1
    with ExitStack() as ctx:
        s = Scope(nc, ctx, "s6r")
        sb = s.sb
        n = Normed(s)
        xn = sb("xn", [P, NT, D])
        xT = sb("xT", [P, U, KT, P])
        rw, rb = sb("rw", [P, KT, E]), sb("rb", [P, E])
        count, below = sb("count", [P, E]), sb("below", [P, E, E])
        earlier = sb("earlier", [P, P])
        tile_before = sb("tile_before", [P, P + E])
        tile_no, row_no, token = sb("tile_no", [P, LISTED]), sb("row_no", [P, P]), sb("token", [P, NT])
        row_is = sb("row_is", [P, 2, NT, P])
        tile_is = sb("tile_is", [P, 2, NT, LISTED])
        ones = sb("ones", [P, 1])
        lg = sb("lg", [P, NT, E])
        best, best_at = sb("best", [P, NT, E]), sb("best_at", [P, NT, E], U32)
        at = sb("at", [P, 2, NT])
        diff, ex = sb("diff", [P, NT]), sb("ex", [P, NT])
        hit = sb("hit", [P, 2, E, NT])
        mask = sb("mask", [P, E, NT])
        counts = sb("counts", [P, P])
        size, sizeu, tiles = sb("size", [P, E]), sb("sizeu", [P, E], U32), sb("tiles", [P, E])
        upto, start = sb("upto", [P, E, E]), sb("start", [P, E])
        place = sb("place", [P, E, NT])
        picked, slotf = sb("picked", [P, 2, E, NT]), sb("slotf", [P, 2, NT])
        row_of, tile_of = sb("row_of", [P, 2, NT], U32), sb("tile_of", [P, 2, NT], U32)
        row_f, tile_f = sb("row_f", [P, 2, NT]), sb("tile_f", [P, 2, NT])
        begun, owned = sb("begun", [P, LISTED, E]), sb("owned", [P, LISTED])
        NCONST = 7
        NG = 4
        (loaded, router_loaded, set_up, stat_ready, rstd_ready, dve_link, xn_ready, xn_stored, x_tr, xT_ready, logits, diff_ready, ex_ready, mask_ready,
         counted, counts_ready, ranked, marked, list_made) = s.sems(
            "loaded router_loaded set_up stat_ready rstd_ready dve_link xn_ready xn_stored x_tr xT_ready logits diff_ready ex_ready mask_ready "
            "counted counts_ready ranked marked list_made")
        block = ctx.enter_context(nc.Block())

        @block.sync
        def _(sp):
            def weights(e):
                sp.dma_start(v["w1"][:, e, :, :], I["p6_w1"][e]).then_inc(v["w_loaded"], 16)
                sp.dma_start(v["w2"][:, e, :, :], I["p6_w2"][e]).then_inc(v["w_loaded"], 16)
            for dst, src in ((rw, "p6_rw"), (rb, "p6_rb")):
                sp.dma_start(dst[:], I[src]).then_inc(router_loaded, 16)
            weights(0)
            for dst, src in ((count, "count8"), (below, "below8"), (earlier, "earlier"), (tile_before, "tile_before"),
                             (tile_no, "tile_no"), (row_no, "row_no"), (token, "token")):
                sp.dma_start(dst[:], I[src]).then_inc(loaded, 16)
            sp.dma_start(v["b1"][:], I["p6_b1"]).then_inc(v["w_loaded"], 16)
            sp.dma_start(v["b2"][:], I["p6_b2"]).then_inc(v["w_loaded"], 16)
            for e in range(1, E):
                if e == 3:
                    for i in range(NT // NG):
                        sp.wait_ge(xn_ready, i + 1)
                        sp.dma_start(rows.rearrange("(t p) d -> p t d", p=P)[:, i * NG:(i + 1) * NG, :], xn[:, i * NG:(i + 1) * NG, :]).then_inc(xn_stored, 16)
                weights(e)
            sp.wait_ge(xn_stored, 16 * (NT // NG))

        @block.gpsimd
        def _(pool):
            pool.memset(ones[:], 1.0)
            pool.memset(n.half[:], -0.5).then_inc(set_up, 1)
            pool.wait_ge(set_up, 1)
            pool.wait_ge(stat_ready, 1)
            pool.tensor_tensor(n.rstd[:], n.var[:], bc(n.half[:], P, NT), ALU.pow).then_inc(rstd_ready, 1)

        @block.tensor
        def _(pe):
            pe.wait_ge(router_loaded, 32)
            for t in range(NT + 1):
                if t < NT:
                    pe.wait_ge(xn_ready, t // NG + 1)
                    after(pe, xT_ready, t - 1)
                    for k in range(KT):
                        mm = pe.transpose(banks[:, t % U, tok(k)], xn[:, t, tok(k)], g.ident[:])
                    mm.then_inc(x_tr, 1)
                if t:
                    pe.wait_ge(xT_ready, t)
                    for k in range(KT):
                        mm = pe.matmul(banks[:, 2, (t - 1) * E:t * E], lhsT=xT[:, (t - 1) % U, k, :], rhs=rw[:, k, :], start=k == 0, stop=k == KT - 1)
                    mm.then_inc(logits, 1)
            pe.wait_ge(loaded, 16 * NCONST)
            pe.wait_ge(mask_ready, 1)
            flat = mask[:].rearrange("p e t -> p (e t)")
            pe.matmul(banks[:, 3, 0:1], lhsT=flat, rhs=ones[:], start=True, stop=True).then_inc(counted, 1)
            pe.matmul(banks[:, 4, 0:P], lhsT=earlier[:], rhs=flat, start=True, stop=False)
            pe.wait_ge(counts_ready, 1)
            pe.matmul(banks[:, 4, 0:P], lhsT=counts[:], rhs=tile_before[:, 0:P], start=False, stop=True)
            pe.matmul(banks[:, 5, 0:E], lhsT=counts[:], rhs=tile_before[:, P:P + E], start=True, stop=True).then_inc(ranked, 1)
            for t in range(NT):
                pe.wait_ge(marked, t // NG + 1)
                for j in range(2):
                    mm = pe.matmul(banks[:, 6, 0:LISTED], lhsT=row_is[:, j, t, :], rhs=tile_is[:, j, t, :],
                                   start=t == 0 and j == 0, stop=t == NT - 1 and j == 1)
            mm.then_inc(list_made, 1)

        @block.scalar
        def _(act):
            for t in range(NT):
                act.wait_ge(x_tr, t + 1)
                after(act, logits, t - 1)
                act.activation(xT[:, t % U, :, :], banks[:, t % U, 0:D].rearrange("p (k q) -> p k q", k=KT), ACT.Copy).then_inc(xT_ready, 1)
            act.wait_ge(diff_ready, 1)
            act.activation(ex[:], diff[:], ACT.Exp).then_inc(ex_ready, 1)

        @block.vector
        def _(dve):
            link = Link(dve, dve_link)
            row_stats(dve, link, g.stats, n.mv, n.var, LN_EPS).then_inc(stat_ready, 1)
            dve.wait_ge(rstd_ready, 1)
            for t in range(NT):
                ins = n.apply(dve, xn[:, t, :], X, t)
                if t % NG == NG - 1:
                    ins.then_inc(xn_ready, 1)
            dve.wait_ge(router_loaded, 32)
            dve.wait_ge(logits, NT)
            link(dve.tensor_tensor(lg[:], banks[:, 2, 0:NT * E].rearrange("p (t e) -> p t e", e=E), bc(rb[:].unsqueeze(1), P, NT, E), ALU.add))
            for t in range(NT):
                ins = dve.max(best[:, t, :], lg[:, t, :])
            link(ins)
            dve.tensor_tensor(diff[:], best[:, :, 1], best[:, :, 0], ALU.subtract).then_inc(diff_ready, 1)
            for t in range(NT):
                ins = dve.max_index(best_at[:, t, :], best[:, t, :], lg[:, t, :])
            link(ins)
            link(dve.tensor_copy(at[:], best_at[:, :, 0:2].rearrange("p t n -> p n t")))
            dve.wait_ge(loaded, 16 * NCONST)
            for j in range(2):
                ins = dve.tensor_tensor(hit[:, j, :, :], bc(count[:].unsqueeze(2), P, E, NT), bc(at[:, j, :].unsqueeze(1), P, E, NT), ALU.is_equal)
            link(ins)
            dve.tensor_tensor(mask[:], hit[:, 0, :, :], hit[:, 1, :, :], ALU.add).then_inc(mask_ready, 1)
            dve.wait_ge(counted, 1)
            dve.tensor_copy(counts[:], bc(banks[:, 3, 0:1], P, P)).then_inc(counts_ready, 1)
            dve.wait_ge(ex_ready, 1)
            link(dve.tensor_scalar(diff[:], ex[:], 1.0, None, ALU.add))
            link(dve.reciprocal(gates[:, 0, :], diff[:]))
            dve.tensor_tensor(gates[:, 1, :], gates[:, 0, :], ex[:], ALU.mult)
            dve.wait_ge(ranked, 1)
            link(dve.tensor_scalar(size[:], banks[:, 5, 0:E], float(P - 1), None, ALU.add))
            link(dve.tensor_copy(sizeu[:], size[:]))
            link(dve.tensor_scalar(sizeu[:], sizeu[:], SHIFT, None, ALU.logical_shift_right))
            link(dve.tensor_copy(tiles[:], sizeu[:]))
            link(dve.tensor_tensor(upto[:], bc(tiles[:].unsqueeze(1), P, E, E), below[:], ALU.mult))
            link(dve.tensor_reduce(start[:], upto[:], AXX, ALU.add))
            link(dve.scalar_tensor_tensor(place[:], bc(start[:].unsqueeze(2), P, E, NT), float(P), banks[:, 4, 0:P].rearrange("p (e t) -> p e t", e=E),
                                          ALU.mult, ALU.add))
            for j in range(2):
                ins = dve.tensor_tensor(picked[:, j, :, :], hit[:, j, :, :], place[:], ALU.mult)
            link(ins)
            link(dve.tensor_reduce(slotf[:], picked[:].rearrange("p j e t -> p j t e"), AXX, ALU.add))
            link(dve.tensor_copy(slots[:], slotf[:]))
            dve.tensor_scalar(row_of[:], slots[:], P - 1, None, ALU.bitwise_and)
            link(dve.tensor_scalar(tile_of[:], slots[:], SHIFT, None, ALU.logical_shift_right))
            dve.tensor_copy(row_f[:], row_of[:])
            link(dve.tensor_copy(tile_f[:], tile_of[:]))
            link(dve.tensor_tensor(tile_is[:], bc(tile_no[:].unsqueeze(1).unsqueeze(1), P, 2, NT, LISTED), bc(tile_f[:].unsqueeze(3), P, 2, NT, LISTED), ALU.is_equal))
            dve.tensor_tensor(tile_is[:], tile_is[:], bc(token[:].unsqueeze(1).unsqueeze(3), P, 2, NT, LISTED), ALU.mult)
            for i in range(NT // NG):
                ts = slice(i * NG, (i + 1) * NG)
                dve.tensor_tensor(row_is[:, :, ts, :], bc(row_no[:].unsqueeze(1).unsqueeze(1), P, 2, NG, P), bc(row_f[:, :, ts].unsqueeze(3), P, 2, NG, P),
                                  ALU.is_equal).then_inc(marked, 1)
            link(dve.tensor_tensor(begun[:], bc(tile_no[:].unsqueeze(2), P, LISTED, E), bc(start[:].unsqueeze(1), P, LISTED, E), ALU.is_ge))
            link(dve.tensor_reduce(owned[:], begun[:], AXX, ALU.add))
            link(dve.tensor_scalar(owned[:], owned[:], -1.0, None, ALU.add))
            link(dve.tensor_copy(owner[:], owned[0:1, :]))
            dve.wait_ge(list_made, 1)
            dve.tensor_copy(listed[:], banks[:, 6, 0:LISTED])


def experts(nc, g, banks, v):
    LISTED, FF = v["LISTED"], v["FF"]
    FT = FF // P
    w1, w2, b1, b2, w_loaded, listed, owner, rows, results = (v[n] for n in "w1 w2 b1 b2 w_loaded listed owner rows results".split())
    E = 8
    with ExitStack() as ctx:
        s = Scope(nc, ctx, "s6e")
        sb = s.sb
        idx = sb("idx", [P, U, 1], U32)
        one, row1 = sb("one", [P, 2]), sb("row1", [1, P])
        xg = sb("xg", [P, U, D])
        xT = sb("xT", [P, U, KT, P])
        w = sb("w", [P, U, KT, FF])
        hT = sb("hT", [P, U, FT, P])
        y = sb("y", [P, U, D])
        gathered = [s.sem(f"gathered{u}") for u in range(U)]
        stored = [s.sem(f"stored{u}") for u in range(U)]
        set_up, carried, idx_ready, w_ready, x_tr, xT_ready, hidden, hT_ready, product, y_ready = s.sems(
            "set_up carried idx_ready w_ready x_tr xT_ready hidden hT_ready product y_ready")
        X_BANK, H_BANK, Y_BANK = 0, 1, 5
        WEIGHTS = 16 * (2 + 2 * E)
        block = ctx.enter_context(nc.Block())

        def expert(engine, t):
            return nc.values_load(owner[0:1, bass.ds(t.b, 1)], engines=[engine], min_val=0, max_val=E - 1,
                                  skip_runtime_bounds_check_because="a count of the eight experts, less one for the first, which always starts at 0")

        @block.sync
        def _(sp):
            def step(item):
                t = item(0)
                sp.wait_ge(y_ready, t.b + 1)
                sp.dma_start(results[bass.ts(t.b, P), :], y[:, t.u, :]).then_inc(stored[t.u], 16)
            skewed(sp, LISTED, 0, step)
            for u, q in enumerate(stored):
                sp.wait_ge(q, 16 * ((LISTED + U - 1 - u) // U))

        @block.gpsimd
        def _(pool):
            pool.memset(row1[:], 1.0).then_inc(set_up, 1)
            pool.memset(one[:], 1.0).then_inc(carried, 1)

            def step(item):
                t = item(0)
                pool.wait_ge(idx_ready, t.b + 1)
                after(pool, x_tr, t.b - 1)
                pool.wait_ge(carried, t.b + 1)
                pool.tensor_tensor(one[:, 1:2], one[:, 0:1], one[:, 0:1], ALU.mult).then_inc(carried, 1)
                pool.indirect_dma_start(xg[:, t.u, :], None, rows, bass.IndirectOffsetOnAxis(idx[:, t.u, :], 0)).then_inc(gathered[t.u], 16)
            skewed(pool, LISTED, 0, step)

        @block.tensor
        def _(pe):
            pe.wait_ge(set_up, 1)

            def step(item):
                x, m, o = item(1), item(2), item(3)
                if m:
                    pe.wait_ge(xT_ready, m.b + 1)
                    pe.wait_ge(w_ready, m.b + 1)
                    after(pe, hT_ready, FT * (m.b - 1))
                    for f in range(FT):
                        for k in range(KT):
                            mm = pe.matmul(banks[:, H_BANK + 2 * m.u + f // 4, tok(f % 4)], lhsT=w[:, m.u, k, tok(f)], rhs=xT[:, m.u, k, :],
                                           start=k == 0, stop=k == KT - 1)
                    mm.then_inc(hidden, 1)
                if x:
                    pe.wait_ge(gathered[x.u], 16 * (x.turn + 1))
                    after(pe, xT_ready, x.b)
                    for k in range(KT):
                        mm = pe.transpose(banks[:, X_BANK, tok(k)], xg[:, x.u, tok(k)], g.ident[:])
                    mm.then_inc(x_tr, 1)
                if o:
                    e = expert(mybir.EngineType.PE, o)
                    pe.wait_ge(hT_ready, FT * (o.b + 1))
                    after(pe, y_ready, o.b)
                    for f in range(FT):
                        pe.matmul(banks[:, Y_BANK, 0:D], lhsT=hT[:, o.u, f, :], rhs=w2[:, bass.ds(e, 1), f, :], start=f == 0, stop=False)
                    pe.matmul(banks[:, Y_BANK, 0:D], lhsT=row1[:], rhs=b2[:, bass.ds(e, 1), :], start=False, stop=True).then_inc(product, 1)
            skewed(pe, LISTED, 3, step)

        @block.scalar
        def _(act):
            def step(item):
                x, m = item(1), item(2)
                if m:
                    e = expert(mybir.EngineType.Activation, m)
                    act.wait_ge(hidden, m.b + 1)
                    after(act, product, m.b - 1)
                    for f in range(FT):
                        act.activation(hT[:, m.u, f, :], banks[:, H_BANK + 2 * m.u + f // 4, tok(f % 4)], ACT.Relu,
                                       bias=b1[:, bass.ds(e, 1), f]).then_inc(hT_ready, 1)
                if x:
                    act.wait_ge(x_tr, x.b + 1)
                    act.activation(xT[:, x.u, :, :], banks[:, X_BANK, 0:D].rearrange("p (k q) -> p k q", k=KT), ACT.Copy).then_inc(xT_ready, 1)
            skewed(act, LISTED, 3, step)

        @block.vector
        def _(dve):
            def step(item):
                n, x, o = item(0), item(1), item(3)
                if n:
                    after(dve, x_tr, n.b - 1)
                    dve.tensor_copy(idx[:, n.u, :], listed[:, bass.ds(n.b, 1)]).then_inc(idx_ready, 1)
                if x:
                    e = expert(mybir.EngineType.DVE, x)
                    dve.wait_ge(w_loaded, WEIGHTS)
                    after(dve, hidden, x.b - 1)
                    dve.tensor_copy(w[:, x.u, :, :], w1[:, bass.ds(e, 1), :, :].rearrange("p e k f -> p (e k) f")).then_inc(w_ready, 1)
                if o:
                    dve.wait_ge(product, o.b + 1)
                    after(dve, stored[o.u], 16 * o.turn)
                    dve.tensor_copy(y[:, o.u, :], banks[:, Y_BANK, 0:D]).then_inc(y_ready, 1)
            skewed(dve, LISTED, 3, step)


def combine(nc, g, slots, gates, results):
    X = g.X
    NG = 4
    with ExitStack() as ctx:
        s = Scope(nc, ctx, "s6c")
        got = s.sb("got", [P, NT, 2, D])
        gathered = [s.sem(f"gathered{t}") for t in range(NT)]
        dve_link, added, stored = s.sems("dve_link added stored")
        block = ctx.enter_context(nc.Block())

        @block.gpsimd
        def _(pool):
            for t in range(NT):
                for j in range(2):
                    pool.indirect_dma_start(got[:, t, j, :], None, results, bass.IndirectOffsetOnAxis(slots[:, j, t:t + 1], 0)).then_inc(gathered[t], 16)

        @block.vector
        def _(dve):
            link = Link(dve, dve_link)
            for t in range(NT):
                dve.wait_ge(gathered[t], 32)
                for j in range(2):
                    ins = dve.scalar_tensor_tensor(X[:, t, :], got[:, t, j, :], gates[:, j, t:t + 1], X[:, t, :], ALU.mult, ALU.add)
                    if not j:
                        link(ins)
                ins.then_inc(added, 1)

        @block.sync
        def _(sp):
            to = g.out.rearrange("(t p) d -> p t d", p=P)
            for i in range(NT // NG):
                ts = slice(i * NG, (i + 1) * NG)
                sp.wait_ge(added, (i + 1) * NG)
                sp.dma_start(to[:, ts, :], X[:, ts, :]).then_inc(stored, 16)
            sp.wait_ge(stored, 16 * (NT // NG))


class Env:

    def __init__(self, inputs, x, ident, stats, x_loaded, out):
        self.I, self.X, self.ident, self.stats, self.x_loaded, self.out = inputs, x, ident, stats, x_loaded, out


def layers(nc, out, inputs):
    with ExitStack() as ctx:
        s = Scope(nc, ctx, "x")
        x_loaded = [s.sem(f"x_loaded{i}") for i in range(4)]
        g = Env(inputs, s.sb("rows", [P, NT, D]), s.sb("ident", [P, P]), s.sb("stats", [P, NT, 6]), x_loaded, out)
        loaded = s.sem("loaded")
        with nc.Block() as block:
            @block.sync
            def _(sp):
                sp.dma_start(g.ident[:], inputs["ident"]).then_inc(loaded, 16)
                for i, q in enumerate(x_loaded):
                    ts = slice(i * NT // 4, (i + 1) * NT // 4)
                    sp.dma_start(g.X[:, ts, :], inputs["x"][:, ts, :]).then_inc(q, 16)
                sp.wait_ge(loaded, 16)
        for phase in (phase1, phase2, phase3, phase4, phase5, phase6):
            before = nc.snapshot_sems()
            phase(nc, g)
            nc.clear_and_free_semaphores(nc.allocated_since(before))
            nc.all_engine_barrier()


def layout(a):
    import numpy as np
    c = np.ascontiguousarray
    P, H1, HD1 = 128, 4, 64
    kp = lambda w, p=P: c(w.reshape(w.shape[0] // p, p, -1).transpose(1, 0, 2))
    col = lambda v, p=P: v.reshape(-1, p).T
    r = {}
    r["x"] = c(a["x"].reshape(16, P, 256).transpose(1, 0, 2))
    r["ctx_768"] = c(a["ctx_768"])
    r["mask_BxS2_bk0"] = c(a["mask_BxS2_bk0"])
    r["ident"] = np.eye(P, dtype=np.float32)
    ch, row = np.arange(256), np.arange(P)
    r["headmask4"] = c((ch[:, None] // HD1 == np.arange(H1)).astype(np.float32).reshape(2, P, H1).transpose(1, 0, 2))
    r["blockmask4"] = (row[:, None] // 32 == ch // HD1).astype(np.float32)
    r["sel"] = (row[:, None] % 32 == np.arange(32)).astype(np.float32)
    p = "L0_xattn_"
    two = lambda v: np.concatenate([v, v])
    r["p1_vec"] = c(np.stack([col(a[p + "ln_l_g"]), col(a[p + "ln_l_b"]), col(np.tile(a[p + "qn_g"], 4)),
                              col(np.tile(a[p + "kn_g"], 4))], axis=1))
    r["p1_bo"], r["p4_bo"] = np.tile(a[p + "bo"], (P, 1)), np.tile(a["L1_xattn_bo"], (P, 1))
    r["p1_cvec"] = c(np.stack([col(a[p + "ln_x_g"], 96), col(a[p + "ln_x_b"], 96)], axis=1))
    r["p1_wq"], r["p1_wlkv"], r["p1_wo"] = (kp(a[p + n].T) for n in ("Wq", "Wlkv", "Wo"))
    r["p1_wkv"] = kp(a[p + "Wkv"].T, 96)
    r["p2_w"] = kp(np.concatenate([a["L0_attn_Wq"], *(a["L0_attn_Wkv"].reshape(256, 16, 80)[:, :, lo:hi].reshape(256, -1)
                                                     for lo, hi in ((0, 16), (16, 80)))], axis=1))
    r["p2_wo"] = kp(a["L0_attn_Wout"])
    r["headmask8"] = (row[:, None] // 16 == np.arange(8)).astype(np.float32)
    r["batchmask"] = (row[:, None] // 32 == row // 32).astype(np.float32)
    p = "L0_ffn_"
    r["p3_wq"], r["p3_wqT"] = kp(a[p + "w_q"]), kp(c(a[p + "w_q"].T))
    r["p3_gb"] = c(np.stack([col(a[p + "bn_gamma"]), col(a[p + "bn_beta"])], axis=1))
    r["p3_keys"] = c(a[p + "keys"].transpose(3, 2, 0, 1).reshape(P, 16, 64))
    r["p3_table"] = np.concatenate([a[p + "down_embed"], a[p + "up_embed"]], axis=1)
    r["count8"] = np.tile(np.arange(8, dtype=np.float32), (P, 1))
    p = "L1_xattn_"
    r["p4_vec"] = c(np.stack([col(a[p + n]) for n in ("bq", "bk", "bv")], axis=1))
    r["p4_wq"], r["p4_wo"] = kp(a[p + "Wq"]), kp(a[p + "Wo"])
    r["p4_wk"], r["p4_wv"] = kp(a[p + "Wk"], 96), kp(a[p + "Wv"], 96)
    r["ctxT"] = c(a["ctx_768"].transpose(0, 2, 1).reshape(64, 2, 96, 257).transpose(0, 2, 1, 3))
    r["p4_lastT"] = c(a["ctx_768"][:, 256, :].T.reshape(2, 96, 64).transpose(1, 0, 2))
    r["blockmask16"] = (row[:, None] // 32 == np.arange(64) // 16).astype(np.float32)
    p = "L1_attn_"
    r["p5_vec"] = c(np.stack([col(v) for v in (*a[p + "W_conv"], a[p + "b_conv"], a[p + "b_dt"], a[p + "D"])], axis=2))
    r["p5_win"] = c(a[p + "W_in"].reshape(2, P, 2, 4, P).transpose(1, 3, 0, 2, 4))
    r["p5_wo"], r["p5_wx"], r["p5_wdt"] = kp(a[p + "W_out"]), kp(a[p + "W_xproj"]), c(a[p + "W_dt"])
    r["p5_alog"] = kp(a[p + "A_log"])
    r["p6_rw"], r["p6_rb"] = kp(a["L1_ffn_router_w"]), np.tile(a["L1_ffn_router_b"], (P, 1))
    r["p6_b2"] = c(a["L1_ffn_b2"].reshape(1, 8, 256))
    r["below8"] = np.tile(np.tril(np.ones((8, 8), np.float32), -1), (P, 1, 1))
    r["earlier"] = np.triu(np.ones((P, P), np.float32), 1)
    same, before = row[:, None] // 16 == row // 16, row[:, None] % 16 < row % 16
    r["tile_before"] = np.concatenate([same & before, row[:, None] // 16 == np.arange(8)], axis=1).astype(np.float32)
    r["tile_no"] = np.tile(np.arange(39, dtype=np.float32), (P, 1))
    r["row_no"] = np.tile(np.arange(P, dtype=np.float32), (P, 1))
    r["token"] = c(np.arange(2048, dtype=np.float32).reshape(16, P).T)
    r["p6_w1"] = c(a["L1_ffn_W1"].reshape(8, 2, P, 1024).transpose(0, 2, 1, 3))
    r["p6_w2"] = c(a["L1_ffn_W2"].reshape(8, 8, P, 256).transpose(0, 2, 1, 3))
    r["p6_b1"] = c(a["L1_ffn_b1"].reshape(8, 8, P).transpose(2, 0, 1))
    return r


def kernel(**inputs):
    import numpy as _np
    import concourse.bacc as _bacc
    from concourse import mybir as _mybir
    from concourse.bass_utils import run_bass_kernel_spmd as _run

    nc = _bacc.Bacc("TRN2", target_bir_lowering=False, num_devices=1)
    arrays = layout({name: _np.asarray(a) for name, a in inputs.items()})
    aps = {name: nc.dram_tensor(name, a.shape, _mybir.dt.from_np(a.dtype), kind="ExternalInput").ap() for name, a in arrays.items()}
    out = nc.dram_tensor("out", (T, D), _mybir.dt.float32, kind="ExternalOutput").ap()
    layers(nc, out, aps)
    r = _run(nc, [arrays], core_ids=[0])
    return _np.asarray(r.results[0]["out"]).reshape(B, S, D)
```
